# Optimizing a Trainium2 kernel written in Bass

```python
import numpy as np
import jax
import jax.numpy as jnp

def _softmax(x, axis=-1):
    return jax.nn.softmax(x, axis=axis)

def _gelu(x):
    return jax.nn.gelu(x, approximate=True)

def _silu(x):
    return jax.nn.silu(x)

def _sigmoid(x):
    return jax.nn.sigmoid(x)

def _layernorm(x, axis=-1, eps=1e-05):
    m = jnp.mean(x, axis=axis, keepdims=True)
    v = jnp.var(x, axis=axis, keepdims=True)
    return (x - m) / jnp.sqrt(v + eps)

def _scatter_add(tgt, idx, src, axis=0):
    return tgt.at[idx].add(src)

def _segment_sum(src, seg, n):
    return jax.ops.segment_sum(src, seg, n)
kernel_name = 'mk_recurrent_d4_jaxref_r4_345885'

def setup_inputs(seed: int=0):
    np.random.seed(seed)
    _w = jnp.asarray

    def _L0_attn_setup():
        import jax, jax.numpy as jnp
        import numpy as np
        D_MODEL = 256
        D_STATE = 16
        D_CONV = 4
        EXPAND = 2
        D_INNER = D_MODEL * EXPAND
        BATCH = 4
        SEQ_LEN = 1024

        def _silu(v):
            return v * jax.nn.sigmoid(v)
        key = jax.random.key(seed)
        ks = jax.random.split(key, 6)

        def rn(k, shape, scale):
            return jax.random.normal(k, shape, dtype=jnp.float32) * scale
        x = rn(ks[0], (BATCH, SEQ_LEN, D_MODEL), 1.0)
        in_proj_w = rn(ks[1], (2 * D_INNER, D_MODEL), D_MODEL ** (-0.5))
        conv_w = rn(ks[2], (D_INNER, 1, D_CONV), D_CONV ** (-0.5))
        conv_b = rn(ks[3], (D_INNER,), 0.02)
        x_proj_w = rn(ks[4], (2 * D_STATE + 1, D_INNER), D_INNER ** (-0.5))
        A_log = jnp.log(jnp.arange(1, D_STATE + 1, dtype=jnp.float32))
        D = jnp.ones((D_INNER,), jnp.float32)
        out_proj_w = rn(ks[5], (D_MODEL, D_INNER), D_INNER ** (-0.5))
        return dict(x=x, in_proj_w=in_proj_w, conv_w=conv_w, conv_b=conv_b, x_proj_w=x_proj_w, A_log=A_log, D=D, out_proj_w=out_proj_w)
    _L0_attn_in = _L0_attn_setup()

    def _L0_ffn_setup():
        import jax, jax.numpy as jnp
        import numpy as np
        B, S, D, E, H, K = (64, 512, 256, 32, 1024, 8)
        key = jax.random.key(seed)
        k0, k1, k2, k3 = jax.random.split(key, 4)
        x = jax.random.normal(k0, (B, S, D), jnp.float32)
        gate_w = jax.random.normal(k1, (E, D), jnp.float32) * (1.0 / np.sqrt(D))
        gate_b = jnp.zeros((E,), jnp.float32)
        w1 = jax.random.normal(k2, (E, D + 1, H), jnp.float32) * (1.0 / np.sqrt(D + 1))
        w2 = jax.random.normal(k3, (E, H + 1, D), jnp.float32) * (1.0 / np.sqrt(H + 1))
        return {'x': x, 'gate_w': gate_w, 'gate_b': gate_b, 'w1': w1, 'w2': w2}
    _L0_ffn_in = _L0_ffn_setup()

    def _L1_attn_setup():
        import jax, jax.numpy as jnp
        import numpy as np
        DIM = 256
        H = 16
        HD = DIM // H // 2
        LAMBDA_INIT = 0.8 - 0.6 * float(np.exp(-0.3 * 0))
        EPS = 1e-05

        def _rms_norm(x, w, eps):
            return x * jax.lax.rsqrt(jnp.mean(jnp.square(x), axis=-1, keepdims=True) + eps) * w
        key = jax.random.key(seed)
        ks = jax.random.split(key, 9)
        B, N = (4, 1024)
        return {'x': jax.random.normal(ks[0], (B, N, DIM), jnp.float32), 'w_qkv': jax.random.normal(ks[1], (3 * DIM, DIM), jnp.float32) * 0.02, 'w_proj': jax.random.normal(ks[2], (DIM, DIM), jnp.float32) * 0.02, 'b_proj': jnp.zeros((DIM,), jnp.float32), 'lambda_q1': jax.random.normal(ks[3], (HD,), jnp.float32) * 0.1, 'lambda_k1': jax.random.normal(ks[4], (HD,), jnp.float32) * 0.1, 'lambda_q2': jax.random.normal(ks[5], (HD,), jnp.float32) * 0.1, 'lambda_k2': jax.random.normal(ks[6], (HD,), jnp.float32) * 0.1, 'sub_norm_w': jnp.ones((2 * HD,), jnp.float32)}
    _L1_attn_in = _L1_attn_setup()

    def _L1_ffn_setup():
        import jax, jax.numpy as jnp
        import numpy as np
        MICRO_BATCHES = 2
        TOP_K = 2
        NUM_EXPERTS = 8
        B, S, D = (4, 1024, 256)
        H = 4 * D
        key = jax.random.key(seed)
        ks = jax.random.split(key, 8)
        s = 0.02
        return {'x': jax.random.normal(ks[0], (B, S, D), jnp.float32), 'ln_scale': jnp.ones((D,), jnp.float32), 'ln_bias': jnp.zeros((D,), jnp.float32), 'attn_w': jax.random.normal(ks[1], (D, D), jnp.float32) * s, 'attn_b': jnp.zeros((D,), jnp.float32), 'gate_w': jax.random.normal(ks[2], (NUM_EXPERTS, D), jnp.float32) * s, 'w1': jax.random.normal(ks[3], (NUM_EXPERTS, D, H), jnp.float32) * s, 'b1': jnp.zeros((NUM_EXPERTS, H), jnp.float32), 'w2': jax.random.normal(ks[4], (NUM_EXPERTS, H, D), jnp.float32) * s, 'b2': jnp.zeros((NUM_EXPERTS, D), jnp.float32), 'next_w': jax.random.normal(ks[5], (D, D), jnp.float32) * s, 'next_b': jnp.zeros((D,), jnp.float32)}
    _L1_ffn_in = _L1_ffn_setup()

    def _L2_attn_setup():
        import jax, jax.numpy as jnp
        import numpy as np
        H = 16

        def _pairwise_l2(pos):
            sq = jnp.sum((pos[:, :, None, :] - pos[:, None, :, :]) ** 2, axis=-1)
            safe = jnp.where(sq > 0, sq, 1.0)
            return jnp.where(sq > 0, jnp.sqrt(safe), 0.0)
        key = jax.random.key(seed)
        ks = jax.random.split(key, 12)
        B, S, D = (2, 512, 256)
        init = lambda k, shape: jax.random.normal(k, shape, dtype=jnp.float32) * 0.02
        return {'x': jax.random.normal(ks[0], (B, S, D), dtype=jnp.float32), 'wq': init(ks[1], (D, D)), 'bq': init(ks[2], (D,)), 'wk': init(ks[3], (D, D)), 'bk': init(ks[4], (D,)), 'wv': init(ks[5], (D, D)), 'bv': init(ks[6], (D,)), 'wo': init(ks[7], (D, D)), 'bo': init(ks[8], (D,)), 'w3d': init(ks[9], (3, D)), 'b3d': init(ks[10], (3,))}
    _L2_attn_in = _L2_attn_setup()

    def _L2_ffn_setup():
        import jax, jax.numpy as jnp
        import numpy as np
        B, S, H = (2, 256, 256)
        E, I, SI = (8, 128, 512)
        TOP_K, N_GROUP, TOPK_GROUP = (2, 2, 1)
        ROUTED_SCALE = 2.5

        def _route(x2d, gate_weight, gate_bias):
            T = x2d.shape[0]
            logits = x2d @ gate_weight.T
            scores = jax.nn.sigmoid(logits)
            sfc = scores + gate_bias[None, :]
            g = sfc.reshape(T, N_GROUP, E // N_GROUP)
            group_scores = jax.lax.top_k(g, 2)[0].sum(-1)
            _, gidx = jax.lax.top_k(group_scores, TOPK_GROUP)
            gmask = jnp.zeros((T, N_GROUP), sfc.dtype).at[jnp.arange(T)[:, None], gidx].set(1.0)
            smask = jnp.repeat(gmask, E // N_GROUP, axis=1)
            masked = jnp.where(smask > 0, sfc, 0.0)
            _, topk_idx = jax.lax.top_k(masked, TOP_K)
            topk_w = jnp.take_along_axis(scores, topk_idx, axis=1)
            topk_w = topk_w / (topk_w.sum(-1, keepdims=True) + 1e-20)
            topk_w = topk_w * ROUTED_SCALE
            return (topk_idx, topk_w)
        key = jax.random.key(seed)
        ks = jax.random.split(key, 7)

        def w(k, shape, sc=0.02):
            return jax.random.normal(k, shape, jnp.float32) * sc
        return {'hidden_states': jax.random.normal(ks[0], (B, S, H), jnp.float32), 'gate_weight': w(ks[1], (E, H)), 'gate_bias': w(ks[2], (E,), 0.01), 'up_weights': w(ks[3], (E, I, H)), 'down_weights': w(ks[4], (E, H, I)), 'shared_up_weight': w(ks[5], (SI, H)), 'shared_down_weight': w(ks[6], (H, SI))}
    _L2_ffn_in = _L2_ffn_setup()

    def _L3_attn_setup():
        import jax, jax.numpy as jnp
        import numpy as np
        B, S, D, NF = (4, 2048, 256, 64)
        key = jax.random.key(seed)
        k1, k2, k3, k4 = jax.random.split(key, 4)
        x = jax.random.normal(k1, (B, S, D), dtype=jnp.float32)
        W_in = jax.random.normal(k2, (2 * NF, D), dtype=jnp.float32) * 0.02
        W_out = jax.random.normal(k3, (D, 2 * NF), dtype=jnp.float32) * 0.02
        log_decay = jnp.linspace(-3.0, -0.001, NF).astype(jnp.float32)
        frequencies = jax.random.normal(k4, (NF,), dtype=jnp.float32)
        return {'x': x, 'W_in': W_in, 'W_out': W_out, 'log_decay': log_decay, 'frequencies': frequencies}
    _L3_attn_in = _L3_attn_setup()

    def _L3_ffn_setup():
        import jax, jax.numpy as jnp
        import numpy as np
        import math
        B, S, D = (4, 512, 256)
        E, DFF = (16, 512)
        CAP_FACTOR = 2.0
        ROUTER_HIDDEN = 128
        CAPACITY = int(math.ceil(S * CAP_FACTOR / E))
        key = jax.random.key(seed)
        ks = jax.random.split(key, 6)

        def uinit(k, shape, fan_in):
            bound = math.sqrt(3.0) * math.sqrt(1.0 / 3.0) / math.sqrt(fan_in)
            return jax.random.uniform(k, shape, jnp.float32, -bound, bound)
        return {'hidden_states': jax.random.normal(ks[0], (B, S, D), jnp.float32), 'router_w1': jax.random.normal(ks[1], (D, ROUTER_HIDDEN), jnp.float32) / math.sqrt(D), 'router_w2': jax.random.normal(ks[2], (ROUTER_HIDDEN, E), jnp.float32) / math.sqrt(ROUTER_HIDDEN), 'w1': uinit(ks[3], (E, D, DFF), D), 'w2': uinit(ks[4], (E, D, DFF), D), 'w3': uinit(ks[5], (E, DFF, D), DFF)}
    _L3_ffn_in = _L3_ffn_setup()
    _d = {'L0_attn_x': _L0_attn_in['x'], 'L0_attn_in_proj_w': _L0_attn_in['in_proj_w'], 'L0_attn_conv_w': _L0_attn_in['conv_w'], 'L0_attn_conv_b': _L0_attn_in['conv_b'], 'L0_attn_x_proj_w': _L0_attn_in['x_proj_w'], 'L0_attn_A_log': _L0_attn_in['A_log'], 'L0_attn_D': _L0_attn_in['D'], 'L0_attn_out_proj_w': _L0_attn_in['out_proj_w'], 'L0_ffn_gate_w': _L0_ffn_in['gate_w'], 'L0_ffn_gate_b': _L0_ffn_in['gate_b'], 'L0_ffn_w1': _L0_ffn_in['w1'], 'L0_ffn_w2': _L0_ffn_in['w2'], 'L1_attn_w_qkv': _L1_attn_in['w_qkv'], 'L1_attn_w_proj': _L1_attn_in['w_proj'], 'L1_attn_b_proj': _L1_attn_in['b_proj'], 'L1_attn_lambda_q1': _L1_attn_in['lambda_q1'], 'L1_attn_lambda_k1': _L1_attn_in['lambda_k1'], 'L1_attn_lambda_q2': _L1_attn_in['lambda_q2'], 'L1_attn_lambda_k2': _L1_attn_in['lambda_k2'], 'L1_attn_sub_norm_w': _L1_attn_in['sub_norm_w'], 'L1_ffn_ln_scale': _L1_ffn_in['ln_scale'], 'L1_ffn_ln_bias': _L1_ffn_in['ln_bias'], 'L1_ffn_attn_w': _L1_ffn_in['attn_w'], 'L1_ffn_attn_b': _L1_ffn_in['attn_b'], 'L1_ffn_gate_w': _L1_ffn_in['gate_w'], 'L1_ffn_w1': _L1_ffn_in['w1'], 'L1_ffn_b1': _L1_ffn_in['b1'], 'L1_ffn_w2': _L1_ffn_in['w2'], 'L1_ffn_b2': _L1_ffn_in['b2'], 'L1_ffn_next_w': _L1_ffn_in['next_w'], 'L1_ffn_next_b': _L1_ffn_in['next_b'], 'L2_attn_wq': _L2_attn_in['wq'], 'L2_attn_bq': _L2_attn_in['bq'], 'L2_attn_wk': _L2_attn_in['wk'], 'L2_attn_bk': _L2_attn_in['bk'], 'L2_attn_wv': _L2_attn_in['wv'], 'L2_attn_bv': _L2_attn_in['bv'], 'L2_attn_wo': _L2_attn_in['wo'], 'L2_attn_bo': _L2_attn_in['bo'], 'L2_attn_w3d': _L2_attn_in['w3d'], 'L2_attn_b3d': _L2_attn_in['b3d'], 'L2_ffn_gate_weight': _L2_ffn_in['gate_weight'], 'L2_ffn_gate_bias': _L2_ffn_in['gate_bias'], 'L2_ffn_up_weights': _L2_ffn_in['up_weights'], 'L2_ffn_down_weights': _L2_ffn_in['down_weights'], 'L2_ffn_shared_up_weight': _L2_ffn_in['shared_up_weight'], 'L2_ffn_shared_down_weight': _L2_ffn_in['shared_down_weight'], 'L3_attn_W_in': _L3_attn_in['W_in'], 'L3_attn_W_out': _L3_attn_in['W_out'], 'L3_attn_log_decay': _L3_attn_in['log_decay'], 'L3_attn_frequencies': _L3_attn_in['frequencies'], 'L3_ffn_router_w1': _L3_ffn_in['router_w1'], 'L3_ffn_router_w2': _L3_ffn_in['router_w2'], 'L3_ffn_w1': _L3_ffn_in['w1'], 'L3_ffn_w2': _L3_ffn_in['w2'], 'L3_ffn_w3': _L3_ffn_in['w3']}
    _x0 = _d['L0_attn_x']
    _d['L0_attn_x'] = jax.random.normal(jax.random.fold_in(jax.random.key(seed), 1), (16, 512, 256), dtype=_x0.dtype)
    del _x0
    return _d

def reference(L0_attn_x, L0_attn_in_proj_w, L0_attn_conv_w, L0_attn_conv_b, L0_attn_x_proj_w, L0_attn_A_log, L0_attn_D, L0_attn_out_proj_w, L0_ffn_gate_w, L0_ffn_gate_b, L0_ffn_w1, L0_ffn_w2, L1_attn_w_qkv, L1_attn_w_proj, L1_attn_b_proj, L1_attn_lambda_q1, L1_attn_lambda_k1, L1_attn_lambda_q2, L1_attn_lambda_k2, L1_attn_sub_norm_w, L1_ffn_ln_scale, L1_ffn_ln_bias, L1_ffn_attn_w, L1_ffn_attn_b, L1_ffn_gate_w, L1_ffn_w1, L1_ffn_b1, L1_ffn_w2, L1_ffn_b2, L1_ffn_next_w, L1_ffn_next_b, L2_attn_wq, L2_attn_bq, L2_attn_wk, L2_attn_bk, L2_attn_wv, L2_attn_bv, L2_attn_wo, L2_attn_bo, L2_attn_w3d, L2_attn_b3d, L2_ffn_gate_weight, L2_ffn_gate_bias, L2_ffn_up_weights, L2_ffn_down_weights, L2_ffn_shared_up_weight, L2_ffn_shared_down_weight, L3_attn_W_in, L3_attn_W_out, L3_attn_log_decay, L3_attn_frequencies, L3_ffn_router_w1, L3_ffn_router_w2, L3_ffn_w1, L3_ffn_w2, L3_ffn_w3):

    def _L0_attn_ref(x, in_proj_w, conv_w, conv_b, x_proj_w, A_log, D, out_proj_w):
        import jax, jax.numpy as jnp
        import numpy as np
        D_MODEL = 256
        D_STATE = 16
        D_CONV = 4
        EXPAND = 2
        D_INNER = D_MODEL * EXPAND
        BATCH = 4
        SEQ_LEN = 1024

        def _silu(v):
            return v * jax.nn.sigmoid(v)
        b, l, _ = x.shape
        xz = jnp.einsum('bld,ed->ble', x, in_proj_w)
        x_inner, z = jnp.split(xz, 2, axis=-1)
        xc = jnp.transpose(x_inner, (0, 2, 1))
        xc = jax.lax.conv_general_dilated(xc, conv_w, window_strides=(1,), padding=[(D_CONV - 1, 0)], feature_group_count=D_INNER, dimension_numbers=('NCH', 'OIH', 'NCH'))
        xc = xc + conv_b[None, :, None]
        x_conv = _silu(jnp.transpose(xc, (0, 2, 1)))
        x_dbl = jnp.einsum('bld,ed->ble', x_conv, x_proj_w)
        delta = jax.nn.softplus(x_dbl[..., 0])
        B_ssm = x_dbl[..., 1:D_STATE + 1]
        C_ssm = x_dbl[..., D_STATE + 1:]
        A = -jnp.exp(A_log)

        def step(h, inp):
            x_t, d_t, B_t, C_t = inp
            dA = jnp.exp(d_t[:, None, None] * A)
            dB = d_t[:, None, None] * B_t[:, None, :]
            h = h * dA + x_t[:, :, None] * dB
            y_t = jnp.einsum('bdn,bn->bd', h, C_t)
            return (h, y_t)
        h0 = jnp.zeros((b, D_INNER, D_STATE), x.dtype)
        xs = (jnp.swapaxes(x_conv, 0, 1), jnp.swapaxes(delta, 0, 1), jnp.swapaxes(B_ssm, 0, 1), jnp.swapaxes(C_ssm, 0, 1))
        _, ys = jax.lax.scan(step, h0, xs)
        y = jnp.swapaxes(ys, 0, 1)
        y = y + x_conv * D
        y = y * _silu(z)
        return jnp.einsum('bld,od->blo', y, out_proj_w)

    def _L0_ffn_ref(x, gate_w, gate_b, w1, w2):
        import jax, jax.numpy as jnp
        import numpy as np
        B, S, D, E, H, K = (64, 512, 256, 32, 1024, 8)
        b, s, d = x.shape
        logits = jnp.einsum('bsd,ed->bse', x, gate_w) + gate_b
        probs = jax.nn.softmax(logits, axis=-2)
        vals_t, idx_t = jax.lax.top_k(probs.transpose(0, 2, 1), K)
        vals = vals_t.transpose(0, 2, 1)
        idx = idx_t.transpose(0, 2, 1)
        flat_idx = idx.reshape(b, K * E)
        tok = jnp.take_along_axis(x, flat_idx[:, :, None], axis=1)
        tok = tok.reshape(b, K, E, d)
        merged = jnp.einsum('bked,bke->bed', tok, vals)
        ones = jnp.ones(merged.shape[:-1] + (1,), merged.dtype)
        h = jnp.einsum('bei,eih->beh', jnp.concatenate([merged, ones], -1), w1)
        h = jax.nn.gelu(h, approximate=False)
        o = jnp.einsum('bej,ejo->beo', jnp.concatenate([h, ones], -1), w2)
        out_tok = jnp.einsum('beo,bke->bkeo', o, vals).reshape(b, K * E, d)
        out = jnp.zeros_like(x).at[jnp.arange(b)[:, None], flat_idx].add(out_tok)
        return out

    def _L1_attn_ref(x, w_qkv, w_proj, b_proj, lambda_q1, lambda_k1, lambda_q2, lambda_k2, sub_norm_w):
        import jax, jax.numpy as jnp
        import numpy as np
        DIM = 256
        H = 16
        HD = DIM // H // 2
        LAMBDA_INIT = 0.8 - 0.6 * float(np.exp(-0.3 * 0))
        EPS = 1e-05

        def _rms_norm(x, w, eps):
            return x * jax.lax.rsqrt(jnp.mean(jnp.square(x), axis=-1, keepdims=True) + eps) * w
        B, N, C = x.shape
        scale = HD ** (-0.5)
        qkv = x @ w_qkv.T
        q, k, v = jnp.split(qkv, 3, axis=-1)
        q = q.reshape(B, N, H, 2, HD)
        k = k.reshape(B, N, H, 2, HD)
        v = v.reshape(B, N, H, 2 * HD)
        lam = jnp.exp(jnp.sum(lambda_q1 * lambda_k1)) - jnp.exp(jnp.sum(lambda_q2 * lambda_k2)) + LAMBDA_INIT

        def sdpa(qi, ki):
            s = jnp.einsum('bnhd,bmhd->bhnm', qi, ki) * scale
            p = jax.nn.softmax(s, axis=-1)
            return jnp.einsum('bhnm,bmhe->bhne', p, v)
        a1 = sdpa(q[:, :, :, 0], k[:, :, :, 0])
        a2 = sdpa(q[:, :, :, 1], k[:, :, :, 1])
        o = a1 - lam * a2
        o = _rms_norm(o, sub_norm_w, EPS) * (1.0 - LAMBDA_INIT)
        o = o.transpose(0, 2, 1, 3).reshape(B, N, C)
        return o @ w_proj.T + b_proj

    def _L1_ffn_ref(x, ln_scale, ln_bias, attn_w, attn_b, gate_w, w1, b1, w2, b2, next_w, next_b):
        import jax, jax.numpy as jnp
        import numpy as np
        MICRO_BATCHES = 2
        TOP_K = 2
        NUM_EXPERTS = 8
        B, S, D = (4, 1024, 256)
        H = 4 * D
        b, s, d = x.shape
        flat = x.reshape(b * s, d)
        mu = jnp.mean(flat, axis=-1, keepdims=True)
        var = jnp.mean((flat - mu) ** 2, axis=-1, keepdims=True)
        xn = (flat - mu) * jax.lax.rsqrt(var + 1e-05) * ln_scale + ln_bias
        x_attn = xn @ attn_w.T + attn_b + flat
        logits = x_attn @ gate_w.T
        _vals, _idx = jax.lax.top_k(logits, TOP_K)
        e = w1.shape[0]
        n = b * s // (MICRO_BATCHES * e)
        xe = x_attn.reshape(MICRO_BATCHES, e, n, d)
        h = jax.nn.gelu(jnp.einsum('mend,edh->menh', xe, w1) + b1[None, :, None, :], approximate=False)
        eo = jnp.einsum('menh,ehd->mend', h, w2) + b2[None, :, None, :]
        eo = eo.reshape(b * s, d)
        out = jax.nn.gelu(eo @ next_w.T + next_b, approximate=False)
        return out.reshape(b, s, d)

    def _L2_attn_ref(x, wq, bq, wk, bk, wv, bv, wo, bo, w3d, b3d):
        import jax, jax.numpy as jnp
        import numpy as np
        H = 16

        def _pairwise_l2(pos):
            sq = jnp.sum((pos[:, :, None, :] - pos[:, None, :, :]) ** 2, axis=-1)
            safe = jnp.where(sq > 0, sq, 1.0)
            return jnp.where(sq > 0, jnp.sqrt(safe), 0.0)
        B, S, D = x.shape
        hd = D // H
        scale = 1.0 / hd ** 0.5
        V = (x @ wv.T + bv).reshape(B, S, H, hd).transpose(0, 2, 1, 3)
        pos = x @ w3d.T + b3d
        dist = _pairwise_l2(pos)
        scores = -dist[:, None, :, :] * scale
        causal = jnp.triu(jnp.ones((S, S), dtype=bool), k=1)
        scores = jnp.where(causal[None, None], -jnp.inf, scores)
        attn = jax.nn.softmax(scores, axis=-1)
        attn = jnp.nan_to_num(attn, nan=0.0)
        out = jnp.einsum('bhqk,bhkd->bhqd', attn, V)
        out = out.transpose(0, 2, 1, 3).reshape(B, S, D)
        return out @ wo.T + bo

    def _L2_ffn_ref(hidden_states, gate_weight, gate_bias, up_weights, down_weights, shared_up_weight, shared_down_weight):
        import jax, jax.numpy as jnp
        import numpy as np
        B, S, H = (2, 256, 256)
        E, I, SI = (8, 128, 512)
        TOP_K, N_GROUP, TOPK_GROUP = (2, 2, 1)
        ROUTED_SCALE = 2.5

        def _route(x2d, gate_weight, gate_bias):
            T = x2d.shape[0]
            logits = x2d @ gate_weight.T
            scores = jax.nn.sigmoid(logits)
            sfc = scores + gate_bias[None, :]
            g = sfc.reshape(T, N_GROUP, E // N_GROUP)
            group_scores = jax.lax.top_k(g, 2)[0].sum(-1)
            _, gidx = jax.lax.top_k(group_scores, TOPK_GROUP)
            gmask = jnp.zeros((T, N_GROUP), sfc.dtype).at[jnp.arange(T)[:, None], gidx].set(1.0)
            smask = jnp.repeat(gmask, E // N_GROUP, axis=1)
            masked = jnp.where(smask > 0, sfc, 0.0)
            _, topk_idx = jax.lax.top_k(masked, TOP_K)
            topk_w = jnp.take_along_axis(scores, topk_idx, axis=1)
            topk_w = topk_w / (topk_w.sum(-1, keepdims=True) + 1e-20)
            topk_w = topk_w * ROUTED_SCALE
            return (topk_idx, topk_w)
        Bv, Sv, Hv = hidden_states.shape
        x = hidden_states.reshape(-1, Hv)
        T = x.shape[0]
        topk_idx, topk_w = _route(x, gate_weight, gate_bias)
        cw = jnp.zeros((T, E), x.dtype).at[jnp.arange(T)[:, None], topk_idx].add(topk_w)
        h = jnp.einsum('th,eih->tei', x, up_weights)
        r = jnp.maximum(h, 0.0)
        r2 = r * r
        routed = jnp.einsum('tei,ehi,te->th', r2, down_weights, cw)
        sh = jnp.maximum(x @ shared_up_weight.T, 0.0)
        shared = sh * sh @ shared_down_weight.T
        return (routed + shared).reshape(Bv, Sv, Hv)

    def _L3_attn_ref(x, W_in, W_out, log_decay, frequencies):
        import jax, jax.numpy as jnp
        import numpy as np
        B, S, D, NF = (4, 2048, 256, 64)
        b, s, d = x.shape
        nf = log_decay.shape[0]
        dt = jnp.float32(1.0)
        decay = jax.nn.sigmoid(log_decay)
        omega = frequencies * 0.1 * dt
        rot = jax.lax.complex(jnp.cos(omega), jnp.sin(omega))
        A = decay * rot
        spectral = jnp.einsum('bsd,fd->bsf', x, W_in)
        u = jax.lax.complex(spectral[..., :nf], spectral[..., nf:])
        ones = jnp.ones((1, nf), dtype=A.dtype)
        A_rep = jnp.broadcast_to(A[None, :], (s - 1, nf))
        powers = jnp.cumprod(jnp.concatenate([ones, A_rep], axis=0), axis=0)
        kernel = powers * rot[None, :]
        n_fft = 2 * s
        U_f = jnp.fft.fft(u, n=n_fft, axis=1)
        K_f = jnp.fft.fft(kernel, n=n_fft, axis=0)
        y = jnp.fft.ifft(U_f * K_f[None, :, :], axis=1)[:, :s, :]
        feats = jnp.concatenate([y.real, y.imag], axis=-1)
        return jnp.einsum('bsf,df->bsd', feats, W_out)

    def _L3_ffn_ref(hidden_states, router_w1, router_w2, w1, w2, w3):
        import jax, jax.numpy as jnp
        import numpy as np
        import math
        B, S, D = (4, 512, 256)
        E, DFF = (16, 512)
        CAP_FACTOR = 2.0
        ROUTER_HIDDEN = 128
        CAPACITY = int(math.ceil(S * CAP_FACTOR / E))
        b, s, d = hidden_states.shape
        e = w1.shape[0]
        cap = CAPACITY
        router_logits = jax.nn.silu(hidden_states @ router_w1) @ router_w2
        expert_probs = jax.nn.softmax(router_logits.transpose(0, 2, 1), axis=-1)
        expert_weights, token_indices = jax.lax.top_k(expert_probs, cap)
        expert_weights = expert_weights / (expert_weights.sum(-1, keepdims=True) + 1e-09)
        expert_inputs = jax.vmap(lambda h, i: h[i])(hidden_states, token_indices)
        gate = jax.nn.silu(jnp.einsum('becd,edf->becf', expert_inputs, w1))
        value = jnp.einsum('becd,edf->becf', expert_inputs, w2)
        expert_out = jnp.einsum('becf,efd->becd', gate * value, w3)
        weighted = expert_out * expert_weights[..., None]

        def combine(idx, vals):
            return jnp.zeros((s, d), vals.dtype).at[idx.reshape(-1)].add(vals.reshape(-1, d))
        output = jax.vmap(combine)(token_indices, weighted)
        return output
    x = L0_attn_x
    xn = _layernorm(x, axis=-1)
    s = _L0_attn_ref(xn, L0_attn_in_proj_w, L0_attn_conv_w, L0_attn_conv_b, L0_attn_x_proj_w, L0_attn_A_log, L0_attn_D, L0_attn_out_proj_w)
    g = _silu(_L0_ffn_ref(xn, L0_ffn_gate_w, L0_ffn_gate_b, L0_ffn_w1, L0_ffn_w2))
    x = x + s * g
    xn = _layernorm(x, axis=-1)
    s = _L1_attn_ref(xn, L1_attn_w_qkv, L1_attn_w_proj, L1_attn_b_proj, L1_attn_lambda_q1, L1_attn_lambda_k1, L1_attn_lambda_q2, L1_attn_lambda_k2, L1_attn_sub_norm_w)
    g = _silu(_L1_ffn_ref(xn, L1_ffn_ln_scale, L1_ffn_ln_bias, L1_ffn_attn_w, L1_ffn_attn_b, L1_ffn_gate_w, L1_ffn_w1, L1_ffn_b1, L1_ffn_w2, L1_ffn_b2, L1_ffn_next_w, L1_ffn_next_b))
    x = x + s * g
    xn = _layernorm(x, axis=-1)
    s = _L2_attn_ref(xn, L2_attn_wq, L2_attn_bq, L2_attn_wk, L2_attn_bk, L2_attn_wv, L2_attn_bv, L2_attn_wo, L2_attn_bo, L2_attn_w3d, L2_attn_b3d)
    g = _silu(_L2_ffn_ref(xn, L2_ffn_gate_weight, L2_ffn_gate_bias, L2_ffn_up_weights, L2_ffn_down_weights, L2_ffn_shared_up_weight, L2_ffn_shared_down_weight))
    x = x + s * g
    xn = _layernorm(x, axis=-1)
    s = _L3_attn_ref(xn, L3_attn_W_in, L3_attn_W_out, L3_attn_log_decay, L3_attn_frequencies)
    g = _silu(_L3_ffn_ref(xn, L3_ffn_router_w1, L3_ffn_router_w2, L3_ffn_w1, L3_ffn_w2, L3_ffn_w3))
    x = x + s * g
    return x

_drawn_inputs = setup_inputs


def setup_inputs(seed=0):
    import zlib

    import numpy as np

    out = dict(_drawn_inputs(seed))
    spreads = {'L0_attn_D': (1.0, 0.6),
     'L0_ffn_gate_b': (0.0, 0.8),
     'L1_attn_b_proj': (0.0, 0.8),
     'L1_attn_sub_norm_w': (1.0, 0.6),
     'L1_ffn_ln_scale': (1.0, 0.6),
     'L1_ffn_ln_bias': (0.0, 0.8),
     'L1_ffn_attn_b': (0.0, 0.8),
     'L1_ffn_b1': (0.0, 0.8),
     'L1_ffn_b2': (0.0, 0.8),
     'L1_ffn_next_b': (0.0, 0.8)}
    factors = {'L0_attn_in_proj_w': 2.801,
     'L0_attn_conv_b': 8.0,
     'L0_attn_A_log': 8.0,
     'L0_ffn_gate_w': 3.052,
     'L1_attn_w_qkv': 7.921,
     'L1_attn_w_proj': 8.0,
     'L1_attn_lambda_q1': 8.0,
     'L1_attn_lambda_k1': 8.0,
     'L1_attn_lambda_q2': 8.0,
     'L1_attn_lambda_k2': 8.0,
     'L1_ffn_attn_w': 8.0,
     'L1_ffn_w1': 8.0,
     'L1_ffn_w2': 8.0,
     'L1_ffn_next_w': 8.0,
     'L2_attn_wv': 8.0,
     'L2_attn_bv': 8.0,
     'L2_attn_wo': 8.0,
     'L2_attn_bo': 8.0,
     'L2_attn_w3d': 8.0,
     'L2_attn_b3d': 8.0,
     'L2_ffn_gate_weight': 8.0,
     'L2_ffn_gate_bias': 8.0,
     'L2_ffn_up_weights': 8.0,
     'L2_ffn_down_weights': 8.0,
     'L2_ffn_shared_up_weight': 8.0,
     'L2_ffn_shared_down_weight': 8.0,
     'L3_attn_W_in': 8.0,
     'L3_attn_W_out': 8.0,
     'L3_attn_log_decay': 8.0,
     'L3_attn_frequencies': 8.0,
     'L3_ffn_router_w1': 8.0,
     'L3_ffn_router_w2': 8.0,
     'L3_ffn_w1': 8.0,
     'L3_ffn_w2': 8.0,
     'L3_ffn_w3': 8.0}
    for name, (base, spread) in spreads.items():
        noise = np.random.default_rng([zlib.crc32(name.encode()), seed]).standard_normal(out[name].shape)
        drawn = base * np.exp(spread * noise) if base else spread * noise
        out[name] = jnp.asarray(drawn.astype(out[name].dtype))
    for name, factor in factors.items():
        out[name] = (out[name] * factor).astype(out[name].dtype)
    return out
```

```python
import math
from contextlib import ExitStack

import concourse.bass as bass
from concourse import mybir

F32 = mybir.dt.float32
BF16 = mybir.dt.bfloat16
U32 = mybir.dt.uint32
ALU = mybir.AluOpType
ACT = mybir.ActivationFunctionType
AX = mybir.AxisListType
P = 128
B, S, DM = 16, 512, 256
Q = S // P
KD = DM // P
EPS = 1e-5


class Signal:

    def __init__(self, nc, ctx, name):
        self.sem = ctx.enter_context(nc.semaphore(name))
        self.n = 0

    def __call__(self, instruction, by=1):
        instruction.then_inc(self.sem, by)
        self.n += by
        return self.n


def link(engine, signal, instruction):
    n = signal(instruction)
    engine.wait_ge(signal.sem, n)
    return n


class Phase:

    def __init__(self, nc, ctx, name):
        self.nc, self.ctx, self.name = nc, ctx, name
        self.signals, self.pool_dma, self.buffers = [], [], {}

    def sb(self, name, shape, dt=F32):
        if name not in self.buffers:
            self.buffers[name] = self.ctx.enter_context(self.nc.sbuf_tensor(f"{self.name}_{name}", shape, dt))
        return self.buffers[name]

    def psum(self):
        return self.ctx.enter_context(self.nc.psum_tensor(f"{self.name}_psum", [P, 8, 512], F32))

    def counter(self, name):
        s = Signal(self.nc, self.ctx, f"{self.name}_{name}")
        self.signals.append(s)
        return s

    def clear(self):
        with self.nc.Block() as block:
            @block.sync
            def _(sp):
                for s in self.signals:
                    if s not in self.pool_dma:
                        sp.sem_clear(s.sem)

            if self.pool_dma:
                @block.gpsimd
                def _(pool):
                    for s in self.pool_dma:
                        pool.dma_reset(range(s.sem.num, s.sem.num + 1))
                        pool.sem_clear(s.sem)
        for s in self.signals:
            s.n = 0


SLOTS = 2


class Job:

    def __init__(self, j):
        self.j, self.slot = j, j % SLOTS
        self.block = self.b = None
        self.before, self.done = None, []

    def wait_for_buffers(self, *more):
        waits = self.before.done if self.before else []
        if waits:
            def wait(engine):
                for sem, n in waits:
                    engine.wait_ge(sem, n)
            for on in (self.block.sync, self.block.tensor, self.block.scalar, self.block.vector) + more:
                on(wait)


def pipeline(bodies, jobs, lag):
    step, left = 0, set(range(len(bodies)))
    while left:
        for j, body in enumerate(bodies):
            if j in left and step >= j * lag:
                before = jobs[j].before
                assert before is None or before.done, "the buffers' last user is still at work"
                if next(body, left) is left:
                    left.remove(j)
        step += 1


def run_sequences(nc, ph, sequence, count, per_pass, lag):
    jobs = [Job(j) for j in range(per_pass)]
    for job in jobs[SLOTS:]:
        job.before = jobs[job.j - SLOTS]
    bodies = [sequence(job) for job in jobs]
    for body in bodies:
        next(body)
    yield
    with nc.Fori(0, count // per_pass) as g:
        with nc.Block() as block:
            for job in jobs:
                job.block, job.b = block, g * per_pass + job.j
            pipeline(bodies, jobs, lag)
        ph.clear()


def load_once(nc, ph, pairs):
    loaded = ph.counter("weights_loaded")
    with nc.Block() as block:
        @block.sync
        def _(sp):
            for dst, src in pairs:
                loaded(sp.dma_start(dst, src), 16)
            sp.wait_ge(loaded.sem, loaded.n)
    ph.clear()


def make_constants(nc, ctx):
    c = {}
    for name in ("ident", "ones", "upto", "after"):
        c[name] = ctx.enter_context(nc.sbuf_tensor(f"c_{name}", [P, P], F32))
    ph = Phase(nc, ctx, "const")
    done = ph.counter("pool_done")
    with nc.Block() as block:
        @block.gpsimd
        def _(pool):
            nc.gpsimd.memset(c["ident"][:, :], 0.0).then_inc(done.sem, 1)
            nc.gpsimd.memset(c["ones"][:, :], 1.0).then_inc(done.sem, 1)
            pool.wait_ge(done.sem, 2)
            nc.gpsimd.affine_select(out=c["ident"][:, :], in_=c["ident"][:, :], compare_op=ALU.not_equal, fill=1.0,
                                    base=0, pattern=[[-1, P]], channel_multiplier=1).then_inc(done.sem, 1)
            nc.gpsimd.affine_select(out=c["upto"][:, :], in_=c["ones"][:, :], compare_op=ALU.is_ge, fill=0.0,
                                    base=0, pattern=[[1, P]], channel_multiplier=-1).then_inc(done.sem, 1)
            nc.gpsimd.affine_select(out=c["after"][:, :], in_=c["ones"][:, :], compare_op=ALU.is_gt, fill=0.0,
                                    base=0, pattern=[[-1, P]], channel_multiplier=1).then_inc(done.sem, 1)
            pool.wait_ge(done.sem, 5)
    done.n = 5
    ph.clear()
    return c


class Norm:

    def __init__(self, ph, tag):
        self.stats = ph.sb(f"{tag}_stats", [P, Q, 6])
        self.mv = ph.sb(f"{tag}_mv", [P, Q, 2])
        self.std = ph.sb(f"{tag}_std", [P, Q])
        self.rstd = ph.sb(f"{tag}_rstd", [P, Q])


def layer_norm(nc, block, nm, x, xn, V, A, ready):
    at = {}

    @block.vector
    def _(dve):
        dve.wait_ge(*ready)
        for q in range(Q):
            V(nc.vector.bn_stats(nm.stats[:, q, :], x[:, q, :]))
        dve.wait_ge(V.sem, V.n)
        for q in range(Q):
            V(nc.vector.bn_aggr(nm.mv[:, q, :], nm.stats[:, q, :]))
        dve.wait_ge(V.sem, V.n)
        at["var"] = V(nc.vector.tensor_scalar(nm.std[:, :], nm.mv[:, :, 1], EPS, None, ALU.add))

    @block.scalar
    def _(act):
        act.wait_ge(V.sem, at["var"])
        at["std"] = A(nc.scalar.activation(nm.std[:, :], nm.std[:, :], ACT.Sqrt))

    @block.vector
    def _(dve):
        dve.wait_ge(A.sem, at["std"])
        link(dve, V, nc.vector.reciprocal(nm.rstd[:, :], nm.std[:, :]))
        for q in range(Q):
            V(nc.vector.tensor_scalar(xn[:, q, :], x[:, q, :], nm.mv[:, q, 0:1], nm.rstd[:, q:q + 1],
                                      ALU.subtract, ALU.mult))
        at["xn"] = V.n
    return at["xn"]


def transpose_rows(nc, block, ps, banks, ident, xn, xnT, T, V, ready, free, eng="vector", kd=KD):
    at = {}

    @block.tensor
    def _(pe):
        pe.wait_ge(*ready)
        for k in range(kd):
            bank = banks[k % len(banks)]
            assert len(banks) >= kd
            if bank in free:
                pe.wait_ge(*free[bank])
            for q in range(Q):
                last = nc.tensor.transpose(ps[:, bank, q * P:(q + 1) * P], xn[:, q, k * P:(k + 1) * P], ident[:, :])
            at[k] = T(last)

    def copies(e, copy):
        for k in range(kd):
            e.wait_ge(T.sem, at[k])
            n = V(copy(xnT[:, k, :], ps[:, banks[k], :]))
            free[banks[k]] = (V.sem, n)
    if eng == "vector":
        block.vector(lambda dve: copies(dve, nc.vector.tensor_copy))
    else:
        block.scalar(lambda act: copies(act, nc.scalar.copy))
    return (V.sem, V.n)


DI, NS, KC = 512, 16, 4
RT = 3
LAG_A = 5
SEQS = 4
KC3 = 96
KST = 96
CI = DI // P
E0, K0 = 32, 8


def phase_a(nc, c, d, mergedT, count=B):
    with ExitStack() as ctx:
        ph = Phase(nc, ctx, "a")
        ps = ph.psum()
        ident, upto, after = c["ident"], c["upto"], c["after"]
        w_in = ph.sb("w_in", [P, KD, 2 * DI])
        w_conv = ph.sb("w_conv", [P, CI, KC])
        b_conv = ph.sb("b_conv", [P, CI])
        w_x = ph.sb("w_x", [P, CI, 2 * NS + 1])
        skip = ph.sb("skip", [P, CI])
        w_out = ph.sb("w_out", [P, CI, DM])
        w_gate = ph.sb("w_gate", [P, KD, E0])
        b_gate = ph.sb("b_gate", [E0, 1])
        a_row = ph.sb("a_row", [P, NS])
        a_col = ph.sb("a_col", [NS, 1])
        pick = ph.sb("pick", [KC3, NS, P], BF16)
        load_once(nc, ph, [
            (w_in[:, :, :], d["w_in"].rearrange("(k p) e -> p k e", p=P)),
            (w_conv[:, :, :], d["w_conv"].rearrange("(c p) o k -> p c (o k)", p=P)),
            (b_conv[:, :], d["b_conv"]),
            (w_x[:, :, :], d["w_x"].rearrange("(c p) e -> p c e", p=P)),
            (skip[:, :], d["skip"]),
            (w_out[:, :, :], d["w_out"].rearrange("(c p) e -> p c e", p=P)),
            (w_gate[:, :, :], d["w_gate0"].rearrange("(k p) e -> p k e", p=P)),
            (b_gate[:, :], d["b_gate0"].rearrange("(e o) -> e o", o=1)),
            (a_row[:, :], d["a_log"].partition_broadcast(P)),
            (a_col[:, :], d["a_log"].rearrange("(n o) -> n o", o=1)),
        ])
        V, A, T, G = (ph.counter(n) for n in ("vector_done", "scalar_done", "tensor_done", "pool_done"))


        def sequence(job):
            i, j = job.slot, job.j
            c3 = ph.sb(f"c3_{i}", [KC3, S], BF16)
            cr = ph.sb(f"cr_{i}", [NS, 1, S])
            crb = ph.sb(f"crb_{i}", [NS, S], BF16)
            cw = ph.sb(f"cw_{i}", [KST, S])
            st = ph.sb(f"st_{i}", [KST, Q, DI])
            x = ph.sb(f"x_{i}", [P, Q, DM])
            xn = ph.sb(f"xn_{i}", [P, Q, DM])
            xnT = ph.sb(f"xnT_{i}", [P, KD, S])
            nm = Norm(ph, f"ln{i}")
            xi = ph.sb(f"xi_{i}", [P, CI, KC - 1 + S])
            cv = ph.sb(f"cv_{i}", [P, CI, S])
            xc = ph.sb(f"xc_{i}", [P, CI, S])
            xct = ph.sb(f"xct_{i}", [P, Q, DI])
            zs = ph.sb(f"zs_{i}", [P, CI, S])
            lg = ph.sb(f"lg_{i}", [E0, S])
            pr = ph.sb(f"pr_{i}", [E0, S])
            rest = lg
            top = ph.sb(f"top_{i}", [E0, K0])
            g1 = ph.sb(f"g1_{i}", [E0, 4])
            pT = ph.sb(f"pT_{i}", [P, Q, E0])
            xd = ph.sb(f"xd_{i}", [P, Q, 2 * NS + 1])
            cT = ph.sb(f"cT_{i}", [NS, S])
            sp1 = ph.sb(f"sp1_{i}", [P, Q])
            sp2 = ph.sb(f"sp2_{i}", [P, Q])
            dl = ph.sb(f"dl_{i}", [P, Q])
            dla = ph.sb(f"dla_{i}", [P, Q, P])
            dlr = ph.sb(f"dlr_{i}", [P, Q, NS])
            bdt = ph.sb(f"bdt_{i}", [P, Q, NS])
            bw = ph.sb(f"bw_{i}", [P, Q, NS])
            edec = ph.sb(f"edec_{i}", [NS, Q])
            span = ph.sb(f"span_{i}", [P, S])
            ex = ph.sb(f"ex_{i}", [P, 2, S])
            t1 = ph.sb(f"t1_{i}", [P, RT, S])
            gm = ph.sb(f"gm_{i}", [P, S])
            yg = cv
            so = x
            x_in, stored = ph.counter(f"x_in{j}"), ph.counter(f"stored{j}")
            spread_read, summed, spread_made, exp_made = (ph.counter(f"{n}{j}") for n in ("spread_read", "summed", "spread_made", "exp_made"))

            if j < SLOTS:
                seqs.append((c3, st, cw))
            yield
            block, b = job.block, job.b
            job.wait_for_buffers(block.gpsimd)
            free, at = {}, {}
            b0, b1, b2, b3 = range(4 * i, 4 * i + 4)
            @block.sync
            def _(sp):
                x_in(sp.dma_start(x[:, :, :], d["x"][b].rearrange("(q p) e -> p q e", p=P)), 16)

            n = layer_norm(nc, block, nm, x, xn, V, A, (x_in.sem, 16))
            at["xn"] = n
            at["xnT"] = transpose_rows(nc, block, ps, [b0, b1], ident, xn, xnT, T, V, (V.sem, n), free)

            yield

            ring = (b3, b0, b1)

            @block.tensor
            def _(pe):
                pe.wait_ge(*at["xnT"])
                for k in range(KD):
                    last = nc.tensor.matmul(ps[0:E0, b2, :], w_gate[:, k, :], xnT[:, k, :], start=k == 0, stop=k == KD - 1)
                at["logits"] = T(last)
                at["proj"] = T.n
                base = A.n
                for e in range(8):
                    if e >= 3:
                        pe.wait_ge(A.sem, base + e - 2)
                    for k in range(KD):
                        last = nc.tensor.matmul(ps[:, ring[e % 3], :], w_in[:, k, e * P:(e + 1) * P], xnT[:, k, :],
                                                start=k == 0, stop=k == KD - 1)
                    T(last)

            @block.vector
            def _(dve):
                at["pad"] = V(nc.vector.memset(xi[:, :, 0:KC - 1], 0.0))
                dve.wait_ge(T.sem, at["logits"])
                n = link(dve, V, nc.vector.tensor_scalar(lg[:, :], ps[0:E0, b2, :], b_gate[:, 0:1], None, ALU.add))
                free[b2] = (V.sem, n)
                at["gmax"] = link(dve, V, nc.vector.tensor_reduce(g1[:, 0:1], lg[:, :], AX.X, ALU.max, negate=True))

            @block.scalar
            def _(act):
                for e in range(8):
                    act.wait_ge(T.sem, at["proj"] + e + 1)
                    if e < 4:
                        A(nc.scalar.copy(xi[:, e, KC - 1:], ps[:, ring[e % 3], :]))
                        if e == 3:
                            at["xi"] = A.n
                    else:
                        A(nc.scalar.activation(zs[:, e - 4, :], ps[:, ring[e % 3], :], ACT.Silu))
                        free[ring[e % 3]] = (A.sem, A.n)
                at["zs"] = A.n

            yield

            @block.vector
            def _(dve):
                dve.wait_ge(V.sem, at["pad"])
                base = V.n
                for k in range(KC):
                    for e in range(CI):
                        if k == 0:
                            dve.wait_ge(A.sem, at["xi"] - 3 + e)
                            V(nc.vector.tensor_scalar(cv[:, e, :], xi[:, e, 0:S], w_conv[:, e, 0:1], b_conv[:, e:e + 1],
                                                      ALU.mult, ALU.add))
                        else:
                            dve.wait_ge(V.sem, base + 4 * (k - 1) + e + 1)
                            V(nc.vector.scalar_tensor_tensor(cv[:, e, :], xi[:, e, k:k + S], w_conv[:, e, k:k + 1],
                                                             cv[:, e, :], ALU.mult, ALU.add))
                at["cv"] = V.n - CI

            @block.scalar
            def _(act):
                for e in range(CI):
                    act.wait_ge(V.sem, at["cv"] + e + 1)
                    A(nc.scalar.activation(xc[:, e, :], cv[:, e, :], ACT.Silu))
                at["xc"] = A.n
                act.wait_ge(V.sem, at["gmax"])
                at["gexp"] = A(nc.scalar.activation(pr[:, :], lg[:, :], ACT.Exp, bias=g1[:, 0:1], accum_out=g1[:, 1:2]))

            @block.vector
            def _(dve):
                dve.wait_ge(A.sem, at["gexp"])
                link(dve, V, nc.vector.reciprocal(g1[:, 2:3], g1[:, 1:2]))
                link(dve, V, nc.vector.tensor_scalar(pr[:, :], pr[:, :], g1[:, 2:3], None, ALU.mult))
                link(dve, V, nc.vector.max(top[:, :], pr[:, :]))
                link(dve, V, nc.vector.match_replace(rest[:, :], top[:, :], pr[:, :], 0.0))
                at["picked"] = link(dve, V, nc.vector.tensor_tensor(pr[:, :], pr[:, :], rest[:, :], ALU.subtract))

            yield

            @block.tensor
            def _(pe):
                pe.wait_ge(A.sem, at["xc"])
                pe.wait_ge(*free[b0])
                for q in range(Q):
                    for e in range(CI):
                        last = nc.tensor.matmul(ps[:, b0, q * 64:q * 64 + 33], xc[:, e, q * P:(q + 1) * P], w_x[:, e, :],
                                                start=e == 0, stop=e == CI - 1)
                at["xd"] = T(last)
                pe.wait_ge(*free[b1])
                for e in range(CI):
                    last = nc.tensor.matmul(ps[0:NS, b1, :], w_x[:, e, NS + 1:], xc[:, e, :], start=e == 0, stop=e == CI - 1)
                at["cT"] = T(last)
                for q in range(Q):
                    pe.wait_ge(*(free[(b2, b3)[q]] if q < 2 else (A.sem, A.n + q - 1)))
                    for e in range(CI):
                        last = nc.tensor.transpose(ps[:, (b2, b3)[q % 2], e * P:(e + 1) * P], xc[:, e, q * P:(q + 1) * P], ident[:, :])
                    T(last)
                at["xct_ps"] = T.n - Q
                pe.wait_ge(V.sem, at["picked"])
                pe.wait_ge(V.sem, V.n + 1)
                for q in range(Q):
                    last = nc.tensor.transpose(ps[:, b0, q * E0:(q + 1) * E0], pr[:, q * P:(q + 1) * P], ident[0:E0, 0:E0])
                at["pT_ps"] = T(last)

            @block.scalar
            def _(act):
                for q in range(Q):
                    act.wait_ge(T.sem, at["xct_ps"] + q + 1)
                    A(nc.scalar.copy(xct[:, q, :], ps[:, (b2, b3)[q % 2], :]))
                    free[(b2, b3)[q % 2]] = (A.sem, A.n)
                at["xct"] = A.n

            @block.vector
            def _(dve):
                dve.wait_ge(T.sem, at["xd"])
                link(dve, V, nc.vector.tensor_copy(
                    xd[:, :, :], ps[:, b0, 0:256].rearrange("p (q e) -> p q e", q=Q)[:, :, 0:33]))
                at["sp1"] = link(dve, V, nc.vector.scalar_tensor_tensor(
                    sp1[:, :], xd[:, :, 0], -1.0, xd[:, :, 0], ALU.mult, ALU.min))
                dve.wait_ge(T.sem, at["cT"])
                link(dve, V, nc.vector.tensor_copy(cT[:, :], ps[0:NS, b1, :]))
                link(dve, V, nc.vector.tensor_copy(c3[0:NS, :], cT[:, :]))
                link(dve, V, nc.vector.tensor_tensor(cr[:, 0, :], cT[:, :], c3[0:NS, :], ALU.subtract))
                V(nc.vector.tensor_copy(c3[32:32 + NS, :], cr[:, 0, :]))
                link(dve, V, nc.vector.tensor_copy(crb[:, :], cr[:, 0, :]))
                at["cT_sb"] = V(nc.vector.tensor_tensor(c3[64:64 + NS, :], cr[:, 0, :], crb[:, :], ALU.subtract))
                free[b1] = (V.sem, V.n)
                dve.wait_ge(T.sem, at["pT_ps"])
                at["pT"] = V(nc.vector.tensor_copy(pT[:, :, :], ps[:, b0, 0:Q * E0]))
                free[b0] = (V.sem, V.n)

            yield

            @block.scalar
            def _(act):
                act.wait_ge(V.sem, at["sp1"])
                link(act, A, nc.scalar.activation(sp2[:, :], sp1[:, :], ACT.Exp))
                at["sp2"] = link(act, A, nc.scalar.activation(sp2[:, :], sp2[:, :], ACT.Ln, bias=1.0))

            @block.vector
            def _(dve):
                dve.wait_ge(A.sem, at["sp2"])
                link(dve, V, nc.vector.scalar_tensor_tensor(dl[:, :], xd[:, :, 0], 0.0, sp2[:, :], ALU.max, ALU.add))
                V(nc.vector.tensor_tensor(dla[:, :, :], after[:, :].unsqueeze(1).broadcast_to([P, Q, P]),
                                          dl[:, :].unsqueeze(2).broadcast_to([P, Q, P]), ALU.mult))
                V(nc.vector.tensor_copy(dlr[:, :, :], dl[:, :].unsqueeze(2).broadcast_to([P, Q, NS])))
                at["dla"] = V.n
                V(nc.vector.tensor_tensor(bdt[:, :, :], xd[:, :, 1:NS + 1], dl[:, :].unsqueeze(2).broadcast_to([P, Q, NS]),
                                          ALU.mult))
                at["bdt"] = V.n

            yield

            @block.tensor
            def _(pe):
                pe.wait_ge(V.sem, at["dla"])
                pe.wait_ge(*free[b3])
                for q in range(Q):
                    last = nc.tensor.matmul(ps[:, b3, q * P:(q + 1) * P], dla[:, q, :], upto[:, :], start=True, stop=True)
                at["span"] = T(last)
                pe.wait_ge(*free[b1])
                for q in range(Q):
                    last = nc.tensor.matmul(ps[0:NS, b1, q * P:(q + 1) * P], dlr[:, q, :], upto[:, :], start=True, stop=True)
                at["upto"] = T(last)
                pe.wait_ge(*free[b2])
                for k in range(KD):
                    for q in range(Q):
                        last = nc.tensor.matmul(ps[:, b2, k * E0:(k + 1) * E0], xn[:, q, k * P:(k + 1) * P], pT[:, q, :],
                                                start=q == 0, stop=q == Q - 1)
                at["merged"] = T(last)

            @block.vector
            def _(dve):
                dve.wait_ge(T.sem, at["span"])
                at["span_sb"] = V(nc.vector.tensor_copy(span[:, :], ps[:, b3, :]))
                free[b3] = (V.sem, V.n)
                dve.wait_ge(T.sem, at["merged"])
                V(nc.vector.tensor_copy(mergedT[:, :, :, bass.ds(b, 1)],
                                        ps[:, b2, 0:KD * E0].rearrange("p (k e o) -> p k e o", k=KD, o=1)))
                free[b2] = (V.sem, V.n)

            spread = (b0, b3)

            @block.tensor
            def _(pe):
                pe.wait_ge(*free[b0])
                pe.wait_ge(*free[b3])
                pe.wait_ge(V.sem, at["cT_sb"])
                for n in range(NS):
                    if n >= 2:
                        pe.wait_ge(spread_read.sem, n - 1)
                    spread_made(nc.tensor.matmul(ps[:, spread[n % 2], :], pick[:, n, :], c3[:, :], start=True, stop=True))

            @block.scalar
            def _(act):
                act.wait_ge(V.sem, at["span_sb"])
                for n in range(NS):
                    if n >= 2:
                        act.wait_ge(spread_read.sem, n - 1)
                    exp_made(nc.scalar.activation(ex[:, n % 2, :], span[:, :], ACT.Exp, scale=a_row[:, n:n + 1]))
                act.wait_ge(T.sem, at["upto"])
                A(nc.scalar.activation(cw[0:NS, :], ps[0:NS, b1, :], ACT.Exp, scale=a_col[:, 0:1]))
                at["cwe"] = A.n
                A(nc.scalar.activation(edec[:, :], ps[0:NS, b1, P - 1:S:P], ACT.Exp, scale=a_col[:, 0:1]))
                at["edec"] = A.n

            @block.vector
            def _(dve):
                dve.wait_ge(V.sem, at["span_sb"])
                at["bwa"] = link(dve, V, nc.vector.tensor_tensor(
                    bw[:, :, :], a_row[:, :].unsqueeze(1).broadcast_to([P, Q, NS]),
                    span[:, P - 1:S:P].unsqueeze(2).broadcast_to([P, Q, NS]), ALU.mult))
                for n in range(NS):
                    dve.wait_ge(exp_made.sem, n + 1)
                    dve.wait_ge(spread_made.sem, n + 1)
                    if n >= RT:
                        dve.wait_ge(summed.sem, n - RT + 1)
                    for q in range(Q):
                        cut = slice(q * P, (q + 1) * P)
                        last = nc.vector.scalar_tensor_tensor(t1[:, n % RT, cut], ex[:, n % 2, cut], bdt[:, q, n:n + 1],
                                                              ps[:, spread[n % 2], cut], ALU.mult, ALU.mult)
                    spread_read(last)
                free[b0] = free[b3] = (spread_read.sem, NS)

            @block.gpsimd
            def _(pool):
                for n in range(NS):
                    pool.wait_ge(spread_read.sem, n + 1)
                    if n == 0:
                        summed(nc.gpsimd.tensor_copy(gm[:, :], t1[:, 0, :]))
                    else:
                        pool.wait_ge(summed.sem, n)
                        summed(nc.gpsimd.tensor_tensor(gm[:, :], gm[:, :], t1[:, n % RT, :], ALU.add))
                pool.wait_ge(summed.sem, NS)
                g3 = gm[:, :].rearrange("p (q t) -> p q t", q=Q)
                summed(nc.gpsimd.tensor_tensor(g3, g3, upto[:, :].unsqueeze(1).broadcast_to([P, Q, P]), ALU.mult))

            @block.scalar
            def _(act):
                act.wait_ge(V.sem, at["bwa"])
                at["bwe"] = A(nc.scalar.activation(bw[:, :, :], bw[:, :, :], ACT.Exp))

            @block.vector
            def _(dve):
                dve.wait_ge(A.sem, at["bwe"])
                at["bw"] = V(nc.vector.tensor_tensor(bw[:, :, :], bw[:, :, :], bdt[:, :, :], ALU.mult))
                at["cw"] = V(nc.vector.tensor_tensor(cw[0:NS, :], cw[0:NS, :], cT[:, :], ALU.mult))
                free[b1] = (V.sem, V.n)

            yield

            @block.tensor
            def _(pe):
                pe.wait_ge(V.sem, at["bw"])
                pe.wait_ge(A.sem, at["xct"])
                at["u"] = T.n
                for q in range(Q - 1):
                    bank = (b2, b0, b3)[q]
                    pe.wait_ge(*free[bank])
                    T(nc.tensor.matmul(ps[0:NS, bank, :], bw[:, q, :], xct[:, q, :], start=True, stop=True))

            @block.vector
            def _(dve):
                dve.wait_ge(A.sem, at["edec"])
                for q in range(Q - 1):
                    bank = (b2, b0, b3)[q]
                    dve.wait_ge(T.sem, at["u"] + q + 1)
                    if q == 0:
                        link(dve, V, nc.vector.tensor_copy(st[0:NS, 1, :], ps[0:NS, bank, :]))
                    else:
                        link(dve, V, nc.vector.scalar_tensor_tensor(st[0:NS, q + 1, :], st[0:NS, q, :], edec[:, q:q + 1],
                                                                    ps[0:NS, bank, :], ALU.mult, ALU.add))
                    free[bank] = (V.sem, V.n)
                at["st"] = V.n

            yield

            @block.tensor
            def _(pe):
                pe.wait_ge(V.sem, at["st"])
                pe.wait_ge(summed.sem, NS + 1)
                at["y"] = T.n
                for e in range(CI):
                    pe.wait_ge(*free[4 * i + e])
                    for q in range(Q):
                        out = ps[:, 4 * i + e, q * P:(q + 1) * P]
                        last = nc.tensor.matmul(out, xct[:, q, e * P:(e + 1) * P], gm[:, q * P:(q + 1) * P],
                                                start=True, stop=q == 0)
                        if q:
                            last = nc.tensor.matmul(out, st[:, q, e * P:(e + 1) * P], cw[:, q * P:(q + 1) * P],
                                                    start=False, stop=True)
                    T(last)

            @block.vector
            def _(dve):
                dve.wait_ge(A.sem, at["zs"])
                for e in range(CI):
                    dve.wait_ge(T.sem, at["y"] + e + 1)
                    link(dve, V, nc.vector.scalar_tensor_tensor(yg[:, e, :], xc[:, e, :], skip[:, e:e + 1], ps[:, 4 * i + e, :],
                                                                ALU.mult, ALU.add))
                    free[4 * i + e] = (V.sem, V.n)
                    V(nc.vector.tensor_tensor(yg[:, e, :], yg[:, e, :], zs[:, e, :], ALU.mult))
                at["yg"] = V.n

            @block.tensor
            def _(pe):
                pe.wait_ge(V.sem, at["yg"])
                at["out"] = T.n
                for q in range(Q):
                    if q % 2 == 0:
                        pe.wait_ge(*free[4 * i + q // 2])
                    for e in range(CI):
                        last = nc.tensor.matmul(ps[:, 4 * i + q // 2, q % 2 * DM:(q % 2 + 1) * DM], yg[:, e, q * P:(q + 1) * P],
                                                w_out[:, e, :], start=e == 0, stop=e == CI - 1)
                    T(last)

            @block.scalar
            def _(act):
                for q in range(0, Q, 2):
                    act.wait_ge(T.sem, at["out"] + q + 2)
                    A(nc.scalar.copy(so[:, q:q + 2, :], ps[:, 4 * i + q // 2, :]))
                at["so"] = A.n

            @block.sync
            def _(sp):
                sp.wait_ge(V.sem, at["picked"])
                stored(sp.dma_start(d["picked"][b], pr[:, :]), 16)
                sp.wait_ge(A.sem, at["so"])
                stored(sp.dma_start(d["s0"][b].rearrange("(q p) e -> p q e", p=P), so[:, :, :]), 16)
                sp.wait_ge(stored.sem, 32)
            job.done = [(c.sem, c.n) for c in (V, A, T, stored, summed)]

        seqs = []
        loop = run_sequences(nc, ph, sequence, count, min(count, SEQS), LAG_A)
        next(loop)

        with nc.Block() as block:
            @block.scalar
            def _(act):
                A(nc.scalar.activation(a_row[:, :], a_row[:, :], ACT.Exp))
                A(nc.scalar.activation(a_col[:, :], a_col[:, :], ACT.Exp))

            @block.vector
            def _(dve):
                dve.wait_ge(A.sem, 2)
                V(nc.vector.tensor_scalar(a_row[:, :], a_row[:, :], -1.0, None, ALU.mult))
                V(nc.vector.tensor_scalar(a_col[:, :], a_col[:, :], -1.0, None, ALU.mult))

            @block.gpsimd
            def _(pool):
                link(pool, G, nc.gpsimd.memset(pick[:, :, :], 0.0))
                for part in range(3):
                    rows = pick[32 * part:32 * part + 32, :, :]
                    link(pool, G, nc.gpsimd.affine_select(out=rows, in_=rows, compare_op=ALU.not_equal, fill=1.0,
                                                          base=0, pattern=[[-1, NS], [0, P]], channel_multiplier=1))
                for c3, st, cw in seqs:
                    link(pool, G, nc.gpsimd.memset(c3[:, :], 0.0))
                    link(pool, G, nc.gpsimd.memset(st[:, :, :], 0.0))
                    link(pool, G, nc.gpsimd.memset(cw[:, :], 0.0))
        ph.clear()

        next(loop, None)


H0 = 1024
EG = 4
HK = H0 // P


def phase_b(nc, c, d, mergedT, count=E0 // EG):
    with ExitStack() as ctx:
        ph = Phase(nc, ctx, "b")
        ps = ph.psum()
        ident = c["ident"]
        w1 = ph.sb("w1", [P, EG, KD, H0])
        w2 = ph.sb("w2", [P, EG, HK, DM])
        w1b = ph.sb("w1b", [B, EG, H0])
        w2b = ph.sb("w2b", [B, EG, DM])
        mt = ph.sb("mt", [P, KD, EG, B])
        hb = ph.sb("hb", [B, 2, H0])
        h = ph.sb("h", [B, 2, H0])
        hT = ph.sb("hT", [P, 2, HK, B])
        o = ph.sb("o", [B, EG, DM])
        V, T = ph.counter("vector_done"), ph.counter("tensor_done")
        w1_in = [ph.counter(f"w1_in{j}") for j in range(EG)]
        w2_in = [ph.counter(f"w2_in{j}") for j in range(EG)]
        hidden_made, biased, hidden_done, turned_made, turned, out_made, out_done, stored = (ph.counter(n) for n in (
            "hidden_made", "biased", "hidden_done", "turned_made", "turned", "out_made", "out_done", "stored"))
        with nc.Fori(0, count) as g:
            with nc.Block() as block:
                @block.sync
                def _(sp):
                    for j in range(EG):
                        w1_in[j](sp.dma_start(w1[:, j, :, :], d["w1_0"][g * EG + j, 0:DM].rearrange("(k p) h -> p k h", p=P)), 16)
                        w1_in[j](sp.dma_start(w1b[:, j, :], d["w1_0"][g * EG + j, DM].partition_broadcast(B)), 16)
                        w2_in[j](sp.dma_start(w2[:, j, :, :], d["w2_0"][g * EG + j, 0:H0].rearrange("(k p) h -> p k h", p=P)), 16)
                        w2_in[j](sp.dma_start(w2b[:, j, :], d["w2_0"][g * EG + j, H0].partition_broadcast(B)), 16)
                    sp.wait_ge(out_done.sem, EG)
                    stored(sp.dma_start(d["o0"][:, bass.ds(g * EG, EG), :], o[:, :, :]), 16)
                    sp.wait_ge(stored.sem, 16)

                @block.tensor
                def _(pe):
                    def hidden(j):
                        pe.wait_ge(w1_in[j].sem, 32)
                        if j >= 2:
                            pe.wait_ge(biased.sem, j - 1)
                        for half in range(2):
                            out = ps[0:B, 2 * (j % 2) + half, :]
                            cols = slice(half * 512, half * 512 + 512)
                            for k in range(KD):
                                last = nc.tensor.matmul(out, mt[:, k, j, :], w1[:, j, k, cols], start=k == 0, stop=k == KD - 1)
                        hidden_made(last)

                    pe.wait_ge(V.sem, 1)
                    hidden(0)
                    for j in range(EG):
                        if j + 1 < EG:
                            hidden(j + 1)
                        pe.wait_ge(hidden_done.sem, j + 1)
                        if j >= 2:
                            pe.wait_ge(turned.sem, j - 1)
                        for k in range(HK):
                            last = nc.tensor.transpose(ps[:, 4 + j % 2, k * B:(k + 1) * B], h[:, j % 2, k * P:(k + 1) * P],
                                                       ident[0:B, 0:B])
                        turned_made(last)
                        pe.wait_ge(turned.sem, j + 1)
                        pe.wait_ge(w2_in[j].sem, 32)
                        if j >= 2:
                            pe.wait_ge(out_done.sem, j - 1)
                        out = ps[0:B, 6 + j % 2, 0:DM]
                        for k in range(HK):
                            last = nc.tensor.matmul(out, hT[:, j % 2, k, :], w2[:, j, k, :], start=k == 0, stop=k == HK - 1)
                        out_made(last)

                @block.scalar
                def _(act):
                    for j in range(EG):
                        act.wait_ge(biased.sem, j + 1)
                        if j >= 2:
                            act.wait_ge(turned_made.sem, j - 1)
                        hidden_done(nc.scalar.activation(h[:, j % 2, :], hb[:, j % 2, :], ACT.Gelu))

                @block.vector
                def _(dve):
                    V(nc.vector.tensor_copy(mt[:, :, :, :], mergedT[:, :, bass.ds(g * EG, EG), :]))
                    def bias(j):
                        dve.wait_ge(w1_in[j].sem, 32)
                        dve.wait_ge(hidden_made.sem, j + 1)
                        if j >= 2:
                            dve.wait_ge(hidden_done.sem, j - 1)
                        b0 = 2 * (j % 2)
                        biased(nc.vector.tensor_tensor(hb[:, j % 2, :].rearrange("p (a n) -> p a n", a=2), ps[0:B, b0:b0 + 2, :],
                                                       w1b[:, j, :].rearrange("p (a n) -> p a n", a=2), ALU.add))

                    bias(0)
                    for j in range(EG):
                        if j + 1 < EG:
                            bias(j + 1)
                        dve.wait_ge(turned_made.sem, j + 1)
                        if j >= 2:
                            dve.wait_ge(out_made.sem, j - 1)
                        turned(nc.vector.tensor_copy(hT[:, j % 2, :, :], ps[:, 4 + j % 2, 0:HK * B]))
                        dve.wait_ge(w2_in[j].sem, 32)
                        dve.wait_ge(out_made.sem, j + 1)
                        out_done(nc.vector.tensor_tensor(o[:, j, :], ps[0:B, 6 + j % 2, 0:DM], w2b[:, j, :], ALU.add))
            ph.clear()


HEADS, HD = 16, 8
HV = 2 * HD
LAMBDA_INIT = 0.8 - 0.6
SPLIT = 3
PRODUCTS = ((0, 0), (0, 1), (1, 0), (1, 1), (0, 2), (2, 0))
KROWS = len(PRODUCTS) * HD
SROWS = 2 * KROWS
AROWS = SROWS + 2 * SPLIT
GH = 4
NG = HEADS // GH
UNITS = HEADS * Q
LAG = 2 * GH * Q // 2 + 5
RING = 6


def phase_c1(nc, c, d, count=B):
    with ExitStack() as ctx:
        ph = Phase(nc, ctx, "c1")
        ps = ph.psum()
        ident = c["ident"]
        w_qkv = ph.sb("w_qkv", [P, KD, 3 * DM])
        w_proj = ph.sb("w_proj", [P, KD, DM])
        b_proj = ph.sb("b_proj", [P, DM])
        w_sub = ph.sb("w_sub", [P, HV])
        lams = ph.sb("lams", [P, 4, HD])
        load_once(nc, ph, [
            (w_qkv[:, :, :], d["w_qkv"].rearrange("(k p) e -> p k e", p=P)),
            (w_proj[:, :, :], d["w_proj"].rearrange("(k p) e -> p k e", p=P)),
            (b_proj[:, :], d["b_proj"].partition_broadcast(P)),
            (w_sub[:, :], d["sub_norm_w"].partition_broadcast(P)),
        ] + [(lams[:, i, :], d[n].partition_broadcast(P)) for i, n in enumerate(
            ("lambda_q1", "lambda_k1", "lambda_q2", "lambda_k2"))])
        V, A, T, G = (ph.counter(n) for n in ("vector_done", "scalar_done", "tensor_done", "pool_done"))
        lp = ph.sb("lp", [P, 2, HD])
        le = ph.sb("le", [P, 2])
        lam = ph.sb("lam", [P, 1])
        identb = ph.sb("identb", [P, P], BF16)
        qs = ph.sb("qs", [AROWS, HEADS, S], BF16)
        ks = ph.sb("ks", [AROWS, 2, HEADS, S], BF16)
        v1 = ph.sb("v1", [P, Q, HEADS, 32])

        with nc.Block() as block:
            @block.vector
            def _(dve):
                V(nc.vector.memset(ks[0:SROWS, :, :, :], 0.0))
                V(nc.vector.memset(qs[:, :, :], 0.0))
                V(nc.vector.memset(v1[:, :, :, HV:], 0.0))
                V(nc.vector.tensor_copy(identb[:, :], ident[:, :]))
                V(nc.vector.tensor_scalar(w_sub[:, :], w_sub[:, :], 1.0 - LAMBDA_INIT, None, ALU.mult))
                link(dve, V, nc.vector.tensor_tensor(lp[:, :, :], lams[:, 0:4:2, :], lams[:, 1:4:2, :], ALU.mult))
                V(nc.vector.memset(v1[:, :, :, HV:HV + 1], 1.0))
                link(dve, V, nc.vector.tensor_reduce(le[:, :], lp[:, :, :], AX.X, ALU.add))

            @block.gpsimd
            def _(pool):
                rows = ks[SROWS:AROWS]
                link(pool, G, nc.gpsimd.memset(rows[:, :, :, :], 1.0))
                for half, base, mult in ((0, SPLIT - 1, -1), (1, -SPLIT, 1)):
                    link(pool, G, nc.gpsimd.affine_select(out=rows[:, half], in_=rows[:, half], compare_op=ALU.is_ge, fill=0.0, base=base,
                                                          pattern=[[0, HEADS], [0, S]], channel_multiplier=mult))

            @block.scalar
            def _(act):
                act.wait_ge(V.sem, V.n)
                A(nc.scalar.activation(le[:, :], le[:, :], ACT.Exp))

            @block.vector
            def _(dve):
                dve.wait_ge(A.sem, 1)
                V(nc.vector.scalar_tensor_tensor(lam[:, :], le[:, 0:1], LAMBDA_INIT, le[:, 1:2], ALU.add, ALU.subtract))
        ph.clear()

        x = ph.sb("x", [P, Q, DM])
        s0 = ph.sb("s0", [P, Q, DM])
        pick = ph.sb("pick", [E0, S])
        o0 = ph.sb("o0", [E0, DM])
        g0 = ph.sb("g0", [P, Q, DM])
        xn = ph.sb("xn", [P, Q, DM])
        xnT = ph.sb("xnT", [P, KD, S])
        nm = Norm(ph, "ln")
        parts = ph.sb("parts", [P, 4, SPLIT, S], BF16)
        rem = ph.sb("rem", [P, 2, S])
        mx = ph.sb("mx", [P, 2, Q, 2, GH])
        mrem = ph.sb("mrem", [P, 2, Q, 2, GH])
        mparts = ph.sb("mparts", [P, 2, Q, 2, SPLIT, GH], BF16)
        mT = ph.sb("mT", [2 * SPLIT * GH, 2, S], BF16)
        pT = ph.sb("pT", [P, RING, 2, S])
        ao = ph.sb("ao", [P, 2, S])
        ot = ph.sb("ot", [P, Q, HEADS, 2, 32])
        rr = ph.sb("rr", [P, Q * HEADS, 2])
        oh = ph.sb("oh", [P, Q * HEADS, HV])
        o2 = ph.sb("o2", [P, Q * HEADS, HV])
        ms = ph.sb("ms", [P, Q * HEADS])
        oT = ph.sb("oT", [P, KD, S])
        so = ph.sb("so", [P, Q, DM])
        ins = {n: ph.counter(n) for n in ("x_in", "s0_in", "pick_in", "qk_in", "max_in0", "max_in1")}
        max_in = [ins["max_in0"], ins["max_in1"]]
        parts_out, stored = ph.counter("parts_out"), ph.counter("stored")
        maxrem = ph.counter("max_remainder")
        (score_made, score_read, maxT_made, maxT_done, logit_made, prob_made, mixed, mixed_read, turned_made,
         turned_read) = (ph.counter(n) for n in (
             "score_made", "score_read", "maxT_made", "maxT_done", "logit_made", "prob_made", "mixed", "mixed_read",
             "turned_made", "turned_read"))

        with nc.Fori(0, count) as b:
            free, at = {}, {}
            with nc.Block() as block:
                @block.sync
                def _(sp):
                    ins["pick_in"](sp.dma_start(pick[:, :], d["picked"][b]), 16)
                    ins["pick_in"](sp.dma_start(o0[:, :], d["o0"][b]), 16)
                    ins["x_in"](sp.dma_start(x[:, :, :], d["x"][b].rearrange("(q p) e -> p q e", p=P)), 16)
                    ins["s0_in"](sp.dma_start(s0[:, :, :], d["s0"][b].rearrange("(q p) e -> p q e", p=P)), 16)

                @block.tensor
                def _(pe):
                    pe.wait_ge(ins["pick_in"].sem, 32)
                    for q in range(Q):
                        last = nc.tensor.matmul(ps[:, q // 2, q % 2 * DM:(q % 2 + 1) * DM], pick[:, q * P:(q + 1) * P], o0[:, :],
                                                start=True, stop=True)
                    at["ffn0"] = T(last)

                @block.scalar
                def _(act):
                    act.wait_ge(T.sem, at["ffn0"])
                    at["g0"] = A(nc.scalar.activation(g0[:, :, :], ps[:, 0:2, :], ACT.Silu))
                    free[0] = free[1] = (A.sem, A.n)

                @block.vector
                def _(dve):
                    dve.wait_ge(A.sem, at["g0"])
                    dve.wait_ge(ins["s0_in"].sem, 16)
                    dve.wait_ge(ins["x_in"].sem, 16)
                    link(dve, V, nc.vector.tensor_tensor(g0[:, :, :], g0[:, :, :], s0[:, :, :], ALU.mult))
                    at["x1"] = V(nc.vector.tensor_tensor(x[:, :, :], x[:, :, :], g0[:, :, :], ALU.add))

                n = layer_norm(nc, block, nm, x, xn, V, A, (V.sem, at["x1"]))
                at["xn"] = n
                at["xnT"] = transpose_rows(nc, block, ps, [0, 1], ident, xn, xnT, T, V, (V.sem, n), free)

                @block.tensor
                def _(pe):
                    pe.wait_ge(*at["xnT"])
                    at["qk"] = T.n
                    for e in range(4):
                        for k in range(KD):
                            last = nc.tensor.matmul(ps[:, 2 + e, :], w_qkv[:, k, e * P:(e + 1) * P], xnT[:, k, :],
                                                    start=k == 0, stop=k == KD - 1)
                        T(last)
                    for q in range(Q):
                        for k in range(KD):
                            last = nc.tensor.matmul(ps[:, 6 + q // 2, q % 2 * DM:(q % 2 + 1) * DM], xnT[:, k, q * P:(q + 1) * P],
                                                    w_qkv[:, k, 2 * DM:], start=k == 0, stop=k == KD - 1)
                    at["v"] = T(last)

                @block.scalar
                def _(act):
                    base = V.n
                    for e in range(4):
                        act.wait_ge(T.sem, at["qk"] + e + 1)
                        A(nc.scalar.copy(parts[:, e, 0, :], ps[:, 2 + e, :]))
                    at["hi"] = A.n - 4
                    for e in range(4):
                        act.wait_ge(V.sem, base + 2 * e + 1)
                        A(nc.scalar.copy(parts[:, e, 1, :], rem[:, e % 2, :]))
                    at["mid"] = A.n - 4

                @block.vector
                def _(dve):
                    for e in range(4):
                        dve.wait_ge(A.sem, at["hi"] + e + 1)
                        V(nc.vector.tensor_tensor(rem[:, e % 2, :], ps[:, 2 + e, :], parts[:, e, 0, :], ALU.subtract))
                        free[2 + e] = (V.sem, V.n)
                        dve.wait_ge(V.sem, V.n)
                        dve.wait_ge(A.sem, at["mid"] + e + 1)
                        link(dve, V, nc.vector.tensor_tensor(parts[:, e, 2, :], rem[:, e % 2, :], parts[:, e, 1, :], ALU.subtract))
                    at["parts"] = V.n
                    dve.wait_ge(T.sem, at["v"])
                    for q in range(0, Q, 2):
                        V(nc.vector.tensor_copy(v1[:, q:q + 2, :, 0:HV],
                                                ps[:, 6 + q // 2, :].rearrange("p (q h e) -> p q h e", q=2, h=HEADS)))
                    at["v1"] = V.n
                    free[6] = free[7] = (V.sem, V.n)

                @block.sync
                def _(sp):
                    sp.wait_ge(V.sem, at["x1"])
                    stored(sp.dma_start(d["x1"][b].rearrange("(q p) e -> p q e", p=P), x[:, :, :]), 16)
                    sp.wait_ge(V.sem, at["xn"])
                    stored(sp.dma_start(d["xn1"][b].rearrange("(q p) e -> p q e", p=P), xn[:, :, :]), 16)
                    sp.wait_ge(V.sem, at["parts"])
                    for e in range(4):
                        parts_out(sp.dma_start(d["qk_parts"][e].rearrange("s p n -> p s n"), parts[:, e, :, :]), 16)
                    sp.wait_ge(parts_out.sem, 64)

                def gather(queue, side, tile):
                    for half in range(2):
                        for r, pair in enumerate(PRODUCTS):
                            row = KROWS * half + HD * r
                            dst = tile(half)[row:row + HD]
                            part = pair[1] if side == 0 else pair[0]
                            for blk in range(2):
                                src = d["qk_parts"][2 * side + blk, part].rearrange("(h c r) n -> c r h n", c=2, r=HD)[half]
                                ins["qk_in"](queue.dma_start(dst[:, 8 * blk:8 * blk + 8, :], src), 16)

                @block.sync
                def _(sp):
                    gather(sp, 0, lambda half: qs)

                @block.scalar
                def _(act):
                    act.wait_ge(parts_out.sem, 64)
                    gather(act, 1, lambda half: ks[:, half])

                def unit(u):
                    pair, m, i = u // (2 * Q), u // 2 % Q, u % 2
                    return 2 * pair + i, m

                STEPS = UNITS + LAG

                def g_before(p):
                    return sum(1 for g in range(NG) if 16 * (g + 1) + 1 <= LAG + 12 + 8 * p)

                def g_turned(g):
                    return sum(1 for p in range(HEADS // 2) if LAG + 12 + 8 * p < 16 * (g + 1) + 1)

                @block.tensor
                def _(pe):
                    pe.wait_ge(ins["qk_in"].sem, ins["qk_in"].n)
                    for bank in range(8):
                        if bank in free:
                            pe.wait_ge(*free[bank])
                    pe.wait_ge(V.sem, at["v1"])

                    def score(k):
                        if k >= 2:
                            pe.wait_ge(score_read.sem, k - 1)
                        hc, j = k // Q, k % Q
                        head, half = hc // 2, hc % 2
                        score_made(nc.tensor.matmul(ps[:, k % 2, :], qs[0:SROWS, head, j * P:(j + 1) * P], ks[0:SROWS, half, head, :],
                                                    start=True, stop=True))

                    def turn_max(g):
                        pe.wait_ge(V.sem, at["v1"] + 3 * (g + 1))
                        if g >= 1:
                            pe.wait_ge(turned_read.sem, g_turned(g))
                            pe.wait_ge(maxT_done.sem, g)
                        psb = ps[:, 7, :].bitcast(BF16)
                        for j in range(Q):
                            last = nc.tensor.transpose(psb[0:2 * SPLIT * GH, j * P:(j + 1) * P],
                                                       mparts[:, g % 2, j, :, :, :].rearrange("p a b c -> p (a b c)"),
                                                       identb[:, :])
                        maxT_made(last)

                    def logits(u):
                        head, m = unit(u)
                        if u % (GH * Q) == 0:
                            g = u // (GH * Q)
                            pe.wait_ge(max_in[g % 2].sem, 32 * (g // 2 + 1))
                        if u >= 2:
                            pe.wait_ge(prob_made.sem, u - 1)
                        for half in range(2):
                            last = nc.tensor.matmul(ps[:, 2 + 2 * (u % 2) + half, :], ks[:, half, head, m * P:(m + 1) * P],
                                                    qs[:, head, :], start=True, stop=True)
                        logit_made(last)

                    def mix(w):
                        m = w % Q
                        pe.wait_ge(prob_made.sem, 2 * w + 2)
                        if m == 0 and w >= Q:
                            pe.wait_ge(mixed_read.sem, w // Q)
                        for i in range(2):
                            head, _ = unit(2 * w + i)
                            for half in range(2):
                                row = 32 * (2 * i + half)
                                last = nc.tensor.matmul(ps[row:row + 32, 6, :], v1[:, m, head, :],
                                                        pT[:, (2 * w + i) % RING, half, :], start=m == 0, stop=m == Q - 1,
                                                        skip_group_check=True)
                        mixed(last)

                    def turn_pair(p):
                        pe.wait_ge(mixed_read.sem, p + 1)
                        if p >= 1:
                            pe.wait_ge(turned_read.sem, p)
                        pe.wait_ge(maxT_done.sem, min(NG, g_before(p)))
                        for j in range(Q):
                            last = nc.tensor.transpose(ps[:, 7, j * P:(j + 1) * P], ao[:, p % 2, j * P:(j + 1) * P], ident[:, :])
                        turned_made(last)

                    for s in range(STEPS + 6):
                        for k in (2 * s, 2 * s + 1):
                            if k < 2 * UNITS:
                                score(k)
                        if s % (2 * GH * Q // 2) == 1 and 1 < s <= UNITS + 1:
                            turn_max(s // (2 * GH * Q // 2) - 1)
                        u = s - LAG
                        if 0 <= u < UNITS:
                            logits(u)
                        if u >= 3 and (u - 3) % 2 == 0 and (u - 3) // 2 < UNITS // 2:
                            mix((u - 3) // 2)
                        if u >= 12 and (u - 12) % 8 == 0 and (u - 12) // 8 < HEADS // 2:
                            turn_pair((u - 12) // 8)

                @block.scalar
                def _(act):
                    for u in range(UNITS + 8):
                        if u < UNITS:
                            act.wait_ge(logit_made.sem, u + 1)
                            if u >= RING:
                                act.wait_ge(mixed.sem, (u - RING) // 2 + 1)
                            b0 = 2 + 2 * (u % 2)
                            prob_made(nc.scalar.activation(pT[:, u % RING, :, :], ps[:, b0:b0 + 2, :], ACT.Exp, scale=HD ** -0.5))
                        if u >= 10 and (u - 10) % 8 == 0 and (u - 10) // 8 < HEADS // 2:
                            p = (u - 10) // 8
                            act.wait_ge(mixed.sem, Q * (p + 1))
                            if p >= 2:
                                act.wait_ge(turned_made.sem, p - 1)
                            mixed_read(nc.scalar.copy(ao[:, p % 2, :], ps[:, 6, :]))

                @block.vector
                def _(dve):
                    def maximum(k):
                        dve.wait_ge(score_made.sem, k + 1)
                        hc, j = k // Q, k % Q
                        head, half = hc // 2, hc % 2
                        score_read(nc.vector.tensor_reduce(mx[:, head // GH % 2, j, half, head % GH:head % GH + 1], ps[:, k % 2, :],
                                                           AX.X, ALU.max, negate=True))

                    def split_max(g):
                        m, r = mx[:, g % 2], mrem[:, g % 2]
                        hi, mid, lo = (mparts[:, g % 2, :, :, i, :] for i in range(SPLIT))
                        dve.wait_ge(score_read.sem, 2 * GH * Q * (g + 1))
                        link(dve, V, nc.vector.tensor_copy(hi, m))
                        k = link(dve, maxrem, nc.vector.tensor_tensor(r, m, hi, ALU.subtract))
                        link(dve, V, nc.vector.tensor_copy(mid, r))
                        V(nc.vector.tensor_tensor(lo, r, mid, ALU.subtract))

                    def store_max(g):
                        dve.wait_ge(maxT_made.sem, g + 1)
                        if g >= 2:
                            dve.wait_ge(max_in[g % 2].sem, 32 * (g // 2))
                        psb = ps[:, 7, :].bitcast(BF16)
                        maxT_done(nc.vector.tensor_copy(mT[:, g % 2, :], psb[0:2 * SPLIT * GH, 0:S]))

                    def turned(p):
                        dve.wait_ge(turned_made.sem, p + 1)
                        turned_read(nc.vector.tensor_copy(
                            ot[:, :, 2 * p:2 * p + 2, :, :].rearrange("p q h c e -> p q (h c e)"),
                            ps[:, 7, :].rearrange("p (q r) -> p q r", q=Q)))

                    for s in range(STEPS + 6):
                        for k in (2 * s, 2 * s + 1):
                            if k < 2 * UNITS:
                                maximum(k)
                        if s % 16 == 15 and s < UNITS:
                            split_max(s // 16)
                        if s % 16 == 1 and 1 < s <= UNITS + 1:
                            store_max(s // 16 - 1)
                        u = s - LAG
                        if u >= 12 and (u - 12) % 8 == 0 and (u - 12) // 8 < HEADS // 2:
                            turned((u - 12) // 8)
                    at["ot"] = HEADS // 2

                @block.sync
                def _(sp):
                    for g in range(NG):
                        sp.wait_ge(maxT_done.sem, g + 1)
                        for half in range(2):
                            n = SPLIT * GH
                            row = SROWS + SPLIT * half
                            max_in[g % 2](sp.dma_start(qs[row:row + SPLIT, GH * g:GH * (g + 1), :],
                                                       mT[n * half:n * (half + 1), g % 2, :]), 16)

                @block.vector
                def _(dve):
                    dve.wait_ge(turned_read.sem, HEADS // 2)
                    o5 = ot[:, :, :, :, :].rearrange("p q h c e -> p (q h) c e")
                    link(dve, V, nc.vector.reciprocal(rr[:, :, :], o5[:, :, :, HV]))
                    link(dve, V, nc.vector.tensor_scalar(rr[:, :, 1], rr[:, :, 1], lam[:, 0:1], None, ALU.mult))
                    bc = [P, Q * HEADS, HV]
                    V(nc.vector.tensor_tensor(oh[:, :, :], o5[:, :, 0, 0:HV], rr[:, :, 0:1].broadcast_to(bc), ALU.mult))
                    link(dve, V, nc.vector.tensor_tensor(o2[:, :, :], o5[:, :, 1, 0:HV], rr[:, :, 1:2].broadcast_to(bc), ALU.mult))
                    link(dve, V, nc.vector.tensor_tensor(oh[:, :, :], oh[:, :, :], o2[:, :, :], ALU.subtract))
                    link(dve, V, nc.vector.tensor_tensor(o2[:, :, :], oh[:, :, :], oh[:, :, :], ALU.mult))
                    link(dve, V, nc.vector.tensor_reduce(ms[:, :], o2[:, :, :], AX.X, ALU.add))
                    at["ms"] = link(dve, V, nc.vector.tensor_scalar(ms[:, :], ms[:, :], 1.0 / HV, EPS, ALU.mult, ALU.add))

                @block.scalar
                def _(act):
                    act.wait_ge(V.sem, at["ms"])
                    at["rms"] = A(nc.scalar.activation(ms[:, :], ms[:, :], ACT.Sqrt))

                @block.vector
                def _(dve):
                    bc = [P, Q * HEADS, HV]
                    dve.wait_ge(A.sem, at["rms"])
                    link(dve, V, nc.vector.reciprocal(ms[:, :], ms[:, :]))
                    link(dve, V, nc.vector.tensor_tensor(oh[:, :, :], oh[:, :, :], ms[:, :].unsqueeze(2).broadcast_to(bc), ALU.mult))
                    at["o"] = link(dve, V, nc.vector.tensor_tensor(
                        oh[:, :, :], oh[:, :, :], w_sub[:, :].unsqueeze(1).broadcast_to(bc), ALU.mult))

                free.clear()
                free[0] = free[1] = (score_read.sem, 2 * UNITS)
                oq = oh[:, :, :].rearrange("p (q h) e -> p q (h e)", q=Q)
                at["oT"] = transpose_rows(nc, block, ps, [0, 1], ident, oq, oT, T, V, (V.sem, at["o"]), free)

                @block.tensor
                def _(pe):
                    pe.wait_ge(*at["oT"])
                    pe.wait_ge(prob_made.sem, UNITS)
                    for q in range(Q):
                        for k in range(KD):
                            last = nc.tensor.matmul(ps[:, 2 + q // 2, q % 2 * DM:(q % 2 + 1) * DM], oT[:, k, q * P:(q + 1) * P],
                                                    w_proj[:, k, :], start=k == 0, stop=k == KD - 1)
                    at["s1"] = T(last)

                @block.vector
                def _(dve):
                    dve.wait_ge(T.sem, at["s1"])
                    at["so"] = V(nc.vector.tensor_tensor(
                        so[:, :, :], ps[:, 2:4, :].rearrange("p a (q e) -> p (a q) e", q=2),
                        b_proj[:, :].unsqueeze(1).broadcast_to([P, Q, DM]), ALU.add))

                @block.sync
                def _(sp):
                    sp.wait_ge(V.sem, at["so"])
                    stored(sp.dma_start(d["s1"][b].rearrange("(q p) e -> p q e", p=P), so[:, :, :]), 16)
                    sp.wait_ge(stored.sem, 48)
            ph.clear()


E1, H1 = 8, 4 * DM
HK1 = H1 // P
MB = B // E1


def phase_c2(nc, c, d, count=E1):
    with ExitStack() as ctx:
        ph = Phase(nc, ctx, "c2")
        ps = ph.psum()
        ident = c["ident"]
        w_attn = ph.sb("w_attn", [P, KD, DM])
        w_next = ph.sb("w_next", [P, KD, DM])
        b_next = ph.sb("b_next", [P, DM])
        cols = {n: ph.sb(n, [P, KD]) for n in ("ln_scale", "ln_bias", "attn_b")}
        load_once(nc, ph, [
            (w_attn[:, :, :], d["attn_w"].rearrange("(k p) e -> p k e", p=P)),
            (w_next[:, :, :], d["next_w"].rearrange("(k p) e -> p k e", p=P)),
            (b_next[:, :], d["next_b"].partition_broadcast(P)),
        ] + [(t[:, :], d[n]) for n, t in cols.items()])
        V, A, T = (ph.counter(n) for n in ("vector_done", "scalar_done", "tensor_done"))
        w1 = ph.sb("w1", [P, KD, H1])
        w2 = ph.sb("w2", [P, HK1, DM])
        b1 = ph.sb("b1", [P, HK1])
        b2 = ph.sb("b2", [P, KD])
        nm = Norm(ph, "ln")
        f = ph.sb("f", [P, MB, Q, DM])
        z = ph.sb("z", [P, MB, Q, DM])
        fT = ph.sb("fT", [P, MB, KD, S])
        zT = ph.sb("zT", [P, MB, KD, S])
        hT = ph.sb("hT", [P, HK1, S])
        eT = ph.sb("eT", [P, KD, S])
        x1 = ph.sb("x1", [P, MB, Q, DM])
        s1 = ph.sb("s1", [P, MB, Q, DM])
        g = ph.sb("g", [P, Q, DM])
        w_in, stored = ph.counter("w_in"), ph.counter("stored")
        f_in, x1_in, s1_in = ([ph.counter(f"{n}{i}") for i in range(MB)] for n in ("f_in", "x1_in", "s1_in"))
        hidden_made, hidden_done = ph.counter("hidden_made"), ph.counter("hidden_done")
        RH = 4
        with nc.Fori(0, count) as e:
            free, at = {}, {}
            with nc.Block() as block:
                @block.sync
                def _(sp):
                    tiles = lambda n, i: d[n][e + i * E1].rearrange("(q p) e -> p q e", p=P)
                    for i in range(MB):
                        f_in[i](sp.dma_start(f[:, i, :, :], tiles("xn1", i)), 16)
                    w_in(sp.dma_start(w1[:, :, :], d["w1_1"][e].rearrange("(k p) h -> p k h", p=P)), 16)
                    w_in(sp.dma_start(w2[:, :, :], d["w2_1"][e].rearrange("(k p) h -> p k h", p=P)), 16)
                    w_in(sp.dma_start(b1[:, :], d["b1_1"][e]), 16)
                    w_in(sp.dma_start(b2[:, :], d["b2_1"][e]), 16)
                    for i in range(MB):
                        x1_in[i](sp.dma_start(x1[:, i, :, :], tiles("x1", i)), 16)
                        s1_in[i](sp.dma_start(s1[:, i, :, :], tiles("s1", i)), 16)

                for i in range(MB):
                    n = layer_norm(nc, block, nm, f[:, i, :, :], z[:, i, :, :], V, A, (f_in[i].sem, 16))
                    at["fT", i] = transpose_rows(nc, block, ps, [0, 1], ident, f[:, i, :, :], fT[:, i, :, :], T, A,
                                                 (f_in[i].sem, 16), free, eng="scalar")

                    @block.tensor
                    def _(pe):
                        pe.wait_ge(V.sem, n)
                        for k in range(KD):
                            if 2 + k in free:
                                pe.wait_ge(*free[2 + k])
                            for q in range(Q):
                                last = nc.tensor.transpose(ps[:, 2 + k, q * P:(q + 1) * P], z[:, i, q, k * P:(k + 1) * P],
                                                           ident[:, :])
                            T(last)
                        at["zT_ps"] = T.n

                    @block.vector
                    def _(dve):
                        for k in range(KD):
                            dve.wait_ge(T.sem, at["zT_ps"] - 1 + k)
                            V(nc.vector.tensor_scalar(zT[:, i, k, :], ps[:, 2 + k, :], cols["ln_scale"][:, k:k + 1],
                                                      cols["ln_bias"][:, k:k + 1], ALU.mult, ALU.add))
                            free[2 + k] = (V.sem, V.n)
                        at["zT", i] = V.n

                for i in range(MB):
                    @block.tensor
                    def _(pe):
                        pe.wait_ge(V.sem, at["zT", i])
                        for e2 in range(KD):
                            pe.wait_ge(*free[e2 + 2 * i])
                            for k in range(KD):
                                last = nc.tensor.matmul(ps[:, e2 + 2 * i, :], w_attn[:, k, e2 * P:(e2 + 1) * P], zT[:, i, k, :],
                                                        start=k == 0, stop=k == KD - 1)
                            T(last)
                        at["xa_ps"] = T.n

                    @block.vector
                    def _(dve):
                        dve.wait_ge(*at["fT", i])
                        for e2 in range(KD):
                            dve.wait_ge(T.sem, at["xa_ps"] - 1 + e2)
                            V(nc.vector.scalar_tensor_tensor(fT[:, i, e2, :], ps[:, e2 + 2 * i, :], cols["attn_b"][:, e2:e2 + 1],
                                                             fT[:, i, e2, :], ALU.add, ALU.add))
                            free[e2 + 2 * i] = (V.sem, V.n)
                        at["xa", i] = V.n

                for i in range(MB):
                    @block.tensor
                    def _(pe):
                        pe.wait_ge(V.sem, at["xa", i])
                        if i == 0:
                            pe.wait_ge(w_in.sem, 64)
                        for h in range(HK1):
                            n = i * HK1 + h
                            if n >= RH:
                                pe.wait_ge(hidden_done.sem, n - RH + 1)
                            for k in range(KD):
                                last = nc.tensor.matmul(ps[:, 4 + n % RH, :], w1[:, k, h * P:(h + 1) * P], fT[:, i, k, :],
                                                        start=k == 0, stop=k == KD - 1)
                            hidden_made(last)
                        for e2 in range(KD):
                            pe.wait_ge(*free[e2])
                            for h in range(HK1):
                                pe.wait_ge(hidden_done.sem, i * HK1 + h + 1)
                                last = nc.tensor.matmul(ps[:, e2, :], w2[:, h, e2 * P:(e2 + 1) * P], hT[:, h, :],
                                                        start=h == 0, stop=h == HK1 - 1)
                            T(last)
                        at["eT_ps"] = T.n

                    @block.scalar
                    def _(act):
                        if i:
                            act.wait_ge(T.sem, at["hT_read"])
                        else:
                            act.wait_ge(w_in.sem, 64)
                        for h in range(HK1):
                            n = i * HK1 + h
                            act.wait_ge(hidden_made.sem, n + 1)
                            hidden_done(nc.scalar.activation(hT[:, h, :], ps[:, 4 + n % RH, :], ACT.Gelu, bias=b1[:, h:h + 1]))
                    at["hT_read"] = at["eT_ps"]

                    @block.vector
                    def _(dve):
                        if i == 0:
                            dve.wait_ge(w_in.sem, 64)
                        else:
                            dve.wait_ge(T.sem, at["out_ps"])
                        for e2 in range(KD):
                            dve.wait_ge(T.sem, at["eT_ps"] - 1 + e2)
                            V(nc.vector.tensor_scalar(eT[:, e2, :], ps[:, e2, :], b2[:, e2:e2 + 1], None, ALU.add))
                            free[e2] = (V.sem, V.n)
                        at["eT"] = V.n

                    @block.tensor
                    def _(pe):
                        pe.wait_ge(V.sem, at["eT"])
                        pe.wait_ge(*free[2])
                        pe.wait_ge(*free[3])
                        for q in range(Q):
                            for k in range(KD):
                                last = nc.tensor.matmul(ps[:, 2 + q // 2, q % 2 * DM:(q % 2 + 1) * DM],
                                                        eT[:, k, q * P:(q + 1) * P], w_next[:, k, :], start=k == 0, stop=k == KD - 1)
                        at["out_ps"] = T(last)

                    @block.vector
                    def _(dve):
                        dve.wait_ge(T.sem, at["out_ps"])
                        if i:
                            dve.wait_ge(V.sem, at["x2"])
                        at["g"] = V(nc.vector.tensor_tensor(
                            g[:, :, :], ps[:, 2:4, :].rearrange("p a (q e) -> p (a q) e", q=2),
                            b_next[:, :].unsqueeze(1).broadcast_to([P, Q, DM]), ALU.add))
                        free[2] = free[3] = (V.sem, V.n)

                    @block.scalar
                    def _(act):
                        act.wait_ge(V.sem, at["g"])
                        link(act, A, nc.scalar.activation(g[:, :, :], g[:, :, :], ACT.Gelu))
                        at["sg"] = A(nc.scalar.activation(g[:, :, :], g[:, :, :], ACT.Silu))

                    @block.vector
                    def _(dve):
                        dve.wait_ge(A.sem, at["sg"])
                        dve.wait_ge(s1_in[i].sem, 16)
                        dve.wait_ge(x1_in[i].sem, 16)
                        link(dve, V, nc.vector.tensor_tensor(s1[:, i, :, :], s1[:, i, :, :], g[:, :, :], ALU.mult))
                        at["x2"] = V(nc.vector.tensor_tensor(x1[:, i, :, :], x1[:, i, :, :], s1[:, i, :, :], ALU.add))

                    @block.sync
                    def _(sp):
                        sp.wait_ge(V.sem, at["x2"])
                        stored(sp.dma_start(d["x2"][e + i * E1].rearrange("(q p) e -> p q e", p=P), x1[:, i, :, :]), 16)
                        if i == MB - 1:
                            sp.wait_ge(stored.sem, 16 * MB)
            ph.clear()


HEADS2 = 16
E2, I2, SI2 = 8, 128, 512
GROUPS, TOPK2, SCALE2 = 2, 2, 2.5
GE = E2 // GROUPS
SB2 = SI2 // P
TINY = 2.0 ** -100
KP2 = 96


def phase_c3(nc, c, d, count=B):
    with ExitStack() as ctx:
        ph = Phase(nc, ctx, "c3")
        ps = ph.psum()
        ident, ones, upto = c["ident"], c["ones"], c["upto"]
        wv, wo = ph.sb("wv", [P, KD, DM]), ph.sb("wo", [P, KD, DM])
        bv, bo = ph.sb("bv", [P, DM]), ph.sb("bo", [P, DM])
        w3, b3 = ph.sb("w3", [P, KD, 3]), ph.sb("b3", [P, 3])
        w3r = ph.sb("w3r", [P, KD, 3, P])
        gw, gb = ph.sb("gw", [P, KD, E2]), ph.sb("gb", [P, E2])
        up = ph.sb("up", [P, KD, E2 * I2])
        down = ph.sb("down", [P, E2, DM])
        sup = ph.sb("sup", [P, KD, SI2])
        sdown = ph.sb("sdown", [P, SB2, DM])
        pick = ph.sb("pick", [KP2, E2, P], BF16)
        early = ph.sb("early", [P, E2, E2])
        rows = lambda n: d[n].rearrange("(k p) e -> p k e", p=P)
        load_once(nc, ph, [
            (wv[:, :, :], rows("wv")), (wo[:, :, :], rows("wo")),
            (bv[:, :], d["bv"].partition_broadcast(P)), (bo[:, :], d["bo"].partition_broadcast(P)),
            (w3[:, :, :], rows("w3d")), (b3[:, :], d["b3d"].partition_broadcast(P)),
            (gw[:, :, :], rows("gate_w2")), (gb[:, :], d["gate_b2"].partition_broadcast(P)),
            (up[:, :, :], rows("up2")), (down[:, :, :], d["down2"]),
            (sup[:, :, :], rows("sup2")), (sdown[:, :, :], rows("sdown2")),
        ])
        cwp = ph.sb("cwp", [P, Q, KP2], BF16)
        identb = ph.sb("identb", [P, P], BF16)
        V, A, T, G = (ph.counter(n) for n in ("vector_done", "scalar_done", "tensor_done", "pool_done"))
        with nc.Block() as block:
            @block.gpsimd
            def _(pool):
                G(nc.gpsimd.memset(pick[:, :, :], 0.0))
                link(pool, G, nc.gpsimd.memset(early[:, :, :], 1.0))
                for part in range(3):
                    rows3 = pick[32 * part:32 * part + 32, :, :]
                    link(pool, G, nc.gpsimd.affine_select(out=rows3, in_=rows3, compare_op=ALU.not_equal, fill=1.0,
                                                          base=0, pattern=[[-1, E2], [0, P]], channel_multiplier=1))
                G(nc.gpsimd.affine_select(out=early[:, :, :], in_=early[:, :, :], compare_op=ALU.is_gt, fill=0.0,
                                          base=0, pattern=[[1, E2], [-1, E2]], channel_multiplier=0))

            @block.vector
            def _(dve):
                V(nc.vector.memset(cwp[:, :, :], 0.0))
                V(nc.vector.tensor_copy(identb[:, :], ident[:, :]))
                V(nc.vector.tensor_copy(w3r[:, :, :, :], w3[:, :, :].unsqueeze(3).broadcast_to([P, KD, 3, P])))
        ph.clear()

        x = ph.sb("x", [P, Q, DM])
        xn = ph.sb("xn", [P, Q, DM])
        xnT = ph.sb("xnT", [P, KD, S])
        nm = Norm(ph, "ln")
        v = ph.sb("v", [P, Q, DM])
        pb = ph.sb("pb", [P, 3, S])
        npk = ph.sb("npk", [P, Q, 3])
        sq = ph.sb("sq", [P, 3, S])
        pr = ph.sb("pr", [P, Q, S])
        rs = ph.sb("rs", [P, S])
        oT = ph.sb("oT", [P, KD, S])
        so = ph.sb("so", [P, Q, DM])
        sc = ph.sb("sc", [P, Q, E2])
        sf = ph.sb("sf", [P, Q, E2])
        hi2, lo2 = ph.sb("hi2", [P, Q * GROUPS, 2]), ph.sb("lo2", [P, Q * GROUPS, 2])
        t2 = ph.sb("t2", [P, Q * GROUPS, 4])
        gm = ph.sb("gm", [P, Q, GROUPS])
        cmp, eq = ph.sb("cmp", [P, Q, E2 * E2]), ph.sb("eq", [P, Q, E2 * E2])
        rank = ph.sb("rank", [P, Q, E2])
        den = ph.sb("den", [P, Q])
        cw = ph.sb("cw", [P, Q, E2])
        cwT = ph.sb("cwT", [KP2, S], BF16)
        cwr = ph.sb("cwr", [P, Q, E2])
        r = ph.sb("r", [P, 2, S])
        r2 = ph.sb("r2", [P, E2 + SB2, S])
        g = ph.sb("g", [P, Q, DM])
        x_in, stored = ph.counter("x_in"), ph.counter("stored")
        (sq_made, sq_read, up_made, relu_made, squared, weighted) = (ph.counter(n) for n in (
            "sq_made", "sq_read", "up_made", "relu_made", "squared", "weighted"))
        with nc.Fori(0, count) as b:
            free, at = {}, {}
            with nc.Block() as block:
                @block.sync
                def _(sp):
                    x_in(sp.dma_start(x[:, :, :], d["x2"][b].rearrange("(q p) e -> p q e", p=P)), 16)

                n = layer_norm(nc, block, nm, x, xn, V, A, (x_in.sem, 16))
                at["xnT"] = transpose_rows(nc, block, ps, [0, 1], ident, xn, xnT, T, V, (V.sem, n), free)

                @block.tensor
                def _(pe):
                    pe.wait_ge(*at["xnT"])
                    for q in range(Q):
                        for k in range(KD):
                            nc.tensor.matmul(ps[:, 5, q * 8:q * 8 + 8], xnT[:, k, q * P:(q + 1) * P], gw[:, k, :],
                                             start=k == 0, stop=k == KD - 1)
                        for k in range(KD):
                            last = nc.tensor.matmul(ps[:, 5, 64 + q * 4:64 + q * 4 + 3], xnT[:, k, q * P:(q + 1) * P], w3[:, k, :],
                                                    start=k == 0, stop=k == KD - 1)
                    at["pk"] = T(last)
                    for i in range(3):
                        for k in range(KD):
                            last = nc.tensor.matmul(ps[:, 2 + i, :], w3r[:, k, i, :], xnT[:, k, :], start=k == 0, stop=k == KD - 1)
                        T(last)
                    at["pb"] = T.n
                    for q in range(Q):
                        for k in range(KD):
                            last = nc.tensor.matmul(ps[:, 6 + q // 2, q % 2 * DM:(q % 2 + 1) * DM], xnT[:, k, q * P:(q + 1) * P],
                                                    wv[:, k, :], start=k == 0, stop=k == KD - 1)
                    at["v"] = T(last)

                @block.vector
                def _(dve):
                    dve.wait_ge(T.sem, at["pk"])
                    V(nc.vector.tensor_copy(sc[:, :, :], ps[:, 5, 0:Q * 8].rearrange("p (q e) -> p q e", q=Q)))
                    at["sc_raw"] = V.n
                    link(dve, V, nc.vector.tensor_tensor(npk[:, :, :], ps[:, 5, 64:64 + Q * 4].rearrange("p (q e) -> p q e", q=Q)[:, :, 0:3],
                                                         b3[:, :].unsqueeze(1).broadcast_to([P, Q, 3]), ALU.add))
                    free[5] = (V.sem, V.n)
                    V(nc.vector.tensor_scalar(npk[:, :, :], npk[:, :, :], -1.0, None, ALU.mult))
                    for i in range(3):
                        dve.wait_ge(T.sem, at["pb"] - 2 + i)
                        V(nc.vector.tensor_scalar(pb[:, i, :], ps[:, 2 + i, :], b3[:, i:i + 1], None, ALU.add))
                        free[2 + i] = (V.sem, V.n)
                    at["pb_sb"] = V.n
                    dve.wait_ge(T.sem, at["v"])
                    at["v_sb"] = V(nc.vector.tensor_tensor(
                        v[:, :, :], ps[:, 6:8, :].rearrange("p a (q e) -> p (a q) e", q=2),
                        bv[:, :].unsqueeze(1).broadcast_to([P, Q, DM]), ALU.add))
                    free[6] = free[7] = (V.sem, V.n)

                @block.scalar
                def _(act):
                    act.wait_ge(V.sem, at["sc_raw"])
                    at["sig"] = A(nc.scalar.activation(sc[:, :, :], sc[:, :, :], ACT.Sigmoid))
                    act.wait_ge(V.sem, at["pb_sb"])
                    for m in range(Q):
                        if m:
                            act.wait_ge(sq_read.sem, m)
                        for i in range(3):
                            sq_made(nc.scalar.activation(sq[:, i, m * P:], pb[:, i, m * P:], ACT.Square, bias=npk[:, m, i:i + 1]))

                @block.vector
                def _(dve):
                    for m in range(Q):
                        dve.wait_ge(sq_made.sem, 3 * m + 3)
                        link(dve, V, nc.vector.tensor_tensor(pr[:, m, m * P:], sq[:, 0, m * P:], sq[:, 1, m * P:], ALU.add))
                        k = sq_read(nc.vector.tensor_tensor(pr[:, m, m * P:], pr[:, m, m * P:], sq[:, 2, m * P:], ALU.add))
                        dve.wait_ge(sq_read.sem, k)
                        V(nc.vector.tensor_scalar(pr[:, m, m * P:], pr[:, m, m * P:], TINY, None, ALU.max))
                    at["sq"] = V.n

                @block.scalar
                def _(act):
                    act.wait_ge(V.sem, at["sq"])
                    for m in range(Q):
                        A(nc.scalar.activation(pr[:, m, m * P:], pr[:, m, m * P:], ACT.Sqrt))
                    act.wait_ge(A.sem, A.n)
                    for m in range(Q):
                        A(nc.scalar.activation(pr[:, m, m * P:], pr[:, m, m * P:], ACT.Exp, scale=-1.0 / (DM // HEADS2) ** 0.5))
                    at["exp"] = A.n

                @block.vector
                def _(dve):
                    dve.wait_ge(A.sem, at["sig"])
                    tt, mul = nc.vector.tensor_tensor, ALU.mult
                    link(dve, V, tt(sf[:, :, :], sc[:, :, :], gb[:, :].unsqueeze(1).broadcast_to([P, Q, E2]), ALU.add))
                    s4 = sf[:, :, :].rearrange("p q (g a b) -> p (q g) a b", g=GROUPS, a=2)
                    V(tt(hi2[:, :, :], s4[:, :, :, 0], s4[:, :, :, 1], ALU.max))
                    link(dve, V, tt(lo2[:, :, :], s4[:, :, :, 0], s4[:, :, :, 1], ALU.min))
                    V(tt(t2[:, :, 0:1], hi2[:, :, 0:1], hi2[:, :, 1:2], ALU.max))
                    V(tt(t2[:, :, 1:2], hi2[:, :, 0:1], hi2[:, :, 1:2], ALU.min))
                    link(dve, V, tt(t2[:, :, 2:3], lo2[:, :, 0:1], lo2[:, :, 1:2], ALU.max))
                    link(dve, V, tt(t2[:, :, 3:4], t2[:, :, 1:2], t2[:, :, 2:3], ALU.max))
                    link(dve, V, tt(t2[:, :, 1:2], t2[:, :, 0:1], t2[:, :, 3:4], ALU.add))
                    gs = t2[:, :, 1].rearrange("p (q g) -> p q g", g=GROUPS)
                    V(tt(gm[:, :, 1:2], gs[:, :, 1:2], gs[:, :, 0:1], ALU.is_gt))
                    link(dve, V, tt(gm[:, :, 0:1], gs[:, :, 1:2], gs[:, :, 0:1], ALU.is_le))
                    sg = sf[:, :, :].rearrange("p q (g e) -> p (q g) e", g=GROUPS)
                    link(dve, V, tt(sg, sg, gm[:, :, :].rearrange("p q g -> p (q g)").unsqueeze(2).broadcast_to([P, Q * GROUPS, GE]), mul))
                    for q in range(Q):
                        mi = sf[:, q, :].unsqueeze(1).broadcast_to([P, E2, E2])
                        mj = sf[:, q, :].unsqueeze(2).broadcast_to([P, E2, E2])
                        V(tt(cmp[:, q, :].rearrange("p (j i) -> p j i", j=E2), mi, mj, ALU.is_gt))
                        V(tt(eq[:, q, :].rearrange("p (j i) -> p j i", j=E2), mi, mj, ALU.is_equal))
                    dve.wait_ge(V.sem, V.n)
                    link(dve, V, tt(eq[:, :, :], eq[:, :, :], early[:, :, :].rearrange("p j i -> p (j i)").unsqueeze(1).broadcast_to([P, Q, E2 * E2]), mul))
                    link(dve, V, tt(cmp[:, :, :], cmp[:, :, :], eq[:, :, :], ALU.add))
                    link(dve, V, nc.vector.tensor_reduce(rank[:, :, :], cmp[:, :, :].rearrange("p q (j i) -> p (q j) i", i=E2), AX.X, ALU.add))
                    link(dve, V, nc.vector.scalar_tensor_tensor(cw[:, :, :], rank[:, :, :], float(TOPK2), sc[:, :, :], ALU.is_lt, mul))
                    link(dve, V, nc.vector.tensor_reduce(den[:, :], cw[:, :, :], AX.X, ALU.add))
                    link(dve, V, nc.vector.tensor_scalar(den[:, :], den[:, :], 1e-20, None, ALU.add))
                    link(dve, V, nc.vector.reciprocal(den[:, :], den[:, :]))
                    link(dve, V, tt(cw[:, :, :], cw[:, :, :], den[:, :].unsqueeze(2).broadcast_to([P, Q, E2]), mul))
                    link(dve, V, nc.vector.tensor_scalar(cw[:, :, :], cw[:, :, :], SCALE2, None, mul))
                    link(dve, V, nc.vector.tensor_copy(cwp[:, :, 0:E2], cw[:, :, :]))
                    link(dve, V, tt(cwr[:, :, :], cw[:, :, :], cwp[:, :, 0:E2], ALU.subtract))
                    link(dve, V, nc.vector.tensor_copy(cwp[:, :, 32:32 + E2], cwr[:, :, :]))
                    at["cw"] = V(tt(cwp[:, :, 64:64 + E2], cwr[:, :, :], cwp[:, :, 32:32 + E2], ALU.subtract))

                @block.tensor
                def _(pe):
                    pe.wait_ge(*free[5])
                    pe.wait_ge(V.sem, at["cw"])
                    for q in range(Q):
                        last = nc.tensor.transpose(ps[0:KP2, 5, :].bitcast(BF16)[:, q * P:(q + 1) * P], cwp[:, q, :], identb[:, :])
                    at["cwT"] = T(last)

                @block.vector
                def _(dve):
                    dve.wait_ge(T.sem, at["cwT"])
                    at["cwT_sb"] = V(nc.vector.tensor_copy(cwT[:, :], ps[0:KP2, 5, :].bitcast(BF16)[:, 0:S]))
                    free[5] = (V.sem, V.n)
                    dve.wait_ge(A.sem, at["exp"])
                    for m in range(Q):
                        V(nc.vector.tensor_tensor(pr[:, m, m * P:(m + 1) * P], pr[:, m, m * P:(m + 1) * P], upto[:, :], ALU.mult))
                    at["pr"] = V.n

                @block.tensor
                def _(pe):
                    pe.wait_ge(V.sem, at["pr"])
                    for bank in (0, 1, 2):
                        for m in range(Q):
                            lhs = ones[:, :] if bank == 2 else v[:, m, bank * P:(bank + 1) * P]
                            last = nc.tensor.matmul(ps[:, bank, m * P:], lhs, pr[:, m, m * P:], start=m == 0, stop=m == Q - 1)
                    at["mix"] = T(last)

                @block.vector
                def _(dve):
                    dve.wait_ge(T.sem, at["mix"])
                    link(dve, V, nc.vector.reciprocal(rs[:, :], ps[:, 2, :]))
                    free[2] = (V.sem, V.n)
                    for k in range(KD):
                        V(nc.vector.tensor_tensor(oT[:, k, :], ps[:, k, :], rs[:, :], ALU.mult))
                        free[k] = (V.sem, V.n)
                    at["oT"] = V.n

                @block.tensor
                def _(pe):
                    pe.wait_ge(V.sem, at["oT"])
                    for q in range(Q):
                        for k in range(KD):
                            last = nc.tensor.matmul(ps[:, q // 2, q % 2 * DM:(q % 2 + 1) * DM], oT[:, k, q * P:(q + 1) * P],
                                                    wo[:, k, :], start=k == 0, stop=k == KD - 1)
                    at["s2"] = T(last)

                @block.vector
                def _(dve):
                    dve.wait_ge(T.sem, at["s2"])
                    at["so"] = V(nc.vector.tensor_tensor(
                        so[:, :, :], ps[:, 0:2, :].rearrange("p a (q e) -> p (a q) e", q=2),
                        bo[:, :].unsqueeze(1).broadcast_to([P, Q, DM]), ALU.add))
                    free[0] = free[1] = (V.sem, V.n)

                N = E2 + SB2

                @block.tensor
                def _(pe):
                    for bank in (4, 5, 6, 7):
                        pe.wait_ge(*free[bank])
                    pe.wait_ge(V.sem, at["cwT_sb"])
                    for e in range(N):
                        if e >= 2:
                            pe.wait_ge(squared.sem, e - 1)
                        for k in range(KD):
                            w = up[:, k, e * P:(e + 1) * P] if e < E2 else sup[:, k, (e - E2) * P:(e - E2 + 1) * P]
                            last = nc.tensor.matmul(ps[:, 4 + e % 2, :], w, xnT[:, k, :], start=k == 0, stop=k == KD - 1)
                        if e < E2:
                            if e >= 2:
                                pe.wait_ge(weighted.sem, e - 1)
                            last = nc.tensor.matmul(ps[:, 6 + e % 2, :], pick[:, e, :], cwT[:, :], start=True, stop=True)
                        up_made(last)

                @block.scalar
                def _(act):
                    for e in range(N):
                        act.wait_ge(up_made.sem, e + 1)
                        if e >= 2:
                            act.wait_ge(squared.sem, e - 1)
                        relu_made(nc.scalar.activation(r[:, e % 2, :], ps[:, 4 + e % 2, :], ACT.Relu))

                @block.vector
                def _(dve):
                    for e in range(N):
                        dve.wait_ge(relu_made.sem, e + 1)
                        k = squared(nc.vector.tensor_tensor(r2[:, e, :], r[:, e % 2, :], r[:, e % 2, :], ALU.mult))
                        if e < E2:
                            dve.wait_ge(squared.sem, k)
                            weighted(nc.vector.tensor_tensor(r2[:, e, :], r2[:, e, :], ps[:, 6 + e % 2, :], ALU.mult))

                @block.tensor
                def _(pe):
                    pe.wait_ge(weighted.sem, E2)
                    pe.wait_ge(squared.sem, N)
                    for q in range(Q):
                        if q % 2 == 0:
                            pe.wait_ge(*free[(2, 3)[q // 2]])
                        for e in range(N):
                            w = down[:, e, :] if e < E2 else sdown[:, e - E2, :]
                            last = nc.tensor.matmul(ps[:, 2 + q // 2, q % 2 * DM:(q % 2 + 1) * DM], r2[:, e, q * P:(q + 1) * P], w,
                                                    start=e == 0, stop=e == N - 1)
                    at["ffn"] = T(last)

                @block.scalar
                def _(act):
                    act.wait_ge(T.sem, at["ffn"])
                    at["g"] = A(nc.scalar.activation(g[:, :, :], ps[:, 2:4, :], ACT.Silu))

                @block.vector
                def _(dve):
                    dve.wait_ge(A.sem, at["g"])
                    link(dve, V, nc.vector.tensor_tensor(g[:, :, :], g[:, :, :], so[:, :, :], ALU.mult))
                    at["x3"] = V(nc.vector.tensor_tensor(x[:, :, :], x[:, :, :], g[:, :, :], ALU.add))

                @block.sync
                def _(sp):
                    sp.wait_ge(V.sem, at["x3"])
                    stored(sp.dma_start(d["x3"][b].rearrange("(q p) e -> p q e", p=P), x[:, :, :]), 16)
                    sp.wait_ge(stored.sem, 16)
            ph.clear()


NF = 64
E3, D3, RH3 = 16, 512, 128
CAP = math.ceil(S * 2.0 / E3)
DK3 = D3 // P
ROUND = 1.5 * 2.0 ** 23


def phase_c4(nc, c, d, count=B):
    with ExitStack() as ctx:
        ph = Phase(nc, ctx, "c4")
        ps = ph.psum()
        ident = c["ident"]
        w_in = ph.sb("w_in", [P, KD, 2, 2 * NF])
        w_out = ph.sb("w_out", [P, 2, DM])
        rw1, rw2 = ph.sb("rw1", [P, KD, RH3]), ph.sb("rw2", [P, E3])
        col = ph.sb("col", [P, 16])
        omega, decay, turns, half, sh, ch, fix = (col[:, i:i + 1] for i in range(7))
        a_col, b_col = col[:, 7:8], col[:, 8:9]
        ld = []
        wi = d["W_in"].rearrange("(k p) e -> p k e", p=P)
        for i in range(2):
            for h in range(2):
                ld.append((w_in[:, :, i, h * NF:(h + 1) * NF], wi[:, :, (h ^ i) * NF:((h ^ i) + 1) * NF]))
                ld.append((w_out[h * NF:(h + 1) * NF, i, :], d["W_out"][(h ^ i) * NF:((h ^ i) + 1) * NF]))
        for h in range(2):
            ld.append((omega[h * NF:(h + 1) * NF], d["frequencies"].rearrange("(f o) -> f o", o=1)))
            ld.append((decay[h * NF:(h + 1) * NF], d["log_decay"].rearrange("(f o) -> f o", o=1)))
        ld += [(rw1[:, :, :], d["router_w1"].rearrange("(k p) e -> p k e", p=P)), (rw2[:, :], d["router_w2"])]
        load_once(nc, ph, ld)
        V, A, T = (ph.counter(n) for n in ("vector_done", "scalar_done", "tensor_done"))
        cs, sn = ph.sb("cs", [P, S + 1]), ph.sb("sn", [P, S + 1])
        tt = ph.sb("tt", [P, S])
        dk = ph.sb("dk", [P, S])
        at = {}

        with nc.Block() as block:
            @block.vector
            def _(dve):
                ts = lambda o, i, a, b, f, g: link(dve, V, nc.vector.tensor_scalar(o, i, a, b, f, g))
                ts(omega, omega, 0.1, None, ALU.mult, ALU.bypass)
                ts(turns, omega, 1 / (2 * math.pi), None, ALU.mult, ALU.bypass)
                ts(turns, turns, ROUND, None, ALU.add, ALU.bypass)
                ts(turns, turns, ROUND, None, ALU.subtract, ALU.bypass)
                for part in (6.28125, 2 * math.pi - 6.28125):
                    link(dve, V, nc.vector.scalar_tensor_tensor(omega, turns, -part, omega, ALU.mult, ALU.add))
                ts(half, omega, 0.5, None, ALU.mult, ALU.bypass)
                link(dve, V, nc.vector.scalar_tensor_tensor(ch, half, -1.0, half, ALU.mult, ALU.min))
                at["half"] = link(dve, V, nc.vector.tensor_scalar(ch, ch, math.pi / 2, 0.0, ALU.add, ALU.max))

            @block.scalar
            def _(act):
                act.wait_ge(V.sem, at["half"])
                A(nc.scalar.activation(sh, half, ACT.Sin))
                A(nc.scalar.activation(ch, ch, ACT.Sin))
                A(nc.scalar.activation(decay, decay, ACT.Sigmoid))

            @block.vector
            def _(dve):
                dve.wait_ge(A.sem, 3)
                st = nc.vector.scalar_tensor_tensor
                V(nc.vector.memset(cs[:, 0:1], 1.0))
                V(nc.vector.memset(sn[:, 0:1], 0.0))
                link(dve, V, nc.vector.memset(dk[:, :], 1.0))
                link(dve, V, nc.vector.tensor_scalar(dk[:, :], dk[:, :], decay, None, ALU.mult))
                link(dve, V, st(sn[:, 1:2], sh, 2.0, ch, ALU.mult, ALU.mult))
                link(dve, V, st(cs[:, 1:2], sh, -2.0, sh, ALU.mult, ALU.mult))
                link(dve, V, nc.vector.tensor_scalar(cs[:, 1:2], cs[:, 1:2], 1.0, None, ALU.add))
                link(dve, V, nc.vector.tensor_tensor(a_col, cs[:, 1:2], cs[:, 1:2], ALU.mult))
                link(dve, V, nc.vector.tensor_tensor(b_col, sn[:, 1:2], sn[:, 1:2], ALU.mult))
                link(dve, V, nc.vector.tensor_tensor(fix, a_col, b_col, ALU.add))
                link(dve, V, nc.vector.tensor_scalar(fix, fix, -0.5, 1.5, ALU.mult, ALU.add))
                link(dve, V, nc.vector.tensor_tensor(cs[:, 1:2], cs[:, 1:2], fix, ALU.mult))
                link(dve, V, nc.vector.tensor_tensor(sn[:, 1:2], sn[:, 1:2], fix, ALU.mult))
                n = 1
                while n < S:
                    ck, sk = cs[:, n:n + 1], sn[:, n:n + 1]
                    lo, hi = slice(1, n + 1), slice(n + 1, 2 * n + 1)
                    link(dve, V, nc.vector.tensor_scalar(tt[:, 0:n], sn[:, lo], sk, None, ALU.mult))
                    link(dve, V, st(cs[:, hi], cs[:, lo], ck, tt[:, 0:n], ALU.mult, ALU.subtract))
                    link(dve, V, nc.vector.tensor_scalar(tt[:, 0:n], cs[:, lo], sk, None, ALU.mult))
                    link(dve, V, st(sn[:, hi], sn[:, lo], ck, tt[:, 0:n], ALU.mult, ALU.add))
                    n *= 2
                link(dve, V, nc.vector.tensor_scalar(sn[NF:, :], sn[NF:, :], -1.0, None, ALU.mult))
        ph.clear()

        x = ph.sb("x", [P, Q, DM])
        xn = ph.sb("xn", [P, Q, DM])
        xnT = ph.sb("xnT", [P, KD, S])
        nm = Norm(ph, "ln")
        u, u2, gs = ph.sb("u", [P, S]), ph.sb("u2", [P, S]), ph.sb("gs", [P, S])
        f = ph.sb("f", [P, 2, S])
        so = ph.sb("so", [P, Q, DM])
        rT = ph.sb("rT", [RH3, S])
        pr = ph.sb("pr", [E3, S])
        g1 = ph.sb("g1", [E3, 4])
        x_in, stored = ph.counter("x_in"), ph.counter("stored")
        with nc.Fori(0, count) as b:
            free, at = {}, {}
            with nc.Block() as block:
                @block.sync
                def _(sp):
                    x_in(sp.dma_start(x[:, :, :], d["x3"][b].rearrange("(q p) e -> p q e", p=P)), 16)

                n = layer_norm(nc, block, nm, x, xn, V, A, (x_in.sem, 16))
                at["xn"] = n
                at["xnT"] = transpose_rows(nc, block, ps, [0, 1], ident, xn, xnT, T, V, (V.sem, n), free)

                @block.tensor
                def _(pe):
                    pe.wait_ge(*at["xnT"])
                    for i in range(2):
                        for k in range(KD):
                            last = nc.tensor.matmul(ps[:, 2 + i, :], w_in[:, k, i, :], xnT[:, k, :], start=k == 0, stop=k == KD - 1)
                    at["u"] = T(last)
                    for k in range(KD):
                        last = nc.tensor.matmul(ps[:, 4, :], rw1[:, k, :], xnT[:, k, :], start=k == 0, stop=k == KD - 1)
                    at["r1"] = T(last)

                @block.scalar
                def _(act):
                    act.wait_ge(T.sem, at["r1"])
                    at["rT"] = A(nc.scalar.activation(rT[:, :], ps[:, 4, :], ACT.Silu))

                @block.vector
                def _(dve):
                    dve.wait_ge(T.sem, at["u"])
                    V(nc.vector.tensor_tensor(u[:, :], ps[:, 2, :], cs[:, 0:S], ALU.mult))
                    link(dve, V, nc.vector.tensor_tensor(u2[:, :], ps[:, 3, :], sn[:, 0:S], ALU.mult))
                    link(dve, V, nc.vector.tensor_tensor(u[:, :], u[:, :], u2[:, :], ALU.add))
                    link(dve, V, nc.vector.tensor_tensor_scan(gs[:, :], dk[:, :], u[:, :], 0.0, ALU.mult, ALU.add))
                    V(nc.vector.tensor_tensor(f[:, 0, :], gs[:, :], cs[:, 1:], ALU.mult))
                    at["f"] = V(nc.vector.tensor_tensor(f[:, 1, :], gs[:, :], sn[:, 1:], ALU.mult))

                @block.tensor
                def _(pe):
                    pe.wait_ge(A.sem, at["rT"])
                    at["lg"] = T(nc.tensor.matmul(ps[0:E3, 5, :], rw2[:, :], rT[:, :], start=True, stop=True))
                    pe.wait_ge(V.sem, at["f"])
                    for q in range(Q):
                        for i in range(2):
                            last = nc.tensor.matmul(ps[:, 6 + q // 2, q % 2 * DM:(q % 2 + 1) * DM], f[:, i, q * P:(q + 1) * P],
                                                    w_out[:, i, :], start=i == 0, stop=i == 1)
                    at["s3"] = T(last)

                @block.vector
                def _(dve):
                    dve.wait_ge(T.sem, at["lg"])
                    at["max"] = V(nc.vector.tensor_reduce(g1[:, 0:1], ps[0:E3, 5, :], AX.X, ALU.max, negate=True))

                @block.scalar
                def _(act):
                    act.wait_ge(V.sem, at["max"])
                    at["exp"] = A(nc.scalar.activation(pr[:, :], ps[0:E3, 5, :], ACT.Exp, bias=g1[:, 0:1], accum_out=g1[:, 1:2]))
                    act.wait_ge(T.sem, at["s3"])
                    at["so"] = A(nc.scalar.copy(so[:, :, :], ps[:, 6:8, :]))

                @block.vector
                def _(dve):
                    dve.wait_ge(A.sem, at["exp"])
                    link(dve, V, nc.vector.reciprocal(g1[:, 2:3], g1[:, 1:2]))
                    at["pr"] = V(nc.vector.tensor_scalar(pr[:, :], pr[:, :], g1[:, 2:3], None, ALU.mult))

                @block.sync
                def _(sp):
                    sp.wait_ge(V.sem, at["xn"])
                    stored(sp.dma_start(d["xn3"][b].rearrange("(q p) e -> p q e", p=P), xn[:, :, :]), 16)
                    sp.wait_ge(V.sem, at["pr"])
                    stored(sp.dma_start(d["probs3"][b], pr[:, :]), 16)
                    sp.wait_ge(A.sem, at["so"])
                    stored(sp.dma_start(d["s3"][b].rearrange("(q p) e -> p q e", p=P), so[:, :, :]), 16)
                    sp.wait_ge(stored.sem, 48)
            ph.clear()


RB = P // E3


def phase_r(nc, c, d, keep):
    with ExitStack() as ctx:
        ph = Phase(nc, ctx, "r")
        ps = ph.psum()
        N = B // RB
        pr = ph.sb("pr", [P, N, S])
        val = ph.sb("val", [P, N, 2, CAP])
        ix = ph.sb("ix", [P, N, CAP], U32)
        ixf = ph.sb("ixf", [P, N, 2, CAP])
        sm = ph.sb("sm", [P, N])
        V, T, p_in = ph.counter("vector_done"), ph.counter("tensor_done"), ph.counter("probs_in")
        rows = d["probs3"].rearrange("b e s -> (b e) s")
        at = {}
        with nc.Block() as block:
            @block.sync
            def _(sp):
                p_in(sp.dma_start(pr[:, :, :], rows.rearrange("(n p) s -> p n s", p=P)), 16)

            @block.vector
            def _(dve):
                dve.wait_ge(p_in.sem, 16)
                for r in range(CAP // 8):
                    cut = slice(8 * r, 8 * r + 8)
                    for n in range(N):
                        V(nc.vector.max(val[:, n, 0, cut], pr[:, n, :]))
                    dve.wait_ge(V.sem, V.n)
                    for n in range(N):
                        V(nc.vector.max_index(ix[:, n, cut], val[:, n, 0, cut], pr[:, n, :]))
                    dve.wait_ge(V.sem, V.n)
                    if r < CAP // 8 - 1:
                        for n in range(N):
                            V(nc.vector.match_replace(pr[:, n, :], val[:, n, 0, cut], pr[:, n, :], -1.0))
                        dve.wait_ge(V.sem, V.n)
                V(nc.vector.tensor_reduce(sm[:, :], val[:, :, 0, :], AX.X, ALU.add))
                for h in range(2):
                    V(nc.vector.tensor_copy(ixf[:, :, h, :], ix[:, :, :]))
                dve.wait_ge(V.sem, V.n)
                link(dve, V, nc.vector.tensor_scalar(sm[:, :], sm[:, :], 1e-9, None, ALU.add))
                link(dve, V, nc.vector.reciprocal(sm[:, :], sm[:, :]))
                for n in range(N):
                    V(nc.vector.tensor_scalar(val[:, n, 0, :], val[:, n, 0, :], sm[:, n:n + 1], None, ALU.mult))
                dve.wait_ge(V.sem, V.n)
                at["val"] = link(dve, V, nc.vector.tensor_copy(val[:, :, 1, :], val[:, :, 0, :]))

            @block.tensor
            def _(pe):
                pe.wait_ge(V.sem, at["val"])
                for n in range(N):
                    for i, t in enumerate((ixf, val)):
                        last = nc.tensor.transpose(ps[:, i, n * P:(n + 1) * P], t[:, n, :, :].rearrange("p a b -> p (a b)"),
                                                   c["ident"][:, :])
                at["turned"] = T(last)

            @block.vector
            def _(dve):
                dve.wait_ge(T.sem, at["turned"])
                for h in range(2):
                    part = slice(h * CAP, (h + 1) * CAP)
                    for i, t in enumerate((keep["slot_ix"], keep["slot_w"])):
                        v = ps[part, i, 0:N * P].rearrange("p (b e a) -> p b e a", b=B, a=2)
                        V(nc.vector.tensor_copy(t[part, :, :], v[:, :, :, h]))
                    v = ps[part, 0, 0:N * P].rearrange("p (b a e) -> p e b a", a=2, e=E3)
                    V(nc.vector.tensor_copy(keep["row_f"][part, :, :], v[:, :, :, h]))
                dve.wait_ge(V.sem, V.n)
                dve.wait_ge(keep["base_sem"].sem, 1)
                link(dve, V, nc.vector.tensor_tensor(keep["row_f"][:, :, :], keep["row_f"][:, :, :],
                                                     keep["base"][:, :].unsqueeze(1).broadcast_to([P, E3, B // 2]), ALU.add))
                V(nc.vector.tensor_copy(keep["row_ix"][:, :, :], keep["row_f"][:, :, :]))

            @block.gpsimd
            def _(pool):
                n = keep["iota_sem"]
                for h in range(2):
                    link(pool, n, nc.gpsimd.iota(keep["base_i"][h * CAP:(h + 1) * CAP, :], pattern=[[2 * S, B // 2]],
                                                 base=h * S, channel_multiplier=0))
                link(pool, n, nc.gpsimd.iota(keep["iota_i"][:, :], pattern=[[1, S]], base=0, channel_multiplier=0))
                link(pool, keep["base_sem"], nc.gpsimd.tensor_copy(keep["base"][:, :], keep["base_i"][:, :]))
                link(pool, n, nc.gpsimd.tensor_copy(keep["iota"][:, :], keep["iota_i"][:, :]))
        keep["ph"].clear()
        ph.clear()


def keep_slots(nc, ctx):
    ph = Phase(nc, ctx, "keep")
    I32 = mybir.dt.int32
    return dict(ph=ph, iota_sem=ph.counter("iota_done"), base_sem=ph.counter("base_done"),
                slot_ix=ph.sb("slot_ix", [P, B, E3 // 2]), slot_w=ph.sb("slot_w", [P, B, E3 // 2]),
                row_f=ph.sb("row_f", [P, E3, B // 2]), row_ix=ph.sb("row_ix", [P, E3, B // 2], U32),
                base_i=ph.sb("base_i", [P, B // 2], I32), base=ph.sb("base", [P, B // 2]),
                iota_i=ph.sb("iota_i", [P, S], I32), iota=ph.sb("iota", [P, S]))


EU = 2


def phase_d(nc, c, d, keep, count=E3 // EU):
    with ExitStack() as ctx:
        ph = Phase(nc, ctx, "d")
        ps = ph.psum()
        ident = c["ident"]
        NT = B * CAP
        NP = NT // P
        NH = NT // 512
        w1, w2 = ph.sb("w1", [P, EU, KD, D3]), ph.sb("w2", [P, EU, KD, D3])
        w3 = ph.sb("w3", [P, EU, DK3, DM])
        rix = ph.sb("rix", [P, EU, NP], U32)
        xg = ph.sb("xg", [P, EU, NP, DM])
        xT = ph.sb("xT", [P, EU, KD, NT])
        gate = ph.sb("gate", [P, 2, 512])
        hT = ph.sb("hT", [P, EU, DK3, NT])
        eo = ph.sb("eo", [P, EU, NP, DM])
        w_in = [ph.counter(f"w_in{j}") for j in range(EU)]
        x_in = [ph.counter(f"x_in{j}_{n}") for j in range(EU) for n in range(NP)]
        ph.pool_dma = x_in
        V, T, stored = ph.counter("vector_done"), ph.counter("tensor_done"), ph.counter("stored")
        (turned_made, turned, gate_made, value_made, gated, hidden_done, out_made, out_done) = (ph.counter(n) for n in (
            "turned_made", "turned", "gate_made", "value_made", "gated", "hidden_done", "out_made", "out_done"))
        with nc.Fori(0, count) as g:
            with nc.Block() as block:
                @block.sync
                def _(sp):
                    for j in range(EU):
                        for t, n in ((w1, "w1_3"), (w2, "w2_3"), (w3, "w3_3")):
                            w_in[j](sp.dma_start(t[:, j, :, :], d[n][g * EU + j].rearrange("(k p) e -> p k e", p=P)), 16)
                    for j in range(EU):
                        for h in range(2):
                            sp.wait_ge(out_done.sem, j * NP + NP // 2 * (h + 1))
                            half = slice(NP // 2 * h, NP // 2 * (h + 1))
                            for a in range(2):
                                dst = d["eo3"][a::2, g * EU + j, :, :].rearrange("n c e -> c n e")[:, half, :]
                                stored(sp.dma_start(dst, eo[a * CAP:(a + 1) * CAP, j, half, :]), 16)
                    sp.wait_ge(stored.sem, 64 * EU)

                @block.vector
                def _(dve):
                    V(nc.vector.tensor_copy(rix[:, :, :], keep["row_ix"][:, bass.ds(g * EU, EU), :]))

                @block.gpsimd
                def _(pool):
                    pool.wait_ge(V.sem, 1)
                    for j in range(EU):
                        for n in range(NP):
                            x_in[j * NP + n](nc.gpsimd.indirect_dma_start(
                                xg[:, j, n, :], None, d["xn3"].rearrange("b s e -> (b s) e"),
                                bass.IndirectOffsetOnAxis(ap=rix[:, j, n:n + 1], axis=0)), 16)
                    for s in x_in:
                        pool.wait_ge(s.sem, 16)

                def turn(pe, j):
                    for n in range(NP * KD // 4):
                        k, n0 = n % KD, n // KD * 4
                        if j * NP * KD // 4 + n >= 2:
                            pe.wait_ge(turned.sem, j * NP * KD // 4 + n - 1)
                        for i in range(4):
                            if k == 0:
                                pe.wait_ge(x_in[j * NP + n0 + i].sem, 16)
                            last = nc.tensor.transpose(ps[:, n % 2, i * P:(i + 1) * P], xg[:, j, n0 + i, k * P:(k + 1) * P], ident[:, :])
                        turned_made(last)

                @block.tensor
                def _(pe):
                    turn(pe, 0)
                    for j in range(EU):
                        pe.wait_ge(w_in[j].sem, 48)
                        pe.wait_ge(turned.sem, (j + 1) * NP * KD // 4)
                        for m in range(DK3 * NH):
                            h, f = m // DK3, m % DK3
                            i = j * DK3 * NH + m
                            if i >= 2:
                                pe.wait_ge(hidden_done.sem, i - 1)
                            for w, bank, made in ((w1, 2, gate_made), (w2, 4, value_made)):
                                for k in range(KD):
                                    last = nc.tensor.matmul(ps[:, bank + i % 2, :], w[:, j, k, f * P:(f + 1) * P],
                                                            xT[:, j, k, h * 512:(h + 1) * 512], start=k == 0, stop=k == KD - 1)
                                made(last)
                        if j + 1 < EU:
                            turn(pe, j + 1)
                        for n in range(NP):
                            i = j * NP + n
                            pe.wait_ge(hidden_done.sem, j * DK3 * NH + DK3 * (n // (NP // NH) + 1))
                            if i >= 2:
                                pe.wait_ge(out_done.sem, i - 1)
                            for k in range(DK3):
                                last = nc.tensor.matmul(ps[:, 6 + i % 2, 0:DM], hT[:, j, k, n * P:(n + 1) * P], w3[:, j, k, :],
                                                        start=k == 0, stop=k == DK3 - 1)
                            out_made(last)

                def copy_turned(dve, j):
                    for n in range(NP * KD // 4):
                        k, n0 = n % KD, n // KD * 4
                        dve.wait_ge(turned_made.sem, j * NP * KD // 4 + n + 1)
                        turned(nc.vector.tensor_copy(xT[:, j, k, n0 * P:(n0 + 4) * P], ps[:, n % 2, :]))

                @block.scalar
                def _(act):
                    for i in range(EU * DK3 * NH):
                        act.wait_ge(gate_made.sem, i + 1)
                        if i >= 2:
                            act.wait_ge(hidden_done.sem, i - 1)
                        gated(nc.scalar.activation(gate[:, i % 2, :], ps[:, 2 + i % 2, :], ACT.Silu))

                @block.vector
                def _(dve):
                    copy_turned(dve, 0)
                    for j in range(EU):
                        for m in range(DK3 * NH):
                            h, f = m // DK3, m % DK3
                            i = j * DK3 * NH + m
                            dve.wait_ge(gated.sem, i + 1)
                            dve.wait_ge(value_made.sem, i + 1)
                            hidden_done(nc.vector.tensor_tensor(hT[:, j, f, h * 512:(h + 1) * 512], gate[:, i % 2, :],
                                                                ps[:, 4 + i % 2, :], ALU.mult))
                        if j + 1 < EU:
                            copy_turned(dve, j + 1)
                        for n in range(NP):
                            i = j * NP + n
                            dve.wait_ge(out_made.sem, i + 1)
                            out_done(nc.vector.tensor_copy(eo[:, j, n, :], ps[:, 6 + i % 2, 0:DM]))
            ph.clear()


def phase_e(nc, c, d, keep, count=B):
    with ExitStack() as ctx:
        ph = Phase(nc, ctx, "e")
        ps = ph.psum()
        EP = E3 // 2
        x, s3 = ph.sb("x", [P, Q, DM]), ph.sb("s3", [P, Q, DM])
        eo = ph.sb("eo", [P, EP, DM])
        ix, w = ph.sb("ix", [P, EP]), ph.sb("w", [P, EP])
        sel = ph.sb("sel", [P, EP, S])
        g = ph.sb("g", [P, Q, DM])
        x_in, eo_in, stored = ph.counter("x_in"), ph.counter("eo_in"), ph.counter("stored")
        V, A, T = (ph.counter(n) for n in ("vector_done", "scalar_done", "tensor_done"))
        with nc.Fori(0, count) as b:
            at = {}
            with nc.Block() as block:
                @block.sync
                def _(sp):
                    for a in range(2):
                        eo_in(sp.dma_start(eo[a * CAP:(a + 1) * CAP, :, :],
                                           d["eo3"][b].rearrange("(n a) c e -> a c n e", a=2)[a]), 16)
                    x_in(sp.dma_start(x[:, :, :], d["x3"][b].rearrange("(q p) e -> p q e", p=P)), 16)
                    x_in(sp.dma_start(s3[:, :, :], d["s3"][b].rearrange("(q p) e -> p q e", p=P)), 16)

                @block.vector
                def _(dve):
                    V(nc.vector.tensor_copy(ix[:, :], keep["slot_ix"][:, bass.ds(b, 1), :]))
                    link(dve, V, nc.vector.tensor_copy(w[:, :], keep["slot_w"][:, bass.ds(b, 1), :]))
                    at["sel"] = V.n
                    for e in range(EP):
                        V(nc.vector.tensor_scalar(sel[:, e, :], keep["iota"][:, :], ix[:, e:e + 1], w[:, e:e + 1],
                                                  ALU.is_equal, ALU.mult))

                @block.tensor
                def _(pe):
                    pe.wait_ge(eo_in.sem, 32)
                    pe.wait_ge(V.sem, at["sel"] + EP)
                    for q in range(Q):
                        for e in range(EP):
                            last = nc.tensor.matmul(ps[:, q // 2, q % 2 * DM:(q % 2 + 1) * DM], sel[:, e, q * P:(q + 1) * P],
                                                    eo[:, e, :], start=e == 0, stop=e == EP - 1)
                    at["ffn"] = T(last)

                @block.scalar
                def _(act):
                    act.wait_ge(T.sem, at["ffn"])
                    at["g"] = A(nc.scalar.activation(g[:, :, :], ps[:, 0:2, :], ACT.Silu))

                @block.vector
                def _(dve):
                    dve.wait_ge(A.sem, at["g"])
                    dve.wait_ge(x_in.sem, 32)
                    link(dve, V, nc.vector.tensor_tensor(g[:, :, :], g[:, :, :], s3[:, :, :], ALU.mult))
                    at["out"] = V(nc.vector.tensor_tensor(x[:, :, :], x[:, :, :], g[:, :, :], ALU.add))

                @block.sync
                def _(sp):
                    sp.wait_ge(V.sem, at["out"])
                    stored(sp.dma_start(d["out"][b].rearrange("(q p) e -> p q e", p=P), x[:, :, :]), 16)
                    sp.wait_ge(stored.sem, 16)
            ph.clear()



def _same(a):
    return a


def _T(a):
    return a.T


def _columns(a):
    return a.reshape(*a.shape[:-1], -1, P).swapaxes(-1, -2)


INPUTS = {
    "x": ("L0_attn_x", _same),
    "w_in": ("L0_attn_in_proj_w", _T), "w_conv": ("L0_attn_conv_w", _same), "b_conv": ("L0_attn_conv_b", _columns),
    "w_x": ("L0_attn_x_proj_w", _T), "skip": ("L0_attn_D", _columns), "w_out": ("L0_attn_out_proj_w", _T),
    "a_log": ("L0_attn_A_log", _same),
    "w_gate0": ("L0_ffn_gate_w", _T), "b_gate0": ("L0_ffn_gate_b", _same),
    "w1_0": ("L0_ffn_w1", _same), "w2_0": ("L0_ffn_w2", _same),
    "w_qkv": ("L1_attn_w_qkv", _T), "w_proj": ("L1_attn_w_proj", _T), "b_proj": ("L1_attn_b_proj", _same),
    "lambda_q1": ("L1_attn_lambda_q1", _same), "lambda_k1": ("L1_attn_lambda_k1", _same),
    "lambda_q2": ("L1_attn_lambda_q2", _same), "lambda_k2": ("L1_attn_lambda_k2", _same),
    "sub_norm_w": ("L1_attn_sub_norm_w", _same),
    "ln_scale": ("L1_ffn_ln_scale", _columns), "ln_bias": ("L1_ffn_ln_bias", _columns),
    "attn_w": ("L1_ffn_attn_w", _T), "attn_b": ("L1_ffn_attn_b", _columns),
    "w1_1": ("L1_ffn_w1", _same), "b1_1": ("L1_ffn_b1", _columns), "w2_1": ("L1_ffn_w2", _same),
    "b2_1": ("L1_ffn_b2", _columns), "next_w": ("L1_ffn_next_w", _T), "next_b": ("L1_ffn_next_b", _same),
    "wv": ("L2_attn_wv", _T), "bv": ("L2_attn_bv", _same), "wo": ("L2_attn_wo", _T), "bo": ("L2_attn_bo", _same),
    "w3d": ("L2_attn_w3d", _T), "b3d": ("L2_attn_b3d", _same),
    "gate_w2": ("L2_ffn_gate_weight", _T), "gate_b2": ("L2_ffn_gate_bias", _same),
    "up2": ("L2_ffn_up_weights", lambda a: a.reshape(E2 * I2, DM).T),
    "down2": ("L2_ffn_down_weights", lambda a: a.transpose(2, 0, 1)),
    "sup2": ("L2_ffn_shared_up_weight", _T), "sdown2": ("L2_ffn_shared_down_weight", _T),
    "W_in": ("L3_attn_W_in", _T), "W_out": ("L3_attn_W_out", _T),
    "frequencies": ("L3_attn_frequencies", _same), "log_decay": ("L3_attn_log_decay", _same),
    "router_w1": ("L3_ffn_router_w1", _same), "router_w2": ("L3_ffn_router_w2", _same),
    "w1_3": ("L3_ffn_w1", _same), "w2_3": ("L3_ffn_w2", _same), "w3_3": ("L3_ffn_w3", _same),
}
SCRATCH = {
    "s0": ((B, S, DM), F32), "picked": ((B, E0, S), F32), "o0": ((B, E0, DM), F32),
    "qk_parts": ((4, SPLIT, P, S), BF16),
    "x1": ((B, S, DM), F32), "xn1": ((B, S, DM), F32), "s1": ((B, S, DM), F32),
    "x2": ((B, S, DM), F32), "x3": ((B, S, DM), F32),
    "xn3": ((B, S, DM), F32), "s3": ((B, S, DM), F32), "probs3": ((B, E3, S), F32), "eo3": ((B, E3, CAP, DM), F32),
}


def program(nc, d):
    with ExitStack() as ctx:
        c = make_constants(nc, ctx)
        with ExitStack() as layer0:
            mergedT = layer0.enter_context(nc.sbuf_tensor("mergedT", [P, KD, E0, B], F32))
            phase_a(nc, c, d, mergedT)
            phase_b(nc, c, d, mergedT)
        phase_c1(nc, c, d)
        phase_c2(nc, c, d)
        phase_c3(nc, c, d)
        keep = keep_slots(nc, ctx)
        phase_c4(nc, c, d)
        phase_r(nc, c, d, keep)
        phase_d(nc, c, d, keep)
        phase_e(nc, c, d, keep)


def kernel(**inputs):
    import numpy as _np
    import concourse.bacc as _bacc
    from concourse import mybir as _mybir
    from concourse.bass_utils import run_bass_kernel_spmd as _run

    nc = _bacc.Bacc("TRN2", target_bir_lowering=False, num_devices=1)
    arrays, d = {}, {}
    for name, (source, lay) in INPUTS.items():
        a = _np.ascontiguousarray(lay(_np.asarray(inputs[source])))
        arrays[f"in_{name}"] = a
        d[name] = nc.dram_tensor(f"in_{name}", a.shape, _mybir.dt.from_np(a.dtype), kind="ExternalInput").ap()
    for name, (shape, dt) in SCRATCH.items():
        d[name] = nc.dram_tensor(f"scratch_{name}", shape, dt, kind="Internal").ap()
    d["out"] = nc.dram_tensor("out", (B, S, DM), F32, kind="ExternalOutput").ap()
    program(nc, d)
    r = _run(nc, [arrays], core_ids=[0])
    return r.results[0]["out"]
```

```python
import math
from contextlib import ExitStack

import concourse.bass as bass
from concourse import mybir

F32 = mybir.dt.float32
BF16 = mybir.dt.bfloat16
U32 = mybir.dt.uint32
ALU = mybir.AluOpType
ACT = mybir.ActivationFunctionType
AX = mybir.AxisListType
P = 128
B, S, DM = 16, 512, 256
Q = S // P
KD = DM // P
EPS = 1e-5


class Signal:

    def __init__(self, nc, ctx, name):
        self.sem = ctx.enter_context(nc.semaphore(name))
        self.n = 0

    def __call__(self, instruction, by=1):
        instruction.then_inc(self.sem, by)
        self.n += by
        return self.n


def link(engine, signal, instruction):
    n = signal(instruction)
    engine.wait_ge(signal.sem, n)
    return n


class Phase:

    def __init__(self, nc, ctx, name):
        self.nc, self.ctx, self.name = nc, ctx, name
        self.signals, self.pool_dma, self.buffers = [], [], {}

    def sb(self, name, shape, dt=F32):
        if name not in self.buffers:
            self.buffers[name] = self.ctx.enter_context(self.nc.sbuf_tensor(f"{self.name}_{name}", shape, dt))
        return self.buffers[name]

    def psum(self):
        return self.ctx.enter_context(self.nc.psum_tensor(f"{self.name}_psum", [P, 8, 512], F32))

    def counter(self, name):
        s = Signal(self.nc, self.ctx, f"{self.name}_{name}")
        self.signals.append(s)
        return s

    def clear(self):
        with self.nc.Block() as block:
            @block.sync
            def _(sp):
                for s in self.signals:
                    if s not in self.pool_dma:
                        sp.sem_clear(s.sem)

            if self.pool_dma:
                @block.gpsimd
                def _(pool):
                    for s in self.pool_dma:
                        pool.dma_reset(range(s.sem.num, s.sem.num + 1))
                        pool.sem_clear(s.sem)
        for s in self.signals:
            s.n = 0


SLOTS = 2


class Job:

    def __init__(self, j):
        self.j, self.slot = j, j % SLOTS
        self.block = self.b = None
        self.before, self.done = None, []

    def wait_for_buffers(self, *more):
        waits = self.before.done if self.before else []
        if waits:
            def wait(engine):
                for sem, n in waits:
                    engine.wait_ge(sem, n)
            for on in (self.block.sync, self.block.tensor, self.block.scalar, self.block.vector) + more:
                on(wait)


def pipeline(bodies, jobs, lag):
    step, left = 0, set(range(len(bodies)))
    while left:
        for j, body in enumerate(bodies):
            if j in left and step >= j * lag:
                before = jobs[j].before
                assert before is None or before.done, "the buffers' last user is still at work"
                if next(body, left) is left:
                    left.remove(j)
        step += 1


def run_sequences(nc, ph, sequence, count, per_pass, lag):
    jobs = [Job(j) for j in range(per_pass)]
    for job in jobs[SLOTS:]:
        job.before = jobs[job.j - SLOTS]
    bodies = [sequence(job) for job in jobs]
    for body in bodies:
        next(body)
    yield
    with nc.Fori(0, count // per_pass) as g:
        with nc.Block() as block:
            for job in jobs:
                job.block, job.b = block, g * per_pass + job.j
            pipeline(bodies, jobs, lag)
        ph.clear()


def load_once(nc, ph, pairs):
    loaded = ph.counter("weights_loaded")
    with nc.Block() as block:
        @block.sync
        def _(sp):
            for dst, src in pairs:
                loaded(sp.dma_start(dst, src), 16)
            sp.wait_ge(loaded.sem, loaded.n)
    ph.clear()


def make_constants(nc, ctx):
    c = {}
    for name in ("ident", "ones", "upto", "after"):
        c[name] = ctx.enter_context(nc.sbuf_tensor(f"c_{name}", [P, P], F32))
    ph = Phase(nc, ctx, "const")
    done = ph.counter("pool_done")
    with nc.Block() as block:
        @block.gpsimd
        def _(pool):
            nc.gpsimd.memset(c["ident"][:, :], 0.0).then_inc(done.sem, 1)
            nc.gpsimd.memset(c["ones"][:, :], 1.0).then_inc(done.sem, 1)
            pool.wait_ge(done.sem, 2)
            nc.gpsimd.affine_select(out=c["ident"][:, :], in_=c["ident"][:, :], compare_op=ALU.not_equal, fill=1.0,
                                    base=0, pattern=[[-1, P]], channel_multiplier=1).then_inc(done.sem, 1)
            nc.gpsimd.affine_select(out=c["upto"][:, :], in_=c["ones"][:, :], compare_op=ALU.is_ge, fill=0.0,
                                    base=0, pattern=[[1, P]], channel_multiplier=-1).then_inc(done.sem, 1)
            nc.gpsimd.affine_select(out=c["after"][:, :], in_=c["ones"][:, :], compare_op=ALU.is_gt, fill=0.0,
                                    base=0, pattern=[[-1, P]], channel_multiplier=1).then_inc(done.sem, 1)
            pool.wait_ge(done.sem, 5)
    done.n = 5
    ph.clear()
    return c


class Norm:

    def __init__(self, ph, tag):
        self.stats = ph.sb(f"{tag}_stats", [P, Q, 6])
        self.mv = ph.sb(f"{tag}_mv", [P, Q, 2])
        self.std = ph.sb(f"{tag}_std", [P, Q])
        self.rstd = ph.sb(f"{tag}_rstd", [P, Q])


def layer_norm(nc, block, nm, x, xn, V, A, ready):
    at = {}

    @block.vector
    def _(dve):
        dve.wait_ge(*ready)
        for q in range(Q):
            V(nc.vector.bn_stats(nm.stats[:, q, :], x[:, q, :]))
        dve.wait_ge(V.sem, V.n)
        for q in range(Q):
            V(nc.vector.bn_aggr(nm.mv[:, q, :], nm.stats[:, q, :]))
        dve.wait_ge(V.sem, V.n)
        at["var"] = V(nc.vector.tensor_scalar(nm.std[:, :], nm.mv[:, :, 1], EPS, None, ALU.add))

    @block.scalar
    def _(act):
        act.wait_ge(V.sem, at["var"])
        at["std"] = A(nc.scalar.activation(nm.std[:, :], nm.std[:, :], ACT.Sqrt))

    @block.vector
    def _(dve):
        dve.wait_ge(A.sem, at["std"])
        link(dve, V, nc.vector.reciprocal(nm.rstd[:, :], nm.std[:, :]))
        for q in range(Q):
            V(nc.vector.tensor_scalar(xn[:, q, :], x[:, q, :], nm.mv[:, q, 0:1], nm.rstd[:, q:q + 1],
                                      ALU.subtract, ALU.mult))
        at["xn"] = V.n
    return at["xn"]


def transpose_rows(nc, block, ps, banks, ident, xn, xnT, T, V, ready, free, eng="vector", kd=KD):
    at = {}

    @block.tensor
    def _(pe):
        pe.wait_ge(*ready)
        for k in range(kd):
            bank = banks[k % len(banks)]
            assert len(banks) >= kd
            if bank in free:
                pe.wait_ge(*free[bank])
            for q in range(Q):
                last = nc.tensor.transpose(ps[:, bank, q * P:(q + 1) * P], xn[:, q, k * P:(k + 1) * P], ident[:, :])
            at[k] = T(last)

    def copies(e, copy):
        for k in range(kd):
            e.wait_ge(T.sem, at[k])
            n = V(copy(xnT[:, k, :], ps[:, banks[k], :]))
            free[banks[k]] = (V.sem, n)
    if eng == "vector":
        block.vector(lambda dve: copies(dve, nc.vector.tensor_copy))
    else:
        block.scalar(lambda act: copies(act, nc.scalar.copy))
    return (V.sem, V.n)


DI, NS, KC = 512, 16, 4
RT = 3
LAG_A = 5
SEQS = 4
KC3 = 96
KST = 96
CI = DI // P
E0, K0 = 32, 8


def phase_a(nc, c, d, mergedT, count=B):
    with ExitStack() as ctx:
        ph = Phase(nc, ctx, "a")
        ps = ph.psum()
        ident, upto, after = c["ident"], c["upto"], c["after"]
        w_in = ph.sb("w_in", [P, KD, 2 * DI])
        w_conv = ph.sb("w_conv", [P, CI, KC])
        b_conv = ph.sb("b_conv", [P, CI])
        w_x = ph.sb("w_x", [P, CI, 2 * NS + 1])
        skip = ph.sb("skip", [P, CI])
        w_out = ph.sb("w_out", [P, CI, DM])
        w_gate = ph.sb("w_gate", [P, KD, E0])
        b_gate = ph.sb("b_gate", [E0, 1])
        a_row = ph.sb("a_row", [P, NS])
        a_col = ph.sb("a_col", [NS, 1])
        pick = ph.sb("pick", [KC3, NS, P], BF16)
        load_once(nc, ph, [
            (w_in[:, :, :], d["w_in"].rearrange("(k p) e -> p k e", p=P)),
            (w_conv[:, :, :], d["w_conv"].rearrange("(c p) o k -> p c (o k)", p=P)),
            (b_conv[:, :], d["b_conv"]),
            (w_x[:, :, :], d["w_x"].rearrange("(c p) e -> p c e", p=P)),
            (skip[:, :], d["skip"]),
            (w_out[:, :, :], d["w_out"].rearrange("(c p) e -> p c e", p=P)),
            (w_gate[:, :, :], d["w_gate0"].rearrange("(k p) e -> p k e", p=P)),
            (b_gate[:, :], d["b_gate0"].rearrange("(e o) -> e o", o=1)),
            (a_row[:, :], d["a_log"].partition_broadcast(P)),
            (a_col[:, :], d["a_log"].rearrange("(n o) -> n o", o=1)),
        ])
        V, A, T, G = (ph.counter(n) for n in ("vector_done", "scalar_done", "tensor_done", "pool_done"))


        def sequence(job):
            i, j = job.slot, job.j
            c3 = ph.sb(f"c3_{i}", [KC3, S], BF16)
            cr = ph.sb(f"cr_{i}", [NS, 1, S])
            crb = ph.sb(f"crb_{i}", [NS, S], BF16)
            cw = ph.sb(f"cw_{i}", [KST, S])
            st = ph.sb(f"st_{i}", [KST, Q, DI])
            x = ph.sb(f"x_{i}", [P, Q, DM])
            xn = ph.sb(f"xn_{i}", [P, Q, DM])
            xnT = ph.sb(f"xnT_{i}", [P, KD, S])
            nm = Norm(ph, f"ln{i}")
            xi = ph.sb(f"xi_{i}", [P, CI, KC - 1 + S])
            cv = ph.sb(f"cv_{i}", [P, CI, S])
            xc = ph.sb(f"xc_{i}", [P, CI, S])
            xct = ph.sb(f"xct_{i}", [P, Q, DI])
            zs = ph.sb(f"zs_{i}", [P, CI, S])
            lg = ph.sb(f"lg_{i}", [E0, S])
            pr = ph.sb(f"pr_{i}", [E0, S])
            rest = lg
            top = ph.sb(f"top_{i}", [E0, K0])
            g1 = ph.sb(f"g1_{i}", [E0, 4])
            pT = ph.sb(f"pT_{i}", [P, Q, E0])
            xd = ph.sb(f"xd_{i}", [P, Q, 2 * NS + 1])
            cT = ph.sb(f"cT_{i}", [NS, S])
            sp1 = ph.sb(f"sp1_{i}", [P, Q])
            sp2 = ph.sb(f"sp2_{i}", [P, Q])
            dl = ph.sb(f"dl_{i}", [P, Q])
            dla = ph.sb(f"dla_{i}", [P, Q, P])
            dlr = ph.sb(f"dlr_{i}", [P, Q, NS])
            bdt = ph.sb(f"bdt_{i}", [P, Q, NS])
            bw = ph.sb(f"bw_{i}", [P, Q, NS])
            edec = ph.sb(f"edec_{i}", [NS, Q])
            span = ph.sb(f"span_{i}", [P, S])
            ex = ph.sb(f"ex_{i}", [P, 2, S])
            t1 = ph.sb(f"t1_{i}", [P, RT, S])
            gm = ph.sb(f"gm_{i}", [P, S])
            yg = cv
            so = x
            x_in, stored = ph.counter(f"x_in{j}"), ph.counter(f"stored{j}")
            spread_read, summed, spread_made, exp_made = (ph.counter(f"{n}{j}") for n in ("spread_read", "summed", "spread_made", "exp_made"))

            if j < SLOTS:
                seqs.append((c3, st, cw))
            yield
            block, b = job.block, job.b
            job.wait_for_buffers(block.gpsimd)
            free, at = {}, {}
            b0, b1, b2, b3 = range(4 * i, 4 * i + 4)
            @block.sync
            def _(sp):
                x_in(sp.dma_start(x[:, :, :], d["x"][b].rearrange("(q p) e -> p q e", p=P)), 16)

            n = layer_norm(nc, block, nm, x, xn, V, A, (x_in.sem, 16))
            at["xn"] = n
            at["xnT"] = transpose_rows(nc, block, ps, [b0, b1], ident, xn, xnT, T, V, (V.sem, n), free)

            yield

            ring = (b3, b0, b1)

            @block.tensor
            def _(pe):
                pe.wait_ge(*at["xnT"])
                for k in range(KD):
                    last = nc.tensor.matmul(ps[0:E0, b2, :], w_gate[:, k, :], xnT[:, k, :], start=k == 0, stop=k == KD - 1)
                at["logits"] = T(last)
                at["proj"] = T.n
                base = A.n
                for e in range(8):
                    if e >= 3:
                        pe.wait_ge(A.sem, base + e - 2)
                    for k in range(KD):
                        last = nc.tensor.matmul(ps[:, ring[e % 3], :], w_in[:, k, e * P:(e + 1) * P], xnT[:, k, :],
                                                start=k == 0, stop=k == KD - 1)
                    T(last)

            @block.vector
            def _(dve):
                at["pad"] = V(nc.vector.memset(xi[:, :, 0:KC - 1], 0.0))
                dve.wait_ge(T.sem, at["logits"])
                n = link(dve, V, nc.vector.tensor_scalar(lg[:, :], ps[0:E0, b2, :], b_gate[:, 0:1], None, ALU.add))
                free[b2] = (V.sem, n)
                at["gmax"] = link(dve, V, nc.vector.tensor_reduce(g1[:, 0:1], lg[:, :], AX.X, ALU.max, negate=True))

            @block.scalar
            def _(act):
                for e in range(8):
                    act.wait_ge(T.sem, at["proj"] + e + 1)
                    if e < 4:
                        A(nc.scalar.copy(xi[:, e, KC - 1:], ps[:, ring[e % 3], :]))
                        if e == 3:
                            at["xi"] = A.n
                    else:
                        A(nc.scalar.activation(zs[:, e - 4, :], ps[:, ring[e % 3], :], ACT.Silu))
                        free[ring[e % 3]] = (A.sem, A.n)
                at["zs"] = A.n

            yield

            @block.vector
            def _(dve):
                dve.wait_ge(V.sem, at["pad"])
                base = V.n
                for k in range(KC):
                    for e in range(CI):
                        if k == 0:
                            dve.wait_ge(A.sem, at["xi"] - 3 + e)
                            V(nc.vector.tensor_scalar(cv[:, e, :], xi[:, e, 0:S], w_conv[:, e, 0:1], b_conv[:, e:e + 1],
                                                      ALU.mult, ALU.add))
                        else:
                            dve.wait_ge(V.sem, base + 4 * (k - 1) + e + 1)
                            V(nc.vector.scalar_tensor_tensor(cv[:, e, :], xi[:, e, k:k + S], w_conv[:, e, k:k + 1],
                                                             cv[:, e, :], ALU.mult, ALU.add))
                at["cv"] = V.n - CI

            @block.scalar
            def _(act):
                for e in range(CI):
                    act.wait_ge(V.sem, at["cv"] + e + 1)
                    A(nc.scalar.activation(xc[:, e, :], cv[:, e, :], ACT.Silu))
                at["xc"] = A.n
                act.wait_ge(V.sem, at["gmax"])
                at["gexp"] = A(nc.scalar.activation(pr[:, :], lg[:, :], ACT.Exp, bias=g1[:, 0:1], accum_out=g1[:, 1:2]))

            @block.vector
            def _(dve):
                dve.wait_ge(A.sem, at["gexp"])
                link(dve, V, nc.vector.reciprocal(g1[:, 2:3], g1[:, 1:2]))
                link(dve, V, nc.vector.tensor_scalar(pr[:, :], pr[:, :], g1[:, 2:3], None, ALU.mult))
                link(dve, V, nc.vector.max(top[:, :], pr[:, :]))
                link(dve, V, nc.vector.match_replace(rest[:, :], top[:, :], pr[:, :], 0.0))
                at["picked"] = link(dve, V, nc.vector.tensor_tensor(pr[:, :], pr[:, :], rest[:, :], ALU.subtract))

            yield

            @block.tensor
            def _(pe):
                pe.wait_ge(A.sem, at["xc"])
                pe.wait_ge(*free[b0])
                for q in range(Q):
                    for e in range(CI):
                        last = nc.tensor.matmul(ps[:, b0, q * 64:q * 64 + 33], xc[:, e, q * P:(q + 1) * P], w_x[:, e, :],
                                                start=e == 0, stop=e == CI - 1)
                at["xd"] = T(last)
                pe.wait_ge(*free[b1])
                for e in range(CI):
                    last = nc.tensor.matmul(ps[0:NS, b1, :], w_x[:, e, NS + 1:], xc[:, e, :], start=e == 0, stop=e == CI - 1)
                at["cT"] = T(last)
                for q in range(Q):
                    pe.wait_ge(*(free[(b2, b3)[q]] if q < 2 else (A.sem, A.n + q - 1)))
                    for e in range(CI):
                        last = nc.tensor.transpose(ps[:, (b2, b3)[q % 2], e * P:(e + 1) * P], xc[:, e, q * P:(q + 1) * P], ident[:, :])
                    T(last)
                at["xct_ps"] = T.n - Q
                pe.wait_ge(V.sem, at["picked"])
                pe.wait_ge(V.sem, V.n + 1)
                for q in range(Q):
                    last = nc.tensor.transpose(ps[:, b0, q * E0:(q + 1) * E0], pr[:, q * P:(q + 1) * P], ident[0:E0, 0:E0])
                at["pT_ps"] = T(last)

            @block.scalar
            def _(act):
                for q in range(Q):
                    act.wait_ge(T.sem, at["xct_ps"] + q + 1)
                    A(nc.scalar.copy(xct[:, q, :], ps[:, (b2, b3)[q % 2], :]))
                    free[(b2, b3)[q % 2]] = (A.sem, A.n)
                at["xct"] = A.n

            @block.vector
            def _(dve):
                dve.wait_ge(T.sem, at["xd"])
                link(dve, V, nc.vector.tensor_copy(
                    xd[:, :, :], ps[:, b0, 0:256].rearrange("p (q e) -> p q e", q=Q)[:, :, 0:33]))
                at["sp1"] = link(dve, V, nc.vector.scalar_tensor_tensor(
                    sp1[:, :], xd[:, :, 0], -1.0, xd[:, :, 0], ALU.mult, ALU.min))
                dve.wait_ge(T.sem, at["cT"])
                link(dve, V, nc.vector.tensor_copy(cT[:, :], ps[0:NS, b1, :]))
                link(dve, V, nc.vector.tensor_copy(c3[0:NS, :], cT[:, :]))
                link(dve, V, nc.vector.tensor_tensor(cr[:, 0, :], cT[:, :], c3[0:NS, :], ALU.subtract))
                V(nc.vector.tensor_copy(c3[32:32 + NS, :], cr[:, 0, :]))
                link(dve, V, nc.vector.tensor_copy(crb[:, :], cr[:, 0, :]))
                at["cT_sb"] = V(nc.vector.tensor_tensor(c3[64:64 + NS, :], cr[:, 0, :], crb[:, :], ALU.subtract))
                free[b1] = (V.sem, V.n)
                dve.wait_ge(T.sem, at["pT_ps"])
                at["pT"] = V(nc.vector.tensor_copy(pT[:, :, :], ps[:, b0, 0:Q * E0]))
                free[b0] = (V.sem, V.n)

            yield

            @block.scalar
            def _(act):
                act.wait_ge(V.sem, at["sp1"])
                link(act, A, nc.scalar.activation(sp2[:, :], sp1[:, :], ACT.Exp))
                at["sp2"] = link(act, A, nc.scalar.activation(sp2[:, :], sp2[:, :], ACT.Ln, bias=1.0))

            @block.vector
            def _(dve):
                dve.wait_ge(A.sem, at["sp2"])
                link(dve, V, nc.vector.scalar_tensor_tensor(dl[:, :], xd[:, :, 0], 0.0, sp2[:, :], ALU.max, ALU.add))
                V(nc.vector.tensor_tensor(dla[:, :, :], after[:, :].unsqueeze(1).broadcast_to([P, Q, P]),
                                          dl[:, :].unsqueeze(2).broadcast_to([P, Q, P]), ALU.mult))
                V(nc.vector.tensor_copy(dlr[:, :, :], dl[:, :].unsqueeze(2).broadcast_to([P, Q, NS])))
                at["dla"] = V.n
                V(nc.vector.tensor_tensor(bdt[:, :, :], xd[:, :, 1:NS + 1], dl[:, :].unsqueeze(2).broadcast_to([P, Q, NS]),
                                          ALU.mult))
                at["bdt"] = V.n

            yield

            @block.tensor
            def _(pe):
                pe.wait_ge(V.sem, at["dla"])
                pe.wait_ge(*free[b3])
                for q in range(Q):
                    last = nc.tensor.matmul(ps[:, b3, q * P:(q + 1) * P], dla[:, q, :], upto[:, :], start=True, stop=True)
                at["span"] = T(last)
                pe.wait_ge(*free[b1])
                for q in range(Q):
                    last = nc.tensor.matmul(ps[0:NS, b1, q * P:(q + 1) * P], dlr[:, q, :], upto[:, :], start=True, stop=True)
                at["upto"] = T(last)
                pe.wait_ge(*free[b2])
                for k in range(KD):
                    for q in range(Q):
                        last = nc.tensor.matmul(ps[:, b2, k * E0:(k + 1) * E0], xn[:, q, k * P:(k + 1) * P], pT[:, q, :],
                                                start=q == 0, stop=q == Q - 1)
                at["merged"] = T(last)

            @block.vector
            def _(dve):
                dve.wait_ge(T.sem, at["span"])
                at["span_sb"] = V(nc.vector.tensor_copy(span[:, :], ps[:, b3, :]))
                free[b3] = (V.sem, V.n)
                dve.wait_ge(T.sem, at["merged"])
                V(nc.vector.tensor_copy(mergedT[:, :, :, bass.ds(b, 1)],
                                        ps[:, b2, 0:KD * E0].rearrange("p (k e o) -> p k e o", k=KD, o=1)))
                free[b2] = (V.sem, V.n)

            spread = (b0, b3)

            @block.tensor
            def _(pe):
                pe.wait_ge(*free[b0])
                pe.wait_ge(*free[b3])
                pe.wait_ge(V.sem, at["cT_sb"])
                for n in range(NS):
                    if n >= 2:
                        pe.wait_ge(spread_read.sem, n - 1)
                    spread_made(nc.tensor.matmul(ps[:, spread[n % 2], :], pick[:, n, :], c3[:, :], start=True, stop=True))

            @block.scalar
            def _(act):
                act.wait_ge(V.sem, at["span_sb"])
                for n in range(NS):
                    if n >= 2:
                        act.wait_ge(spread_read.sem, n - 1)
                    exp_made(nc.scalar.activation(ex[:, n % 2, :], span[:, :], ACT.Exp, scale=a_row[:, n:n + 1]))
                act.wait_ge(T.sem, at["upto"])
                A(nc.scalar.activation(cw[0:NS, :], ps[0:NS, b1, :], ACT.Exp, scale=a_col[:, 0:1]))
                at["cwe"] = A.n
                A(nc.scalar.activation(edec[:, :], ps[0:NS, b1, P - 1:S:P], ACT.Exp, scale=a_col[:, 0:1]))
                at["edec"] = A.n

            @block.vector
            def _(dve):
                dve.wait_ge(V.sem, at["span_sb"])
                at["bwa"] = link(dve, V, nc.vector.tensor_tensor(
                    bw[:, :, :], a_row[:, :].unsqueeze(1).broadcast_to([P, Q, NS]),
                    span[:, P - 1:S:P].unsqueeze(2).broadcast_to([P, Q, NS]), ALU.mult))
                for n in range(NS):
                    dve.wait_ge(exp_made.sem, n + 1)
                    dve.wait_ge(spread_made.sem, n + 1)
                    if n >= RT:
                        dve.wait_ge(summed.sem, n - RT + 1)
                    for q in range(Q):
                        cut = slice(q * P, (q + 1) * P)
                        last = nc.vector.scalar_tensor_tensor(t1[:, n % RT, cut], ex[:, n % 2, cut], bdt[:, q, n:n + 1],
                                                              ps[:, spread[n % 2], cut], ALU.mult, ALU.mult)
                    spread_read(last)
                free[b0] = free[b3] = (spread_read.sem, NS)

            @block.gpsimd
            def _(pool):
                for n in range(NS):
                    pool.wait_ge(spread_read.sem, n + 1)
                    if n == 0:
                        summed(nc.gpsimd.tensor_copy(gm[:, :], t1[:, 0, :]))
                    else:
                        pool.wait_ge(summed.sem, n)
                        summed(nc.gpsimd.tensor_tensor(gm[:, :], gm[:, :], t1[:, n % RT, :], ALU.add))
                pool.wait_ge(summed.sem, NS)
                g3 = gm[:, :].rearrange("p (q t) -> p q t", q=Q)
                summed(nc.gpsimd.tensor_tensor(g3, g3, upto[:, :].unsqueeze(1).broadcast_to([P, Q, P]), ALU.mult))

            @block.scalar
            def _(act):
                act.wait_ge(V.sem, at["bwa"])
                at["bwe"] = A(nc.scalar.activation(bw[:, :, :], bw[:, :, :], ACT.Exp))

            @block.vector
            def _(dve):
                dve.wait_ge(A.sem, at["bwe"])
                at["bw"] = V(nc.vector.tensor_tensor(bw[:, :, :], bw[:, :, :], bdt[:, :, :], ALU.mult))
                at["cw"] = V(nc.vector.tensor_tensor(cw[0:NS, :], cw[0:NS, :], cT[:, :], ALU.mult))
                free[b1] = (V.sem, V.n)

            yield

            @block.tensor
            def _(pe):
                pe.wait_ge(V.sem, at["bw"])
                pe.wait_ge(A.sem, at["xct"])
                at["u"] = T.n
                for q in range(Q - 1):
                    bank = (b2, b0, b3)[q]
                    pe.wait_ge(*free[bank])
                    T(nc.tensor.matmul(ps[0:NS, bank, :], bw[:, q, :], xct[:, q, :], start=True, stop=True))

            @block.vector
            def _(dve):
                dve.wait_ge(A.sem, at["edec"])
                for q in range(Q - 1):
                    bank = (b2, b0, b3)[q]
                    dve.wait_ge(T.sem, at["u"] + q + 1)
                    if q == 0:
                        link(dve, V, nc.vector.tensor_copy(st[0:NS, 1, :], ps[0:NS, bank, :]))
                    else:
                        link(dve, V, nc.vector.scalar_tensor_tensor(st[0:NS, q + 1, :], st[0:NS, q, :], edec[:, q:q + 1],
                                                                    ps[0:NS, bank, :], ALU.mult, ALU.add))
                    free[bank] = (V.sem, V.n)
                at["st"] = V.n

            yield

            @block.tensor
            def _(pe):
                pe.wait_ge(V.sem, at["st"])
                pe.wait_ge(summed.sem, NS + 1)
                at["y"] = T.n
                for e in range(CI):
                    pe.wait_ge(*free[4 * i + e])
                    for q in range(Q):
                        out = ps[:, 4 * i + e, q * P:(q + 1) * P]
                        last = nc.tensor.matmul(out, xct[:, q, e * P:(e + 1) * P], gm[:, q * P:(q + 1) * P],
                                                start=True, stop=q == 0)
                        if q:
                            last = nc.tensor.matmul(out, st[:, q, e * P:(e + 1) * P], cw[:, q * P:(q + 1) * P],
                                                    start=False, stop=True)
                    T(last)

            @block.vector
            def _(dve):
                dve.wait_ge(A.sem, at["zs"])
                for e in range(CI):
                    dve.wait_ge(T.sem, at["y"] + e + 1)
                    link(dve, V, nc.vector.scalar_tensor_tensor(yg[:, e, :], xc[:, e, :], skip[:, e:e + 1], ps[:, 4 * i + e, :],
                                                                ALU.mult, ALU.add))
                    free[4 * i + e] = (V.sem, V.n)
                    V(nc.vector.tensor_tensor(yg[:, e, :], yg[:, e, :], zs[:, e, :], ALU.mult))
                at["yg"] = V.n

            @block.tensor
            def _(pe):
                pe.wait_ge(V.sem, at["yg"])
                at["out"] = T.n
                for q in range(Q):
                    if q % 2 == 0:
                        pe.wait_ge(*free[4 * i + q // 2])
                    for e in range(CI):
                        last = nc.tensor.matmul(ps[:, 4 * i + q // 2, q % 2 * DM:(q % 2 + 1) * DM], yg[:, e, q * P:(q + 1) * P],
                                                w_out[:, e, :], start=e == 0, stop=e == CI - 1)
                    T(last)

            @block.scalar
            def _(act):
                for q in range(0, Q, 2):
                    act.wait_ge(T.sem, at["out"] + q + 2)
                    A(nc.scalar.copy(so[:, q:q + 2, :], ps[:, 4 * i + q // 2, :]))
                at["so"] = A.n

            @block.sync
            def _(sp):
                sp.wait_ge(V.sem, at["picked"])
                stored(sp.dma_start(d["picked"][b], pr[:, :]), 16)
                sp.wait_ge(A.sem, at["so"])
                stored(sp.dma_start(d["s0"][b].rearrange("(q p) e -> p q e", p=P), so[:, :, :]), 16)
                sp.wait_ge(stored.sem, 32)
            job.done = [(c.sem, c.n) for c in (V, A, T, stored, summed)]

        seqs = []
        loop = run_sequences(nc, ph, sequence, count, min(count, SEQS), LAG_A)
        next(loop)

        with nc.Block() as block:
            @block.scalar
            def _(act):
                A(nc.scalar.activation(a_row[:, :], a_row[:, :], ACT.Exp))
                A(nc.scalar.activation(a_col[:, :], a_col[:, :], ACT.Exp))

            @block.vector
            def _(dve):
                dve.wait_ge(A.sem, 2)
                V(nc.vector.tensor_scalar(a_row[:, :], a_row[:, :], -1.0, None, ALU.mult))
                V(nc.vector.tensor_scalar(a_col[:, :], a_col[:, :], -1.0, None, ALU.mult))

            @block.gpsimd
            def _(pool):
                link(pool, G, nc.gpsimd.memset(pick[:, :, :], 0.0))
                for part in range(3):
                    rows = pick[32 * part:32 * part + 32, :, :]
                    link(pool, G, nc.gpsimd.affine_select(out=rows, in_=rows, compare_op=ALU.not_equal, fill=1.0,
                                                          base=0, pattern=[[-1, NS], [0, P]], channel_multiplier=1))
                for c3, st, cw in seqs:
                    link(pool, G, nc.gpsimd.memset(c3[:, :], 0.0))
                    link(pool, G, nc.gpsimd.memset(st[:, :, :], 0.0))
                    link(pool, G, nc.gpsimd.memset(cw[:, :], 0.0))
        ph.clear()

        next(loop, None)


H0 = 1024
EG = 4
HK = H0 // P


def phase_b(nc, c, d, mergedT, count=E0 // EG):
    with ExitStack() as ctx:
        ph = Phase(nc, ctx, "b")
        ps = ph.psum()
        ident = c["ident"]
        w1 = ph.sb("w1", [P, EG, KD, H0])
        w2 = ph.sb("w2", [P, EG, HK, DM])
        w1b = ph.sb("w1b", [B, EG, H0])
        w2b = ph.sb("w2b", [B, EG, DM])
        mt = ph.sb("mt", [P, KD, EG, B])
        hb = ph.sb("hb", [B, 2, H0])
        h = ph.sb("h", [B, 2, H0])
        hT = ph.sb("hT", [P, 2, HK, B])
        o = ph.sb("o", [B, EG, DM])
        V, T = ph.counter("vector_done"), ph.counter("tensor_done")
        w1_in = [ph.counter(f"w1_in{j}") for j in range(EG)]
        w2_in = [ph.counter(f"w2_in{j}") for j in range(EG)]
        hidden_made, biased, hidden_done, turned_made, turned, out_made, out_done, stored = (ph.counter(n) for n in (
            "hidden_made", "biased", "hidden_done", "turned_made", "turned", "out_made", "out_done", "stored"))
        with nc.Fori(0, count) as g:
            with nc.Block() as block:
                @block.sync
                def _(sp):
                    for j in range(EG):
                        w1_in[j](sp.dma_start(w1[:, j, :, :], d["w1_0"][g * EG + j, 0:DM].rearrange("(k p) h -> p k h", p=P)), 16)
                        w1_in[j](sp.dma_start(w1b[:, j, :], d["w1_0"][g * EG + j, DM].partition_broadcast(B)), 16)
                        w2_in[j](sp.dma_start(w2[:, j, :, :], d["w2_0"][g * EG + j, 0:H0].rearrange("(k p) h -> p k h", p=P)), 16)
                        w2_in[j](sp.dma_start(w2b[:, j, :], d["w2_0"][g * EG + j, H0].partition_broadcast(B)), 16)
                    sp.wait_ge(out_done.sem, EG)
                    stored(sp.dma_start(d["o0"][:, bass.ds(g * EG, EG), :], o[:, :, :]), 16)
                    sp.wait_ge(stored.sem, 16)

                @block.tensor
                def _(pe):
                    def hidden(j):
                        pe.wait_ge(w1_in[j].sem, 32)
                        if j >= 2:
                            pe.wait_ge(biased.sem, j - 1)
                        for half in range(2):
                            out = ps[0:B, 2 * (j % 2) + half, :]
                            cols = slice(half * 512, half * 512 + 512)
                            for k in range(KD):
                                last = nc.tensor.matmul(out, mt[:, k, j, :], w1[:, j, k, cols], start=k == 0, stop=k == KD - 1)
                        hidden_made(last)

                    pe.wait_ge(V.sem, 1)
                    hidden(0)
                    for j in range(EG):
                        if j + 1 < EG:
                            hidden(j + 1)
                        pe.wait_ge(hidden_done.sem, j + 1)
                        if j >= 2:
                            pe.wait_ge(turned.sem, j - 1)
                        for k in range(HK):
                            last = nc.tensor.transpose(ps[:, 4 + j % 2, k * B:(k + 1) * B], h[:, j % 2, k * P:(k + 1) * P],
                                                       ident[0:B, 0:B])
                        turned_made(last)
                        pe.wait_ge(turned.sem, j + 1)
                        pe.wait_ge(w2_in[j].sem, 32)
                        if j >= 2:
                            pe.wait_ge(out_done.sem, j - 1)
                        out = ps[0:B, 6 + j % 2, 0:DM]
                        for k in range(HK):
                            last = nc.tensor.matmul(out, hT[:, j % 2, k, :], w2[:, j, k, :], start=k == 0, stop=k == HK - 1)
                        out_made(last)

                @block.scalar
                def _(act):
                    for j in range(EG):
                        act.wait_ge(biased.sem, j + 1)
                        if j >= 2:
                            act.wait_ge(turned_made.sem, j - 1)
                        hidden_done(nc.scalar.activation(h[:, j % 2, :], hb[:, j % 2, :], ACT.Gelu))

                @block.vector
                def _(dve):
                    V(nc.vector.tensor_copy(mt[:, :, :, :], mergedT[:, :, bass.ds(g * EG, EG), :]))
                    def bias(j):
                        dve.wait_ge(w1_in[j].sem, 32)
                        dve.wait_ge(hidden_made.sem, j + 1)
                        if j >= 2:
                            dve.wait_ge(hidden_done.sem, j - 1)
                        b0 = 2 * (j % 2)
                        biased(nc.vector.tensor_tensor(hb[:, j % 2, :].rearrange("p (a n) -> p a n", a=2), ps[0:B, b0:b0 + 2, :],
                                                       w1b[:, j, :].rearrange("p (a n) -> p a n", a=2), ALU.add))

                    bias(0)
                    for j in range(EG):
                        if j + 1 < EG:
                            bias(j + 1)
                        dve.wait_ge(turned_made.sem, j + 1)
                        if j >= 2:
                            dve.wait_ge(out_made.sem, j - 1)
                        turned(nc.vector.tensor_copy(hT[:, j % 2, :, :], ps[:, 4 + j % 2, 0:HK * B]))
                        dve.wait_ge(w2_in[j].sem, 32)
                        dve.wait_ge(out_made.sem, j + 1)
                        out_done(nc.vector.tensor_tensor(o[:, j, :], ps[0:B, 6 + j % 2, 0:DM], w2b[:, j, :], ALU.add))
            ph.clear()


HEADS, HD = 16, 8
HV = 2 * HD
LAMBDA_INIT = 0.8 - 0.6
SPLIT = 3
PRODUCTS = ((0, 0), (0, 1), (1, 0), (1, 1), (0, 2), (2, 0))
KROWS = len(PRODUCTS) * HD
SROWS = 2 * KROWS
AROWS = SROWS + 2 * SPLIT
GH = 4
NG = HEADS // GH
UNITS = HEADS * Q
GSTEPS = GH * Q
LAG = GSTEPS + 5
RING = 6
LAG_C1 = 5
RUN = 4


def phase_c1a(nc, c, d, count=B):
    with ExitStack() as ctx:
        ph = Phase(nc, ctx, "c1a")
        ps = ph.psum()
        ident = c["ident"]
        w_qkv = ph.sb("w_qkv", [P, KD, 3 * DM])
        load_once(nc, ph, [(w_qkv[:, :, :], d["w_qkv"].rearrange("(k p) e -> p k e", p=P))])
        V, A, T, G = (ph.counter(n) for n in ("vector_done", "scalar_done", "tensor_done", "pool_done"))
        padded = []

        def sequence(job):
            i, j = job.slot, job.j
            x = ph.sb(f"x_{i}", [P, Q, DM])
            s0 = ph.sb(f"s0_{i}", [P, Q, DM])
            pick = ph.sb(f"pick_{i}", [P, S])
            o0 = ph.sb(f"o0_{i}", [P, DM])
            g0 = ph.sb(f"g0_{i}", [P, Q, DM])
            xn = ph.sb(f"xn_{i}", [P, Q, DM])
            xnT = ph.sb(f"xnT_{i}", [P, KD, S])
            nm = Norm(ph, f"ln{i}")
            parts = ph.sb(f"parts_{i}", [P, 4, SPLIT, S], BF16)
            rem = ph.sb(f"rem_{i}", [P, 4, S])
            vo = ph.sb(f"vo_{i}", [P, Q, DM])
            x_in, s0_in, pick_in, stored = (ph.counter(f"{n}{j}") for n in ("x_in", "s0_in", "pick_in", "stored"))
            if j < SLOTS:
                padded.extend((pick, o0))
            yield
            block, b = job.block, job.b
            job.wait_for_buffers(block.gpsimd)
            free, at = {}, {}
            b0, b1, b2, b3 = range(4 * i, 4 * i + 4)

            @block.sync
            def _(sp):
                pick_in(sp.dma_start(pick[0:E0, :], d["picked"][b]), 16)
                pick_in(sp.dma_start(o0[0:E0, :], d["o0"][b]), 16)
                x_in(sp.dma_start(x[:, :, :], d["x"][b].rearrange("(q p) e -> p q e", p=P)), 16)
                s0_in(sp.dma_start(s0[:, :, :], d["s0"][b].rearrange("(q p) e -> p q e", p=P)), 16)

            @block.tensor
            def _(pe):
                pe.wait_ge(pick_in.sem, 32)
                for q in range(Q):
                    last = nc.tensor.matmul(ps[:, b0 + q // 2, q % 2 * DM:(q % 2 + 1) * DM], pick[:, q * P:(q + 1) * P], o0[:, :],
                                            start=True, stop=True)
                at["ffn0"] = T(last)

            @block.scalar
            def _(act):
                act.wait_ge(T.sem, at["ffn0"])
                at["g0"] = A(nc.scalar.activation(g0[:, :, :], ps[:, b0:b0 + 2, :], ACT.Silu))
                free[b0] = free[b1] = (A.sem, A.n)

            yield

            @block.gpsimd
            def _(pool):
                pool.wait_ge(A.sem, at["g0"])
                pool.wait_ge(s0_in.sem, 16)
                pool.wait_ge(x_in.sem, 16)
                link(pool, G, nc.gpsimd.tensor_tensor(g0[:, :, :], g0[:, :, :], s0[:, :, :], ALU.mult))
                at["x1"] = G(nc.gpsimd.tensor_tensor(x[:, :, :], x[:, :, :], g0[:, :, :], ALU.add))

            yield
            n = layer_norm(nc, block, nm, x, xn, V, A, (G.sem, at["x1"]))
            at["xn"] = n

            @block.sync
            def _(sp):
                sp.wait_ge(G.sem, at["x1"])
                stored(sp.dma_start(d["x1"][b].rearrange("(q p) e -> p q e", p=P), x[:, :, :]), 16)
                sp.wait_ge(V.sem, at["xn"])
                stored(sp.dma_start(d["xn1"][b].rearrange("(q p) e -> p q e", p=P), xn[:, :, :]), 16)

            yield
            at["xnT"] = transpose_rows(nc, block, ps, [b2, b3], ident, xn, xnT, T, V, (V.sem, n), free)

            for e in range(4):
                yield
                bank = b0 + e

                @block.tensor
                def _(pe):
                    if e == 0:
                        pe.wait_ge(*at["xnT"])
                    pe.wait_ge(*free[bank])
                    for k in range(KD):
                        last = nc.tensor.matmul(ps[:, bank, :], w_qkv[:, k, e * P:(e + 1) * P], xnT[:, k, :],
                                                start=k == 0, stop=k == KD - 1)
                    at["qk"] = T(last)

                @block.scalar
                def _(act):
                    act.wait_ge(T.sem, at["qk"])
                    at["hi"] = A(nc.scalar.copy(parts[:, e, 0, :], ps[:, bank, :]))

                @block.vector
                def _(dve):
                    dve.wait_ge(A.sem, at["hi"])
                    at["rem"] = V(nc.vector.tensor_tensor(rem[:, e, :], ps[:, bank, :], parts[:, e, 0, :], ALU.subtract))
                    free[bank] = (V.sem, V.n)

                @block.scalar
                def _(act):
                    act.wait_ge(V.sem, at["rem"])
                    at["mid"] = A(nc.scalar.copy(parts[:, e, 1, :], rem[:, e, :]))

                @block.gpsimd
                def _(pool):
                    pool.wait_ge(A.sem, at["mid"])
                    at["lo"] = G(nc.gpsimd.tensor_tensor(parts[:, e, 2, :], rem[:, e, :], parts[:, e, 1, :], ALU.subtract))

                @block.sync
                def _(sp):
                    sp.wait_ge(G.sem, at["lo"])
                    stored(sp.dma_start(d["qk_parts"][b, e // 2, :, e % 2 * P:(e % 2 + 1) * P].rearrange("s p n -> p s n"),
                                        parts[:, e, :, :]), 16)

            yield

            @block.tensor
            def _(pe):
                for q in range(Q):
                    if q % 2 == 0:
                        pe.wait_ge(*free[b0 + q // 2])
                    for k in range(KD):
                        last = nc.tensor.matmul(ps[:, b0 + q // 2, q % 2 * DM:(q % 2 + 1) * DM], xnT[:, k, q * P:(q + 1) * P],
                                                w_qkv[:, k, 2 * DM:], start=k == 0, stop=k == KD - 1)
                at["v"] = T(last)

            @block.scalar
            def _(act):
                act.wait_ge(T.sem, at["v"])
                at["vo"] = A(nc.scalar.copy(vo[:, :, :], ps[:, b0:b0 + 2, :].rearrange("p a (q e) -> p (a q) e", q=2)))

            @block.sync
            def _(sp):
                sp.wait_ge(A.sem, at["vo"])
                stored(sp.dma_start(d["v1"][b].rearrange("(q p) e -> p q e", p=P), vo[:, :, :]), 16)
                sp.wait_ge(stored.sem, stored.n)
            job.done = [(c.sem, c.n) for c in (V, A, T, G, stored)]

        loop = run_sequences(nc, ph, sequence, count, min(count, 4), LAG_C1)
        next(loop)
        with nc.Block() as block:
            @block.vector
            def _(dve):
                for t in padded:
                    link(dve, V, nc.vector.memset(t[:, :], 0.0))
        ph.clear()
        next(loop, None)


def phase_c1b(nc, c, d, count=B):
    with ExitStack() as ctx:
        ph = Phase(nc, ctx, "c1b")
        ps = ph.psum()
        ident = c["ident"]
        w_proj = ph.sb("w_proj", [P, KD, DM])
        b_proj = ph.sb("b_proj", [P, DM])
        w_sub = ph.sb("w_sub", [P, HV])
        lams = ph.sb("lams", [P, 4, HD])
        load_once(nc, ph, [
            (w_proj[:, :, :], d["w_proj"].rearrange("(k p) e -> p k e", p=P)),
            (b_proj[:, :], d["b_proj"].partition_broadcast(P)),
            (w_sub[:, :], d["sub_norm_w"].partition_broadcast(P)),
        ] + [(lams[:, i, :], d[n].partition_broadcast(P)) for i, n in enumerate(
            ("lambda_q1", "lambda_k1", "lambda_q2", "lambda_k2"))])
        V, A, G = (ph.counter(n) for n in ("vector_done", "scalar_done", "pool_done"))
        lp = ph.sb("lp", [P, 2, HD])
        le = ph.sb("le", [P, 2])
        lam = ph.sb("lam", [P, 1])
        identb = ph.sb("identb", [P, P], BF16)
        qs = ph.sb("qs", [AROWS, 2, HEADS, S], BF16)
        ks = ph.sb("ks", [AROWS, 2, 2, HEADS, S], BF16)
        v1 = ph.sb("v1", [P, 2, Q, HEADS, 32])

        with nc.Block() as block:
            @block.vector
            def _(dve):
                V(nc.vector.memset(ks[0:SROWS, :, :, :, :], 0.0))
                V(nc.vector.memset(qs[:, :, :, :], 0.0))
                V(nc.vector.memset(v1[:, :, :, :, HV:], 0.0))
                V(nc.vector.tensor_copy(identb[:, :], ident[:, :]))
                V(nc.vector.tensor_scalar(w_sub[:, :], w_sub[:, :], 1.0 - LAMBDA_INIT, None, ALU.mult))
                link(dve, V, nc.vector.tensor_tensor(lp[:, :, :], lams[:, 0:4:2, :], lams[:, 1:4:2, :], ALU.mult))
                V(nc.vector.memset(v1[:, :, :, :, HV:HV + 1], 1.0))
                link(dve, V, nc.vector.tensor_reduce(le[:, :], lp[:, :, :], AX.X, ALU.add))

            @block.gpsimd
            def _(pool):
                rows = ks[SROWS:AROWS]
                link(pool, G, nc.gpsimd.memset(rows[:, :, :, :, :], 1.0))
                for slot in range(2):
                    for half, base, mult in ((0, SPLIT - 1, -1), (1, -SPLIT, 1)):
                        link(pool, G, nc.gpsimd.affine_select(
                            out=rows[:, slot, half], in_=rows[:, slot, half], compare_op=ALU.is_ge, fill=0.0, base=base,
                            pattern=[[0, HEADS], [0, S]], channel_multiplier=mult))

            @block.scalar
            def _(act):
                act.wait_ge(V.sem, V.n)
                A(nc.scalar.activation(le[:, :], le[:, :], ACT.Exp))

            @block.vector
            def _(dve):
                dve.wait_ge(A.sem, 1)
                V(nc.vector.scalar_tensor_tensor(lam[:, :], le[:, 0:1], LAMBDA_INIT, le[:, 1:2], ALU.add, ALU.subtract))
        ph.clear()

        vin = ph.sb("vin", [P, Q, DM])
        mx = ph.sb("mx", [P, 2, Q, 2, GH])
        mrem = ph.sb("mrem", [P, 2, Q, 2, GH])
        mparts = ph.sb("mparts", [P, 2, Q, 2, SPLIT, GH], BF16)
        mT = ph.sb("mT", [2 * SPLIT * GH, 2, S], BF16)
        pT = ph.sb("pT", [P, RING, 2, S])
        ao = ph.sb("ao", [P, 2, S])
        ot = ph.sb("ot", [P, Q, HEADS, 2, 32])
        rr = ph.sb("rr", [P, Q * HEADS, 2])
        oh = ph.sb("oh", [P, Q * HEADS, HV])
        o2 = ph.sb("o2", [P, Q * HEADS, HV])
        ms = ph.sb("ms", [P, Q * HEADS])
        oT = ph.sb("oT", [P, KD, S])
        so = ph.sb("so", [P, Q, DM])
        qk_in = [ph.counter("qk_in0"), ph.counter("qk_in1")]
        max_in = [ph.counter("max_in0"), ph.counter("max_in1")]
        (v_in, v_ready, stored, max_split, max_remainder, tile_made, tile_read, maxT_made, maxT_done, logit_made, prob_made,
         mixed, mixed_read, turned_made, turned_read, sums_read, squares_made, mean_made, root_made, scale_made,
         scaled) = (ph.counter(n) for n in (
             "v_in", "v_ready", "stored", "max_split", "max_remainder", "tile_made", "tile_read", "maxT_made", "maxT_done",
             "logit_made", "prob_made", "mixed", "mixed_read", "turned_made", "turned_read", "sums_read", "squares_made",
             "mean_made", "root_made", "scale_made", "scaled"))

        run = min(count, RUN)
        groups, units, pairs = run * NG, run * UNITS, run * HEADS // 2
        GATHERS = 2 * 2 * len(PRODUCTS)

        PAIR_AT = 12
        SQUARES, OT_AT, PROJ_AT = 6, 11, 14
        last_pair = [LAG + PAIR_AT + 8 * (8 * n + 7) for n in range(run)]
        steps = last_pair[-1] + PROJ_AT + 1

        def tiles(s):
            out = [("score", k // (2 * UNITS), k % (2 * UNITS)) for k in (2 * s, 2 * s + 1) if k < 2 * units]
            for n in range(run):
                if s == last_pair[n] + OT_AT:
                    out += [("oT", n, 0), ("oT", n, 1)]
                if s == last_pair[n] + PROJ_AT:
                    out += [("proj", n, 0), ("proj", n, 1)]
            return out

        def tiles_until(step):
            return sum(len(tiles(s)) for s in range(step + 1))

        def unit(u):
            n, r = u // UNITS, u % UNITS
            return n, 2 * (r // (2 * Q)) + r % 2, r // 2 % Q

        def pair_at(s):
            u = s - LAG - PAIR_AT
            return u // 8 if u >= 0 and u % 8 == 0 and u // 8 < pairs else None

        def group_at(s):
            return s // GSTEPS - 1 if s % GSTEPS == 1 and s > 1 and s // GSTEPS <= groups else None

        def groups_before(p):
            return sum(1 for g in range(groups) if GSTEPS * (g + 1) + 1 <= LAG + PAIR_AT + 8 * p)

        def pairs_before(g):
            return sum(1 for p in range(pairs) if LAG + PAIR_AT + 8 * p < GSTEPS * (g + 1) + 1)

        with nc.Fori(0, count // run) as trip:
            b, at_sums = trip * run, {}
            with nc.Block() as block:
                def store(sp, n):
                    sp.wait_ge(tile_read.sem, tiles_until(last_pair[n] + PROJ_AT))
                    stored(sp.dma_start(d["s1"][b + n].rearrange("(q p) e -> p q e", p=P), so[:, :, :]), 16)

                @block.sync
                def _(sp):
                    for n in range(run):
                        if n >= 2:
                            sp.wait_ge(prob_made.sem, UNITS * (n - 1))
                        slot = n % 2
                        for half in range(2):
                            for r, pair in enumerate(PRODUCTS):
                                row = KROWS * half + HD * r
                                for side, dst, part in ((0, qs[:, slot], pair[1]), (1, ks[:, slot, half], pair[0])):
                                    src = d["qk_parts"][b + n, side, part].rearrange("(h c r) n -> c r h n", c=2, r=HD)[half]
                                    qk_in[slot](sp.dma_start(dst[row:row + HD], src), 16)
                        if n >= 1:
                            sp.wait_ge(v_ready.sem, n)
                        v_in(sp.dma_start(vin[:, :, :], d["v1"][b + n].rearrange("(q p) e -> p q e", p=P)), 16)
                        if n >= 2:
                            store(sp, n - 2)
                    for n in range(max(0, run - 2), run):
                        store(sp, n)
                    sp.wait_ge(stored.sem, 16 * run)

                @block.tensor
                def _(pe):
                    made = 0

                    def tile(kind, n, k):
                        nonlocal made
                        bank, slot = made % 2, n % 2
                        if made >= 2:
                            pe.wait_ge(tile_read.sem, made - 1)
                        if kind == "score":
                            if k == 0:
                                pe.wait_ge(qk_in[slot].sem, 16 * GATHERS * (n // 2 + 1))
                            hc, m = k // Q, k % Q
                            last = nc.tensor.matmul(ps[:, bank, :], qs[0:SROWS, slot, hc // 2, m * P:(m + 1) * P],
                                                    ks[0:SROWS, slot, hc % 2, hc // 2, :], start=True, stop=True)
                        elif kind == "oT":
                            pe.wait_ge(scaled.sem, 2 * (n + 1))
                            oq = oh[:, :, :].rearrange("p (q h) e -> p q (h e)", q=Q)
                            for q in range(Q):
                                last = nc.tensor.transpose(ps[:, bank, q * P:(q + 1) * P], oq[:, q, k * P:(k + 1) * P], ident[:, :])
                        else:
                            pe.wait_ge(tile_read.sem, tiles_until(last_pair[n] + OT_AT))
                            for q in (2 * k, 2 * k + 1):
                                for kk in range(KD):
                                    last = nc.tensor.matmul(ps[:, bank, q % 2 * DM:(q % 2 + 1) * DM], oT[:, kk, q * P:(q + 1) * P],
                                                            w_proj[:, kk, :], start=kk == 0, stop=kk == KD - 1)
                        tile_made(last)
                        made += 1

                    def turn_max(g):
                        pe.wait_ge(max_split.sem, 3 * (g + 1))
                        if pairs_before(g):
                            pe.wait_ge(turned_read.sem, pairs_before(g))
                        if g:
                            pe.wait_ge(maxT_done.sem, g)
                        psb = ps[:, 7, :].bitcast(BF16)
                        for m in range(Q):
                            last = nc.tensor.transpose(psb[0:2 * SPLIT * GH, m * P:(m + 1) * P],
                                                       mparts[:, g % 2, m, :, :, :].rearrange("p a b c -> p (a b c)"),
                                                       identb[:, :])
                        maxT_made(last)

                    def logits(u):
                        n, head, m = unit(u)
                        if u % (GH * Q) == 0:
                            g = u // (GH * Q)
                            pe.wait_ge(max_in[g % 2].sem, 32 * (g // 2 + 1))
                        if u >= 2:
                            pe.wait_ge(prob_made.sem, u - 1)
                        for half in range(2):
                            last = nc.tensor.matmul(ps[:, 2 + 2 * (u % 2) + half, :], ks[:, n % 2, half, head, m * P:(m + 1) * P],
                                                    qs[:, n % 2, head, :], start=True, stop=True)
                        logit_made(last)

                    def mix(w):
                        m = w % Q
                        pe.wait_ge(prob_made.sem, 2 * w + 2)
                        if m == 0 and w >= Q:
                            pe.wait_ge(mixed_read.sem, w // Q)
                        if 2 * w % UNITS == 0:
                            pe.wait_ge(v_ready.sem, 2 * w // UNITS + 1)
                        for i in range(2):
                            n, head, _ = unit(2 * w + i)
                            for half in range(2):
                                row = 32 * (2 * i + half)
                                last = nc.tensor.matmul(ps[row:row + 32, 6, :], v1[:, n % 2, m, head, :],
                                                        pT[:, (2 * w + i) % RING, half, :], start=m == 0, stop=m == Q - 1,
                                                        skip_group_check=True)
                        mixed(last)

                    def turn_pair(p):
                        pe.wait_ge(mixed_read.sem, p + 1)
                        if p >= 1:
                            pe.wait_ge(turned_read.sem, p)
                        pe.wait_ge(maxT_done.sem, groups_before(p))
                        for q in range(Q):
                            last = nc.tensor.transpose(ps[:, 7, q * P:(q + 1) * P], ao[:, p % 2, q * P:(q + 1) * P], ident[:, :])
                        turned_made(last)

                    for s in range(steps):
                        for t in tiles(s)[:1]:
                            tile(*t)
                        if group_at(s) is not None:
                            turn_max(group_at(s))
                        u = s - LAG
                        if 0 <= u < units:
                            logits(u)
                        for t in tiles(s)[1:]:
                            tile(*t)
                        if u >= 3 and (u - 3) % 2 == 0 and (u - 3) // 2 < units // 2:
                            mix((u - 3) // 2)
                        if pair_at(s) is not None:
                            turn_pair(pair_at(s))

                @block.scalar
                def _(act):
                    for s in range(steps):
                        g = group_at(s - 1)
                        if g is not None:
                            act.wait_ge(maxT_done.sem, g + 1)
                            slot, heads = g // NG % 2, slice(GH * (g % NG), GH * (g % NG + 1))
                            for half in range(2):
                                row, n = SROWS + SPLIT * half, SPLIT * GH
                                max_in[g % 2](act.dma_start(qs[row:row + SPLIT, slot, heads, :],
                                                            mT[n * half:n * (half + 1), g % 2, :]), 16)
                        u = s - LAG
                        if 0 <= u < units:
                            act.wait_ge(logit_made.sem, u + 1)
                            if u >= RING:
                                act.wait_ge(mixed.sem, (u - RING) // 2 + 1)
                            b0 = 2 + 2 * (u % 2)
                            prob_made(nc.scalar.activation(pT[:, u % RING, :, :], ps[:, b0:b0 + 2, :], ACT.Exp, scale=HD ** -0.5))
                        if u >= 10 and (u - 10) % 8 == 0 and (u - 10) // 8 < pairs:
                            p = (u - 10) // 8
                            act.wait_ge(mixed.sem, Q * (p + 1))
                            if p >= 2:
                                act.wait_ge(turned_made.sem, p - 1)
                            mixed_read(nc.scalar.copy(ao[:, p % 2, :], ps[:, 6, :]))
                        for n in range(run):
                            if s == last_pair[n] + SQUARES + 1:
                                act.wait_ge(mean_made.sem, 2 * (n + 1))
                                root_made(nc.scalar.activation(ms[:, :], ms[:, :], ACT.Sqrt))

                @block.vector
                def _(dve):
                    read = 0

                    def tile(kind, n, k):
                        nonlocal read
                        bank = read % 2
                        dve.wait_ge(tile_made.sem, read + 1)
                        if kind == "score":
                            hc, m = k // Q, k % Q
                            head, half, g = hc // 2, hc % 2, NG * n + hc // 2 // GH
                            tile_read(nc.vector.tensor_reduce(mx[:, g % 2, m, half, head % GH:head % GH + 1], ps[:, bank, :],
                                                              AX.X, ALU.max, negate=True))
                        elif kind == "oT":
                            tile_read(nc.vector.tensor_copy(oT[:, k, :], ps[:, bank, :]))
                        else:
                            if n and k == 0:
                                dve.wait_ge(stored.sem, 16 * n)
                            tile_read(nc.vector.tensor_tensor(
                                so[:, 2 * k:2 * k + 2, :], ps[:, bank, :].rearrange("p (q e) -> p q e", q=2),
                                b_proj[:, :].unsqueeze(1).broadcast_to([P, 2, DM]), ALU.add))
                        read += 1

                    def split_max(g):
                        m, r = mx[:, g % 2], mrem[:, g % 2]
                        hi, mid, lo = (mparts[:, g % 2, :, :, i, :] for i in range(SPLIT))
                        dve.wait_ge(tile_read.sem, read)
                        link(dve, max_split, nc.vector.tensor_copy(hi, m))
                        link(dve, max_remainder, nc.vector.tensor_tensor(r, m, hi, ALU.subtract))
                        link(dve, max_split, nc.vector.tensor_copy(mid, r))
                        max_split(nc.vector.tensor_tensor(lo, r, mid, ALU.subtract))

                    def store_max(g):
                        dve.wait_ge(maxT_made.sem, g + 1)
                        if g >= 2:
                            dve.wait_ge(max_in[g % 2].sem, 32 * (g // 2))
                        psb = ps[:, 7, :].bitcast(BF16)
                        maxT_done(nc.vector.tensor_copy(mT[:, g % 2, :], psb[0:2 * SPLIT * GH, 0:S]))

                    def turned(p):
                        dve.wait_ge(turned_made.sem, p + 1)
                        n = p // (HEADS // 2)
                        if n and p % (HEADS // 2) == 0:
                            dve.wait_ge(sums_read.sem, 2 * n)
                        h = 2 * (p % (HEADS // 2))
                        turned_read(nc.vector.tensor_copy(
                            ot[:, :, h:h + 2, :, :].rearrange("p q h c e -> p q (h c e)"),
                            ps[:, 7, :].rearrange("p (q r) -> p q r", q=Q)))

                    for s in range(steps):
                        for t in tiles(s):
                            tile(*t)
                        if s % GSTEPS == GSTEPS - 1 and s < units:
                            split_max(s // GSTEPS)
                        if group_at(s) is not None:
                            store_max(group_at(s))
                        if pair_at(s) is not None:
                            turned(pair_at(s))
                        for n in range(run):
                            if s == last_pair[n]:
                                dve.wait_ge(turned_read.sem, (n + 1) * HEADS // 2)
                                link(dve, V, nc.vector.reciprocal(
                                    rr[:, :, :], ot[:, :, :, :, HV].rearrange("p q h c -> p (q h) c")))
                                at_sums[n] = V(nc.vector.tensor_scalar(rr[:, :, 1], rr[:, :, 1], lam[:, 0:1], None, ALU.mult))
                            if s == last_pair[n] + SQUARES:
                                dve.wait_ge(squares_made.sem, 2 * (n + 1))
                                link(dve, mean_made, nc.vector.tensor_reduce(ms[:, :], o2[:, :, :], AX.X, ALU.add))
                                mean_made(nc.vector.tensor_scalar(ms[:, :], ms[:, :], 1.0 / HV, EPS, ALU.mult, ALU.add))
                            if s == last_pair[n] + SQUARES + 1:
                                dve.wait_ge(root_made.sem, n + 1)
                                scale_made(nc.vector.reciprocal(ms[:, :], ms[:, :]))

                @block.gpsimd
                def _(pool):
                    def values(n):
                        pool.wait_ge(v_in.sem, 16 * (n + 1))
                        if n >= 2:
                            pool.wait_ge(mixed.sem, UNITS // 2 * (n - 1))
                        v_ready(nc.gpsimd.tensor_copy(v1[:, n % 2, :, :, 0:HV], vin[:, :, :].rearrange("p q (h e) -> p q h e", h=HEADS)))

                    def finish(n):
                        o5 = ot[:, :, :, :, :].rearrange("p q h c e -> p (q h) c e")
                        bc = [P, Q * HEADS, HV]
                        pool.wait_ge(V.sem, at_sums[n])
                        if n:
                            pool.wait_ge(tile_read.sem, tiles_until(last_pair[n - 1] + OT_AT))
                        link(pool, sums_read, nc.gpsimd.tensor_tensor(
                            oh[:, :, :], o5[:, :, 0, 0:HV], rr[:, :, 0:1].broadcast_to(bc), ALU.mult))
                        link(pool, sums_read, nc.gpsimd.tensor_tensor(
                            o2[:, :, :], o5[:, :, 1, 0:HV], rr[:, :, 1:2].broadcast_to(bc), ALU.mult))
                        link(pool, squares_made, nc.gpsimd.tensor_tensor(oh[:, :, :], oh[:, :, :], o2[:, :, :], ALU.subtract))
                        squares_made(nc.gpsimd.tensor_tensor(o2[:, :, :], oh[:, :, :], oh[:, :, :], ALU.mult))
                        pool.wait_ge(scale_made.sem, n + 1)
                        link(pool, scaled, nc.gpsimd.tensor_tensor(
                            oh[:, :, :], oh[:, :, :], ms[:, :].unsqueeze(2).broadcast_to(bc), ALU.mult))
                        link(pool, scaled, nc.gpsimd.tensor_tensor(
                            oh[:, :, :], oh[:, :, :], w_sub[:, :].unsqueeze(1).broadcast_to(bc), ALU.mult))

                    values(0)
                    if run > 1:
                        values(1)
                    for n in range(run):
                        finish(n)
                        if n + 2 < run:
                            values(n + 2)
            ph.clear()


E1, H1 = 8, 4 * DM
HK1 = H1 // P
MB = B // E1


def phase_c2(nc, c, d, count=E1):
    with ExitStack() as ctx:
        ph = Phase(nc, ctx, "c2")
        ps = ph.psum()
        ident = c["ident"]
        w_attn = ph.sb("w_attn", [P, KD, DM])
        w_next = ph.sb("w_next", [P, KD, DM])
        b_next = ph.sb("b_next", [P, DM])
        cols = {n: ph.sb(n, [P, KD]) for n in ("ln_scale", "ln_bias", "attn_b")}
        load_once(nc, ph, [
            (w_attn[:, :, :], d["attn_w"].rearrange("(k p) e -> p k e", p=P)),
            (w_next[:, :, :], d["next_w"].rearrange("(k p) e -> p k e", p=P)),
            (b_next[:, :], d["next_b"].partition_broadcast(P)),
        ] + [(t[:, :], d[n]) for n, t in cols.items()])
        V, A, T = (ph.counter(n) for n in ("vector_done", "scalar_done", "tensor_done"))
        w1 = ph.sb("w1", [P, KD, H1])
        w2 = ph.sb("w2", [P, HK1, DM])
        b1 = ph.sb("b1", [P, HK1])
        b2 = ph.sb("b2", [P, KD])
        nm = Norm(ph, "ln")
        f = ph.sb("f", [P, MB, Q, DM])
        z = ph.sb("z", [P, MB, Q, DM])
        fT = ph.sb("fT", [P, MB, KD, S])
        zT = ph.sb("zT", [P, MB, KD, S])
        hT = ph.sb("hT", [P, HK1, S])
        eT = ph.sb("eT", [P, KD, S])
        x1 = ph.sb("x1", [P, MB, Q, DM])
        s1 = ph.sb("s1", [P, MB, Q, DM])
        g = ph.sb("g", [P, Q, DM])
        w_in, stored = ph.counter("w_in"), ph.counter("stored")
        f_in, x1_in, s1_in = ([ph.counter(f"{n}{i}") for i in range(MB)] for n in ("f_in", "x1_in", "s1_in"))
        hidden_made, hidden_done = ph.counter("hidden_made"), ph.counter("hidden_done")
        RH = 4
        with nc.Fori(0, count) as e:
            free, at = {}, {}
            with nc.Block() as block:
                @block.sync
                def _(sp):
                    tiles = lambda n, i: d[n][e + i * E1].rearrange("(q p) e -> p q e", p=P)
                    for i in range(MB):
                        f_in[i](sp.dma_start(f[:, i, :, :], tiles("xn1", i)), 16)
                    w_in(sp.dma_start(w1[:, :, :], d["w1_1"][e].rearrange("(k p) h -> p k h", p=P)), 16)
                    w_in(sp.dma_start(w2[:, :, :], d["w2_1"][e].rearrange("(k p) h -> p k h", p=P)), 16)
                    w_in(sp.dma_start(b1[:, :], d["b1_1"][e]), 16)
                    w_in(sp.dma_start(b2[:, :], d["b2_1"][e]), 16)
                    for i in range(MB):
                        x1_in[i](sp.dma_start(x1[:, i, :, :], tiles("x1", i)), 16)
                        s1_in[i](sp.dma_start(s1[:, i, :, :], tiles("s1", i)), 16)

                for i in range(MB):
                    n = layer_norm(nc, block, nm, f[:, i, :, :], z[:, i, :, :], V, A, (f_in[i].sem, 16))
                    at["fT", i] = transpose_rows(nc, block, ps, [0, 1], ident, f[:, i, :, :], fT[:, i, :, :], T, A,
                                                 (f_in[i].sem, 16), free, eng="scalar")

                    @block.tensor
                    def _(pe):
                        pe.wait_ge(V.sem, n)
                        for k in range(KD):
                            if 2 + k in free:
                                pe.wait_ge(*free[2 + k])
                            for q in range(Q):
                                last = nc.tensor.transpose(ps[:, 2 + k, q * P:(q + 1) * P], z[:, i, q, k * P:(k + 1) * P],
                                                           ident[:, :])
                            T(last)
                        at["zT_ps"] = T.n

                    @block.vector
                    def _(dve):
                        for k in range(KD):
                            dve.wait_ge(T.sem, at["zT_ps"] - 1 + k)
                            V(nc.vector.tensor_scalar(zT[:, i, k, :], ps[:, 2 + k, :], cols["ln_scale"][:, k:k + 1],
                                                      cols["ln_bias"][:, k:k + 1], ALU.mult, ALU.add))
                            free[2 + k] = (V.sem, V.n)
                        at["zT", i] = V.n

                for i in range(MB):
                    @block.tensor
                    def _(pe):
                        pe.wait_ge(V.sem, at["zT", i])
                        for e2 in range(KD):
                            pe.wait_ge(*free[e2 + 2 * i])
                            for k in range(KD):
                                last = nc.tensor.matmul(ps[:, e2 + 2 * i, :], w_attn[:, k, e2 * P:(e2 + 1) * P], zT[:, i, k, :],
                                                        start=k == 0, stop=k == KD - 1)
                            T(last)
                        at["xa_ps"] = T.n

                    @block.vector
                    def _(dve):
                        dve.wait_ge(*at["fT", i])
                        for e2 in range(KD):
                            dve.wait_ge(T.sem, at["xa_ps"] - 1 + e2)
                            V(nc.vector.scalar_tensor_tensor(fT[:, i, e2, :], ps[:, e2 + 2 * i, :], cols["attn_b"][:, e2:e2 + 1],
                                                             fT[:, i, e2, :], ALU.add, ALU.add))
                            free[e2 + 2 * i] = (V.sem, V.n)
                        at["xa", i] = V.n

                for i in range(MB):
                    @block.tensor
                    def _(pe):
                        pe.wait_ge(V.sem, at["xa", i])
                        if i == 0:
                            pe.wait_ge(w_in.sem, 64)
                        for h in range(HK1):
                            n = i * HK1 + h
                            if n >= RH:
                                pe.wait_ge(hidden_done.sem, n - RH + 1)
                            for k in range(KD):
                                last = nc.tensor.matmul(ps[:, 4 + n % RH, :], w1[:, k, h * P:(h + 1) * P], fT[:, i, k, :],
                                                        start=k == 0, stop=k == KD - 1)
                            hidden_made(last)
                        for e2 in range(KD):
                            pe.wait_ge(*free[e2])
                            for h in range(HK1):
                                pe.wait_ge(hidden_done.sem, i * HK1 + h + 1)
                                last = nc.tensor.matmul(ps[:, e2, :], w2[:, h, e2 * P:(e2 + 1) * P], hT[:, h, :],
                                                        start=h == 0, stop=h == HK1 - 1)
                            T(last)
                        at["eT_ps"] = T.n

                    @block.scalar
                    def _(act):
                        if i:
                            act.wait_ge(T.sem, at["hT_read"])
                        else:
                            act.wait_ge(w_in.sem, 64)
                        for h in range(HK1):
                            n = i * HK1 + h
                            act.wait_ge(hidden_made.sem, n + 1)
                            hidden_done(nc.scalar.activation(hT[:, h, :], ps[:, 4 + n % RH, :], ACT.Gelu, bias=b1[:, h:h + 1]))
                    at["hT_read"] = at["eT_ps"]

                    @block.vector
                    def _(dve):
                        if i == 0:
                            dve.wait_ge(w_in.sem, 64)
                        else:
                            dve.wait_ge(T.sem, at["out_ps"])
                        for e2 in range(KD):
                            dve.wait_ge(T.sem, at["eT_ps"] - 1 + e2)
                            V(nc.vector.tensor_scalar(eT[:, e2, :], ps[:, e2, :], b2[:, e2:e2 + 1], None, ALU.add))
                            free[e2] = (V.sem, V.n)
                        at["eT"] = V.n

                    @block.tensor
                    def _(pe):
                        pe.wait_ge(V.sem, at["eT"])
                        pe.wait_ge(*free[2])
                        pe.wait_ge(*free[3])
                        for q in range(Q):
                            for k in range(KD):
                                last = nc.tensor.matmul(ps[:, 2 + q // 2, q % 2 * DM:(q % 2 + 1) * DM],
                                                        eT[:, k, q * P:(q + 1) * P], w_next[:, k, :], start=k == 0, stop=k == KD - 1)
                        at["out_ps"] = T(last)

                    @block.vector
                    def _(dve):
                        dve.wait_ge(T.sem, at["out_ps"])
                        if i:
                            dve.wait_ge(V.sem, at["x2"])
                        at["g"] = V(nc.vector.tensor_tensor(
                            g[:, :, :], ps[:, 2:4, :].rearrange("p a (q e) -> p (a q) e", q=2),
                            b_next[:, :].unsqueeze(1).broadcast_to([P, Q, DM]), ALU.add))
                        free[2] = free[3] = (V.sem, V.n)

                    @block.scalar
                    def _(act):
                        act.wait_ge(V.sem, at["g"])
                        link(act, A, nc.scalar.activation(g[:, :, :], g[:, :, :], ACT.Gelu))
                        at["sg"] = A(nc.scalar.activation(g[:, :, :], g[:, :, :], ACT.Silu))

                    @block.vector
                    def _(dve):
                        dve.wait_ge(A.sem, at["sg"])
                        dve.wait_ge(s1_in[i].sem, 16)
                        dve.wait_ge(x1_in[i].sem, 16)
                        link(dve, V, nc.vector.tensor_tensor(s1[:, i, :, :], s1[:, i, :, :], g[:, :, :], ALU.mult))
                        at["x2"] = V(nc.vector.tensor_tensor(x1[:, i, :, :], x1[:, i, :, :], s1[:, i, :, :], ALU.add))

                    @block.sync
                    def _(sp):
                        sp.wait_ge(V.sem, at["x2"])
                        stored(sp.dma_start(d["x2"][e + i * E1].rearrange("(q p) e -> p q e", p=P), x1[:, i, :, :]), 16)
                        if i == MB - 1:
                            sp.wait_ge(stored.sem, 16 * MB)
            ph.clear()


HEADS2 = 16
E2, I2, SI2 = 8, 128, 512
GROUPS, TOPK2, SCALE2 = 2, 2, 2.5
GE = E2 // GROUPS
SB2 = SI2 // P
TINY = 2.0 ** -100
KP2 = 96


def phase_c3(nc, c, d, count=B):
    with ExitStack() as ctx:
        ph = Phase(nc, ctx, "c3")
        ps = ph.psum()
        ident, ones, upto = c["ident"], c["ones"], c["upto"]
        wv, wo = ph.sb("wv", [P, KD, DM]), ph.sb("wo", [P, KD, DM])
        bv, bo = ph.sb("bv", [P, DM]), ph.sb("bo", [P, DM])
        w3, b3 = ph.sb("w3", [P, KD, 3]), ph.sb("b3", [P, 3])
        w3r = ph.sb("w3r", [P, KD, 3, P])
        gw, gb = ph.sb("gw", [P, KD, E2]), ph.sb("gb", [P, E2])
        up = ph.sb("up", [P, KD, E2 * I2])
        down = ph.sb("down", [P, E2, DM])
        sup = ph.sb("sup", [P, KD, SI2])
        sdown = ph.sb("sdown", [P, SB2, DM])
        pick = ph.sb("pick", [KP2, E2, P], BF16)
        early = ph.sb("early", [P, E2, E2])
        rows = lambda n: d[n].rearrange("(k p) e -> p k e", p=P)
        load_once(nc, ph, [
            (wv[:, :, :], rows("wv")), (wo[:, :, :], rows("wo")),
            (bv[:, :], d["bv"].partition_broadcast(P)), (bo[:, :], d["bo"].partition_broadcast(P)),
            (w3[:, :, :], rows("w3d")), (b3[:, :], d["b3d"].partition_broadcast(P)),
            (gw[:, :, :], rows("gate_w2")), (gb[:, :], d["gate_b2"].partition_broadcast(P)),
            (up[:, :, :], rows("up2")), (down[:, :, :], d["down2"]),
            (sup[:, :, :], rows("sup2")), (sdown[:, :, :], rows("sdown2")),
        ])
        cwp = ph.sb("cwp", [P, Q, KP2], BF16)
        identb = ph.sb("identb", [P, P], BF16)
        V, A, T, G = (ph.counter(n) for n in ("vector_done", "scalar_done", "tensor_done", "pool_done"))
        with nc.Block() as block:
            @block.gpsimd
            def _(pool):
                G(nc.gpsimd.memset(pick[:, :, :], 0.0))
                link(pool, G, nc.gpsimd.memset(early[:, :, :], 1.0))
                for part in range(3):
                    rows3 = pick[32 * part:32 * part + 32, :, :]
                    link(pool, G, nc.gpsimd.affine_select(out=rows3, in_=rows3, compare_op=ALU.not_equal, fill=1.0,
                                                          base=0, pattern=[[-1, E2], [0, P]], channel_multiplier=1))
                G(nc.gpsimd.affine_select(out=early[:, :, :], in_=early[:, :, :], compare_op=ALU.is_gt, fill=0.0,
                                          base=0, pattern=[[1, E2], [-1, E2]], channel_multiplier=0))

            @block.vector
            def _(dve):
                V(nc.vector.memset(cwp[:, :, :], 0.0))
                V(nc.vector.tensor_copy(identb[:, :], ident[:, :]))
                V(nc.vector.tensor_copy(w3r[:, :, :, :], w3[:, :, :].unsqueeze(3).broadcast_to([P, KD, 3, P])))
        ph.clear()

        x = ph.sb("x", [P, Q, DM])
        xn = ph.sb("xn", [P, Q, DM])
        xnT = ph.sb("xnT", [P, KD, S])
        nm = Norm(ph, "ln")
        v = ph.sb("v", [P, Q, DM])
        pb = ph.sb("pb", [P, 3, S])
        npk = ph.sb("npk", [P, Q, 3])
        sq = ph.sb("sq", [P, 3, S])
        pr = ph.sb("pr", [P, Q, S])
        rs = ph.sb("rs", [P, S])
        oT = ph.sb("oT", [P, KD, S])
        so = ph.sb("so", [P, Q, DM])
        sc = ph.sb("sc", [P, Q, E2])
        sf = ph.sb("sf", [P, Q, E2])
        hi2, lo2 = ph.sb("hi2", [P, Q * GROUPS, 2]), ph.sb("lo2", [P, Q * GROUPS, 2])
        t2 = ph.sb("t2", [P, Q * GROUPS, 4])
        gm = ph.sb("gm", [P, Q, GROUPS])
        cmp, eq = ph.sb("cmp", [P, Q, E2 * E2]), ph.sb("eq", [P, Q, E2 * E2])
        rank = ph.sb("rank", [P, Q, E2])
        den = ph.sb("den", [P, Q])
        cw = ph.sb("cw", [P, Q, E2])
        cwT = ph.sb("cwT", [KP2, S], BF16)
        cwr = ph.sb("cwr", [P, Q, E2])
        r = ph.sb("r", [P, 2, S])
        r2 = ph.sb("r2", [P, E2 + SB2, S])
        g = ph.sb("g", [P, Q, DM])
        x_in, stored = ph.counter("x_in"), ph.counter("stored")
        (sq_made, sq_read, up_made, relu_made, squared, weighted) = (ph.counter(n) for n in (
            "sq_made", "sq_read", "up_made", "relu_made", "squared", "weighted"))
        with nc.Fori(0, count) as b:
            free, at = {}, {}
            with nc.Block() as block:
                @block.sync
                def _(sp):
                    x_in(sp.dma_start(x[:, :, :], d["x2"][b].rearrange("(q p) e -> p q e", p=P)), 16)

                n = layer_norm(nc, block, nm, x, xn, V, A, (x_in.sem, 16))
                at["xnT"] = transpose_rows(nc, block, ps, [0, 1], ident, xn, xnT, T, V, (V.sem, n), free)

                @block.tensor
                def _(pe):
                    pe.wait_ge(*at["xnT"])
                    for q in range(Q):
                        for k in range(KD):
                            nc.tensor.matmul(ps[:, 5, q * 8:q * 8 + 8], xnT[:, k, q * P:(q + 1) * P], gw[:, k, :],
                                             start=k == 0, stop=k == KD - 1)
                        for k in range(KD):
                            last = nc.tensor.matmul(ps[:, 5, 64 + q * 4:64 + q * 4 + 3], xnT[:, k, q * P:(q + 1) * P], w3[:, k, :],
                                                    start=k == 0, stop=k == KD - 1)
                    at["pk"] = T(last)
                    for i in range(3):
                        for k in range(KD):
                            last = nc.tensor.matmul(ps[:, 2 + i, :], w3r[:, k, i, :], xnT[:, k, :], start=k == 0, stop=k == KD - 1)
                        T(last)
                    at["pb"] = T.n
                    for q in range(Q):
                        for k in range(KD):
                            last = nc.tensor.matmul(ps[:, 6 + q // 2, q % 2 * DM:(q % 2 + 1) * DM], xnT[:, k, q * P:(q + 1) * P],
                                                    wv[:, k, :], start=k == 0, stop=k == KD - 1)
                    at["v"] = T(last)

                @block.vector
                def _(dve):
                    dve.wait_ge(T.sem, at["pk"])
                    V(nc.vector.tensor_copy(sc[:, :, :], ps[:, 5, 0:Q * 8].rearrange("p (q e) -> p q e", q=Q)))
                    at["sc_raw"] = V.n
                    link(dve, V, nc.vector.tensor_tensor(npk[:, :, :], ps[:, 5, 64:64 + Q * 4].rearrange("p (q e) -> p q e", q=Q)[:, :, 0:3],
                                                         b3[:, :].unsqueeze(1).broadcast_to([P, Q, 3]), ALU.add))
                    free[5] = (V.sem, V.n)
                    V(nc.vector.tensor_scalar(npk[:, :, :], npk[:, :, :], -1.0, None, ALU.mult))
                    for i in range(3):
                        dve.wait_ge(T.sem, at["pb"] - 2 + i)
                        V(nc.vector.tensor_scalar(pb[:, i, :], ps[:, 2 + i, :], b3[:, i:i + 1], None, ALU.add))
                        free[2 + i] = (V.sem, V.n)
                    at["pb_sb"] = V.n
                    dve.wait_ge(T.sem, at["v"])
                    at["v_sb"] = V(nc.vector.tensor_tensor(
                        v[:, :, :], ps[:, 6:8, :].rearrange("p a (q e) -> p (a q) e", q=2),
                        bv[:, :].unsqueeze(1).broadcast_to([P, Q, DM]), ALU.add))
                    free[6] = free[7] = (V.sem, V.n)

                @block.scalar
                def _(act):
                    act.wait_ge(V.sem, at["sc_raw"])
                    at["sig"] = A(nc.scalar.activation(sc[:, :, :], sc[:, :, :], ACT.Sigmoid))
                    act.wait_ge(V.sem, at["pb_sb"])
                    for m in range(Q):
                        if m:
                            act.wait_ge(sq_read.sem, m)
                        for i in range(3):
                            sq_made(nc.scalar.activation(sq[:, i, m * P:], pb[:, i, m * P:], ACT.Square, bias=npk[:, m, i:i + 1]))

                @block.vector
                def _(dve):
                    for m in range(Q):
                        dve.wait_ge(sq_made.sem, 3 * m + 3)
                        link(dve, V, nc.vector.tensor_tensor(pr[:, m, m * P:], sq[:, 0, m * P:], sq[:, 1, m * P:], ALU.add))
                        k = sq_read(nc.vector.tensor_tensor(pr[:, m, m * P:], pr[:, m, m * P:], sq[:, 2, m * P:], ALU.add))
                        dve.wait_ge(sq_read.sem, k)
                        V(nc.vector.tensor_scalar(pr[:, m, m * P:], pr[:, m, m * P:], TINY, None, ALU.max))
                    at["sq"] = V.n

                @block.scalar
                def _(act):
                    act.wait_ge(V.sem, at["sq"])
                    for m in range(Q):
                        A(nc.scalar.activation(pr[:, m, m * P:], pr[:, m, m * P:], ACT.Sqrt))
                    act.wait_ge(A.sem, A.n)
                    for m in range(Q):
                        A(nc.scalar.activation(pr[:, m, m * P:], pr[:, m, m * P:], ACT.Exp, scale=-1.0 / (DM // HEADS2) ** 0.5))
                    at["exp"] = A.n

                @block.vector
                def _(dve):
                    dve.wait_ge(A.sem, at["sig"])
                    tt, mul = nc.vector.tensor_tensor, ALU.mult
                    link(dve, V, tt(sf[:, :, :], sc[:, :, :], gb[:, :].unsqueeze(1).broadcast_to([P, Q, E2]), ALU.add))
                    s4 = sf[:, :, :].rearrange("p q (g a b) -> p (q g) a b", g=GROUPS, a=2)
                    V(tt(hi2[:, :, :], s4[:, :, :, 0], s4[:, :, :, 1], ALU.max))
                    link(dve, V, tt(lo2[:, :, :], s4[:, :, :, 0], s4[:, :, :, 1], ALU.min))
                    V(tt(t2[:, :, 0:1], hi2[:, :, 0:1], hi2[:, :, 1:2], ALU.max))
                    V(tt(t2[:, :, 1:2], hi2[:, :, 0:1], hi2[:, :, 1:2], ALU.min))
                    link(dve, V, tt(t2[:, :, 2:3], lo2[:, :, 0:1], lo2[:, :, 1:2], ALU.max))
                    link(dve, V, tt(t2[:, :, 3:4], t2[:, :, 1:2], t2[:, :, 2:3], ALU.max))
                    link(dve, V, tt(t2[:, :, 1:2], t2[:, :, 0:1], t2[:, :, 3:4], ALU.add))
                    gs = t2[:, :, 1].rearrange("p (q g) -> p q g", g=GROUPS)
                    V(tt(gm[:, :, 1:2], gs[:, :, 1:2], gs[:, :, 0:1], ALU.is_gt))
                    link(dve, V, tt(gm[:, :, 0:1], gs[:, :, 1:2], gs[:, :, 0:1], ALU.is_le))
                    sg = sf[:, :, :].rearrange("p q (g e) -> p (q g) e", g=GROUPS)
                    link(dve, V, tt(sg, sg, gm[:, :, :].rearrange("p q g -> p (q g)").unsqueeze(2).broadcast_to([P, Q * GROUPS, GE]), mul))
                    for q in range(Q):
                        mi = sf[:, q, :].unsqueeze(1).broadcast_to([P, E2, E2])
                        mj = sf[:, q, :].unsqueeze(2).broadcast_to([P, E2, E2])
                        V(tt(cmp[:, q, :].rearrange("p (j i) -> p j i", j=E2), mi, mj, ALU.is_gt))
                        V(tt(eq[:, q, :].rearrange("p (j i) -> p j i", j=E2), mi, mj, ALU.is_equal))
                    dve.wait_ge(V.sem, V.n)
                    link(dve, V, tt(eq[:, :, :], eq[:, :, :], early[:, :, :].rearrange("p j i -> p (j i)").unsqueeze(1).broadcast_to([P, Q, E2 * E2]), mul))
                    link(dve, V, tt(cmp[:, :, :], cmp[:, :, :], eq[:, :, :], ALU.add))
                    link(dve, V, nc.vector.tensor_reduce(rank[:, :, :], cmp[:, :, :].rearrange("p q (j i) -> p (q j) i", i=E2), AX.X, ALU.add))
                    link(dve, V, nc.vector.scalar_tensor_tensor(cw[:, :, :], rank[:, :, :], float(TOPK2), sc[:, :, :], ALU.is_lt, mul))
                    link(dve, V, nc.vector.tensor_reduce(den[:, :], cw[:, :, :], AX.X, ALU.add))
                    link(dve, V, nc.vector.tensor_scalar(den[:, :], den[:, :], 1e-20, None, ALU.add))
                    link(dve, V, nc.vector.reciprocal(den[:, :], den[:, :]))
                    link(dve, V, tt(cw[:, :, :], cw[:, :, :], den[:, :].unsqueeze(2).broadcast_to([P, Q, E2]), mul))
                    link(dve, V, nc.vector.tensor_scalar(cw[:, :, :], cw[:, :, :], SCALE2, None, mul))
                    link(dve, V, nc.vector.tensor_copy(cwp[:, :, 0:E2], cw[:, :, :]))
                    link(dve, V, tt(cwr[:, :, :], cw[:, :, :], cwp[:, :, 0:E2], ALU.subtract))
                    link(dve, V, nc.vector.tensor_copy(cwp[:, :, 32:32 + E2], cwr[:, :, :]))
                    at["cw"] = V(tt(cwp[:, :, 64:64 + E2], cwr[:, :, :], cwp[:, :, 32:32 + E2], ALU.subtract))

                @block.tensor
                def _(pe):
                    pe.wait_ge(*free[5])
                    pe.wait_ge(V.sem, at["cw"])
                    for q in range(Q):
                        last = nc.tensor.transpose(ps[0:KP2, 5, :].bitcast(BF16)[:, q * P:(q + 1) * P], cwp[:, q, :], identb[:, :])
                    at["cwT"] = T(last)

                @block.vector
                def _(dve):
                    dve.wait_ge(T.sem, at["cwT"])
                    at["cwT_sb"] = V(nc.vector.tensor_copy(cwT[:, :], ps[0:KP2, 5, :].bitcast(BF16)[:, 0:S]))
                    free[5] = (V.sem, V.n)
                    dve.wait_ge(A.sem, at["exp"])
                    for m in range(Q):
                        V(nc.vector.tensor_tensor(pr[:, m, m * P:(m + 1) * P], pr[:, m, m * P:(m + 1) * P], upto[:, :], ALU.mult))
                    at["pr"] = V.n

                @block.tensor
                def _(pe):
                    pe.wait_ge(V.sem, at["pr"])
                    for bank in (0, 1, 2):
                        for m in range(Q):
                            lhs = ones[:, :] if bank == 2 else v[:, m, bank * P:(bank + 1) * P]
                            last = nc.tensor.matmul(ps[:, bank, m * P:], lhs, pr[:, m, m * P:], start=m == 0, stop=m == Q - 1)
                    at["mix"] = T(last)

                @block.vector
                def _(dve):
                    dve.wait_ge(T.sem, at["mix"])
                    link(dve, V, nc.vector.reciprocal(rs[:, :], ps[:, 2, :]))
                    free[2] = (V.sem, V.n)
                    for k in range(KD):
                        V(nc.vector.tensor_tensor(oT[:, k, :], ps[:, k, :], rs[:, :], ALU.mult))
                        free[k] = (V.sem, V.n)
                    at["oT"] = V.n

                @block.tensor
                def _(pe):
                    pe.wait_ge(V.sem, at["oT"])
                    for q in range(Q):
                        for k in range(KD):
                            last = nc.tensor.matmul(ps[:, q // 2, q % 2 * DM:(q % 2 + 1) * DM], oT[:, k, q * P:(q + 1) * P],
                                                    wo[:, k, :], start=k == 0, stop=k == KD - 1)
                    at["s2"] = T(last)

                @block.vector
                def _(dve):
                    dve.wait_ge(T.sem, at["s2"])
                    at["so"] = V(nc.vector.tensor_tensor(
                        so[:, :, :], ps[:, 0:2, :].rearrange("p a (q e) -> p (a q) e", q=2),
                        bo[:, :].unsqueeze(1).broadcast_to([P, Q, DM]), ALU.add))
                    free[0] = free[1] = (V.sem, V.n)

                N = E2 + SB2

                @block.tensor
                def _(pe):
                    for bank in (4, 5, 6, 7):
                        pe.wait_ge(*free[bank])
                    pe.wait_ge(V.sem, at["cwT_sb"])
                    for e in range(N):
                        if e >= 2:
                            pe.wait_ge(squared.sem, e - 1)
                        for k in range(KD):
                            w = up[:, k, e * P:(e + 1) * P] if e < E2 else sup[:, k, (e - E2) * P:(e - E2 + 1) * P]
                            last = nc.tensor.matmul(ps[:, 4 + e % 2, :], w, xnT[:, k, :], start=k == 0, stop=k == KD - 1)
                        if e < E2:
                            if e >= 2:
                                pe.wait_ge(weighted.sem, e - 1)
                            last = nc.tensor.matmul(ps[:, 6 + e % 2, :], pick[:, e, :], cwT[:, :], start=True, stop=True)
                        up_made(last)

                @block.scalar
                def _(act):
                    for e in range(N):
                        act.wait_ge(up_made.sem, e + 1)
                        if e >= 2:
                            act.wait_ge(squared.sem, e - 1)
                        relu_made(nc.scalar.activation(r[:, e % 2, :], ps[:, 4 + e % 2, :], ACT.Relu))

                @block.vector
                def _(dve):
                    for e in range(N):
                        dve.wait_ge(relu_made.sem, e + 1)
                        k = squared(nc.vector.tensor_tensor(r2[:, e, :], r[:, e % 2, :], r[:, e % 2, :], ALU.mult))
                        if e < E2:
                            dve.wait_ge(squared.sem, k)
                            weighted(nc.vector.tensor_tensor(r2[:, e, :], r2[:, e, :], ps[:, 6 + e % 2, :], ALU.mult))

                @block.tensor
                def _(pe):
                    pe.wait_ge(weighted.sem, E2)
                    pe.wait_ge(squared.sem, N)
                    for q in range(Q):
                        if q % 2 == 0:
                            pe.wait_ge(*free[(2, 3)[q // 2]])
                        for e in range(N):
                            w = down[:, e, :] if e < E2 else sdown[:, e - E2, :]
                            last = nc.tensor.matmul(ps[:, 2 + q // 2, q % 2 * DM:(q % 2 + 1) * DM], r2[:, e, q * P:(q + 1) * P], w,
                                                    start=e == 0, stop=e == N - 1)
                    at["ffn"] = T(last)

                @block.scalar
                def _(act):
                    act.wait_ge(T.sem, at["ffn"])
                    at["g"] = A(nc.scalar.activation(g[:, :, :], ps[:, 2:4, :], ACT.Silu))

                @block.vector
                def _(dve):
                    dve.wait_ge(A.sem, at["g"])
                    link(dve, V, nc.vector.tensor_tensor(g[:, :, :], g[:, :, :], so[:, :, :], ALU.mult))
                    at["x3"] = V(nc.vector.tensor_tensor(x[:, :, :], x[:, :, :], g[:, :, :], ALU.add))

                @block.sync
                def _(sp):
                    sp.wait_ge(V.sem, at["x3"])
                    stored(sp.dma_start(d["x3"][b].rearrange("(q p) e -> p q e", p=P), x[:, :, :]), 16)
                    sp.wait_ge(stored.sem, 16)
            ph.clear()


NF = 64
E3, D3, RH3 = 16, 512, 128
CAP = math.ceil(S * 2.0 / E3)
DK3 = D3 // P
ROUND = 1.5 * 2.0 ** 23


def phase_c4(nc, c, d, count=B):
    with ExitStack() as ctx:
        ph = Phase(nc, ctx, "c4")
        ps = ph.psum()
        ident = c["ident"]
        w_in = ph.sb("w_in", [P, KD, 2, 2 * NF])
        w_out = ph.sb("w_out", [P, 2, DM])
        rw1, rw2 = ph.sb("rw1", [P, KD, RH3]), ph.sb("rw2", [P, E3])
        col = ph.sb("col", [P, 16])
        omega, decay, turns, half, sh, ch, fix = (col[:, i:i + 1] for i in range(7))
        a_col, b_col = col[:, 7:8], col[:, 8:9]
        ld = []
        wi = d["W_in"].rearrange("(k p) e -> p k e", p=P)
        for i in range(2):
            for h in range(2):
                ld.append((w_in[:, :, i, h * NF:(h + 1) * NF], wi[:, :, (h ^ i) * NF:((h ^ i) + 1) * NF]))
                ld.append((w_out[h * NF:(h + 1) * NF, i, :], d["W_out"][(h ^ i) * NF:((h ^ i) + 1) * NF]))
        for h in range(2):
            ld.append((omega[h * NF:(h + 1) * NF], d["frequencies"].rearrange("(f o) -> f o", o=1)))
            ld.append((decay[h * NF:(h + 1) * NF], d["log_decay"].rearrange("(f o) -> f o", o=1)))
        ld += [(rw1[:, :, :], d["router_w1"].rearrange("(k p) e -> p k e", p=P)), (rw2[:, :], d["router_w2"])]
        load_once(nc, ph, ld)
        V, A, T = (ph.counter(n) for n in ("vector_done", "scalar_done", "tensor_done"))
        cs, sn = ph.sb("cs", [P, S + 1]), ph.sb("sn", [P, S + 1])
        tt = ph.sb("tt", [P, S])
        dk = ph.sb("dk", [P, S])
        at = {}

        with nc.Block() as block:
            @block.vector
            def _(dve):
                ts = lambda o, i, a, b, f, g: link(dve, V, nc.vector.tensor_scalar(o, i, a, b, f, g))
                ts(omega, omega, 0.1, None, ALU.mult, ALU.bypass)
                ts(turns, omega, 1 / (2 * math.pi), None, ALU.mult, ALU.bypass)
                ts(turns, turns, ROUND, None, ALU.add, ALU.bypass)
                ts(turns, turns, ROUND, None, ALU.subtract, ALU.bypass)
                for part in (6.28125, 2 * math.pi - 6.28125):
                    link(dve, V, nc.vector.scalar_tensor_tensor(omega, turns, -part, omega, ALU.mult, ALU.add))
                ts(half, omega, 0.5, None, ALU.mult, ALU.bypass)
                link(dve, V, nc.vector.scalar_tensor_tensor(ch, half, -1.0, half, ALU.mult, ALU.min))
                at["half"] = link(dve, V, nc.vector.tensor_scalar(ch, ch, math.pi / 2, 0.0, ALU.add, ALU.max))

            @block.scalar
            def _(act):
                act.wait_ge(V.sem, at["half"])
                A(nc.scalar.activation(sh, half, ACT.Sin))
                A(nc.scalar.activation(ch, ch, ACT.Sin))
                A(nc.scalar.activation(decay, decay, ACT.Sigmoid))

            @block.vector
            def _(dve):
                dve.wait_ge(A.sem, 3)
                st = nc.vector.scalar_tensor_tensor
                V(nc.vector.memset(cs[:, 0:1], 1.0))
                V(nc.vector.memset(sn[:, 0:1], 0.0))
                link(dve, V, nc.vector.memset(dk[:, :], 1.0))
                link(dve, V, nc.vector.tensor_scalar(dk[:, :], dk[:, :], decay, None, ALU.mult))
                link(dve, V, st(sn[:, 1:2], sh, 2.0, ch, ALU.mult, ALU.mult))
                link(dve, V, st(cs[:, 1:2], sh, -2.0, sh, ALU.mult, ALU.mult))
                link(dve, V, nc.vector.tensor_scalar(cs[:, 1:2], cs[:, 1:2], 1.0, None, ALU.add))
                link(dve, V, nc.vector.tensor_tensor(a_col, cs[:, 1:2], cs[:, 1:2], ALU.mult))
                link(dve, V, nc.vector.tensor_tensor(b_col, sn[:, 1:2], sn[:, 1:2], ALU.mult))
                link(dve, V, nc.vector.tensor_tensor(fix, a_col, b_col, ALU.add))
                link(dve, V, nc.vector.tensor_scalar(fix, fix, -0.5, 1.5, ALU.mult, ALU.add))
                link(dve, V, nc.vector.tensor_tensor(cs[:, 1:2], cs[:, 1:2], fix, ALU.mult))
                link(dve, V, nc.vector.tensor_tensor(sn[:, 1:2], sn[:, 1:2], fix, ALU.mult))
                n = 1
                while n < S:
                    ck, sk = cs[:, n:n + 1], sn[:, n:n + 1]
                    lo, hi = slice(1, n + 1), slice(n + 1, 2 * n + 1)
                    link(dve, V, nc.vector.tensor_scalar(tt[:, 0:n], sn[:, lo], sk, None, ALU.mult))
                    link(dve, V, st(cs[:, hi], cs[:, lo], ck, tt[:, 0:n], ALU.mult, ALU.subtract))
                    link(dve, V, nc.vector.tensor_scalar(tt[:, 0:n], cs[:, lo], sk, None, ALU.mult))
                    link(dve, V, st(sn[:, hi], sn[:, lo], ck, tt[:, 0:n], ALU.mult, ALU.add))
                    n *= 2
                link(dve, V, nc.vector.tensor_scalar(sn[NF:, :], sn[NF:, :], -1.0, None, ALU.mult))
        ph.clear()

        x = ph.sb("x", [P, Q, DM])
        xn = ph.sb("xn", [P, Q, DM])
        xnT = ph.sb("xnT", [P, KD, S])
        nm = Norm(ph, "ln")
        u, u2, gs = ph.sb("u", [P, S]), ph.sb("u2", [P, S]), ph.sb("gs", [P, S])
        f = ph.sb("f", [P, 2, S])
        so = ph.sb("so", [P, Q, DM])
        rT = ph.sb("rT", [RH3, S])
        pr = ph.sb("pr", [E3, S])
        g1 = ph.sb("g1", [E3, 4])
        x_in, stored = ph.counter("x_in"), ph.counter("stored")
        with nc.Fori(0, count) as b:
            free, at = {}, {}
            with nc.Block() as block:
                @block.sync
                def _(sp):
                    x_in(sp.dma_start(x[:, :, :], d["x3"][b].rearrange("(q p) e -> p q e", p=P)), 16)

                n = layer_norm(nc, block, nm, x, xn, V, A, (x_in.sem, 16))
                at["xn"] = n
                at["xnT"] = transpose_rows(nc, block, ps, [0, 1], ident, xn, xnT, T, V, (V.sem, n), free)

                @block.tensor
                def _(pe):
                    pe.wait_ge(*at["xnT"])
                    for i in range(2):
                        for k in range(KD):
                            last = nc.tensor.matmul(ps[:, 2 + i, :], w_in[:, k, i, :], xnT[:, k, :], start=k == 0, stop=k == KD - 1)
                    at["u"] = T(last)
                    for k in range(KD):
                        last = nc.tensor.matmul(ps[:, 4, :], rw1[:, k, :], xnT[:, k, :], start=k == 0, stop=k == KD - 1)
                    at["r1"] = T(last)

                @block.scalar
                def _(act):
                    act.wait_ge(T.sem, at["r1"])
                    at["rT"] = A(nc.scalar.activation(rT[:, :], ps[:, 4, :], ACT.Silu))

                @block.vector
                def _(dve):
                    dve.wait_ge(T.sem, at["u"])
                    V(nc.vector.tensor_tensor(u[:, :], ps[:, 2, :], cs[:, 0:S], ALU.mult))
                    link(dve, V, nc.vector.tensor_tensor(u2[:, :], ps[:, 3, :], sn[:, 0:S], ALU.mult))
                    link(dve, V, nc.vector.tensor_tensor(u[:, :], u[:, :], u2[:, :], ALU.add))
                    link(dve, V, nc.vector.tensor_tensor_scan(gs[:, :], dk[:, :], u[:, :], 0.0, ALU.mult, ALU.add))
                    V(nc.vector.tensor_tensor(f[:, 0, :], gs[:, :], cs[:, 1:], ALU.mult))
                    at["f"] = V(nc.vector.tensor_tensor(f[:, 1, :], gs[:, :], sn[:, 1:], ALU.mult))

                @block.tensor
                def _(pe):
                    pe.wait_ge(A.sem, at["rT"])
                    at["lg"] = T(nc.tensor.matmul(ps[0:E3, 5, :], rw2[:, :], rT[:, :], start=True, stop=True))
                    pe.wait_ge(V.sem, at["f"])
                    for q in range(Q):
                        for i in range(2):
                            last = nc.tensor.matmul(ps[:, 6 + q // 2, q % 2 * DM:(q % 2 + 1) * DM], f[:, i, q * P:(q + 1) * P],
                                                    w_out[:, i, :], start=i == 0, stop=i == 1)
                    at["s3"] = T(last)

                @block.vector
                def _(dve):
                    dve.wait_ge(T.sem, at["lg"])
                    at["max"] = V(nc.vector.tensor_reduce(g1[:, 0:1], ps[0:E3, 5, :], AX.X, ALU.max, negate=True))

                @block.scalar
                def _(act):
                    act.wait_ge(V.sem, at["max"])
                    at["exp"] = A(nc.scalar.activation(pr[:, :], ps[0:E3, 5, :], ACT.Exp, bias=g1[:, 0:1], accum_out=g1[:, 1:2]))
                    act.wait_ge(T.sem, at["s3"])
                    at["so"] = A(nc.scalar.copy(so[:, :, :], ps[:, 6:8, :]))

                @block.vector
                def _(dve):
                    dve.wait_ge(A.sem, at["exp"])
                    link(dve, V, nc.vector.reciprocal(g1[:, 2:3], g1[:, 1:2]))
                    at["pr"] = V(nc.vector.tensor_scalar(pr[:, :], pr[:, :], g1[:, 2:3], None, ALU.mult))

                @block.sync
                def _(sp):
                    sp.wait_ge(V.sem, at["xn"])
                    stored(sp.dma_start(d["xn3"][b].rearrange("(q p) e -> p q e", p=P), xn[:, :, :]), 16)
                    sp.wait_ge(V.sem, at["pr"])
                    stored(sp.dma_start(d["probs3"][b], pr[:, :]), 16)
                    sp.wait_ge(A.sem, at["so"])
                    stored(sp.dma_start(d["s3"][b].rearrange("(q p) e -> p q e", p=P), so[:, :, :]), 16)
                    sp.wait_ge(stored.sem, 48)
            ph.clear()


RB = P // E3


def phase_r(nc, c, d, keep):
    with ExitStack() as ctx:
        ph = Phase(nc, ctx, "r")
        ps = ph.psum()
        N = B // RB
        pr = ph.sb("pr", [P, N, S])
        val = ph.sb("val", [P, N, 2, CAP])
        ix = ph.sb("ix", [P, N, CAP], U32)
        ixf = ph.sb("ixf", [P, N, 2, CAP])
        sm = ph.sb("sm", [P, N])
        V, T, p_in = ph.counter("vector_done"), ph.counter("tensor_done"), ph.counter("probs_in")
        rows = d["probs3"].rearrange("b e s -> (b e) s")
        at = {}
        with nc.Block() as block:
            @block.sync
            def _(sp):
                p_in(sp.dma_start(pr[:, :, :], rows.rearrange("(n p) s -> p n s", p=P)), 16)

            @block.vector
            def _(dve):
                dve.wait_ge(p_in.sem, 16)
                for r in range(CAP // 8):
                    cut = slice(8 * r, 8 * r + 8)
                    for n in range(N):
                        V(nc.vector.max(val[:, n, 0, cut], pr[:, n, :]))
                    dve.wait_ge(V.sem, V.n)
                    for n in range(N):
                        V(nc.vector.max_index(ix[:, n, cut], val[:, n, 0, cut], pr[:, n, :]))
                    dve.wait_ge(V.sem, V.n)
                    if r < CAP // 8 - 1:
                        for n in range(N):
                            V(nc.vector.match_replace(pr[:, n, :], val[:, n, 0, cut], pr[:, n, :], -1.0))
                        dve.wait_ge(V.sem, V.n)
                V(nc.vector.tensor_reduce(sm[:, :], val[:, :, 0, :], AX.X, ALU.add))
                for h in range(2):
                    V(nc.vector.tensor_copy(ixf[:, :, h, :], ix[:, :, :]))
                dve.wait_ge(V.sem, V.n)
                link(dve, V, nc.vector.tensor_scalar(sm[:, :], sm[:, :], 1e-9, None, ALU.add))
                link(dve, V, nc.vector.reciprocal(sm[:, :], sm[:, :]))
                for n in range(N):
                    V(nc.vector.tensor_scalar(val[:, n, 0, :], val[:, n, 0, :], sm[:, n:n + 1], None, ALU.mult))
                dve.wait_ge(V.sem, V.n)
                at["val"] = link(dve, V, nc.vector.tensor_copy(val[:, :, 1, :], val[:, :, 0, :]))

            @block.tensor
            def _(pe):
                pe.wait_ge(V.sem, at["val"])
                for n in range(N):
                    for i, t in enumerate((ixf, val)):
                        last = nc.tensor.transpose(ps[:, i, n * P:(n + 1) * P], t[:, n, :, :].rearrange("p a b -> p (a b)"),
                                                   c["ident"][:, :])
                at["turned"] = T(last)

            @block.vector
            def _(dve):
                dve.wait_ge(T.sem, at["turned"])
                for h in range(2):
                    part = slice(h * CAP, (h + 1) * CAP)
                    for i, t in enumerate((keep["slot_ix"], keep["slot_w"])):
                        v = ps[part, i, 0:N * P].rearrange("p (b e a) -> p b e a", b=B, a=2)
                        V(nc.vector.tensor_copy(t[part, :, :], v[:, :, :, h]))
                    v = ps[part, 0, 0:N * P].rearrange("p (b a e) -> p e b a", a=2, e=E3)
                    V(nc.vector.tensor_copy(keep["row_f"][part, :, :], v[:, :, :, h]))
                dve.wait_ge(V.sem, V.n)
                dve.wait_ge(keep["base_sem"].sem, 1)
                link(dve, V, nc.vector.tensor_tensor(keep["row_f"][:, :, :], keep["row_f"][:, :, :],
                                                     keep["base"][:, :].unsqueeze(1).broadcast_to([P, E3, B // 2]), ALU.add))
                V(nc.vector.tensor_copy(keep["row_ix"][:, :, :], keep["row_f"][:, :, :]))

            @block.gpsimd
            def _(pool):
                n = keep["iota_sem"]
                for h in range(2):
                    link(pool, n, nc.gpsimd.iota(keep["base_i"][h * CAP:(h + 1) * CAP, :], pattern=[[2 * S, B // 2]],
                                                 base=h * S, channel_multiplier=0))
                link(pool, n, nc.gpsimd.iota(keep["iota_i"][:, :], pattern=[[1, S]], base=0, channel_multiplier=0))
                link(pool, keep["base_sem"], nc.gpsimd.tensor_copy(keep["base"][:, :], keep["base_i"][:, :]))
                link(pool, n, nc.gpsimd.tensor_copy(keep["iota"][:, :], keep["iota_i"][:, :]))
        keep["ph"].clear()
        ph.clear()


def keep_slots(nc, ctx):
    ph = Phase(nc, ctx, "keep")
    I32 = mybir.dt.int32
    return dict(ph=ph, iota_sem=ph.counter("iota_done"), base_sem=ph.counter("base_done"),
                slot_ix=ph.sb("slot_ix", [P, B, E3 // 2]), slot_w=ph.sb("slot_w", [P, B, E3 // 2]),
                row_f=ph.sb("row_f", [P, E3, B // 2]), row_ix=ph.sb("row_ix", [P, E3, B // 2], U32),
                base_i=ph.sb("base_i", [P, B // 2], I32), base=ph.sb("base", [P, B // 2]),
                iota_i=ph.sb("iota_i", [P, S], I32), iota=ph.sb("iota", [P, S]))


EU = 2


def phase_d(nc, c, d, keep, count=E3 // EU):
    with ExitStack() as ctx:
        ph = Phase(nc, ctx, "d")
        ps = ph.psum()
        ident = c["ident"]
        NT = B * CAP
        NP = NT // P
        NH = NT // 512
        w1, w2 = ph.sb("w1", [P, EU, KD, D3]), ph.sb("w2", [P, EU, KD, D3])
        w3 = ph.sb("w3", [P, EU, DK3, DM])
        rix = ph.sb("rix", [P, EU, NP], U32)
        xg = ph.sb("xg", [P, EU, NP, DM])
        xT = ph.sb("xT", [P, EU, KD, NT])
        gate = ph.sb("gate", [P, 2, 512])
        hT = ph.sb("hT", [P, EU, DK3, NT])
        eo = ph.sb("eo", [P, EU, NP, DM])
        w_in = [ph.counter(f"w_in{j}") for j in range(EU)]
        x_in = [ph.counter(f"x_in{j}_{n}") for j in range(EU) for n in range(NP)]
        ph.pool_dma = x_in
        V, T, stored = ph.counter("vector_done"), ph.counter("tensor_done"), ph.counter("stored")
        (turned_made, turned, gate_made, value_made, gated, hidden_done, out_made, out_done) = (ph.counter(n) for n in (
            "turned_made", "turned", "gate_made", "value_made", "gated", "hidden_done", "out_made", "out_done"))
        with nc.Fori(0, count) as g:
            with nc.Block() as block:
                @block.sync
                def _(sp):
                    for j in range(EU):
                        for t, n in ((w1, "w1_3"), (w2, "w2_3"), (w3, "w3_3")):
                            w_in[j](sp.dma_start(t[:, j, :, :], d[n][g * EU + j].rearrange("(k p) e -> p k e", p=P)), 16)
                    for j in range(EU):
                        for h in range(2):
                            sp.wait_ge(out_done.sem, j * NP + NP // 2 * (h + 1))
                            half = slice(NP // 2 * h, NP // 2 * (h + 1))
                            for a in range(2):
                                dst = d["eo3"][a::2, g * EU + j, :, :].rearrange("n c e -> c n e")[:, half, :]
                                stored(sp.dma_start(dst, eo[a * CAP:(a + 1) * CAP, j, half, :]), 16)
                    sp.wait_ge(stored.sem, 64 * EU)

                @block.vector
                def _(dve):
                    V(nc.vector.tensor_copy(rix[:, :, :], keep["row_ix"][:, bass.ds(g * EU, EU), :]))

                @block.gpsimd
                def _(pool):
                    pool.wait_ge(V.sem, 1)
                    for j in range(EU):
                        for n in range(NP):
                            x_in[j * NP + n](nc.gpsimd.indirect_dma_start(
                                xg[:, j, n, :], None, d["xn3"].rearrange("b s e -> (b s) e"),
                                bass.IndirectOffsetOnAxis(ap=rix[:, j, n:n + 1], axis=0)), 16)
                    for s in x_in:
                        pool.wait_ge(s.sem, 16)

                def turn(pe, j):
                    for n in range(NP * KD // 4):
                        k, n0 = n % KD, n // KD * 4
                        if j * NP * KD // 4 + n >= 2:
                            pe.wait_ge(turned.sem, j * NP * KD // 4 + n - 1)
                        for i in range(4):
                            if k == 0:
                                pe.wait_ge(x_in[j * NP + n0 + i].sem, 16)
                            last = nc.tensor.transpose(ps[:, n % 2, i * P:(i + 1) * P], xg[:, j, n0 + i, k * P:(k + 1) * P], ident[:, :])
                        turned_made(last)

                @block.tensor
                def _(pe):
                    turn(pe, 0)
                    for j in range(EU):
                        pe.wait_ge(w_in[j].sem, 48)
                        pe.wait_ge(turned.sem, (j + 1) * NP * KD // 4)
                        for m in range(DK3 * NH):
                            h, f = m // DK3, m % DK3
                            i = j * DK3 * NH + m
                            if i >= 2:
                                pe.wait_ge(hidden_done.sem, i - 1)
                            for w, bank, made in ((w1, 2, gate_made), (w2, 4, value_made)):
                                for k in range(KD):
                                    last = nc.tensor.matmul(ps[:, bank + i % 2, :], w[:, j, k, f * P:(f + 1) * P],
                                                            xT[:, j, k, h * 512:(h + 1) * 512], start=k == 0, stop=k == KD - 1)
                                made(last)
                        if j + 1 < EU:
                            turn(pe, j + 1)
                        for n in range(NP):
                            i = j * NP + n
                            pe.wait_ge(hidden_done.sem, j * DK3 * NH + DK3 * (n // (NP // NH) + 1))
                            if i >= 2:
                                pe.wait_ge(out_done.sem, i - 1)
                            for k in range(DK3):
                                last = nc.tensor.matmul(ps[:, 6 + i % 2, 0:DM], hT[:, j, k, n * P:(n + 1) * P], w3[:, j, k, :],
                                                        start=k == 0, stop=k == DK3 - 1)
                            out_made(last)

                def copy_turned(dve, j):
                    for n in range(NP * KD // 4):
                        k, n0 = n % KD, n // KD * 4
                        dve.wait_ge(turned_made.sem, j * NP * KD // 4 + n + 1)
                        turned(nc.vector.tensor_copy(xT[:, j, k, n0 * P:(n0 + 4) * P], ps[:, n % 2, :]))

                @block.scalar
                def _(act):
                    for i in range(EU * DK3 * NH):
                        act.wait_ge(gate_made.sem, i + 1)
                        if i >= 2:
                            act.wait_ge(hidden_done.sem, i - 1)
                        gated(nc.scalar.activation(gate[:, i % 2, :], ps[:, 2 + i % 2, :], ACT.Silu))

                @block.vector
                def _(dve):
                    copy_turned(dve, 0)
                    for j in range(EU):
                        for m in range(DK3 * NH):
                            h, f = m // DK3, m % DK3
                            i = j * DK3 * NH + m
                            dve.wait_ge(gated.sem, i + 1)
                            dve.wait_ge(value_made.sem, i + 1)
                            hidden_done(nc.vector.tensor_tensor(hT[:, j, f, h * 512:(h + 1) * 512], gate[:, i % 2, :],
                                                                ps[:, 4 + i % 2, :], ALU.mult))
                        if j + 1 < EU:
                            copy_turned(dve, j + 1)
                        for n in range(NP):
                            i = j * NP + n
                            dve.wait_ge(out_made.sem, i + 1)
                            out_done(nc.vector.tensor_copy(eo[:, j, n, :], ps[:, 6 + i % 2, 0:DM]))
            ph.clear()


def phase_e(nc, c, d, keep, count=B):
    with ExitStack() as ctx:
        ph = Phase(nc, ctx, "e")
        ps = ph.psum()
        EP = E3 // 2
        x, s3 = ph.sb("x", [P, Q, DM]), ph.sb("s3", [P, Q, DM])
        eo = ph.sb("eo", [P, EP, DM])
        ix, w = ph.sb("ix", [P, EP]), ph.sb("w", [P, EP])
        sel = ph.sb("sel", [P, EP, S])
        g = ph.sb("g", [P, Q, DM])
        x_in, eo_in, stored = ph.counter("x_in"), ph.counter("eo_in"), ph.counter("stored")
        V, A, T = (ph.counter(n) for n in ("vector_done", "scalar_done", "tensor_done"))
        with nc.Fori(0, count) as b:
            at = {}
            with nc.Block() as block:
                @block.sync
                def _(sp):
                    for a in range(2):
                        eo_in(sp.dma_start(eo[a * CAP:(a + 1) * CAP, :, :],
                                           d["eo3"][b].rearrange("(n a) c e -> a c n e", a=2)[a]), 16)
                    x_in(sp.dma_start(x[:, :, :], d["x3"][b].rearrange("(q p) e -> p q e", p=P)), 16)
                    x_in(sp.dma_start(s3[:, :, :], d["s3"][b].rearrange("(q p) e -> p q e", p=P)), 16)

                @block.vector
                def _(dve):
                    V(nc.vector.tensor_copy(ix[:, :], keep["slot_ix"][:, bass.ds(b, 1), :]))
                    link(dve, V, nc.vector.tensor_copy(w[:, :], keep["slot_w"][:, bass.ds(b, 1), :]))
                    at["sel"] = V.n
                    for e in range(EP):
                        V(nc.vector.tensor_scalar(sel[:, e, :], keep["iota"][:, :], ix[:, e:e + 1], w[:, e:e + 1],
                                                  ALU.is_equal, ALU.mult))

                @block.tensor
                def _(pe):
                    pe.wait_ge(eo_in.sem, 32)
                    pe.wait_ge(V.sem, at["sel"] + EP)
                    for q in range(Q):
                        for e in range(EP):
                            last = nc.tensor.matmul(ps[:, q // 2, q % 2 * DM:(q % 2 + 1) * DM], sel[:, e, q * P:(q + 1) * P],
                                                    eo[:, e, :], start=e == 0, stop=e == EP - 1)
                    at["ffn"] = T(last)

                @block.scalar
                def _(act):
                    act.wait_ge(T.sem, at["ffn"])
                    at["g"] = A(nc.scalar.activation(g[:, :, :], ps[:, 0:2, :], ACT.Silu))

                @block.vector
                def _(dve):
                    dve.wait_ge(A.sem, at["g"])
                    dve.wait_ge(x_in.sem, 32)
                    link(dve, V, nc.vector.tensor_tensor(g[:, :, :], g[:, :, :], s3[:, :, :], ALU.mult))
                    at["out"] = V(nc.vector.tensor_tensor(x[:, :, :], x[:, :, :], g[:, :, :], ALU.add))

                @block.sync
                def _(sp):
                    sp.wait_ge(V.sem, at["out"])
                    stored(sp.dma_start(d["out"][b].rearrange("(q p) e -> p q e", p=P), x[:, :, :]), 16)
                    sp.wait_ge(stored.sem, 16)
            ph.clear()



def _same(a):
    return a


def _T(a):
    return a.T


def _columns(a):
    return a.reshape(*a.shape[:-1], -1, P).swapaxes(-1, -2)


INPUTS = {
    "x": ("L0_attn_x", _same),
    "w_in": ("L0_attn_in_proj_w", _T), "w_conv": ("L0_attn_conv_w", _same), "b_conv": ("L0_attn_conv_b", _columns),
    "w_x": ("L0_attn_x_proj_w", _T), "skip": ("L0_attn_D", _columns), "w_out": ("L0_attn_out_proj_w", _T),
    "a_log": ("L0_attn_A_log", _same),
    "w_gate0": ("L0_ffn_gate_w", _T), "b_gate0": ("L0_ffn_gate_b", _same),
    "w1_0": ("L0_ffn_w1", _same), "w2_0": ("L0_ffn_w2", _same),
    "w_qkv": ("L1_attn_w_qkv", _T), "w_proj": ("L1_attn_w_proj", _T), "b_proj": ("L1_attn_b_proj", _same),
    "lambda_q1": ("L1_attn_lambda_q1", _same), "lambda_k1": ("L1_attn_lambda_k1", _same),
    "lambda_q2": ("L1_attn_lambda_q2", _same), "lambda_k2": ("L1_attn_lambda_k2", _same),
    "sub_norm_w": ("L1_attn_sub_norm_w", _same),
    "ln_scale": ("L1_ffn_ln_scale", _columns), "ln_bias": ("L1_ffn_ln_bias", _columns),
    "attn_w": ("L1_ffn_attn_w", _T), "attn_b": ("L1_ffn_attn_b", _columns),
    "w1_1": ("L1_ffn_w1", _same), "b1_1": ("L1_ffn_b1", _columns), "w2_1": ("L1_ffn_w2", _same),
    "b2_1": ("L1_ffn_b2", _columns), "next_w": ("L1_ffn_next_w", _T), "next_b": ("L1_ffn_next_b", _same),
    "wv": ("L2_attn_wv", _T), "bv": ("L2_attn_bv", _same), "wo": ("L2_attn_wo", _T), "bo": ("L2_attn_bo", _same),
    "w3d": ("L2_attn_w3d", _T), "b3d": ("L2_attn_b3d", _same),
    "gate_w2": ("L2_ffn_gate_weight", _T), "gate_b2": ("L2_ffn_gate_bias", _same),
    "up2": ("L2_ffn_up_weights", lambda a: a.reshape(E2 * I2, DM).T),
    "down2": ("L2_ffn_down_weights", lambda a: a.transpose(2, 0, 1)),
    "sup2": ("L2_ffn_shared_up_weight", _T), "sdown2": ("L2_ffn_shared_down_weight", _T),
    "W_in": ("L3_attn_W_in", _T), "W_out": ("L3_attn_W_out", _T),
    "frequencies": ("L3_attn_frequencies", _same), "log_decay": ("L3_attn_log_decay", _same),
    "router_w1": ("L3_ffn_router_w1", _same), "router_w2": ("L3_ffn_router_w2", _same),
    "w1_3": ("L3_ffn_w1", _same), "w2_3": ("L3_ffn_w2", _same), "w3_3": ("L3_ffn_w3", _same),
}
SCRATCH = {
    "s0": ((B, S, DM), F32), "picked": ((B, E0, S), F32), "o0": ((B, E0, DM), F32),
    "qk_parts": ((B, 2, SPLIT, 2 * P, S), BF16), "v1": ((B, S, DM), F32),
    "x1": ((B, S, DM), F32), "xn1": ((B, S, DM), F32), "s1": ((B, S, DM), F32),
    "x2": ((B, S, DM), F32), "x3": ((B, S, DM), F32),
    "xn3": ((B, S, DM), F32), "s3": ((B, S, DM), F32), "probs3": ((B, E3, S), F32), "eo3": ((B, E3, CAP, DM), F32),
}


def program(nc, d):
    with ExitStack() as ctx:
        c = make_constants(nc, ctx)
        with ExitStack() as layer0:
            mergedT = layer0.enter_context(nc.sbuf_tensor("mergedT", [P, KD, E0, B], F32))
            phase_a(nc, c, d, mergedT)
            phase_b(nc, c, d, mergedT)
        phase_c1a(nc, c, d)
        phase_c1b(nc, c, d)
        phase_c2(nc, c, d)
        phase_c3(nc, c, d)
        keep = keep_slots(nc, ctx)
        phase_c4(nc, c, d)
        phase_r(nc, c, d, keep)
        phase_d(nc, c, d, keep)
        phase_e(nc, c, d, keep)


def kernel(**inputs):
    import numpy as _np
    import concourse.bacc as _bacc
    from concourse import mybir as _mybir
    from concourse.bass_utils import run_bass_kernel_spmd as _run

    nc = _bacc.Bacc("TRN2", target_bir_lowering=False, num_devices=1)
    arrays, d = {}, {}
    for name, (source, lay) in INPUTS.items():
        a = _np.ascontiguousarray(lay(_np.asarray(inputs[source])))
        arrays[f"in_{name}"] = a
        d[name] = nc.dram_tensor(f"in_{name}", a.shape, _mybir.dt.from_np(a.dtype), kind="ExternalInput").ap()
    for name, (shape, dt) in SCRATCH.items():
        d[name] = nc.dram_tensor(f"scratch_{name}", shape, dt, kind="Internal").ap()
    d["out"] = nc.dram_tensor("out", (B, S, DM), F32, kind="ExternalOutput").ap()
    program(nc, d)
    r = _run(nc, [arrays], core_ids=[0])
    return r.results[0]["out"]
```

```python
import math
from contextlib import ExitStack

import concourse.bass as bass
from concourse import mybir

F32 = mybir.dt.float32
BF16 = mybir.dt.bfloat16
U32 = mybir.dt.uint32
ALU = mybir.AluOpType
ACT = mybir.ActivationFunctionType
AX = mybir.AxisListType
P = 128
B, S, DM = 16, 512, 256
Q = S // P
KD = DM // P
EPS = 1e-5


class Signal:

    def __init__(self, nc, ctx, name):
        self.sem = ctx.enter_context(nc.semaphore(name))
        self.n = 0

    def __call__(self, instruction, by=1):
        instruction.then_inc(self.sem, by)
        self.n += by
        return self.n


def link(engine, signal, instruction):
    n = signal(instruction)
    engine.wait_ge(signal.sem, n)
    return n


class Phase:

    def __init__(self, nc, ctx, name):
        self.nc, self.ctx, self.name = nc, ctx, name
        self.signals, self.pool_dma, self.buffers = [], [], {}

    def sb(self, name, shape, dt=F32):
        if name not in self.buffers:
            self.buffers[name] = self.ctx.enter_context(self.nc.sbuf_tensor(f"{self.name}_{name}", shape, dt))
        return self.buffers[name]

    def psum(self):
        return self.ctx.enter_context(self.nc.psum_tensor(f"{self.name}_psum", [P, 8, 512], F32))

    def counter(self, name):
        s = Signal(self.nc, self.ctx, f"{self.name}_{name}")
        self.signals.append(s)
        return s

    def clear(self):
        with self.nc.Block() as block:
            @block.sync
            def _(sp):
                for s in self.signals:
                    if s not in self.pool_dma:
                        sp.sem_clear(s.sem)

            if self.pool_dma:
                @block.gpsimd
                def _(pool):
                    for s in self.pool_dma:
                        pool.dma_reset(range(s.sem.num, s.sem.num + 1))
                        pool.sem_clear(s.sem)
        for s in self.signals:
            s.n = 0


class Job:

    def __init__(self, j, slots):
        self.j, self.slot = j, j % slots
        self.block = self.b = None
        self.before, self.done = None, []

    def wait_for_buffers(self, *engines):
        waits = self.before.done if self.before else []
        if waits:
            def wait(engine):
                for sem, n in waits:
                    engine.wait_ge(sem, n)
            for on in engines:
                on(wait)


def pipeline(bodies, jobs, lag):
    step, left = 0, set(range(len(bodies)))
    while left:
        for j, body in enumerate(bodies):
            if j in left and step >= j * lag:
                before = jobs[j].before
                assert before is None or before.done, "the buffers' last user is still at work"
                if next(body, left) is left:
                    left.remove(j)
        step += 1


def run_sequences(nc, ph, sequence, count, per_pass, lag, slots=2):
    jobs = [Job(j, slots) for j in range(per_pass)]
    for job in jobs[slots:]:
        job.before = jobs[job.j - slots]
    bodies = [sequence(job) for job in jobs]
    for body in bodies:
        next(body)
    yield
    with nc.Fori(0, count // per_pass) as g:
        with nc.Block() as block:
            for job in jobs:
                job.block, job.b = block, g * per_pass + job.j
            pipeline(bodies, jobs, lag)
        ph.clear()


def load_once(nc, ph, pairs):
    loaded = ph.counter("weights_loaded")
    with nc.Block() as block:
        @block.sync
        def _(sp):
            for dst, src in pairs:
                loaded(sp.dma_start(dst, src), 16)
            sp.wait_ge(loaded.sem, loaded.n)
    ph.clear()


def make_constants(nc, ctx):
    c = {}
    for name in ("ident", "ones", "upto", "after"):
        c[name] = ctx.enter_context(nc.sbuf_tensor(f"c_{name}", [P, P], F32))
    ph = Phase(nc, ctx, "const")
    done = ph.counter("pool_done")
    with nc.Block() as block:
        @block.gpsimd
        def _(pool):
            nc.gpsimd.memset(c["ident"][:, :], 0.0).then_inc(done.sem, 1)
            nc.gpsimd.memset(c["ones"][:, :], 1.0).then_inc(done.sem, 1)
            pool.wait_ge(done.sem, 2)
            nc.gpsimd.affine_select(out=c["ident"][:, :], in_=c["ident"][:, :], compare_op=ALU.not_equal, fill=1.0,
                                    base=0, pattern=[[-1, P]], channel_multiplier=1).then_inc(done.sem, 1)
            nc.gpsimd.affine_select(out=c["upto"][:, :], in_=c["ones"][:, :], compare_op=ALU.is_ge, fill=0.0,
                                    base=0, pattern=[[1, P]], channel_multiplier=-1).then_inc(done.sem, 1)
            nc.gpsimd.affine_select(out=c["after"][:, :], in_=c["ones"][:, :], compare_op=ALU.is_gt, fill=0.0,
                                    base=0, pattern=[[-1, P]], channel_multiplier=1).then_inc(done.sem, 1)
            pool.wait_ge(done.sem, 5)
    done.n = 5
    ph.clear()
    return c


class Norm:

    def __init__(self, ph, tag):
        self.stats = ph.sb(f"{tag}_stats", [P, Q, 6])
        self.mv = ph.sb(f"{tag}_mv", [P, Q, 2])
        self.std = ph.sb(f"{tag}_std", [P, Q])
        self.rstd = ph.sb(f"{tag}_rstd", [P, Q])


def layer_norm(nc, block, nm, x, xn, V, A, ready):
    at = {}

    @block.vector
    def _(dve):
        dve.wait_ge(*ready)
        for q in range(Q):
            V(nc.vector.bn_stats(nm.stats[:, q, :], x[:, q, :]))
        dve.wait_ge(V.sem, V.n)
        for q in range(Q):
            V(nc.vector.bn_aggr(nm.mv[:, q, :], nm.stats[:, q, :]))
        dve.wait_ge(V.sem, V.n)
        at["var"] = V(nc.vector.tensor_scalar(nm.std[:, :], nm.mv[:, :, 1], EPS, None, ALU.add))

    @block.scalar
    def _(act):
        act.wait_ge(V.sem, at["var"])
        at["std"] = A(nc.scalar.activation(nm.std[:, :], nm.std[:, :], ACT.Sqrt))

    @block.vector
    def _(dve):
        dve.wait_ge(A.sem, at["std"])
        link(dve, V, nc.vector.reciprocal(nm.rstd[:, :], nm.std[:, :]))
        for q in range(Q):
            V(nc.vector.tensor_scalar(xn[:, q, :], x[:, q, :], nm.mv[:, q, 0:1], nm.rstd[:, q:q + 1],
                                      ALU.subtract, ALU.mult))
        at["xn"] = V.n
    return at["xn"]


def transpose_rows(nc, block, ps, banks, ident, xn, xnT, T, V, ready, free, eng="vector", kd=KD):
    at = {}

    @block.tensor
    def _(pe):
        pe.wait_ge(*ready)
        for k in range(kd):
            bank = banks[k % len(banks)]
            assert len(banks) >= kd
            if bank in free:
                pe.wait_ge(*free[bank])
            for q in range(Q):
                last = nc.tensor.transpose(ps[:, bank, q * P:(q + 1) * P], xn[:, q, k * P:(k + 1) * P], ident[:, :])
            at[k] = T(last)

    def copies(e, copy):
        for k in range(kd):
            e.wait_ge(T.sem, at[k])
            n = V(copy(xnT[:, k, :], ps[:, banks[k], :]))
            free[banks[k]] = (V.sem, n)
    if eng == "vector":
        block.vector(lambda dve: copies(dve, nc.vector.tensor_copy))
    else:
        block.scalar(lambda act: copies(act, nc.scalar.copy))
    return (V.sem, V.n)


DI, NS, KC = 512, 16, 4
GSTEP = 2
RE = 3
RT = 3
LAG_A = 15
SEQS = 4
KC3 = 96
KST = 96
CI = DI // P
E0, K0 = 32, 8


def phase_a(nc, c, d, mergedT, count=B):
    with ExitStack() as ctx:
        ph = Phase(nc, ctx, "a")
        ps = ph.psum()
        ident, upto, after = c["ident"], c["upto"], c["after"]
        w_in = ph.sb("w_in", [P, KD, 2 * DI])
        w_conv = ph.sb("w_conv", [P, CI, KC])
        b_conv = ph.sb("b_conv", [P, CI])
        w_x = ph.sb("w_x", [P, CI, 2 * NS + 1])
        skip = ph.sb("skip", [P, CI])
        w_out = ph.sb("w_out", [P, CI, DM])
        w_gate = ph.sb("w_gate", [P, KD, E0])
        b_gate = ph.sb("b_gate", [E0, 1])
        a_row = ph.sb("a_row", [P, NS])
        a_col = ph.sb("a_col", [NS, 1])
        pick = ph.sb("pick", [KC3, NS, P], BF16)
        load_once(nc, ph, [
            (w_in[:, :, :], d["w_in"].rearrange("(k p) e -> p k e", p=P)),
            (w_conv[:, :, :], d["w_conv"].rearrange("(c p) o k -> p c (o k)", p=P)),
            (b_conv[:, :], d["b_conv"]),
            (w_x[:, :, :], d["w_x"].rearrange("(c p) e -> p c e", p=P)),
            (skip[:, :], d["skip"]),
            (w_out[:, :, :], d["w_out"].rearrange("(c p) e -> p c e", p=P)),
            (w_gate[:, :, :], d["w_gate0"].rearrange("(k p) e -> p k e", p=P)),
            (b_gate[:, :], d["b_gate0"].rearrange("(e o) -> e o", o=1)),
            (a_row[:, :], d["a_log"].partition_broadcast(P)),
            (a_col[:, :], d["a_log"].rearrange("(n o) -> n o", o=1)),
        ])
        V, A, T, G = (ph.counter(n) for n in ("vector_done", "scalar_done", "tensor_done", "pool_done"))


        def sequence(job):
            i, j = job.slot, job.j
            c3 = ph.sb(f"c3_{i}", [KC3, S], BF16)
            crb = ph.sb(f"crb_{i}", [NS, S], BF16)
            cw = ph.sb(f"cw_{i}", [KST, S])
            st = ph.sb(f"st_{i}", [KST, Q, DI])
            x = ph.sb(f"x_{i}", [P, Q, DM])
            xn = ph.sb(f"xn_{i}", [P, Q, DM])
            xnT = ph.sb(f"xnT_{i}", [P, KD, S])
            nm = Norm(ph, f"ln{i}")
            xi = ph.sb(f"xi_{i}", [P, CI, KC - 1 + S])
            cv = ph.sb(f"cv_{i}", [P, CI, S])
            xc = ph.sb(f"xc_{i}", [P, CI, S])
            xct = ph.sb(f"xct_{i}", [P, Q, DI])
            zs = ph.sb(f"zs_{i}", [P, CI, S])
            lg = ph.sb(f"lg_{i}", [E0, S])
            pr = ph.sb(f"pr_{i}", [E0, S])
            rest = lg
            cr = lg
            top = ph.sb(f"top_{i}", [E0, K0])
            g1 = ph.sb(f"g1_{i}", [E0, 4])
            pT = ph.sb(f"pT_{i}", [P, Q, E0])
            xd = ph.sb(f"xd_{i}", [P, Q, 2 * NS + 1])
            cT = ph.sb(f"cT_{i}", [NS, S])
            sp1 = ph.sb(f"sp1_{i}", [P, Q])
            sp2 = ph.sb(f"sp2_{i}", [P, Q])
            dl = ph.sb(f"dl_{i}", [P, Q])
            dla = ph.sb(f"dla_{i}", [P, Q, P])
            dlr = ph.sb(f"dlr_{i}", [P, Q, NS])
            bdt = ph.sb(f"bdt_{i}", [P, Q, NS])
            bw = ph.sb(f"bw_{i}", [P, Q, NS])
            edec = ph.sb(f"edec_{i}", [NS, Q])
            span = ph.sb(f"span_{i}", [P, S])
            ex = ph.sb(f"ex_{i}", [P, RE, S])
            t1 = ph.sb(f"t1_{i}", [P, RT, S])
            gm = ph.sb(f"gm_{i}", [P, S])
            yg = cv
            so = x
            x_in, stored = ph.counter(f"x_in{j}"), ph.counter(f"stored{j}")
            spread_read, summed, spread_made, exp_made = (ph.counter(f"{n}{j}") for n in ("spread_read", "summed", "spread_made", "exp_made"))

            if j == i:
                seqs.append((c3, st, cw))
            yield
            block, b = job.block, job.b
            job.wait_for_buffers(block.sync)
            free, at = {}, {}
            b0, b1, b2, b3 = range(4 * i, 4 * i + 4)
            @block.sync
            def _(sp):
                x_in(sp.dma_start(x[:, :, :], d["x"][b].rearrange("(q p) e -> p q e", p=P)), 16)

            yield
            job.wait_for_buffers(block.tensor, block.scalar, block.vector, block.gpsimd)
            n = layer_norm(nc, block, nm, x, xn, V, A, (x_in.sem, 16))
            at["xn"] = n
            yield
            at["xnT"] = transpose_rows(nc, block, ps, [b0, b1], ident, xn, xnT, T, V, (V.sem, n), free)

            yield

            ring = (b3, b0, b1, b2)

            @block.tensor
            def _(pe):
                pe.wait_ge(*at["xnT"])
                for k in range(KD):
                    last = nc.tensor.matmul(ps[0:E0, b2, :], w_gate[:, k, :], xnT[:, k, :], start=k == 0, stop=k == KD - 1)
                at["logits"] = T(last)

            @block.vector
            def _(dve):
                at["pad"] = V(nc.vector.memset(xi[:, :, 0:KC - 1], 0.0))
                dve.wait_ge(T.sem, at["logits"])
                n = link(dve, V, nc.vector.tensor_scalar(lg[:, :], ps[0:E0, b2, :], b_gate[:, 0:1], None, ALU.add))
                free[b2] = (V.sem, n)
                at["gmax"] = link(dve, V, nc.vector.tensor_reduce(g1[:, 0:1], lg[:, :], AX.X, ALU.max, negate=True))

            def project(e, bank):
                @block.tensor
                def _(pe):
                    if bank in free:
                        pe.wait_ge(*free[bank])
                    for k in range(KD):
                        last = nc.tensor.matmul(ps[:, bank, :], w_in[:, k, e * P:(e + 1) * P], xnT[:, k, :],
                                                start=k == 0, stop=k == KD - 1)
                    at[f"proj{e}"] = T(last)

            def projected(e, bank):
                @block.scalar
                def _(act):
                    act.wait_ge(T.sem, at[f"proj{e}"])
                    to = xi[:, e, KC - 1:] if e < CI else zs[:, e - CI, :]
                    at[f"xz{e}"] = A(nc.scalar.copy(to, ps[:, bank, :]))
                    free[bank] = (A.sem, A.n)

            for e in range(CI):
                project(e, ring[e])
                if e % 2:
                    yield
                    projected(e - 1, ring[e - 1])
                    projected(e, ring[e])

            for k in range(KC):
                @block.vector
                def _(dve):
                    if k == 0:
                        dve.wait_ge(V.sem, at["pad"])
                    for e in range(CI):
                        if k == 0:
                            dve.wait_ge(A.sem, at[f"xz{e}"])
                            at[f"cv{e}"] = V(nc.vector.tensor_scalar(cv[:, e, :], xi[:, e, 0:S], w_conv[:, e, 0:1], b_conv[:, e:e + 1],
                                                                     ALU.mult, ALU.add))
                        else:
                            dve.wait_ge(V.sem, at[f"cv{e}"])
                            at[f"cv{e}"] = V(nc.vector.scalar_tensor_tensor(
                                cv[:, e, :], xi[:, e, k:k + S], w_conv[:, e, k:k + 1], cv[:, e, :], ALU.mult, ALU.add))
                if k % 2:
                    yield

            @block.scalar
            def _(act):
                for e in range(CI):
                    act.wait_ge(V.sem, at[f"cv{e}"])
                    A(nc.scalar.activation(xc[:, e, :], cv[:, e, :], ACT.Silu))
                at["xc"] = A.n
                act.wait_ge(V.sem, at["gmax"])
                at["gexp"] = A(nc.scalar.activation(pr[:, :], lg[:, :], ACT.Exp, bias=g1[:, 0:1], accum_out=g1[:, 1:2]))

            yield

            @block.vector
            def _(dve):
                dve.wait_ge(A.sem, at["gexp"])
                link(dve, V, nc.vector.reciprocal(g1[:, 2:3], g1[:, 1:2]))
                link(dve, V, nc.vector.tensor_scalar(pr[:, :], pr[:, :], g1[:, 2:3], None, ALU.mult))
                link(dve, V, nc.vector.max(top[:, :], pr[:, :]))
                link(dve, V, nc.vector.match_replace(rest[:, :], top[:, :], pr[:, :], 0.0))
                at["picked"] = link(dve, V, nc.vector.tensor_tensor(pr[:, :], pr[:, :], rest[:, :], ALU.subtract))

            @block.tensor
            def _(pe):
                pe.wait_ge(A.sem, at["xc"])
                pe.wait_ge(*free[b0])
                for q in range(Q):
                    for e in range(CI):
                        last = nc.tensor.matmul(ps[:, b0, q * 64:q * 64 + 33], xc[:, e, q * P:(q + 1) * P], w_x[:, e, :],
                                                start=e == 0, stop=e == CI - 1)
                at["xd"] = T(last)
                pe.wait_ge(*free[b1])
                for e in range(CI):
                    last = nc.tensor.matmul(ps[0:NS, b1, :], w_x[:, e, NS + 1:], xc[:, e, :], start=e == 0, stop=e == CI - 1)
                at["cT"] = T(last)

            @block.vector
            def _(dve):
                dve.wait_ge(T.sem, at["xd"])
                link(dve, V, nc.vector.tensor_copy(
                    xd[:, :, :], ps[:, b0, 0:256].rearrange("p (q e) -> p q e", q=Q)[:, :, 0:33]))
                free[b0] = (V.sem, V.n)
                at["sp1"] = link(dve, V, nc.vector.scalar_tensor_tensor(
                    sp1[:, :], xd[:, :, 0], -1.0, xd[:, :, 0], ALU.mult, ALU.min))
                dve.wait_ge(T.sem, at["cT"])
                link(dve, V, nc.vector.tensor_copy(cT[:, :], ps[0:NS, b1, :]))
                free[b1] = (V.sem, V.n)

            @block.scalar
            def _(act):
                act.wait_ge(V.sem, at["sp1"])
                link(act, A, nc.scalar.activation(sp2[:, :], sp1[:, :], ACT.Exp))
                at["sp2"] = link(act, A, nc.scalar.activation(sp2[:, :], sp2[:, :], ACT.Ln, bias=1.0))

            yield

            @block.tensor
            def _(pe):
                pe.wait_ge(V.sem, at["picked"])
                pe.wait_ge(*free[b0])
                for q in range(Q):
                    last = nc.tensor.transpose(ps[:, b0, q * E0:(q + 1) * E0], pr[:, q * P:(q + 1) * P], ident[0:E0, 0:E0])
                at["pT_ps"] = T(last)

            @block.vector
            def _(dve):
                link(dve, V, nc.vector.tensor_copy(c3[0:NS, :], cT[:, :]))
                link(dve, V, nc.vector.tensor_tensor(cr[0:NS, :], cT[:, :], c3[0:NS, :], ALU.subtract))
                V(nc.vector.tensor_copy(c3[32:32 + NS, :], cr[0:NS, :]))
                link(dve, V, nc.vector.tensor_copy(crb[:, :], cr[0:NS, :]))
                at["cT_sb"] = V(nc.vector.tensor_tensor(c3[64:64 + NS, :], cr[0:NS, :], crb[:, :], ALU.subtract))
                dve.wait_ge(T.sem, at["pT_ps"])
                at["pT"] = V(nc.vector.tensor_copy(pT[:, :, :], ps[:, b0, 0:Q * E0]))
                free[b0] = (V.sem, V.n)

            yield

            @block.vector
            def _(dve):
                dve.wait_ge(A.sem, at["sp2"])
                link(dve, V, nc.vector.scalar_tensor_tensor(dl[:, :], xd[:, :, 0], 0.0, sp2[:, :], ALU.max, ALU.add))
                V(nc.vector.tensor_tensor(dla[:, :, :], after[:, :].unsqueeze(1).broadcast_to([P, Q, P]),
                                          dl[:, :].unsqueeze(2).broadcast_to([P, Q, P]), ALU.mult))
                V(nc.vector.tensor_copy(dlr[:, :, :], dl[:, :].unsqueeze(2).broadcast_to([P, Q, NS])))
                at["dla"] = V.n
                V(nc.vector.tensor_tensor(bdt[:, :, :], xd[:, :, 1:NS + 1], dl[:, :].unsqueeze(2).broadcast_to([P, Q, NS]),
                                          ALU.mult))
                at["bdt"] = V.n

            yield

            @block.tensor
            def _(pe):
                pe.wait_ge(V.sem, at["dla"])
                pe.wait_ge(*free[b3])
                for q in range(Q):
                    last = nc.tensor.matmul(ps[:, b3, q * P:(q + 1) * P], dla[:, q, :], upto[:, :], start=True, stop=True)
                at["span"] = T(last)
                pe.wait_ge(*free[b1])
                for q in range(Q):
                    last = nc.tensor.matmul(ps[0:NS, b1, q * P:(q + 1) * P], dlr[:, q, :], upto[:, :], start=True, stop=True)
                at["upto"] = T(last)
                pe.wait_ge(*free[b2])
                for k in range(KD):
                    for q in range(Q):
                        last = nc.tensor.matmul(ps[:, b2, k * E0:(k + 1) * E0], xn[:, q, k * P:(k + 1) * P], pT[:, q, :],
                                                start=q == 0, stop=q == Q - 1)
                at["merged"] = T(last)

            @block.vector
            def _(dve):
                dve.wait_ge(T.sem, at["span"])
                at["span_sb"] = V(nc.vector.tensor_copy(span[:, :], ps[:, b3, :]))
                free[b3] = (V.sem, V.n)
                dve.wait_ge(T.sem, at["merged"])
                V(nc.vector.tensor_copy(mergedT[:, :, :, bass.ds(b, 1)],
                                        ps[:, b2, 0:KD * E0].rearrange("p (k e o) -> p k e o", k=KD, o=1)))
                free[b2] = (V.sem, V.n)

            @block.vector
            def _(dve):
                dve.wait_ge(V.sem, at["span_sb"])
                at["bwa"] = V(nc.vector.tensor_tensor(
                    bw[:, :, :], a_row[:, :].unsqueeze(1).broadcast_to([P, Q, NS]),
                    span[:, P - 1:S:P].unsqueeze(2).broadcast_to([P, Q, NS]), ALU.mult))

            @block.scalar
            def _(act):
                act.wait_ge(T.sem, at["upto"])
                at["cwe"] = A(nc.scalar.activation(cw[0:NS, :], ps[0:NS, b1, :], ACT.Exp, scale=a_col[:, 0:1]))
                at["edec"] = A(nc.scalar.activation(edec[:, :], ps[0:NS, b1, P - 1:S:P], ACT.Exp, scale=a_col[:, 0:1]))
                free[b1] = (A.sem, A.n)
                act.wait_ge(V.sem, at["bwa"])
                at["bwe"] = A(nc.scalar.activation(bw[:, :, :], bw[:, :, :], ACT.Exp))

            spread = (b0, b3)

            def turn_x(q, bank):
                @block.tensor
                def _(pe):
                    pe.wait_ge(*free[bank])
                    for e in range(CI):
                        last = nc.tensor.transpose(ps[:, bank, e * P:(e + 1) * P], xc[:, e, q * P:(q + 1) * P], ident[:, :])
                    at["xct_ps"] = T(last)

            def turned_x(q, bank):
                @block.scalar
                def _(act):
                    act.wait_ge(T.sem, at["xct_ps"])
                    at["xct"] = A(nc.scalar.copy(xct[:, q, :], ps[:, bank, :]))
                    free[bank] = (A.sem, A.n)

            for n in range(NS):
                if n % GSTEP == 0:
                    yield
                    step = n // GSTEP
                    bank = (b1, b2)[step % 2]
                    if step < CI:
                        z_or_x, args = project, (CI + step, bank)
                    else:
                        z_or_x, args = turn_x, (step - CI, bank)
                    z_or_x(*args)
                    later = (projected if step < CI else turned_x), args

                @block.tensor
                def _(pe):
                    if n < 2:
                        pe.wait_ge(*free[spread[n]])
                        pe.wait_ge(V.sem, at["cT_sb"])
                    else:
                        pe.wait_ge(spread_read.sem, n - 1)
                    spread_made(nc.tensor.matmul(ps[:, spread[n % 2], :], pick[:, n, :], c3[:, :], start=True, stop=True))

                @block.scalar
                def _(act):
                    if n == 0:
                        act.wait_ge(V.sem, at["span_sb"])
                    if n >= RE:
                        act.wait_ge(spread_read.sem, n - RE + 1)
                    exp_made(nc.scalar.activation(ex[:, n % RE, :], span[:, :], ACT.Exp, scale=a_row[:, n:n + 1]))

                @block.vector
                def _(dve):
                    dve.wait_ge(exp_made.sem, n + 1)
                    dve.wait_ge(spread_made.sem, n + 1)
                    if n == 0:
                        dve.wait_ge(V.sem, at["bdt"])
                    if n >= RT:
                        dve.wait_ge(summed.sem, n - RT + 1)
                    for q in range(Q):
                        cut = slice(q * P, (q + 1) * P)
                        last = nc.vector.scalar_tensor_tensor(t1[:, n % RT, cut], ex[:, n % RE, cut], bdt[:, q, n:n + 1],
                                                              ps[:, spread[n % 2], cut], ALU.mult, ALU.mult)
                    spread_read(last)

                @block.gpsimd
                def _(pool):
                    pool.wait_ge(spread_read.sem, n + 1)
                    if n == 0:
                        summed(nc.gpsimd.tensor_copy(gm[:, :], t1[:, 0, :]))
                    else:
                        pool.wait_ge(summed.sem, n)
                        summed(nc.gpsimd.tensor_tensor(gm[:, :], gm[:, :], t1[:, n % RT, :], ALU.add))
                if n % GSTEP == GSTEP - 1:
                    later[0](*later[1])
            free[b0] = free[b3] = (spread_read.sem, NS)

            yield

            @block.gpsimd
            def _(pool):
                pool.wait_ge(summed.sem, NS)
                g3 = gm[:, :].rearrange("p (q t) -> p q t", q=Q)
                summed(nc.gpsimd.tensor_tensor(g3, g3, upto[:, :].unsqueeze(1).broadcast_to([P, Q, P]), ALU.mult))

            @block.vector
            def _(dve):
                dve.wait_ge(A.sem, at["bwe"])
                at["bw"] = V(nc.vector.tensor_tensor(bw[:, :, :], bw[:, :, :], bdt[:, :, :], ALU.mult))
                at["cw"] = V(nc.vector.tensor_tensor(cw[0:NS, :], cw[0:NS, :], cT[:, :], ALU.mult))

            @block.scalar
            def _(act):
                act.wait_ge(A.sem, at[f"xz{2 * CI - 1}"])
                at["zs"] = A(nc.scalar.activation(zs[:, :, :], zs[:, :, :], ACT.Silu))

            yield

            @block.tensor
            def _(pe):
                pe.wait_ge(V.sem, at["bw"])
                pe.wait_ge(A.sem, at["xct"])
                at["u"] = T.n
                for q in range(Q - 1):
                    bank = (b2, b0, b3)[q]
                    pe.wait_ge(*free[bank])
                    T(nc.tensor.matmul(ps[0:NS, bank, :], bw[:, q, :], xct[:, q, :], start=True, stop=True))

            @block.vector
            def _(dve):
                dve.wait_ge(A.sem, at["edec"])
                for q in range(Q - 1):
                    bank = (b2, b0, b3)[q]
                    dve.wait_ge(T.sem, at["u"] + q + 1)
                    if q == 0:
                        link(dve, V, nc.vector.tensor_copy(st[0:NS, 1, :], ps[0:NS, bank, :]))
                    else:
                        link(dve, V, nc.vector.scalar_tensor_tensor(st[0:NS, q + 1, :], st[0:NS, q, :], edec[:, q:q + 1],
                                                                    ps[0:NS, bank, :], ALU.mult, ALU.add))
                    free[bank] = (V.sem, V.n)
                at["st"] = V.n

            yield

            for e in range(CI):
                if e == 2:
                    yield

                @block.tensor
                def _(pe):
                    if e == 0:
                        pe.wait_ge(V.sem, at["st"])
                        pe.wait_ge(summed.sem, NS + 1)
                    pe.wait_ge(*free[4 * i + e])
                    for q in range(Q):
                        out = ps[:, 4 * i + e, q * P:(q + 1) * P]
                        last = nc.tensor.matmul(out, xct[:, q, e * P:(e + 1) * P], gm[:, q * P:(q + 1) * P],
                                                start=True, stop=q == 0)
                        if q:
                            last = nc.tensor.matmul(out, st[:, q, e * P:(e + 1) * P], cw[:, q * P:(q + 1) * P],
                                                    start=False, stop=True)
                    at["y"] = T(last)

                @block.vector
                def _(dve):
                    if e == 0:
                        dve.wait_ge(A.sem, at["zs"])
                    dve.wait_ge(T.sem, at["y"])
                    link(dve, V, nc.vector.scalar_tensor_tensor(yg[:, e, :], xc[:, e, :], skip[:, e:e + 1], ps[:, 4 * i + e, :],
                                                                ALU.mult, ALU.add))
                    free[4 * i + e] = (V.sem, V.n)
                    at["yg"] = V(nc.vector.tensor_tensor(yg[:, e, :], yg[:, e, :], zs[:, e, :], ALU.mult))

            yield

            @block.tensor
            def _(pe):
                pe.wait_ge(V.sem, at["yg"])
                at["out"] = T.n
                for q in range(Q):
                    if q % 2 == 0:
                        pe.wait_ge(*free[4 * i + q // 2])
                    for e in range(CI):
                        last = nc.tensor.matmul(ps[:, 4 * i + q // 2, q % 2 * DM:(q % 2 + 1) * DM], yg[:, e, q * P:(q + 1) * P],
                                                w_out[:, e, :], start=e == 0, stop=e == CI - 1)
                    T(last)

            @block.scalar
            def _(act):
                for q in range(0, Q, 2):
                    act.wait_ge(T.sem, at["out"] + q + 2)
                    A(nc.scalar.copy(so[:, q:q + 2, :], ps[:, 4 * i + q // 2, :]))
                at["so"] = A.n

            @block.sync
            def _(sp):
                sp.wait_ge(V.sem, at["picked"])
                stored(sp.dma_start(d["picked"][b], pr[:, :]), 16)
                sp.wait_ge(A.sem, at["so"])
                stored(sp.dma_start(d["s0"][b].rearrange("(q p) e -> p q e", p=P), so[:, :, :]), 16)
                sp.wait_ge(stored.sem, 32)
            job.done = [(c.sem, c.n) for c in (V, A, T, stored, summed)]

        seqs = []
        loop = run_sequences(nc, ph, sequence, count, min(count, SEQS), LAG_A)
        next(loop)

        with nc.Block() as block:
            @block.scalar
            def _(act):
                A(nc.scalar.activation(a_row[:, :], a_row[:, :], ACT.Exp))
                A(nc.scalar.activation(a_col[:, :], a_col[:, :], ACT.Exp))

            @block.vector
            def _(dve):
                dve.wait_ge(A.sem, 2)
                V(nc.vector.tensor_scalar(a_row[:, :], a_row[:, :], -1.0, None, ALU.mult))
                V(nc.vector.tensor_scalar(a_col[:, :], a_col[:, :], -1.0, None, ALU.mult))

            @block.gpsimd
            def _(pool):
                link(pool, G, nc.gpsimd.memset(pick[:, :, :], 0.0))
                for part in range(3):
                    rows = pick[32 * part:32 * part + 32, :, :]
                    link(pool, G, nc.gpsimd.affine_select(out=rows, in_=rows, compare_op=ALU.not_equal, fill=1.0,
                                                          base=0, pattern=[[-1, NS], [0, P]], channel_multiplier=1))
                for c3, st, cw in seqs:
                    link(pool, G, nc.gpsimd.memset(c3[:, :], 0.0))
                    link(pool, G, nc.gpsimd.memset(st[:, :, :], 0.0))
                    link(pool, G, nc.gpsimd.memset(cw[:, :], 0.0))
        ph.clear()

        next(loop, None)


H0 = 1024
EG = 4
HK = H0 // P


def phase_b(nc, c, d, mergedT, count=E0 // EG):
    with ExitStack() as ctx:
        ph = Phase(nc, ctx, "b")
        ps = ph.psum()
        ident = c["ident"]
        w1 = ph.sb("w1", [P, EG, KD, H0])
        w2 = ph.sb("w2", [P, EG, HK, DM])
        w1b = ph.sb("w1b", [B, EG, H0])
        w2b = ph.sb("w2b", [B, EG, DM])
        mt = ph.sb("mt", [P, KD, EG, B])
        hb = ph.sb("hb", [B, 2, H0])
        h = ph.sb("h", [B, 2, H0])
        hT = ph.sb("hT", [P, 2, HK, B])
        o = ph.sb("o", [B, EG, DM])
        V, T = ph.counter("vector_done"), ph.counter("tensor_done")
        w1_in = [ph.counter(f"w1_in{j}") for j in range(EG)]
        w2_in = [ph.counter(f"w2_in{j}") for j in range(EG)]
        hidden_made, biased, hidden_done, turned_made, turned, out_made, out_done, stored = (ph.counter(n) for n in (
            "hidden_made", "biased", "hidden_done", "turned_made", "turned", "out_made", "out_done", "stored"))
        with nc.Fori(0, count) as g:
            with nc.Block() as block:
                @block.sync
                def _(sp):
                    for j in range(EG):
                        w1_in[j](sp.dma_start(w1[:, j, :, :], d["w1_0"][g * EG + j, 0:DM].rearrange("(k p) h -> p k h", p=P)), 16)
                        w1_in[j](sp.dma_start(w1b[:, j, :], d["w1_0"][g * EG + j, DM].partition_broadcast(B)), 16)
                        w2_in[j](sp.dma_start(w2[:, j, :, :], d["w2_0"][g * EG + j, 0:H0].rearrange("(k p) h -> p k h", p=P)), 16)
                        w2_in[j](sp.dma_start(w2b[:, j, :], d["w2_0"][g * EG + j, H0].partition_broadcast(B)), 16)
                    sp.wait_ge(out_done.sem, EG)
                    stored(sp.dma_start(d["o0"][:, bass.ds(g * EG, EG), :], o[:, :, :]), 16)
                    sp.wait_ge(stored.sem, 16)

                @block.tensor
                def _(pe):
                    def hidden(j):
                        pe.wait_ge(w1_in[j].sem, 32)
                        if j >= 2:
                            pe.wait_ge(biased.sem, j - 1)
                        for half in range(2):
                            out = ps[0:B, 2 * (j % 2) + half, :]
                            cols = slice(half * 512, half * 512 + 512)
                            for k in range(KD):
                                last = nc.tensor.matmul(out, mt[:, k, j, :], w1[:, j, k, cols], start=k == 0, stop=k == KD - 1)
                        hidden_made(last)

                    pe.wait_ge(V.sem, 1)
                    hidden(0)
                    for j in range(EG):
                        if j + 1 < EG:
                            hidden(j + 1)
                        pe.wait_ge(hidden_done.sem, j + 1)
                        if j >= 2:
                            pe.wait_ge(turned.sem, j - 1)
                        for k in range(HK):
                            last = nc.tensor.transpose(ps[:, 4 + j % 2, k * B:(k + 1) * B], h[:, j % 2, k * P:(k + 1) * P],
                                                       ident[0:B, 0:B])
                        turned_made(last)
                        pe.wait_ge(turned.sem, j + 1)
                        pe.wait_ge(w2_in[j].sem, 32)
                        if j >= 2:
                            pe.wait_ge(out_done.sem, j - 1)
                        out = ps[0:B, 6 + j % 2, 0:DM]
                        for k in range(HK):
                            last = nc.tensor.matmul(out, hT[:, j % 2, k, :], w2[:, j, k, :], start=k == 0, stop=k == HK - 1)
                        out_made(last)

                @block.scalar
                def _(act):
                    for j in range(EG):
                        act.wait_ge(biased.sem, j + 1)
                        if j >= 2:
                            act.wait_ge(turned_made.sem, j - 1)
                        hidden_done(nc.scalar.activation(h[:, j % 2, :], hb[:, j % 2, :], ACT.Gelu))

                @block.vector
                def _(dve):
                    V(nc.vector.tensor_copy(mt[:, :, :, :], mergedT[:, :, bass.ds(g * EG, EG), :]))
                    def bias(j):
                        dve.wait_ge(w1_in[j].sem, 32)
                        dve.wait_ge(hidden_made.sem, j + 1)
                        if j >= 2:
                            dve.wait_ge(hidden_done.sem, j - 1)
                        b0 = 2 * (j % 2)
                        biased(nc.vector.tensor_tensor(hb[:, j % 2, :].rearrange("p (a n) -> p a n", a=2), ps[0:B, b0:b0 + 2, :],
                                                       w1b[:, j, :].rearrange("p (a n) -> p a n", a=2), ALU.add))

                    bias(0)
                    for j in range(EG):
                        if j + 1 < EG:
                            bias(j + 1)
                        dve.wait_ge(turned_made.sem, j + 1)
                        if j >= 2:
                            dve.wait_ge(out_made.sem, j - 1)
                        turned(nc.vector.tensor_copy(hT[:, j % 2, :, :], ps[:, 4 + j % 2, 0:HK * B]))
                        dve.wait_ge(w2_in[j].sem, 32)
                        dve.wait_ge(out_made.sem, j + 1)
                        out_done(nc.vector.tensor_tensor(o[:, j, :], ps[0:B, 6 + j % 2, 0:DM], w2b[:, j, :], ALU.add))
            ph.clear()


HEADS, HD = 16, 8
HV = 2 * HD
LAMBDA_INIT = 0.8 - 0.6
SPLIT = 3
PRODUCTS = ((0, 0), (0, 1), (1, 0), (1, 1), (0, 2), (2, 0))
KROWS = len(PRODUCTS) * HD
SROWS = 2 * KROWS
AROWS = SROWS + 2 * SPLIT
GH = 4
NG = HEADS // GH
UNITS = HEADS * Q
GSTEPS = GH * Q
LAG = GSTEPS + 5
RING = 6
SLOTS_C1, LAG_C1 = 4, 3
RUN = 4


def phase_c1a(nc, c, d, count=B):
    with ExitStack() as ctx:
        ph = Phase(nc, ctx, "c1a")
        ps = ph.psum()
        ident = c["ident"]
        w_qkv = ph.sb("w_qkv", [P, KD, 3 * DM])
        load_once(nc, ph, [(w_qkv[:, :, :], d["w_qkv"].rearrange("(k p) e -> p k e", p=P))])
        V, A, T, G = (ph.counter(n) for n in ("vector_done", "scalar_done", "tensor_done", "pool_done"))
        padded = []

        def sequence(job):
            i, j = job.slot, job.j
            x = ph.sb(f"x_{i}", [P, Q, DM])
            s0 = ph.sb(f"s0_{i}", [P, Q, DM])
            pick = ph.sb(f"pick_{i}", [P, S])
            o0 = ph.sb(f"o0_{i}", [P, DM])
            g0 = ph.sb(f"g0_{i}", [P, Q, DM])
            xn = ph.sb(f"xn_{i}", [P, Q, DM])
            xnT = ph.sb(f"xnT_{i}", [P, KD, S])
            nm = Norm(ph, f"ln{i}")
            parts = ph.sb(f"parts_{i}", [P, 4, SPLIT, S], BF16)
            rem = ph.sb(f"rem_{i}", [P, 2, S])
            vo = s0
            x_in, s0_in, pick_in, stored = (ph.counter(f"{n}{j}") for n in ("x_in", "s0_in", "pick_in", "stored"))
            if j == i:
                padded.extend((pick, o0))
            yield
            block, b = job.block, job.b
            job.wait_for_buffers(block.sync)
            free, at = {}, {}
            b0, b1 = 2 * i, 2 * i + 1

            @block.sync
            def _(sp):
                pick_in(sp.dma_start(pick[0:E0, :], d["picked"][b]), 16)
                pick_in(sp.dma_start(o0[0:E0, :], d["o0"][b]), 16)
                x_in(sp.dma_start(x[:, :, :], d["x"][b].rearrange("(q p) e -> p q e", p=P)), 16)
                s0_in(sp.dma_start(s0[:, :, :], d["s0"][b].rearrange("(q p) e -> p q e", p=P)), 16)

            yield
            yield
            job.wait_for_buffers(block.tensor, block.scalar, block.vector, block.gpsimd)

            @block.tensor
            def _(pe):
                pe.wait_ge(pick_in.sem, 32)
                for q in range(Q):
                    last = nc.tensor.matmul(ps[:, b0 + q // 2, q % 2 * DM:(q % 2 + 1) * DM], pick[:, q * P:(q + 1) * P], o0[:, :],
                                            start=True, stop=True)
                at["ffn0"] = T(last)

            @block.scalar
            def _(act):
                act.wait_ge(T.sem, at["ffn0"])
                at["g0"] = A(nc.scalar.activation(g0[:, :, :], ps[:, b0:b0 + 2, :], ACT.Silu))
                free[b0] = free[b1] = (A.sem, A.n)

            yield

            @block.gpsimd
            def _(pool):
                pool.wait_ge(A.sem, at["g0"])
                pool.wait_ge(s0_in.sem, 16)
                pool.wait_ge(x_in.sem, 16)
                link(pool, G, nc.gpsimd.tensor_tensor(g0[:, :, :], g0[:, :, :], s0[:, :, :], ALU.mult))
                at["x1"] = G(nc.gpsimd.tensor_tensor(x[:, :, :], x[:, :, :], g0[:, :, :], ALU.add))

            yield
            n = layer_norm(nc, block, nm, x, xn, V, A, (G.sem, at["x1"]))
            at["xn"] = n

            @block.sync
            def _(sp):
                sp.wait_ge(G.sem, at["x1"])
                stored(sp.dma_start(d["x1"][b].rearrange("(q p) e -> p q e", p=P), x[:, :, :]), 16)
                sp.wait_ge(V.sem, at["xn"])
                stored(sp.dma_start(d["xn1"][b].rearrange("(q p) e -> p q e", p=P), xn[:, :, :]), 16)

            yield
            at["xnT"] = transpose_rows(nc, block, ps, [b0, b1], ident, xn, xnT, T, V, (V.sem, n), free)

            for e in range(4):
                yield
                bank = (b0, b1)[e % 2]

                @block.tensor
                def _(pe):
                    if e == 0:
                        pe.wait_ge(*at["xnT"])
                    pe.wait_ge(*free[bank])
                    for k in range(KD):
                        last = nc.tensor.matmul(ps[:, bank, :], w_qkv[:, k, e * P:(e + 1) * P], xnT[:, k, :],
                                                start=k == 0, stop=k == KD - 1)
                    at["qk"] = T(last)

                @block.scalar
                def _(act):
                    act.wait_ge(T.sem, at["qk"])
                    at["hi"] = A(nc.scalar.copy(parts[:, e, 0, :], ps[:, bank, :]))

                @block.vector
                def _(dve):
                    dve.wait_ge(A.sem, at["hi"])
                    if e >= 2:
                        dve.wait_ge(G.sem, at[f"lo{e - 2}"])
                    at["rem"] = V(nc.vector.tensor_tensor(rem[:, e % 2, :], ps[:, bank, :], parts[:, e, 0, :], ALU.subtract))
                    free[bank] = (V.sem, V.n)

                @block.scalar
                def _(act):
                    act.wait_ge(V.sem, at["rem"])
                    at["mid"] = A(nc.scalar.copy(parts[:, e, 1, :], rem[:, e % 2, :]))

                @block.gpsimd
                def _(pool):
                    pool.wait_ge(A.sem, at["mid"])
                    at[f"lo{e}"] = G(nc.gpsimd.tensor_tensor(parts[:, e, 2, :], rem[:, e % 2, :], parts[:, e, 1, :], ALU.subtract))

                @block.sync
                def _(sp):
                    sp.wait_ge(G.sem, at[f"lo{e}"])
                    stored(sp.dma_start(d["qk_parts"][b, e // 2, :, e % 2 * P:(e % 2 + 1) * P].rearrange("s p n -> p s n"),
                                        parts[:, e, :, :]), 16)

            yield

            @block.tensor
            def _(pe):
                for q in range(Q):
                    if q % 2 == 0:
                        pe.wait_ge(*free[b0 + q // 2])
                    for k in range(KD):
                        last = nc.tensor.matmul(ps[:, b0 + q // 2, q % 2 * DM:(q % 2 + 1) * DM], xnT[:, k, q * P:(q + 1) * P],
                                                w_qkv[:, k, 2 * DM:], start=k == 0, stop=k == KD - 1)
                at["v"] = T(last)

            @block.scalar
            def _(act):
                act.wait_ge(T.sem, at["v"])
                at["vo"] = A(nc.scalar.copy(vo[:, :, :], ps[:, b0:b0 + 2, :].rearrange("p a (q e) -> p (a q) e", q=2)))

            @block.sync
            def _(sp):
                sp.wait_ge(A.sem, at["vo"])
                stored(sp.dma_start(d["v1"][b].rearrange("(q p) e -> p q e", p=P), vo[:, :, :]), 16)
                sp.wait_ge(stored.sem, stored.n)
            job.done = [(c.sem, c.n) for c in (V, A, T, G, stored)]

        loop = run_sequences(nc, ph, sequence, count, min(count, 8), LAG_C1, SLOTS_C1)
        next(loop)
        with nc.Block() as block:
            @block.vector
            def _(dve):
                for t in padded:
                    link(dve, V, nc.vector.memset(t[:, :], 0.0))
        ph.clear()
        next(loop, None)


def phase_c1b(nc, c, d, count=B):
    with ExitStack() as ctx:
        ph = Phase(nc, ctx, "c1b")
        ps = ph.psum()
        ident = c["ident"]
        w_proj = ph.sb("w_proj", [P, KD, DM])
        b_proj = ph.sb("b_proj", [P, DM])
        w_sub = ph.sb("w_sub", [P, HV])
        lams = ph.sb("lams", [P, 4, HD])
        load_once(nc, ph, [
            (w_proj[:, :, :], d["w_proj"].rearrange("(k p) e -> p k e", p=P)),
            (b_proj[:, :], d["b_proj"].partition_broadcast(P)),
            (w_sub[:, :], d["sub_norm_w"].partition_broadcast(P)),
        ] + [(lams[:, i, :], d[n].partition_broadcast(P)) for i, n in enumerate(
            ("lambda_q1", "lambda_k1", "lambda_q2", "lambda_k2"))])
        V, A, G = (ph.counter(n) for n in ("vector_done", "scalar_done", "pool_done"))
        lp = ph.sb("lp", [P, 2, HD])
        le = ph.sb("le", [P, 2])
        lam = ph.sb("lam", [P, 1])
        identb = ph.sb("identb", [P, P], BF16)
        qs = ph.sb("qs", [AROWS, 2, HEADS, S], BF16)
        ks = ph.sb("ks", [AROWS, 2, 2, HEADS, S], BF16)
        v1 = ph.sb("v1", [P, 2, Q, HEADS, 32])

        with nc.Block() as block:
            @block.vector
            def _(dve):
                V(nc.vector.memset(ks[0:SROWS, :, :, :, :], 0.0))
                V(nc.vector.memset(qs[:, :, :, :], 0.0))
                V(nc.vector.memset(v1[:, :, :, :, HV:], 0.0))
                V(nc.vector.tensor_copy(identb[:, :], ident[:, :]))
                V(nc.vector.tensor_scalar(w_sub[:, :], w_sub[:, :], 1.0 - LAMBDA_INIT, None, ALU.mult))
                link(dve, V, nc.vector.tensor_tensor(lp[:, :, :], lams[:, 0:4:2, :], lams[:, 1:4:2, :], ALU.mult))
                V(nc.vector.memset(v1[:, :, :, :, HV:HV + 1], 1.0))
                link(dve, V, nc.vector.tensor_reduce(le[:, :], lp[:, :, :], AX.X, ALU.add))

            @block.gpsimd
            def _(pool):
                rows = ks[SROWS:AROWS]
                link(pool, G, nc.gpsimd.memset(rows[:, :, :, :, :], 1.0))
                for slot in range(2):
                    for half, base, mult in ((0, SPLIT - 1, -1), (1, -SPLIT, 1)):
                        link(pool, G, nc.gpsimd.affine_select(
                            out=rows[:, slot, half], in_=rows[:, slot, half], compare_op=ALU.is_ge, fill=0.0, base=base,
                            pattern=[[0, HEADS], [0, S]], channel_multiplier=mult))

            @block.scalar
            def _(act):
                act.wait_ge(V.sem, V.n)
                A(nc.scalar.activation(le[:, :], le[:, :], ACT.Exp))

            @block.vector
            def _(dve):
                dve.wait_ge(A.sem, 1)
                V(nc.vector.scalar_tensor_tensor(lam[:, :], le[:, 0:1], LAMBDA_INIT, le[:, 1:2], ALU.add, ALU.subtract))
        ph.clear()

        vin = ph.sb("vin", [P, Q, DM])
        mx = ph.sb("mx", [P, 2, Q, 2, GH])
        mrem = ph.sb("mrem", [P, 2, Q, 2, GH])
        mparts = ph.sb("mparts", [P, 2, Q, 2, SPLIT, GH], BF16)
        mT = ph.sb("mT", [2 * SPLIT * GH, 2, S], BF16)
        pT = ph.sb("pT", [P, RING, 2, S])
        ao = ph.sb("ao", [P, 2, S])
        ot = ph.sb("ot", [P, Q, HEADS, 2, 32])
        rr = ph.sb("rr", [P, Q * HEADS, 2])
        oh = ph.sb("oh", [P, Q * HEADS, HV])
        o2 = ph.sb("o2", [P, Q * HEADS, HV])
        ms = ph.sb("ms", [P, Q * HEADS])
        oT = ph.sb("oT", [P, KD, S])
        so = ph.sb("so", [P, Q, DM])
        qk_in = [ph.counter("qk_in0"), ph.counter("qk_in1")]
        max_in = [ph.counter("max_in0"), ph.counter("max_in1")]
        (v_in, v_ready, stored, max_split, max_remainder, tile_made, tile_read, maxT_made, maxT_done, logit_made, prob_made,
         mixed, mixed_read, turned_made, turned_read, sums_read, squares_made, mean_made, root_made, scale_made,
         scaled) = (ph.counter(n) for n in (
             "v_in", "v_ready", "stored", "max_split", "max_remainder", "tile_made", "tile_read", "maxT_made", "maxT_done",
             "logit_made", "prob_made", "mixed", "mixed_read", "turned_made", "turned_read", "sums_read", "squares_made",
             "mean_made", "root_made", "scale_made", "scaled"))

        run = min(count, RUN)
        groups, units, pairs = run * NG, run * UNITS, run * HEADS // 2
        GATHERS = 2 * 2 * len(PRODUCTS)

        PAIR_AT = 12
        SQUARES, OT_AT, PROJ_AT = 6, 11, 14
        last_pair = [LAG + PAIR_AT + 8 * (8 * n + 7) for n in range(run)]
        steps = last_pair[-1] + PROJ_AT + 1

        def tiles(s):
            out = [("score", k // (2 * UNITS), k % (2 * UNITS)) for k in (2 * s, 2 * s + 1) if k < 2 * units]
            for n in range(run):
                if s == last_pair[n] + OT_AT:
                    out += [("oT", n, 0), ("oT", n, 1)]
                if s == last_pair[n] + PROJ_AT:
                    out += [("proj", n, 0), ("proj", n, 1)]
            return out

        def tiles_until(step):
            return sum(len(tiles(s)) for s in range(step + 1))

        def unit(u):
            n, r = u // UNITS, u % UNITS
            return n, 2 * (r // (2 * Q)) + r % 2, r // 2 % Q

        def pair_at(s):
            u = s - LAG - PAIR_AT
            return u // 8 if u >= 0 and u % 8 == 0 and u // 8 < pairs else None

        def group_at(s):
            return s // GSTEPS - 1 if s % GSTEPS == 1 and s > 1 and s // GSTEPS <= groups else None

        def groups_before(p):
            return sum(1 for g in range(groups) if GSTEPS * (g + 1) + 1 <= LAG + PAIR_AT + 8 * p)

        def pairs_before(g):
            return sum(1 for p in range(pairs) if LAG + PAIR_AT + 8 * p < GSTEPS * (g + 1) + 1)

        with nc.Fori(0, count // run) as trip:
            b, at_sums = trip * run, {}
            with nc.Block() as block:
                def store(sp, n):
                    sp.wait_ge(tile_read.sem, tiles_until(last_pair[n] + PROJ_AT))
                    stored(sp.dma_start(d["s1"][b + n].rearrange("(q p) e -> p q e", p=P), so[:, :, :]), 16)

                @block.sync
                def _(sp):
                    for n in range(run):
                        if n >= 2:
                            sp.wait_ge(prob_made.sem, UNITS * (n - 1))
                        slot = n % 2
                        for half in range(2):
                            for r, pair in enumerate(PRODUCTS):
                                row = KROWS * half + HD * r
                                for side, dst, part in ((0, qs[:, slot], pair[1]), (1, ks[:, slot, half], pair[0])):
                                    src = d["qk_parts"][b + n, side, part].rearrange("(h c r) n -> c r h n", c=2, r=HD)[half]
                                    qk_in[slot](sp.dma_start(dst[row:row + HD], src), 16)
                        if n >= 1:
                            sp.wait_ge(v_ready.sem, n)
                        v_in(sp.dma_start(vin[:, :, :], d["v1"][b + n].rearrange("(q p) e -> p q e", p=P)), 16)
                        if n >= 2:
                            store(sp, n - 2)
                    for n in range(max(0, run - 2), run):
                        store(sp, n)
                    sp.wait_ge(stored.sem, 16 * run)

                @block.tensor
                def _(pe):
                    made = 0

                    def tile(kind, n, k):
                        nonlocal made
                        bank, slot = made % 2, n % 2
                        if made >= 2:
                            pe.wait_ge(tile_read.sem, made - 1)
                        if kind == "score":
                            if k == 0:
                                pe.wait_ge(qk_in[slot].sem, 16 * GATHERS * (n // 2 + 1))
                            hc, m = k // Q, k % Q
                            last = nc.tensor.matmul(ps[:, bank, :], qs[0:SROWS, slot, hc // 2, m * P:(m + 1) * P],
                                                    ks[0:SROWS, slot, hc % 2, hc // 2, :], start=True, stop=True)
                        elif kind == "oT":
                            pe.wait_ge(scaled.sem, 2 * (n + 1))
                            oq = oh[:, :, :].rearrange("p (q h) e -> p q (h e)", q=Q)
                            for q in range(Q):
                                last = nc.tensor.transpose(ps[:, bank, q * P:(q + 1) * P], oq[:, q, k * P:(k + 1) * P], ident[:, :])
                        else:
                            pe.wait_ge(tile_read.sem, tiles_until(last_pair[n] + OT_AT))
                            for q in (2 * k, 2 * k + 1):
                                for kk in range(KD):
                                    last = nc.tensor.matmul(ps[:, bank, q % 2 * DM:(q % 2 + 1) * DM], oT[:, kk, q * P:(q + 1) * P],
                                                            w_proj[:, kk, :], start=kk == 0, stop=kk == KD - 1)
                        tile_made(last)
                        made += 1

                    def turn_max(g):
                        pe.wait_ge(max_split.sem, 3 * (g + 1))
                        if pairs_before(g):
                            pe.wait_ge(turned_read.sem, pairs_before(g))
                        if g:
                            pe.wait_ge(maxT_done.sem, g)
                        psb = ps[:, 7, :].bitcast(BF16)
                        for m in range(Q):
                            last = nc.tensor.transpose(psb[0:2 * SPLIT * GH, m * P:(m + 1) * P],
                                                       mparts[:, g % 2, m, :, :, :].rearrange("p a b c -> p (a b c)"),
                                                       identb[:, :])
                        maxT_made(last)

                    def logits(u):
                        n, head, m = unit(u)
                        if u % (GH * Q) == 0:
                            g = u // (GH * Q)
                            pe.wait_ge(max_in[g % 2].sem, 32 * (g // 2 + 1))
                        if u >= 2:
                            pe.wait_ge(prob_made.sem, u - 1)
                        for half in range(2):
                            last = nc.tensor.matmul(ps[:, 2 + 2 * (u % 2) + half, :], ks[:, n % 2, half, head, m * P:(m + 1) * P],
                                                    qs[:, n % 2, head, :], start=True, stop=True)
                        logit_made(last)

                    def mix(w):
                        m = w % Q
                        pe.wait_ge(prob_made.sem, 2 * w + 2)
                        if m == 0 and w >= Q:
                            pe.wait_ge(mixed_read.sem, w // Q)
                        if 2 * w % UNITS == 0:
                            pe.wait_ge(v_ready.sem, 2 * w // UNITS + 1)
                        for i in range(2):
                            n, head, _ = unit(2 * w + i)
                            for half in range(2):
                                row = 32 * (2 * i + half)
                                last = nc.tensor.matmul(ps[row:row + 32, 6, :], v1[:, n % 2, m, head, :],
                                                        pT[:, (2 * w + i) % RING, half, :], start=m == 0, stop=m == Q - 1,
                                                        skip_group_check=True)
                        mixed(last)

                    def turn_pair(p):
                        pe.wait_ge(mixed_read.sem, p + 1)
                        if p >= 1:
                            pe.wait_ge(turned_read.sem, p)
                        pe.wait_ge(maxT_done.sem, groups_before(p))
                        for q in range(Q):
                            last = nc.tensor.transpose(ps[:, 7, q * P:(q + 1) * P], ao[:, p % 2, q * P:(q + 1) * P], ident[:, :])
                        turned_made(last)

                    for s in range(steps):
                        for t in tiles(s)[:1]:
                            tile(*t)
                        if group_at(s) is not None:
                            turn_max(group_at(s))
                        u = s - LAG
                        if 0 <= u < units:
                            logits(u)
                        for t in tiles(s)[1:]:
                            tile(*t)
                        if u >= 3 and (u - 3) % 2 == 0 and (u - 3) // 2 < units // 2:
                            mix((u - 3) // 2)
                        if pair_at(s) is not None:
                            turn_pair(pair_at(s))

                @block.scalar
                def _(act):
                    for s in range(steps):
                        g = group_at(s - 1)
                        if g is not None:
                            act.wait_ge(maxT_done.sem, g + 1)
                            slot, heads = g // NG % 2, slice(GH * (g % NG), GH * (g % NG + 1))
                            for half in range(2):
                                row, n = SROWS + SPLIT * half, SPLIT * GH
                                max_in[g % 2](act.dma_start(qs[row:row + SPLIT, slot, heads, :],
                                                            mT[n * half:n * (half + 1), g % 2, :]), 16)
                        u = s - LAG
                        if 0 <= u < units:
                            act.wait_ge(logit_made.sem, u + 1)
                            if u >= RING:
                                act.wait_ge(mixed.sem, (u - RING) // 2 + 1)
                            b0 = 2 + 2 * (u % 2)
                            prob_made(nc.scalar.activation(pT[:, u % RING, :, :], ps[:, b0:b0 + 2, :], ACT.Exp, scale=HD ** -0.5))
                        if u >= 10 and (u - 10) % 8 == 0 and (u - 10) // 8 < pairs:
                            p = (u - 10) // 8
                            act.wait_ge(mixed.sem, Q * (p + 1))
                            if p >= 2:
                                act.wait_ge(turned_made.sem, p - 1)
                            mixed_read(nc.scalar.copy(ao[:, p % 2, :], ps[:, 6, :]))
                        for n in range(run):
                            if s == last_pair[n] + SQUARES + 1:
                                act.wait_ge(mean_made.sem, 2 * (n + 1))
                                root_made(nc.scalar.activation(ms[:, :], ms[:, :], ACT.Sqrt))

                @block.vector
                def _(dve):
                    read = 0

                    def tile(kind, n, k):
                        nonlocal read
                        bank = read % 2
                        dve.wait_ge(tile_made.sem, read + 1)
                        if kind == "score":
                            hc, m = k // Q, k % Q
                            head, half, g = hc // 2, hc % 2, NG * n + hc // 2 // GH
                            tile_read(nc.vector.tensor_reduce(mx[:, g % 2, m, half, head % GH:head % GH + 1], ps[:, bank, :],
                                                              AX.X, ALU.max, negate=True))
                        elif kind == "oT":
                            tile_read(nc.vector.tensor_copy(oT[:, k, :], ps[:, bank, :]))
                        else:
                            if n and k == 0:
                                dve.wait_ge(stored.sem, 16 * n)
                            tile_read(nc.vector.tensor_tensor(
                                so[:, 2 * k:2 * k + 2, :], ps[:, bank, :].rearrange("p (q e) -> p q e", q=2),
                                b_proj[:, :].unsqueeze(1).broadcast_to([P, 2, DM]), ALU.add))
                        read += 1

                    def split_max(g):
                        m, r = mx[:, g % 2], mrem[:, g % 2]
                        hi, mid, lo = (mparts[:, g % 2, :, :, i, :] for i in range(SPLIT))
                        dve.wait_ge(tile_read.sem, read)
                        link(dve, max_split, nc.vector.tensor_copy(hi, m))
                        link(dve, max_remainder, nc.vector.tensor_tensor(r, m, hi, ALU.subtract))
                        link(dve, max_split, nc.vector.tensor_copy(mid, r))
                        max_split(nc.vector.tensor_tensor(lo, r, mid, ALU.subtract))

                    def store_max(g):
                        dve.wait_ge(maxT_made.sem, g + 1)
                        if g >= 2:
                            dve.wait_ge(max_in[g % 2].sem, 32 * (g // 2))
                        psb = ps[:, 7, :].bitcast(BF16)
                        maxT_done(nc.vector.tensor_copy(mT[:, g % 2, :], psb[0:2 * SPLIT * GH, 0:S]))

                    def turned(p):
                        dve.wait_ge(turned_made.sem, p + 1)
                        n = p // (HEADS // 2)
                        if n and p % (HEADS // 2) == 0:
                            dve.wait_ge(sums_read.sem, 2 * n)
                        h = 2 * (p % (HEADS // 2))
                        turned_read(nc.vector.tensor_copy(
                            ot[:, :, h:h + 2, :, :].rearrange("p q h c e -> p q (h c e)"),
                            ps[:, 7, :].rearrange("p (q r) -> p q r", q=Q)))

                    for s in range(steps):
                        for t in tiles(s):
                            tile(*t)
                        if s % GSTEPS == GSTEPS - 1 and s < units:
                            split_max(s // GSTEPS)
                        if group_at(s) is not None:
                            store_max(group_at(s))
                        if pair_at(s) is not None:
                            turned(pair_at(s))
                        for n in range(run):
                            if s == last_pair[n]:
                                dve.wait_ge(turned_read.sem, (n + 1) * HEADS // 2)
                                link(dve, V, nc.vector.reciprocal(
                                    rr[:, :, :], ot[:, :, :, :, HV].rearrange("p q h c -> p (q h) c")))
                                at_sums[n] = V(nc.vector.tensor_scalar(rr[:, :, 1], rr[:, :, 1], lam[:, 0:1], None, ALU.mult))
                            if s == last_pair[n] + SQUARES:
                                dve.wait_ge(squares_made.sem, 2 * (n + 1))
                                link(dve, mean_made, nc.vector.tensor_reduce(ms[:, :], o2[:, :, :], AX.X, ALU.add))
                                mean_made(nc.vector.tensor_scalar(ms[:, :], ms[:, :], 1.0 / HV, EPS, ALU.mult, ALU.add))
                            if s == last_pair[n] + SQUARES + 1:
                                dve.wait_ge(root_made.sem, n + 1)
                                scale_made(nc.vector.reciprocal(ms[:, :], ms[:, :]))

                @block.gpsimd
                def _(pool):
                    def values(n):
                        pool.wait_ge(v_in.sem, 16 * (n + 1))
                        if n >= 2:
                            pool.wait_ge(mixed.sem, UNITS // 2 * (n - 1))
                        v_ready(nc.gpsimd.tensor_copy(v1[:, n % 2, :, :, 0:HV], vin[:, :, :].rearrange("p q (h e) -> p q h e", h=HEADS)))

                    def finish(n):
                        o5 = ot[:, :, :, :, :].rearrange("p q h c e -> p (q h) c e")
                        bc = [P, Q * HEADS, HV]
                        pool.wait_ge(V.sem, at_sums[n])
                        if n:
                            pool.wait_ge(tile_read.sem, tiles_until(last_pair[n - 1] + OT_AT))
                        link(pool, sums_read, nc.gpsimd.tensor_tensor(
                            oh[:, :, :], o5[:, :, 0, 0:HV], rr[:, :, 0:1].broadcast_to(bc), ALU.mult))
                        link(pool, sums_read, nc.gpsimd.tensor_tensor(
                            o2[:, :, :], o5[:, :, 1, 0:HV], rr[:, :, 1:2].broadcast_to(bc), ALU.mult))
                        link(pool, squares_made, nc.gpsimd.tensor_tensor(oh[:, :, :], oh[:, :, :], o2[:, :, :], ALU.subtract))
                        squares_made(nc.gpsimd.tensor_tensor(o2[:, :, :], oh[:, :, :], oh[:, :, :], ALU.mult))
                        pool.wait_ge(scale_made.sem, n + 1)
                        link(pool, scaled, nc.gpsimd.tensor_tensor(
                            oh[:, :, :], oh[:, :, :], ms[:, :].unsqueeze(2).broadcast_to(bc), ALU.mult))
                        link(pool, scaled, nc.gpsimd.tensor_tensor(
                            oh[:, :, :], oh[:, :, :], w_sub[:, :].unsqueeze(1).broadcast_to(bc), ALU.mult))

                    values(0)
                    if run > 1:
                        values(1)
                    for n in range(run):
                        finish(n)
                        if n + 2 < run:
                            values(n + 2)
            ph.clear()


E1, H1 = 8, 4 * DM
HK1 = H1 // P
MB = B // E1


def phase_c2(nc, c, d, count=E1):
    with ExitStack() as ctx:
        ph = Phase(nc, ctx, "c2")
        ps = ph.psum()
        ident = c["ident"]
        w_attn = ph.sb("w_attn", [P, KD, DM])
        w_next = ph.sb("w_next", [P, KD, DM])
        b_next = ph.sb("b_next", [P, DM])
        cols = {n: ph.sb(n, [P, KD]) for n in ("ln_scale", "ln_bias", "attn_b")}
        load_once(nc, ph, [
            (w_attn[:, :, :], d["attn_w"].rearrange("(k p) e -> p k e", p=P)),
            (w_next[:, :, :], d["next_w"].rearrange("(k p) e -> p k e", p=P)),
            (b_next[:, :], d["next_b"].partition_broadcast(P)),
        ] + [(t[:, :], d[n]) for n, t in cols.items()])
        V, A, T = (ph.counter(n) for n in ("vector_done", "scalar_done", "tensor_done"))
        w1 = ph.sb("w1", [P, KD, H1])
        w2 = ph.sb("w2", [P, HK1, DM])
        b1 = ph.sb("b1", [P, HK1])
        b2 = ph.sb("b2", [P, KD])
        nm = Norm(ph, "ln")
        f = ph.sb("f", [P, MB, Q, DM])
        z = ph.sb("z", [P, MB, Q, DM])
        fT = ph.sb("fT", [P, MB, KD, S])
        zT = ph.sb("zT", [P, MB, KD, S])
        hT = ph.sb("hT", [P, HK1, S])
        eT = ph.sb("eT", [P, KD, S])
        x1 = ph.sb("x1", [P, MB, Q, DM])
        s1 = ph.sb("s1", [P, MB, Q, DM])
        g = ph.sb("g", [P, Q, DM])
        w_in, stored = ph.counter("w_in"), ph.counter("stored")
        f_in, x1_in, s1_in = ([ph.counter(f"{n}{i}") for i in range(MB)] for n in ("f_in", "x1_in", "s1_in"))
        hidden_made, hidden_done = ph.counter("hidden_made"), ph.counter("hidden_done")
        RH = 4
        with nc.Fori(0, count) as e:
            free, at = {}, {}
            with nc.Block() as block:
                @block.sync
                def _(sp):
                    tiles = lambda n, i: d[n][e + i * E1].rearrange("(q p) e -> p q e", p=P)
                    for i in range(MB):
                        f_in[i](sp.dma_start(f[:, i, :, :], tiles("xn1", i)), 16)
                    w_in(sp.dma_start(w1[:, :, :], d["w1_1"][e].rearrange("(k p) h -> p k h", p=P)), 16)
                    w_in(sp.dma_start(w2[:, :, :], d["w2_1"][e].rearrange("(k p) h -> p k h", p=P)), 16)
                    w_in(sp.dma_start(b1[:, :], d["b1_1"][e]), 16)
                    w_in(sp.dma_start(b2[:, :], d["b2_1"][e]), 16)
                    for i in range(MB):
                        x1_in[i](sp.dma_start(x1[:, i, :, :], tiles("x1", i)), 16)
                        s1_in[i](sp.dma_start(s1[:, i, :, :], tiles("s1", i)), 16)

                for i in range(MB):
                    n = layer_norm(nc, block, nm, f[:, i, :, :], z[:, i, :, :], V, A, (f_in[i].sem, 16))
                    at["fT", i] = transpose_rows(nc, block, ps, [0, 1], ident, f[:, i, :, :], fT[:, i, :, :], T, A,
                                                 (f_in[i].sem, 16), free, eng="scalar")

                    @block.tensor
                    def _(pe):
                        pe.wait_ge(V.sem, n)
                        for k in range(KD):
                            if 2 + k in free:
                                pe.wait_ge(*free[2 + k])
                            for q in range(Q):
                                last = nc.tensor.transpose(ps[:, 2 + k, q * P:(q + 1) * P], z[:, i, q, k * P:(k + 1) * P],
                                                           ident[:, :])
                            T(last)
                        at["zT_ps"] = T.n

                    @block.vector
                    def _(dve):
                        for k in range(KD):
                            dve.wait_ge(T.sem, at["zT_ps"] - 1 + k)
                            V(nc.vector.tensor_scalar(zT[:, i, k, :], ps[:, 2 + k, :], cols["ln_scale"][:, k:k + 1],
                                                      cols["ln_bias"][:, k:k + 1], ALU.mult, ALU.add))
                            free[2 + k] = (V.sem, V.n)
                        at["zT", i] = V.n

                for i in range(MB):
                    @block.tensor
                    def _(pe):
                        pe.wait_ge(V.sem, at["zT", i])
                        for e2 in range(KD):
                            pe.wait_ge(*free[e2 + 2 * i])
                            for k in range(KD):
                                last = nc.tensor.matmul(ps[:, e2 + 2 * i, :], w_attn[:, k, e2 * P:(e2 + 1) * P], zT[:, i, k, :],
                                                        start=k == 0, stop=k == KD - 1)
                            T(last)
                        at["xa_ps"] = T.n

                    @block.vector
                    def _(dve):
                        dve.wait_ge(*at["fT", i])
                        for e2 in range(KD):
                            dve.wait_ge(T.sem, at["xa_ps"] - 1 + e2)
                            V(nc.vector.scalar_tensor_tensor(fT[:, i, e2, :], ps[:, e2 + 2 * i, :], cols["attn_b"][:, e2:e2 + 1],
                                                             fT[:, i, e2, :], ALU.add, ALU.add))
                            free[e2 + 2 * i] = (V.sem, V.n)
                        at["xa", i] = V.n

                for i in range(MB):
                    @block.tensor
                    def _(pe):
                        pe.wait_ge(V.sem, at["xa", i])
                        if i == 0:
                            pe.wait_ge(w_in.sem, 64)
                        for h in range(HK1):
                            n = i * HK1 + h
                            if n >= RH:
                                pe.wait_ge(hidden_done.sem, n - RH + 1)
                            for k in range(KD):
                                last = nc.tensor.matmul(ps[:, 4 + n % RH, :], w1[:, k, h * P:(h + 1) * P], fT[:, i, k, :],
                                                        start=k == 0, stop=k == KD - 1)
                            hidden_made(last)
                        for e2 in range(KD):
                            pe.wait_ge(*free[e2])
                            for h in range(HK1):
                                pe.wait_ge(hidden_done.sem, i * HK1 + h + 1)
                                last = nc.tensor.matmul(ps[:, e2, :], w2[:, h, e2 * P:(e2 + 1) * P], hT[:, h, :],
                                                        start=h == 0, stop=h == HK1 - 1)
                            T(last)
                        at["eT_ps"] = T.n

                    @block.scalar
                    def _(act):
                        if i:
                            act.wait_ge(T.sem, at["hT_read"])
                        else:
                            act.wait_ge(w_in.sem, 64)
                        for h in range(HK1):
                            n = i * HK1 + h
                            act.wait_ge(hidden_made.sem, n + 1)
                            hidden_done(nc.scalar.activation(hT[:, h, :], ps[:, 4 + n % RH, :], ACT.Gelu, bias=b1[:, h:h + 1]))
                    at["hT_read"] = at["eT_ps"]

                    @block.vector
                    def _(dve):
                        if i == 0:
                            dve.wait_ge(w_in.sem, 64)
                        else:
                            dve.wait_ge(T.sem, at["out_ps"])
                        for e2 in range(KD):
                            dve.wait_ge(T.sem, at["eT_ps"] - 1 + e2)
                            V(nc.vector.tensor_scalar(eT[:, e2, :], ps[:, e2, :], b2[:, e2:e2 + 1], None, ALU.add))
                            free[e2] = (V.sem, V.n)
                        at["eT"] = V.n

                    @block.tensor
                    def _(pe):
                        pe.wait_ge(V.sem, at["eT"])
                        pe.wait_ge(*free[2])
                        pe.wait_ge(*free[3])
                        for q in range(Q):
                            for k in range(KD):
                                last = nc.tensor.matmul(ps[:, 2 + q // 2, q % 2 * DM:(q % 2 + 1) * DM],
                                                        eT[:, k, q * P:(q + 1) * P], w_next[:, k, :], start=k == 0, stop=k == KD - 1)
                        at["out_ps"] = T(last)

                    @block.vector
                    def _(dve):
                        dve.wait_ge(T.sem, at["out_ps"])
                        if i:
                            dve.wait_ge(V.sem, at["x2"])
                        at["g"] = V(nc.vector.tensor_tensor(
                            g[:, :, :], ps[:, 2:4, :].rearrange("p a (q e) -> p (a q) e", q=2),
                            b_next[:, :].unsqueeze(1).broadcast_to([P, Q, DM]), ALU.add))
                        free[2] = free[3] = (V.sem, V.n)

                    @block.scalar
                    def _(act):
                        act.wait_ge(V.sem, at["g"])
                        link(act, A, nc.scalar.activation(g[:, :, :], g[:, :, :], ACT.Gelu))
                        at["sg"] = A(nc.scalar.activation(g[:, :, :], g[:, :, :], ACT.Silu))

                    @block.vector
                    def _(dve):
                        dve.wait_ge(A.sem, at["sg"])
                        dve.wait_ge(s1_in[i].sem, 16)
                        dve.wait_ge(x1_in[i].sem, 16)
                        link(dve, V, nc.vector.tensor_tensor(s1[:, i, :, :], s1[:, i, :, :], g[:, :, :], ALU.mult))
                        at["x2"] = V(nc.vector.tensor_tensor(x1[:, i, :, :], x1[:, i, :, :], s1[:, i, :, :], ALU.add))

                    @block.sync
                    def _(sp):
                        sp.wait_ge(V.sem, at["x2"])
                        stored(sp.dma_start(d["x2"][e + i * E1].rearrange("(q p) e -> p q e", p=P), x1[:, i, :, :]), 16)
                        if i == MB - 1:
                            sp.wait_ge(stored.sem, 16 * MB)
            ph.clear()


HEADS2 = 16
E2, I2, SI2 = 8, 128, 512
GROUPS, TOPK2, SCALE2 = 2, 2, 2.5
GE = E2 // GROUPS
SB2 = SI2 // P
TINY = 2.0 ** -100
LAG_C3, PASS_C3 = 10, 4
KP2 = 96


def phase_c3(nc, c, d, count=B):
    with ExitStack() as ctx:
        ph = Phase(nc, ctx, "c3")
        ps = ph.psum()
        ident, ones, upto = c["ident"], c["ones"], c["upto"]
        wv, wo = ph.sb("wv", [P, KD, DM]), ph.sb("wo", [P, KD, DM])
        bv, bo = ph.sb("bv", [P, DM]), ph.sb("bo", [P, DM])
        w3, bias3 = ph.sb("w3", [P, KD, 3]), ph.sb("b3", [P, 3])
        w3r = ph.sb("w3r", [P, KD, 3, P])
        gw, gb = ph.sb("gw", [P, KD, E2]), ph.sb("gb", [P, E2])
        up = ph.sb("up", [P, KD, E2 * I2])
        down = ph.sb("down", [P, E2, DM])
        sup = ph.sb("sup", [P, KD, SI2])
        sdown = ph.sb("sdown", [P, SB2, DM])
        pick = ph.sb("pick", [KP2, E2, P], BF16)
        early = ph.sb("early", [P, E2, E2])
        rows = lambda n: d[n].rearrange("(k p) e -> p k e", p=P)
        load_once(nc, ph, [
            (wv[:, :, :], rows("wv")), (wo[:, :, :], rows("wo")),
            (bv[:, :], d["bv"].partition_broadcast(P)), (bo[:, :], d["bo"].partition_broadcast(P)),
            (w3[:, :, :], rows("w3d")), (bias3[:, :], d["b3d"].partition_broadcast(P)),
            (gw[:, :, :], rows("gate_w2")), (gb[:, :], d["gate_b2"].partition_broadcast(P)),
            (up[:, :, :], rows("up2")), (down[:, :, :], d["down2"]),
            (sup[:, :, :], rows("sup2")), (sdown[:, :, :], rows("sdown2")),
        ])
        identb = ph.sb("identb", [P, P], BF16)
        V, A, T, G = (ph.counter(n) for n in ("vector_done", "scalar_done", "tensor_done", "pool_done"))
        padded = []

        def sequence(job):
            i, j = job.slot, job.j
            x = ph.sb(f"x_{i}", [P, Q, DM])
            xn = ph.sb(f"xn_{i}", [P, Q, DM])
            xnT = ph.sb(f"xnT_{i}", [P, KD, S])
            nm = Norm(ph, f"ln_{i}")
            v = ph.sb(f"v_{i}", [P, Q, DM])
            pb = ph.sb(f"pb_{i}", [P, 3, S])
            npk = ph.sb(f"npk_{i}", [P, Q, 3])
            sq = ph.sb(f"sq_{i}", [P, 3, S])
            pr = ph.sb(f"pr_{i}", [P, Q, S])
            rs = ph.sb(f"rs_{i}", [P, S])
            oT = ph.sb(f"oT_{i}", [P, KD, S])
            so = xn
            sc = ph.sb(f"sc_{i}", [P, Q, E2])
            sf = ph.sb(f"sf_{i}", [P, Q, E2])
            hi2, lo2 = ph.sb(f"hi2_{i}", [P, Q * GROUPS, 2]), ph.sb(f"lo2_{i}", [P, Q * GROUPS, 2])
            t2 = ph.sb(f"t2_{i}", [P, Q * GROUPS, 4])
            gm = ph.sb(f"gm_{i}", [P, Q, GROUPS])
            cwp = ph.sb(f"cwp_{i}", [P, Q, KP2], BF16)
            cmp, eq = ph.sb(f"cmp_{i}", [P, Q, E2 * E2]), ph.sb(f"eq_{i}", [P, Q, E2 * E2])
            rank = ph.sb(f"rank_{i}", [P, Q, E2])
            den = ph.sb(f"den_{i}", [P, Q])
            cw = ph.sb(f"cw_{i}", [P, Q, E2])
            cwT = ph.sb(f"cwT_{i}", [KP2, S], BF16)
            cwr = ph.sb(f"cwr_{i}", [P, Q, E2])
            r = ph.sb(f"r_{i}", [P, 2, S])
            r2 = ph.sb(f"r2_{i}", [P, E2 + SB2, S])
            g = v
            (x_in, stored, sq_made, sq_read, up_made, relu_made, squared, weighted) = (ph.counter(f"{n}{j}") for n in (
                "x_in", "stored", "sq_made", "sq_read", "up_made", "relu_made", "squared", "weighted"))
            if j == i:
                padded.append(cwp)
            yield
            block, b = job.block, job.b
            free, at = {}, {}
            b0, b1, b2, b3 = range(4 * i, 4 * i + 4)
            job.wait_for_buffers(block.sync)

            @block.sync
            def _(sp):
                x_in(sp.dma_start(x[:, :, :], d["x2"][b].rearrange("(q p) e -> p q e", p=P)), 16)

            yield
            job.wait_for_buffers(block.tensor, block.scalar, block.vector)
            n = layer_norm(nc, block, nm, x, xn, V, A, (x_in.sem, 16))
            yield
            at["xnT"] = transpose_rows(nc, block, ps, [b0, b1], ident, xn, xnT, T, V, (V.sem, n), free)

            yield

            pbank = (b3, b0, b1)
            @block.tensor
            def _(pe):
                pe.wait_ge(*at["xnT"])
                for q in range(Q):
                    for k in range(KD):
                        nc.tensor.matmul(ps[:, b2, q * 8:q * 8 + 8], xnT[:, k, q * P:(q + 1) * P], gw[:, k, :],
                                         start=k == 0, stop=k == KD - 1)
                    for k in range(KD):
                        last = nc.tensor.matmul(ps[:, b2, 64 + q * 4:64 + q * 4 + 3], xnT[:, k, q * P:(q + 1) * P], w3[:, k, :],
                                                start=k == 0, stop=k == KD - 1)
                at["pk"] = T(last)
                for r3 in range(3):
                    if r3:
                        pe.wait_ge(*free[pbank[r3]])
                    for k in range(KD):
                        last = nc.tensor.matmul(ps[:, pbank[r3], :], w3r[:, k, r3, :], xnT[:, k, :], start=k == 0, stop=k == KD - 1)
                    T(last)
                at["pb"] = T.n

            @block.vector
            def _(dve):
                dve.wait_ge(T.sem, at["pk"])
                V(nc.vector.tensor_copy(sc[:, :, :], ps[:, b2, 0:Q * 8].rearrange("p (q e) -> p q e", q=Q)))
                at["sc_raw"] = V.n
                link(dve, V, nc.vector.tensor_tensor(npk[:, :, :], ps[:, b2, 64:64 + Q * 4].rearrange("p (q e) -> p q e", q=Q)[:, :, 0:3],
                                                     bias3[:, :].unsqueeze(1).broadcast_to([P, Q, 3]), ALU.add))
                free[b2] = (V.sem, V.n)
                V(nc.vector.tensor_scalar(npk[:, :, :], npk[:, :, :], -1.0, None, ALU.mult))
                for r3 in range(3):
                    dve.wait_ge(T.sem, at["pb"] - 2 + r3)
                    V(nc.vector.tensor_scalar(pb[:, r3, :], ps[:, pbank[r3], :], bias3[:, r3:r3 + 1], None, ALU.add))
                    free[pbank[r3]] = (V.sem, V.n)
                at["pb_sb"] = V.n

            yield

            @block.tensor
            def _(pe):
                for q in range(Q):
                    if q % 2 == 0:
                        pe.wait_ge(*free[b2 + q // 2])
                    for k in range(KD):
                        last = nc.tensor.matmul(ps[:, b2 + q // 2, q % 2 * DM:(q % 2 + 1) * DM], xnT[:, k, q * P:(q + 1) * P],
                                                wv[:, k, :], start=k == 0, stop=k == KD - 1)
                at["v"] = T(last)

            @block.scalar
            def _(act):
                act.wait_ge(V.sem, at["sc_raw"])
                at["sig"] = A(nc.scalar.activation(sc[:, :, :], sc[:, :, :], ACT.Sigmoid))
                act.wait_ge(V.sem, at["pb_sb"])
                for m in range(Q):
                    if m:
                        act.wait_ge(sq_read.sem, m)
                    for r3 in range(3):
                        sq_made(nc.scalar.activation(sq[:, r3, m * P:], pb[:, r3, m * P:], ACT.Square, bias=npk[:, m, r3:r3 + 1]))

            @block.vector
            def _(dve):
                for m in range(Q):
                    dve.wait_ge(sq_made.sem, 3 * m + 3)
                    link(dve, V, nc.vector.tensor_tensor(pr[:, m, m * P:], sq[:, 0, m * P:], sq[:, 1, m * P:], ALU.add))
                    k = sq_read(nc.vector.tensor_tensor(pr[:, m, m * P:], pr[:, m, m * P:], sq[:, 2, m * P:], ALU.add))
                    dve.wait_ge(sq_read.sem, k)
                    V(nc.vector.tensor_scalar(pr[:, m, m * P:], pr[:, m, m * P:], TINY, None, ALU.max))
                at["sq"] = V.n
                dve.wait_ge(T.sem, at["v"])
                V(nc.vector.tensor_tensor(
                    v[:, :, :], ps[:, b2:b2 + 2, :].rearrange("p a (q e) -> p (a q) e", q=2),
                    bv[:, :].unsqueeze(1).broadcast_to([P, Q, DM]), ALU.add))
                free[b2] = free[b3] = (V.sem, V.n)

            yield

            @block.scalar
            def _(act):
                act.wait_ge(V.sem, at["sq"])
                for m in range(Q):
                    A(nc.scalar.activation(pr[:, m, m * P:], pr[:, m, m * P:], ACT.Sqrt))
                act.wait_ge(A.sem, A.n)
                for m in range(Q):
                    A(nc.scalar.activation(pr[:, m, m * P:], pr[:, m, m * P:], ACT.Exp, scale=-1.0 / (DM // HEADS2) ** 0.5))
                at["exp"] = A.n

            yield

            @block.vector
            def _(dve):
                dve.wait_ge(A.sem, at["sig"])
                tt, mul = nc.vector.tensor_tensor, ALU.mult
                link(dve, V, tt(sf[:, :, :], sc[:, :, :], gb[:, :].unsqueeze(1).broadcast_to([P, Q, E2]), ALU.add))
                s4 = sf[:, :, :].rearrange("p q (g a b) -> p (q g) a b", g=GROUPS, a=2)
                V(tt(hi2[:, :, :], s4[:, :, :, 0], s4[:, :, :, 1], ALU.max))
                link(dve, V, tt(lo2[:, :, :], s4[:, :, :, 0], s4[:, :, :, 1], ALU.min))
                V(tt(t2[:, :, 0:1], hi2[:, :, 0:1], hi2[:, :, 1:2], ALU.max))
                V(tt(t2[:, :, 1:2], hi2[:, :, 0:1], hi2[:, :, 1:2], ALU.min))
                link(dve, V, tt(t2[:, :, 2:3], lo2[:, :, 0:1], lo2[:, :, 1:2], ALU.max))
                link(dve, V, tt(t2[:, :, 3:4], t2[:, :, 1:2], t2[:, :, 2:3], ALU.max))
                link(dve, V, tt(t2[:, :, 1:2], t2[:, :, 0:1], t2[:, :, 3:4], ALU.add))
                gs = t2[:, :, 1].rearrange("p (q g) -> p q g", g=GROUPS)
                V(tt(gm[:, :, 1:2], gs[:, :, 1:2], gs[:, :, 0:1], ALU.is_gt))
                link(dve, V, tt(gm[:, :, 0:1], gs[:, :, 1:2], gs[:, :, 0:1], ALU.is_le))
                sg = sf[:, :, :].rearrange("p q (g e) -> p (q g) e", g=GROUPS)
                link(dve, V, tt(sg, sg, gm[:, :, :].rearrange("p q g -> p (q g)").unsqueeze(2).broadcast_to([P, Q * GROUPS, GE]), mul))
                at["group"] = V.n

            yield

            @block.vector
            def _(dve):
                tt, mul = nc.vector.tensor_tensor, ALU.mult
                for q in range(Q):
                    mi = sf[:, q, :].unsqueeze(1).broadcast_to([P, E2, E2])
                    mj = sf[:, q, :].unsqueeze(2).broadcast_to([P, E2, E2])
                    V(tt(cmp[:, q, :].rearrange("p (j i) -> p j i", j=E2), mi, mj, ALU.is_gt))
                    V(tt(eq[:, q, :].rearrange("p (j i) -> p j i", j=E2), mi, mj, ALU.is_equal))
                dve.wait_ge(V.sem, V.n)
                link(dve, V, tt(eq[:, :, :], eq[:, :, :], early[:, :, :].rearrange("p j i -> p (j i)").unsqueeze(1).broadcast_to([P, Q, E2 * E2]), mul))
                link(dve, V, tt(cmp[:, :, :], cmp[:, :, :], eq[:, :, :], ALU.add))
                link(dve, V, nc.vector.tensor_reduce(rank[:, :, :], cmp[:, :, :].rearrange("p q (j i) -> p (q j) i", i=E2), AX.X, ALU.add))
                link(dve, V, nc.vector.scalar_tensor_tensor(cw[:, :, :], rank[:, :, :], float(TOPK2), sc[:, :, :], ALU.is_lt, mul))
                link(dve, V, nc.vector.tensor_reduce(den[:, :], cw[:, :, :], AX.X, ALU.add))
                link(dve, V, nc.vector.tensor_scalar(den[:, :], den[:, :], 1e-20, None, ALU.add))
                link(dve, V, nc.vector.reciprocal(den[:, :], den[:, :]))
                link(dve, V, tt(cw[:, :, :], cw[:, :, :], den[:, :].unsqueeze(2).broadcast_to([P, Q, E2]), mul))
                link(dve, V, nc.vector.tensor_scalar(cw[:, :, :], cw[:, :, :], SCALE2, None, mul))
                link(dve, V, nc.vector.tensor_copy(cwp[:, :, 0:E2], cw[:, :, :]))
                link(dve, V, tt(cwr[:, :, :], cw[:, :, :], cwp[:, :, 0:E2], ALU.subtract))
                link(dve, V, nc.vector.tensor_copy(cwp[:, :, 32:32 + E2], cwr[:, :, :]))
                at["cw"] = V(tt(cwp[:, :, 64:64 + E2], cwr[:, :, :], cwp[:, :, 32:32 + E2], ALU.subtract))

            yield

            @block.tensor
            def _(pe):
                pe.wait_ge(*free[b3])
                pe.wait_ge(V.sem, at["cw"])
                for q in range(Q):
                    last = nc.tensor.transpose(ps[0:KP2, b3, :].bitcast(BF16)[:, q * P:(q + 1) * P], cwp[:, q, :], identb[:, :])
                at["cwT"] = T(last)

            @block.vector
            def _(dve):
                dve.wait_ge(T.sem, at["cwT"])
                at["cwT_sb"] = V(nc.vector.tensor_copy(cwT[:, :], ps[0:KP2, b3, :].bitcast(BF16)[:, 0:S]))
                free[b3] = (V.sem, V.n)
                dve.wait_ge(A.sem, at["exp"])
                for m in range(Q):
                    V(nc.vector.tensor_tensor(pr[:, m, m * P:(m + 1) * P], pr[:, m, m * P:(m + 1) * P], upto[:, :], ALU.mult))
                at["pr"] = V.n

            yield

            @block.tensor
            def _(pe):
                pe.wait_ge(V.sem, at["pr"])
                for n, bank in enumerate((b0, b1, b2)):
                    pe.wait_ge(*free[bank])
                    for m in range(Q):
                        lhs = v[:, m, n * P:(n + 1) * P] if n < KD else ones[:, :]
                        last = nc.tensor.matmul(ps[:, bank, m * P:], lhs, pr[:, m, m * P:], start=m == 0, stop=m == Q - 1)
                at["mix"] = T(last)

            @block.vector
            def _(dve):
                dve.wait_ge(T.sem, at["mix"])
                link(dve, V, nc.vector.reciprocal(rs[:, :], ps[:, b2, :]))
                free[b2] = (V.sem, V.n)
                for k in range(KD):
                    V(nc.vector.tensor_tensor(oT[:, k, :], ps[:, b0 + k, :], rs[:, :], ALU.mult))
                    free[b0 + k] = (V.sem, V.n)
                at["oT"] = V.n

            yield

            @block.tensor
            def _(pe):
                pe.wait_ge(V.sem, at["oT"])
                for q in range(Q):
                    for k in range(KD):
                        last = nc.tensor.matmul(ps[:, b0 + q // 2, q % 2 * DM:(q % 2 + 1) * DM], oT[:, k, q * P:(q + 1) * P],
                                                wo[:, k, :], start=k == 0, stop=k == KD - 1)
                at["s2"] = T(last)

            @block.vector
            def _(dve):
                dve.wait_ge(T.sem, at["s2"])
                at["so"] = V(nc.vector.tensor_tensor(
                    so[:, :, :], ps[:, b0:b0 + 2, :].rearrange("p a (q e) -> p (a q) e", q=2),
                    bo[:, :].unsqueeze(1).broadcast_to([P, Q, DM]), ALU.add))
                free[b0] = free[b1] = (V.sem, V.n)

            N = E2 + SB2
            for e in range(N):
                if e % 2 == 0:
                    yield

                @block.tensor
                def _(pe):
                    if e < 2:
                        pe.wait_ge(V.sem, at["cwT_sb"])
                        pe.wait_ge(*free[b2 + e])
                    else:
                        pe.wait_ge(squared.sem, e - 1)
                    for k in range(KD):
                        w = up[:, k, e * P:(e + 1) * P] if e < E2 else sup[:, k, (e - E2) * P:(e - E2 + 1) * P]
                        last = nc.tensor.matmul(ps[:, b2 + e % 2, :], w, xnT[:, k, :], start=k == 0, stop=k == KD - 1)
                    if e < E2:
                        pe.wait_ge(*free[b0 + e % 2])
                        last = nc.tensor.matmul(ps[:, b0 + e % 2, :], pick[:, e, :], cwT[:, :], start=True, stop=True)
                    up_made(last)

                @block.scalar
                def _(act):
                    act.wait_ge(up_made.sem, e + 1)
                    if e >= 2:
                        act.wait_ge(squared.sem, e - 1)
                    relu_made(nc.scalar.activation(r[:, e % 2, :], ps[:, b2 + e % 2, :], ACT.Relu))

                @block.vector
                def _(dve):
                    dve.wait_ge(relu_made.sem, e + 1)
                    k = squared(nc.vector.tensor_tensor(r2[:, e, :], r[:, e % 2, :], r[:, e % 2, :], ALU.mult))
                    if e < E2:
                        dve.wait_ge(squared.sem, k)
                        k = weighted(nc.vector.tensor_tensor(r2[:, e, :], r2[:, e, :], ps[:, b0 + e % 2, :], ALU.mult))
                        free[b0 + e % 2] = (weighted.sem, k)

            for q in range(Q):
                yield

                @block.tensor
                def _(pe):
                    if q == 0:
                        pe.wait_ge(weighted.sem, E2)
                        pe.wait_ge(squared.sem, N)
                    for e in range(N):
                        w = down[:, e, :] if e < E2 else sdown[:, e - E2, :]
                        last = nc.tensor.matmul(ps[:, b0 + q // 2, q % 2 * DM:(q % 2 + 1) * DM], r2[:, e, q * P:(q + 1) * P], w,
                                                start=e == 0, stop=e == N - 1)
                    at["ffn"] = T(last)

            @block.scalar
            def _(act):
                act.wait_ge(T.sem, at["ffn"])
                at["g"] = A(nc.scalar.activation(g[:, :, :], ps[:, b0:b0 + 2, :], ACT.Silu))

            @block.vector
            def _(dve):
                dve.wait_ge(A.sem, at["g"])
                link(dve, V, nc.vector.tensor_tensor(g[:, :, :], g[:, :, :], so[:, :, :], ALU.mult))
                at["x3"] = V(nc.vector.tensor_tensor(x[:, :, :], x[:, :, :], g[:, :, :], ALU.add))

            @block.sync
            def _(sp):
                sp.wait_ge(V.sem, at["x3"])
                stored(sp.dma_start(d["x3"][b].rearrange("(q p) e -> p q e", p=P), x[:, :, :]), 16)
                sp.wait_ge(stored.sem, 16)
            job.done = [(c.sem, c.n) for c in (V, A, T, stored)]

        run = run_sequences(nc, ph, sequence, count, min(count, PASS_C3), LAG_C3)
        next(run)
        with nc.Block() as block:
            @block.gpsimd
            def _(pool):
                G(nc.gpsimd.memset(pick[:, :, :], 0.0))
                link(pool, G, nc.gpsimd.memset(early[:, :, :], 1.0))
                for part in range(3):
                    rows3 = pick[32 * part:32 * part + 32, :, :]
                    link(pool, G, nc.gpsimd.affine_select(out=rows3, in_=rows3, compare_op=ALU.not_equal, fill=1.0,
                                                          base=0, pattern=[[-1, E2], [0, P]], channel_multiplier=1))
                G(nc.gpsimd.affine_select(out=early[:, :, :], in_=early[:, :, :], compare_op=ALU.is_gt, fill=0.0,
                                          base=0, pattern=[[1, E2], [-1, E2]], channel_multiplier=0))

            @block.vector
            def _(dve):
                for cwp in padded:
                    V(nc.vector.memset(cwp[:, :, :], 0.0))
                V(nc.vector.tensor_copy(identb[:, :], ident[:, :]))
                V(nc.vector.tensor_copy(w3r[:, :, :, :], w3[:, :, :].unsqueeze(3).broadcast_to([P, KD, 3, P])))
        ph.clear()

        next(run, None)


NF = 64
E3, D3, RH3 = 16, 512, 128
CAP = math.ceil(S * 2.0 / E3)
DK3 = D3 // P
SLOTS_C4, LAG_C4 = 4, 3
SLOTS_E, LAG_E = 4, 2
ROUND = 1.5 * 2.0 ** 23


def phase_c4(nc, c, d, count=B):
    with ExitStack() as ctx:
        ph = Phase(nc, ctx, "c4")
        ps = ph.psum()
        ident = c["ident"]
        w_in = ph.sb("w_in", [P, KD, 2, 2 * NF])
        w_out = ph.sb("w_out", [P, 2, DM])
        rw1, rw2 = ph.sb("rw1", [P, KD, RH3]), ph.sb("rw2", [P, E3])
        col = ph.sb("col", [P, 16])
        omega, decay, turns, half, sh, ch, fix = (col[:, i:i + 1] for i in range(7))
        a_col, b_col = col[:, 7:8], col[:, 8:9]
        ld = []
        wi = d["W_in"].rearrange("(k p) e -> p k e", p=P)
        for i in range(2):
            for h in range(2):
                ld.append((w_in[:, :, i, h * NF:(h + 1) * NF], wi[:, :, (h ^ i) * NF:((h ^ i) + 1) * NF]))
                ld.append((w_out[h * NF:(h + 1) * NF, i, :], d["W_out"][(h ^ i) * NF:((h ^ i) + 1) * NF]))
        for h in range(2):
            ld.append((omega[h * NF:(h + 1) * NF], d["frequencies"].rearrange("(f o) -> f o", o=1)))
            ld.append((decay[h * NF:(h + 1) * NF], d["log_decay"].rearrange("(f o) -> f o", o=1)))
        ld += [(rw1[:, :, :], d["router_w1"].rearrange("(k p) e -> p k e", p=P)), (rw2[:, :], d["router_w2"])]
        load_once(nc, ph, ld)
        V, A, T = (ph.counter(n) for n in ("vector_done", "scalar_done", "tensor_done"))
        cs, sn = ph.sb("cs", [P, S + 1]), ph.sb("sn", [P, S + 1])
        tt = ph.sb("tt", [P, S])
        dk = ph.sb("dk", [P, S])
        at = {}

        with nc.Block() as block:
            @block.vector
            def _(dve):
                ts = lambda o, i, a, b, f, g: link(dve, V, nc.vector.tensor_scalar(o, i, a, b, f, g))
                ts(omega, omega, 0.1, None, ALU.mult, ALU.bypass)
                ts(turns, omega, 1 / (2 * math.pi), None, ALU.mult, ALU.bypass)
                ts(turns, turns, ROUND, None, ALU.add, ALU.bypass)
                ts(turns, turns, ROUND, None, ALU.subtract, ALU.bypass)
                for part in (6.28125, 2 * math.pi - 6.28125):
                    link(dve, V, nc.vector.scalar_tensor_tensor(omega, turns, -part, omega, ALU.mult, ALU.add))
                ts(half, omega, 0.5, None, ALU.mult, ALU.bypass)
                link(dve, V, nc.vector.scalar_tensor_tensor(ch, half, -1.0, half, ALU.mult, ALU.min))
                at["half"] = link(dve, V, nc.vector.tensor_scalar(ch, ch, math.pi / 2, 0.0, ALU.add, ALU.max))

            @block.scalar
            def _(act):
                act.wait_ge(V.sem, at["half"])
                A(nc.scalar.activation(sh, half, ACT.Sin))
                A(nc.scalar.activation(ch, ch, ACT.Sin))
                A(nc.scalar.activation(decay, decay, ACT.Sigmoid))

            @block.vector
            def _(dve):
                dve.wait_ge(A.sem, 3)
                st = nc.vector.scalar_tensor_tensor
                V(nc.vector.memset(cs[:, 0:1], 1.0))
                V(nc.vector.memset(sn[:, 0:1], 0.0))
                link(dve, V, nc.vector.memset(dk[:, :], 1.0))
                link(dve, V, nc.vector.tensor_scalar(dk[:, :], dk[:, :], decay, None, ALU.mult))
                link(dve, V, st(sn[:, 1:2], sh, 2.0, ch, ALU.mult, ALU.mult))
                link(dve, V, st(cs[:, 1:2], sh, -2.0, sh, ALU.mult, ALU.mult))
                link(dve, V, nc.vector.tensor_scalar(cs[:, 1:2], cs[:, 1:2], 1.0, None, ALU.add))
                link(dve, V, nc.vector.tensor_tensor(a_col, cs[:, 1:2], cs[:, 1:2], ALU.mult))
                link(dve, V, nc.vector.tensor_tensor(b_col, sn[:, 1:2], sn[:, 1:2], ALU.mult))
                link(dve, V, nc.vector.tensor_tensor(fix, a_col, b_col, ALU.add))
                link(dve, V, nc.vector.tensor_scalar(fix, fix, -0.5, 1.5, ALU.mult, ALU.add))
                link(dve, V, nc.vector.tensor_tensor(cs[:, 1:2], cs[:, 1:2], fix, ALU.mult))
                link(dve, V, nc.vector.tensor_tensor(sn[:, 1:2], sn[:, 1:2], fix, ALU.mult))
                n = 1
                while n < S:
                    ck, sk = cs[:, n:n + 1], sn[:, n:n + 1]
                    lo, hi = slice(1, n + 1), slice(n + 1, 2 * n + 1)
                    link(dve, V, nc.vector.tensor_scalar(tt[:, 0:n], sn[:, lo], sk, None, ALU.mult))
                    link(dve, V, st(cs[:, hi], cs[:, lo], ck, tt[:, 0:n], ALU.mult, ALU.subtract))
                    link(dve, V, nc.vector.tensor_scalar(tt[:, 0:n], cs[:, lo], sk, None, ALU.mult))
                    link(dve, V, st(sn[:, hi], sn[:, lo], ck, tt[:, 0:n], ALU.mult, ALU.add))
                    n *= 2
                link(dve, V, nc.vector.tensor_scalar(sn[NF:, :], sn[NF:, :], -1.0, None, ALU.mult))
        ph.clear()


        def sequence(job):
            i, j = job.slot, job.j
            x = ph.sb(f"x_{i}", [P, Q, DM])
            xn = ph.sb(f"xn_{i}", [P, Q, DM])
            xnT = ph.sb(f"xnT_{i}", [P, KD, S])
            nm = Norm(ph, f"ln_{i}")
            u, u2, gs = (ph.sb(f"{n}_{i}", [P, S]) for n in ("u", "u2", "gs"))
            f = ph.sb(f"f_{i}", [P, 2, S])
            so = ph.sb(f"so_{i}", [P, Q, DM])
            rT = ph.sb(f"rT_{i}", [RH3, S])
            pr = ph.sb(f"pr_{i}", [E3, S])
            g1 = ph.sb(f"g1_{i}", [E3, 4])
            x_in, stored = ph.counter(f"x_in{j}"), ph.counter(f"stored{j}")
            yield
            block, b = job.block, job.b
            free, at = {}, {}
            b0, b1 = 2 * i, 2 * i + 1
            job.wait_for_buffers(block.sync)

            @block.sync
            def _(sp):
                x_in(sp.dma_start(x[:, :, :], d["x3"][b].rearrange("(q p) e -> p q e", p=P)), 16)

            yield
            yield
            job.wait_for_buffers(block.tensor, block.scalar, block.vector)
            n = layer_norm(nc, block, nm, x, xn, V, A, (x_in.sem, 16))
            at["xn"] = n

            @block.sync
            def _(sp):
                sp.wait_ge(V.sem, at["xn"])
                stored(sp.dma_start(d["xn3"][b].rearrange("(q p) e -> p q e", p=P), xn[:, :, :]), 16)

            yield
            at["xnT"] = transpose_rows(nc, block, ps, [b0, b1], ident, xn, xnT, T, V, (V.sem, n), free)

            yield

            @block.tensor
            def _(pe):
                pe.wait_ge(*at["xnT"])
                for h in range(2):
                    for k in range(KD):
                        last = nc.tensor.matmul(ps[:, b0 + h, :], w_in[:, k, h, :], xnT[:, k, :], start=k == 0, stop=k == KD - 1)
                at["u"] = T(last)

            @block.vector
            def _(dve):
                dve.wait_ge(T.sem, at["u"])
                V(nc.vector.tensor_tensor(u[:, :], ps[:, b0, :], cs[:, 0:S], ALU.mult))
                link(dve, V, nc.vector.tensor_tensor(u2[:, :], ps[:, b1, :], sn[:, 0:S], ALU.mult))
                free[b0] = free[b1] = (V.sem, V.n)

            @block.gpsimd
            def _(pool):
                pool.wait_ge(*free[b1])
                at["usum"] = G(nc.gpsimd.tensor_tensor(u[:, :], u[:, :], u2[:, :], ALU.add))

            yield

            @block.tensor
            def _(pe):
                pe.wait_ge(*free[b0])
                for k in range(KD):
                    last = nc.tensor.matmul(ps[:, b0, :], rw1[:, k, :], xnT[:, k, :], start=k == 0, stop=k == KD - 1)
                at["r1"] = T(last)

            @block.scalar
            def _(act):
                act.wait_ge(T.sem, at["r1"])
                at["rT"] = A(nc.scalar.activation(rT[:, :], ps[:, b0, :], ACT.Silu))
                free[b0] = (A.sem, A.n)

            @block.vector
            def _(dve):
                dve.wait_ge(G.sem, at["usum"])
                at["gs"] = link(dve, V, nc.vector.tensor_tensor_scan(gs[:, :], dk[:, :], u[:, :], 0.0, ALU.mult, ALU.add))
                V(nc.vector.tensor_tensor(f[:, 0, :], gs[:, :], cs[:, 1:], ALU.mult))
                at["f"] = V(nc.vector.tensor_tensor(f[:, 1, :], gs[:, :], sn[:, 1:], ALU.mult))

            yield

            @block.tensor
            def _(pe):
                pe.wait_ge(A.sem, at["rT"])
                pe.wait_ge(*free[b1])
                at["lg"] = T(nc.tensor.matmul(ps[0:E3, b1, :], rw2[:, :], rT[:, :], start=True, stop=True))

            @block.vector
            def _(dve):
                dve.wait_ge(T.sem, at["lg"])
                at["max"] = V(nc.vector.tensor_reduce(g1[:, 0:1], ps[0:E3, b1, :], AX.X, ALU.max, negate=True))

            @block.scalar
            def _(act):
                act.wait_ge(V.sem, at["max"])
                at["exp"] = A(nc.scalar.activation(pr[:, :], ps[0:E3, b1, :], ACT.Exp, bias=g1[:, 0:1], accum_out=g1[:, 1:2]))
                free[b1] = (A.sem, A.n)

            yield

            @block.tensor
            def _(pe):
                pe.wait_ge(V.sem, at["f"])
                for q in range(Q):
                    if q % 2 == 0:
                        pe.wait_ge(*free[b0 + q // 2])
                    for h in range(2):
                        last = nc.tensor.matmul(ps[:, b0 + q // 2, q % 2 * DM:(q % 2 + 1) * DM], f[:, h, q * P:(q + 1) * P],
                                                w_out[:, h, :], start=h == 0, stop=h == 1)
                at["s3"] = T(last)

            @block.vector
            def _(dve):
                dve.wait_ge(A.sem, at["exp"])
                link(dve, V, nc.vector.reciprocal(g1[:, 2:3], g1[:, 1:2]))
                at["pr"] = V(nc.vector.tensor_scalar(pr[:, :], pr[:, :], g1[:, 2:3], None, ALU.mult))

            yield

            @block.scalar
            def _(act):
                act.wait_ge(T.sem, at["s3"])
                at["so"] = A(nc.scalar.copy(so[:, :, :], ps[:, b0:b0 + 2, :]))

            @block.sync
            def _(sp):
                sp.wait_ge(V.sem, at["pr"])
                stored(sp.dma_start(d["probs3"][b], pr[:, :]), 16)
                sp.wait_ge(A.sem, at["so"])
                stored(sp.dma_start(d["s3"][b].rearrange("(q p) e -> p q e", p=P), so[:, :, :]), 16)

            yield

            @block.sync
            def _(sp):
                sp.wait_ge(stored.sem, 48)
            job.done = [(c.sem, c.n) for c in (V, A, T, G, stored)]

        G = ph.counter("pool_done")
        loop = run_sequences(nc, ph, sequence, count, min(count, 8), LAG_C4, SLOTS_C4)
        next(loop)
        next(loop, None)


RB = P // E3


def phase_r(nc, c, d, keep):
    with ExitStack() as ctx:
        ph = Phase(nc, ctx, "r")
        ps = ph.psum()
        N = B // RB
        pr = ph.sb("pr", [P, N, S])
        val = ph.sb("val", [P, N, 2, CAP])
        ix = ph.sb("ix", [P, N, CAP], U32)
        ixf = ph.sb("ixf", [P, N, 2, CAP])
        sm = ph.sb("sm", [P, N])
        V, T, p_in = ph.counter("vector_done"), ph.counter("tensor_done"), ph.counter("probs_in")
        rows = d["probs3"].rearrange("b e s -> (b e) s")
        at = {}
        with nc.Block() as block:
            @block.sync
            def _(sp):
                p_in(sp.dma_start(pr[:, :, :], rows.rearrange("(n p) s -> p n s", p=P)), 16)

            @block.vector
            def _(dve):
                dve.wait_ge(p_in.sem, 16)
                for r in range(CAP // 8):
                    cut = slice(8 * r, 8 * r + 8)
                    for n in range(N):
                        V(nc.vector.max(val[:, n, 0, cut], pr[:, n, :]))
                    dve.wait_ge(V.sem, V.n)
                    for n in range(N):
                        V(nc.vector.max_index(ix[:, n, cut], val[:, n, 0, cut], pr[:, n, :]))
                    dve.wait_ge(V.sem, V.n)
                    if r < CAP // 8 - 1:
                        for n in range(N):
                            V(nc.vector.match_replace(pr[:, n, :], val[:, n, 0, cut], pr[:, n, :], -1.0))
                        dve.wait_ge(V.sem, V.n)
                V(nc.vector.tensor_reduce(sm[:, :], val[:, :, 0, :], AX.X, ALU.add))
                for h in range(2):
                    V(nc.vector.tensor_copy(ixf[:, :, h, :], ix[:, :, :]))
                dve.wait_ge(V.sem, V.n)
                link(dve, V, nc.vector.tensor_scalar(sm[:, :], sm[:, :], 1e-9, None, ALU.add))
                link(dve, V, nc.vector.reciprocal(sm[:, :], sm[:, :]))
                for n in range(N):
                    V(nc.vector.tensor_scalar(val[:, n, 0, :], val[:, n, 0, :], sm[:, n:n + 1], None, ALU.mult))
                dve.wait_ge(V.sem, V.n)
                at["val"] = link(dve, V, nc.vector.tensor_copy(val[:, :, 1, :], val[:, :, 0, :]))

            @block.tensor
            def _(pe):
                pe.wait_ge(V.sem, at["val"])
                for n in range(N):
                    for i, t in enumerate((ixf, val)):
                        last = nc.tensor.transpose(ps[:, i, n * P:(n + 1) * P], t[:, n, :, :].rearrange("p a b -> p (a b)"),
                                                   c["ident"][:, :])
                at["turned"] = T(last)

            @block.vector
            def _(dve):
                dve.wait_ge(T.sem, at["turned"])
                for h in range(2):
                    part = slice(h * CAP, (h + 1) * CAP)
                    for i, t in enumerate((keep["slot_ix"], keep["slot_w"])):
                        v = ps[part, i, 0:N * P].rearrange("p (b e a) -> p b e a", b=B, a=2)
                        V(nc.vector.tensor_copy(t[part, :, :], v[:, :, :, h]))
                    v = ps[part, 0, 0:N * P].rearrange("p (b a e) -> p e b a", a=2, e=E3)
                    V(nc.vector.tensor_copy(keep["row_f"][part, :, :], v[:, :, :, h]))
                dve.wait_ge(V.sem, V.n)
                dve.wait_ge(keep["base_sem"].sem, 1)
                link(dve, V, nc.vector.tensor_tensor(keep["row_f"][:, :, :], keep["row_f"][:, :, :],
                                                     keep["base"][:, :].unsqueeze(1).broadcast_to([P, E3, B // 2]), ALU.add))
                V(nc.vector.tensor_copy(keep["row_ix"][:, :, :], keep["row_f"][:, :, :]))

            @block.gpsimd
            def _(pool):
                n = keep["iota_sem"]
                for h in range(2):
                    link(pool, n, nc.gpsimd.iota(keep["base_i"][h * CAP:(h + 1) * CAP, :], pattern=[[2 * S, B // 2]],
                                                 base=h * S, channel_multiplier=0))
                link(pool, n, nc.gpsimd.iota(keep["iota_i"][:, :], pattern=[[1, S]], base=0, channel_multiplier=0))
                link(pool, keep["base_sem"], nc.gpsimd.tensor_copy(keep["base"][:, :], keep["base_i"][:, :]))
                link(pool, n, nc.gpsimd.tensor_copy(keep["iota"][:, :], keep["iota_i"][:, :]))
        keep["ph"].clear()
        ph.clear()


def keep_slots(nc, ctx):
    ph = Phase(nc, ctx, "keep")
    I32 = mybir.dt.int32
    return dict(ph=ph, iota_sem=ph.counter("iota_done"), base_sem=ph.counter("base_done"),
                slot_ix=ph.sb("slot_ix", [P, B, E3 // 2]), slot_w=ph.sb("slot_w", [P, B, E3 // 2]),
                row_f=ph.sb("row_f", [P, E3, B // 2]), row_ix=ph.sb("row_ix", [P, E3, B // 2], U32),
                base_i=ph.sb("base_i", [P, B // 2], I32), base=ph.sb("base", [P, B // 2]),
                iota_i=ph.sb("iota_i", [P, S], I32), iota=ph.sb("iota", [P, S]))


EU = 4


def phase_d(nc, c, d, keep, count=E3 // EU):
    with ExitStack() as ctx:
        ph = Phase(nc, ctx, "d")
        ps = ph.psum()
        ident = c["ident"]
        NT = B * CAP
        NP = NT // P
        NH = NT // 512
        w1, w2 = ph.sb("w1", [P, 2, KD, D3]), ph.sb("w2", [P, 2, KD, D3])
        w3 = ph.sb("w3", [P, 2, DK3, DM])
        rix = ph.sb("rix", [P, EU, NP], U32)
        xg = ph.sb("xg", [P, 2, NP, DM])
        xT = ph.sb("xT", [P, 2, KD, NT])
        gate = ph.sb("gate", [P, 2, 512])
        hT = ph.sb("hT", [P, 2, DK3, NT])
        eo = ph.sb("eo", [P, 2, NP, DM])
        w_in = [ph.counter(f"w_in{j}") for j in range(EU)]
        x_in = [ph.counter(f"x_in{j}_{n}") for j in range(2) for n in range(NP)]
        ph.pool_dma = x_in
        V, T, stored = ph.counter("vector_done"), ph.counter("tensor_done"), ph.counter("stored")
        (turned_made, turned, gate_made, value_made, gated, hidden_done, out_made, out_done) = (ph.counter(n) for n in (
            "turned_made", "turned", "gate_made", "value_made", "gated", "hidden_done", "out_made", "out_done"))
        with nc.Fori(0, count) as g:
            with nc.Block() as block:
                @block.sync
                def _(sp):
                    def weights(j):
                        if j >= 2:
                            sp.wait_ge(out_made.sem, (j - 1) * NP)
                        for t, n in ((w1, "w1_3"), (w2, "w2_3"), (w3, "w3_3")):
                            w_in[j](sp.dma_start(t[:, j % 2, :, :], d[n][g * EU + j].rearrange("(k p) e -> p k e", p=P)), 16)

                    weights(0)
                    weights(1)
                    for j in range(EU):
                        if 1 <= j < EU - 1:
                            weights(j + 1)
                        for h in range(2):
                            sp.wait_ge(out_done.sem, j * NP + NP // 2 * (h + 1))
                            half = slice(NP // 2 * h, NP // 2 * (h + 1))
                            for a in range(2):
                                dst = d["eo3"][a::2, g * EU + j, :, :].rearrange("n c e -> c n e")[:, half, :]
                                stored(sp.dma_start(dst, eo[a * CAP:(a + 1) * CAP, j % 2, half, :]), 16)
                    sp.wait_ge(stored.sem, 64 * EU)

                @block.vector
                def _(dve):
                    V(nc.vector.tensor_copy(rix[:, :, :], keep["row_ix"][:, bass.ds(g * EU, EU), :]))

                @block.gpsimd
                def _(pool):
                    pool.wait_ge(V.sem, 1)
                    for j in range(EU):
                        if j >= 2:
                            pool.wait_ge(turned_made.sem, (j - 1) * NP * KD // 4)
                        for n in range(NP):
                            x_in[j % 2 * NP + n](nc.gpsimd.indirect_dma_start(
                                xg[:, j % 2, n, :], None, d["xn3"].rearrange("b s e -> (b s) e"),
                                bass.IndirectOffsetOnAxis(ap=rix[:, j, n:n + 1], axis=0)), 16)
                    for s in x_in:
                        pool.wait_ge(s.sem, 16 * (EU // 2))

                def turn(pe, j):
                    for n in range(NP * KD // 4):
                        k, n0 = n % KD, n // KD * 4
                        if j * NP * KD // 4 + n >= 2:
                            pe.wait_ge(turned.sem, j * NP * KD // 4 + n - 1)
                        for i in range(4):
                            if k == 0:
                                pe.wait_ge(x_in[j % 2 * NP + n0 + i].sem, 16 * (j // 2 + 1))
                            last = nc.tensor.transpose(ps[:, n % 2, i * P:(i + 1) * P], xg[:, j % 2, n0 + i, k * P:(k + 1) * P], ident[:, :])
                        turned_made(last)

                @block.tensor
                def _(pe):
                    turn(pe, 0)
                    for j in range(EU):
                        pe.wait_ge(w_in[j].sem, 48)
                        pe.wait_ge(turned.sem, (j + 1) * NP * KD // 4)
                        for m in range(DK3 * NH):
                            h, f = m // DK3, m % DK3
                            i = j * DK3 * NH + m
                            if i >= 2:
                                pe.wait_ge(hidden_done.sem, i - 1)
                            for w, bank, made in ((w1, 2, gate_made), (w2, 4, value_made)):
                                for k in range(KD):
                                    last = nc.tensor.matmul(ps[:, bank + i % 2, :], w[:, j % 2, k, f * P:(f + 1) * P],
                                                            xT[:, j % 2, k, h * 512:(h + 1) * 512], start=k == 0, stop=k == KD - 1)
                                made(last)
                        if j + 1 < EU:
                            turn(pe, j + 1)
                        for n in range(NP):
                            i = j * NP + n
                            pe.wait_ge(hidden_done.sem, j * DK3 * NH + DK3 * (n // (NP // NH) + 1))
                            if i >= 2:
                                pe.wait_ge(out_done.sem, i - 1)
                            for k in range(DK3):
                                last = nc.tensor.matmul(ps[:, 6 + i % 2, 0:DM], hT[:, j % 2, k, n * P:(n + 1) * P], w3[:, j % 2, k, :],
                                                        start=k == 0, stop=k == DK3 - 1)
                            out_made(last)

                def copy_turned(dve, j):
                    for n in range(NP * KD // 4):
                        k, n0 = n % KD, n // KD * 4
                        dve.wait_ge(turned_made.sem, j * NP * KD // 4 + n + 1)
                        turned(nc.vector.tensor_copy(xT[:, j % 2, k, n0 * P:(n0 + 4) * P], ps[:, n % 2, :]))

                @block.scalar
                def _(act):
                    for i in range(EU * DK3 * NH):
                        act.wait_ge(gate_made.sem, i + 1)
                        if i >= 2:
                            act.wait_ge(hidden_done.sem, i - 1)
                        gated(nc.scalar.activation(gate[:, i % 2, :], ps[:, 2 + i % 2, :], ACT.Silu))

                @block.vector
                def _(dve):
                    copy_turned(dve, 0)
                    for j in range(EU):
                        for m in range(DK3 * NH):
                            h, f = m // DK3, m % DK3
                            i = j * DK3 * NH + m
                            dve.wait_ge(gated.sem, i + 1)
                            dve.wait_ge(value_made.sem, i + 1)
                            hidden_done(nc.vector.tensor_tensor(hT[:, j % 2, f, h * 512:(h + 1) * 512], gate[:, i % 2, :],
                                                                ps[:, 4 + i % 2, :], ALU.mult))
                        if j + 1 < EU:
                            copy_turned(dve, j + 1)
                        for n in range(NP):
                            i = j * NP + n
                            if j >= 2 and n == 0:
                                dve.wait_ge(stored.sem, 64 * (j - 1))
                            dve.wait_ge(out_made.sem, i + 1)
                            out_done(nc.vector.tensor_copy(eo[:, j % 2, n, :], ps[:, 6 + i % 2, 0:DM]))
            ph.clear()


def phase_e(nc, c, d, keep, count=B):
    with ExitStack() as ctx:
        ph = Phase(nc, ctx, "e")
        ps = ph.psum()
        EP = E3 // 2
        V, A, T, G = (ph.counter(n) for n in ("vector_done", "scalar_done", "tensor_done", "pool_done"))

        def sequence(job):
            i, j = job.slot, job.j
            x, s3, g = (ph.sb(f"{n}_{i}", [P, Q, DM]) for n in ("x", "s3", "g"))
            eo = ph.sb(f"eo_{i}", [P, EP, DM])
            ix, w = ph.sb(f"ix_{i}", [P, EP]), ph.sb(f"w_{i}", [P, EP])
            sel = ph.sb(f"sel_{i}", [P, EP, S])
            x_in, eo_in, stored = (ph.counter(f"{n}{j}") for n in ("x_in", "eo_in", "stored"))
            yield
            block, b, at = job.block, job.b, {}
            b0 = 2 * i
            job.wait_for_buffers(block.sync, block.vector)

            @block.sync
            def _(sp):
                for a in range(2):
                    eo_in(sp.dma_start(eo[a * CAP:(a + 1) * CAP, :, :],
                                       d["eo3"][b].rearrange("(n a) c e -> a c n e", a=2)[a]), 16)
                x_in(sp.dma_start(x[:, :, :], d["x3"][b].rearrange("(q p) e -> p q e", p=P)), 16)
                x_in(sp.dma_start(s3[:, :, :], d["s3"][b].rearrange("(q p) e -> p q e", p=P)), 16)

            @block.vector
            def _(dve):
                V(nc.vector.tensor_copy(ix[:, :], keep["slot_ix"][:, bass.ds(b, 1), :]))
                link(dve, V, nc.vector.tensor_copy(w[:, :], keep["slot_w"][:, bass.ds(b, 1), :]))
                for e in range(EP):
                    V(nc.vector.tensor_scalar(sel[:, e, :], keep["iota"][:, :], ix[:, e:e + 1], w[:, e:e + 1],
                                              ALU.is_equal, ALU.mult))
                at["sel"] = V.n

            yield
            yield
            yield
            job.wait_for_buffers(block.tensor, block.scalar, block.gpsimd)

            @block.tensor
            def _(pe):
                pe.wait_ge(eo_in.sem, 32)
                pe.wait_ge(V.sem, at["sel"])
                for q in range(Q):
                    for e in range(EP):
                        last = nc.tensor.matmul(ps[:, b0 + q // 2, q % 2 * DM:(q % 2 + 1) * DM], sel[:, e, q * P:(q + 1) * P],
                                                eo[:, e, :], start=e == 0, stop=e == EP - 1)
                at["ffn"] = T(last)

            @block.scalar
            def _(act):
                act.wait_ge(T.sem, at["ffn"])
                at["g"] = A(nc.scalar.activation(g[:, :, :], ps[:, b0:b0 + 2, :], ACT.Silu))

            yield

            @block.gpsimd
            def _(pool):
                pool.wait_ge(A.sem, at["g"])
                pool.wait_ge(x_in.sem, 32)
                link(pool, G, nc.gpsimd.tensor_tensor(g[:, :, :], g[:, :, :], s3[:, :, :], ALU.mult))
                at["out"] = G(nc.gpsimd.tensor_tensor(x[:, :, :], x[:, :, :], g[:, :, :], ALU.add))

            yield

            @block.sync
            def _(sp):
                sp.wait_ge(G.sem, at["out"])
                stored(sp.dma_start(d["out"][b].rearrange("(q p) e -> p q e", p=P), x[:, :, :]), 16)

            yield

            @block.sync
            def _(sp):
                sp.wait_ge(stored.sem, 16)
            job.done = [(c.sem, c.n) for c in (V, A, T, G, stored)]

        loop = run_sequences(nc, ph, sequence, count, min(count, 8), LAG_E, SLOTS_E)
        next(loop)
        next(loop, None)



def _same(a):
    return a


def _T(a):
    return a.T


def _columns(a):
    return a.reshape(*a.shape[:-1], -1, P).swapaxes(-1, -2)


INPUTS = {
    "x": ("L0_attn_x", _same),
    "w_in": ("L0_attn_in_proj_w", _T), "w_conv": ("L0_attn_conv_w", _same), "b_conv": ("L0_attn_conv_b", _columns),
    "w_x": ("L0_attn_x_proj_w", _T), "skip": ("L0_attn_D", _columns), "w_out": ("L0_attn_out_proj_w", _T),
    "a_log": ("L0_attn_A_log", _same),
    "w_gate0": ("L0_ffn_gate_w", _T), "b_gate0": ("L0_ffn_gate_b", _same),
    "w1_0": ("L0_ffn_w1", _same), "w2_0": ("L0_ffn_w2", _same),
    "w_qkv": ("L1_attn_w_qkv", _T), "w_proj": ("L1_attn_w_proj", _T), "b_proj": ("L1_attn_b_proj", _same),
    "lambda_q1": ("L1_attn_lambda_q1", _same), "lambda_k1": ("L1_attn_lambda_k1", _same),
    "lambda_q2": ("L1_attn_lambda_q2", _same), "lambda_k2": ("L1_attn_lambda_k2", _same),
    "sub_norm_w": ("L1_attn_sub_norm_w", _same),
    "ln_scale": ("L1_ffn_ln_scale", _columns), "ln_bias": ("L1_ffn_ln_bias", _columns),
    "attn_w": ("L1_ffn_attn_w", _T), "attn_b": ("L1_ffn_attn_b", _columns),
    "w1_1": ("L1_ffn_w1", _same), "b1_1": ("L1_ffn_b1", _columns), "w2_1": ("L1_ffn_w2", _same),
    "b2_1": ("L1_ffn_b2", _columns), "next_w": ("L1_ffn_next_w", _T), "next_b": ("L1_ffn_next_b", _same),
    "wv": ("L2_attn_wv", _T), "bv": ("L2_attn_bv", _same), "wo": ("L2_attn_wo", _T), "bo": ("L2_attn_bo", _same),
    "w3d": ("L2_attn_w3d", _T), "b3d": ("L2_attn_b3d", _same),
    "gate_w2": ("L2_ffn_gate_weight", _T), "gate_b2": ("L2_ffn_gate_bias", _same),
    "up2": ("L2_ffn_up_weights", lambda a: a.reshape(E2 * I2, DM).T),
    "down2": ("L2_ffn_down_weights", lambda a: a.transpose(2, 0, 1)),
    "sup2": ("L2_ffn_shared_up_weight", _T), "sdown2": ("L2_ffn_shared_down_weight", _T),
    "W_in": ("L3_attn_W_in", _T), "W_out": ("L3_attn_W_out", _T),
    "frequencies": ("L3_attn_frequencies", _same), "log_decay": ("L3_attn_log_decay", _same),
    "router_w1": ("L3_ffn_router_w1", _same), "router_w2": ("L3_ffn_router_w2", _same),
    "w1_3": ("L3_ffn_w1", _same), "w2_3": ("L3_ffn_w2", _same), "w3_3": ("L3_ffn_w3", _same),
}
SCRATCH = {
    "s0": ((B, S, DM), F32), "picked": ((B, E0, S), F32), "o0": ((B, E0, DM), F32),
    "qk_parts": ((B, 2, SPLIT, 2 * P, S), BF16), "v1": ((B, S, DM), F32),
    "x1": ((B, S, DM), F32), "xn1": ((B, S, DM), F32), "s1": ((B, S, DM), F32),
    "x2": ((B, S, DM), F32), "x3": ((B, S, DM), F32),
    "xn3": ((B, S, DM), F32), "s3": ((B, S, DM), F32), "probs3": ((B, E3, S), F32), "eo3": ((B, E3, CAP, DM), F32),
}


def program(nc, d):
    with ExitStack() as ctx:
        c = make_constants(nc, ctx)
        with ExitStack() as layer0:
            mergedT = layer0.enter_context(nc.sbuf_tensor("mergedT", [P, KD, E0, B], F32))
            phase_a(nc, c, d, mergedT)
            phase_b(nc, c, d, mergedT)
        phase_c1a(nc, c, d)
        phase_c1b(nc, c, d)
        phase_c2(nc, c, d)
        phase_c3(nc, c, d)
        keep = keep_slots(nc, ctx)
        phase_c4(nc, c, d)
        phase_r(nc, c, d, keep)
        phase_d(nc, c, d, keep)
        phase_e(nc, c, d, keep)


def kernel(**inputs):
    import numpy as _np
    import concourse.bacc as _bacc
    from concourse import mybir as _mybir
    from concourse.bass_utils import run_bass_kernel_spmd as _run

    nc = _bacc.Bacc("TRN2", target_bir_lowering=False, num_devices=1)
    arrays, d = {}, {}
    for name, (source, lay) in INPUTS.items():
        a = _np.ascontiguousarray(lay(_np.asarray(inputs[source])))
        arrays[f"in_{name}"] = a
        d[name] = nc.dram_tensor(f"in_{name}", a.shape, _mybir.dt.from_np(a.dtype), kind="ExternalInput").ap()
    for name, (shape, dt) in SCRATCH.items():
        d[name] = nc.dram_tensor(f"scratch_{name}", shape, dt, kind="Internal").ap()
    d["out"] = nc.dram_tensor("out", (B, S, DM), F32, kind="ExternalOutput").ap()
    program(nc, d)
    r = _run(nc, [arrays], core_ids=[0])
    return r.results[0]["out"]
```
